# Optimizing a Trainium2 kernel written in Bass

```python
import numpy as np
import jax
import jax.numpy as jnp

def _softmax(x, axis=-1):
    return jax.nn.softmax(x, axis=axis)

def _gelu(x):
    return jax.nn.gelu(x, approximate=True)

def _silu(x):
    return jax.nn.silu(x)

def _sigmoid(x):
    return jax.nn.sigmoid(x)

def _layernorm(x, axis=-1, eps=1e-05):
    m = jnp.mean(x, axis=axis, keepdims=True)
    v = jnp.var(x, axis=axis, keepdims=True)
    return (x - m) / jnp.sqrt(v + eps)

def _scatter_add(tgt, idx, src, axis=0):
    return tgt.at[idx].add(src)

def _segment_sum(src, seg, n):
    return jax.ops.segment_sum(src, seg, n)
kernel_name = 'mk_xattn_ffn_d4_seqx_r8_132787'

def setup_inputs(seed: int=0):
    np.random.seed(seed)
    _w = jnp.asarray

    def _rec_inputs():
        import jax
        import jax.numpy as jnp
        _rk = jax.random.key(seed)
        x = 6.313e-05 + 0.9998 * jax.random.normal(jax.random.fold_in(_rk, 1), (2, 512, 128), jnp.float32)
        _lenS = 512 - jax.random.randint(jax.random.fold_in(_rk, 7), (2,), 0, max(1, 512 // 4) + 1, jnp.int32)
        _lenS2 = 77 - jax.random.randint(jax.random.fold_in(_rk, 8), (2,), 0, max(1, 77 // 4) + 1, jnp.int32)
        _ctx_1024P = jax.random.normal(jax.random.fold_in(_rk, 11), (2, 16, 128), jnp.float32)
        _ctx_1024c = jax.random.dirichlet(jax.random.fold_in(_rk, 511), 0.3 * jnp.ones((16,), jnp.float32), (2, 77))
        _ctx_1024t = jnp.einsum('bsk,bkd->bsd', _ctx_1024c, _ctx_1024P)
        _ctx_1024t = _ctx_1024t * jax.lax.rsqrt(jnp.mean(jnp.square(_ctx_1024t)) + 1e-12) * 0.953939
        ctx_1024 = -0.000214406 + 1.00034 * (_ctx_1024t + 0.3 * jax.random.normal(jax.random.fold_in(_rk, 611), (2, 77, 128), jnp.float32))
        _validS = jnp.arange(512)[None, :] < _lenS[:, None]
        _validS2 = jnp.arange(77)[None, :] < _lenS2[:, None]
        _causal = jnp.tril(jnp.ones((512, 512), dtype=bool))
        mask_1x1xSxS2_ik0 = jnp.where(jnp.broadcast_to(_validS2[0:1, None, None, :], (1, 1, 512, 77)), 0, 1).astype(jnp.int32)
        mask_1x1xSxS2_fk1 = jnp.where(jnp.broadcast_to(_validS2[0:1, None, None, :], (1, 1, 512, 77)), 1.0, 0.0).astype(jnp.float32)
        mask_BxS2_bk0 = jnp.logical_not(jnp.broadcast_to(_validS2[:, :], (2, 77)))
        return (x, ctx_1024, mask_1x1xSxS2_ik0, mask_1x1xSxS2_fk1, mask_BxS2_bk0)
    x, ctx_1024, mask_1x1xSxS2_ik0, mask_1x1xSxS2_fk1, mask_BxS2_bk0 = _rec_inputs()

    def _L0_xattn_setup():
        import jax, jax.numpy as jnp
        import numpy as np
        from jax import lax
        BIG = jnp.float32(1e+30)

        def _pairwise_euclidean(a, b):
            aa = jnp.sum(a * a, axis=-1)[:, None]
            bb = jnp.sum(b * b, axis=-1)[None, :]
            ab = a @ b.T
            return jnp.sqrt(jnp.maximum(aa + bb - 2.0 * ab, 0.0))

        def _dtw_cost(D):
            row0 = jnp.cumsum(D[0])

            def row_step(prev_row, d_row):
                first = d_row[0] + prev_row[0]

                def col_step(left, inp):
                    d_ij, up, diag = inp
                    r = d_ij + jnp.minimum(jnp.minimum(up, left), diag)
                    return (r, r)
                _, rest = lax.scan(col_step, first, (d_row[1:], prev_row[1:], prev_row[:-1]))
                row = jnp.concatenate([first[None], rest])
                return (row, row)
            _, rows = lax.scan(row_step, row0, D[1:])
            return jnp.concatenate([row0[None], rows], axis=0)

        def _backtrack(R, T1, T2):
            L = T1 + T2 - 1

            def step(carry, _):
                i, j, done = carry
                valid = jnp.logical_not(done)
                cd = jnp.where((i > 0) & (j > 0), R[jnp.maximum(i - 1, 0), jnp.maximum(j - 1, 0)], BIG)
                cu = jnp.where(i > 0, R[jnp.maximum(i - 1, 0), j], BIG)
                cl = jnp.where(j > 0, R[i, jnp.maximum(j - 1, 0)], BIG)
                choice = jnp.argmin(jnp.stack([cd, cu, cl]))
                ni = jnp.where(choice <= 1, i - 1, i)
                nj = jnp.where((choice == 0) | (choice == 2), j - 1, j)
                at_origin = (i == 0) & (j == 0)
                ni = jnp.where(at_origin, 0, ni)
                nj = jnp.where(at_origin, 0, nj)
                return ((ni, nj, done | at_origin), (i, j, valid))
            init = (jnp.int32(T1 - 1), jnp.int32(T2 - 1), jnp.bool_(False))
            _, (i_idx, j_idx, valid) = lax.scan(step, init, None, length=L)
            return (i_idx, j_idx, valid)

        def _align_one(small, large):
            T_small, d = small.shape
            T_large = large.shape[0]
            D = _pairwise_euclidean(small, large)
            R = _dtw_cost(D)
            i_idx, j_idx, valid = _backtrack(R, T_small, T_large)
            contrib = small[i_idx] * valid[:, None].astype(small.dtype)
            expanded = jnp.zeros((T_large, d), dtype=small.dtype).at[j_idx].add(contrib)
            return expanded
        key = jax.random.key(seed)
        k1, k2 = jax.random.split(key)
        teacher = jax.random.normal(k1, (16, 50, 128), dtype=jnp.float32)
        student = jax.random.normal(k2, (16, 75, 128), dtype=jnp.float32)
        return {'teacher_features': teacher, 'student_features': student}
    _L0_xattn_all = _L0_xattn_setup()
    _L0_xattn_in = {k: v for k, v in _L0_xattn_all.items() if k in ()}
    del _L0_xattn_all

    def _L0_ffn_setup():
        import jax, jax.numpy as jnp
        import numpy as np
        BLOCK = 32
        W_BITS = 4
        ACT_BITS = 16

        def act_qdq(x):
            qmax = 2.0 ** (ACT_BITS - 1) - 1.0
            scale = jnp.maximum(jnp.max(jnp.abs(x)) / qmax, 1e-12)
            return jnp.clip(jnp.round(x / scale), -qmax - 1.0, qmax) * scale

        def fixed_qdq_u16(x):
            scale = 1.0 / 65536.0
            return jnp.clip(jnp.round(x / scale), 0.0, 65535.0) * scale

        def lpbq_dequant(w):
            O, I = w.shape
            qmax = 2.0 ** (W_BITS - 1) - 1.0
            wb = w.reshape(O, I // BLOCK, BLOCK)
            s = jnp.maximum(jnp.max(jnp.abs(wb), axis=-1, keepdims=True) / qmax, 1e-12)
            wq = jnp.clip(jnp.round(wb / s), -qmax - 1.0, qmax) * s
            return wq.reshape(O, I)
        key = jax.random.key(seed)
        k1, k2, k3, k4 = jax.random.split(key, 4)
        B, S, H, I = (2, 512, 128, 384)
        x = jax.random.normal(k1, (B, S, H), jnp.float32)
        w_gate = jax.random.normal(k2, (I, H), jnp.float32) * 0.02
        w_up = jax.random.normal(k3, (I, H), jnp.float32) * 0.02
        w_down = jax.random.normal(k4, (H, I), jnp.float32) * 0.02
        return {'x': x, 'w_gate': w_gate, 'w_up': w_up, 'w_down': w_down}
    _L0_ffn_all = _L0_ffn_setup()
    _L0_ffn_in = {k: v for k, v in _L0_ffn_all.items() if k in ('w_gate', 'w_up', 'w_down')}
    del _L0_ffn_all

    def _L1_xattn_setup():
        import jax, jax.numpy as jnp
        import numpy as np
        D_MODEL = 128
        NUM_HEADS = 16
        D_K = D_MODEL // NUM_HEADS
        B, S = (4, 256)
        key = jax.random.key(seed)
        ks = jax.random.split(key, 12)
        scale = 1.0 / np.sqrt(D_MODEL)
        inp = {'query': jax.random.normal(ks[0], (B, S, D_MODEL), jnp.float32), 'key': jax.random.normal(ks[1], (B, S, D_MODEL), jnp.float32), 'value': jax.random.normal(ks[2], (B, S, D_MODEL), jnp.float32), 'mask': jnp.tril(jnp.ones((S, S), jnp.int32))[None, None, :, :], 'Wq': jax.random.normal(ks[3], (D_MODEL, D_MODEL), jnp.float32) * scale, 'bq': jnp.zeros((D_MODEL,), jnp.float32), 'Wk': jax.random.normal(ks[4], (D_MODEL, D_MODEL), jnp.float32) * scale, 'bk': jnp.zeros((D_MODEL,), jnp.float32), 'Wv': jax.random.normal(ks[5], (D_MODEL, D_MODEL), jnp.float32) * scale, 'bv': jnp.zeros((D_MODEL,), jnp.float32), 'Wo': jax.random.normal(ks[6], (D_MODEL, D_MODEL), jnp.float32) * scale, 'bo': jnp.zeros((D_MODEL,), jnp.float32)}
        return inp
    _L1_xattn_all = _L1_xattn_setup()
    _L1_xattn_in = {k: v for k, v in _L1_xattn_all.items() if k in ('Wq', 'bq', 'Wk', 'bk', 'Wv', 'bv', 'Wo', 'bo')}
    del _L1_xattn_all

    def _L1_ffn_setup():
        import jax, jax.numpy as jnp
        import numpy as np
        S_LEN, BATCH, HIDDEN = (256, 2, 128)
        N_HEADS, N_KV = (16, 8)
        N_EXP, TOP_K, CAP_F = (8, 2, 1.25)
        FFN = 512
        HEAD_DIM = HIDDEN // N_HEADS
        Q_PER_KV = N_HEADS // N_KV
        EPS = 1e-05
        NEG = -1000000000.0

        def _ln(x, w, b):
            mu = jnp.mean(x, -1, keepdims=True)
            var = jnp.var(x, -1, keepdims=True)
            return (x - mu) * jax.lax.rsqrt(var + EPS) * w + b

        def _forward(hidden_states, ln1_weight, ln1_bias, ln2_weight, ln2_bias, qkv_weight, proj_weight, router_weight, moe_w1, moe_w2):
            S, B, H = hidden_states.shape
            ln1 = _ln(hidden_states, ln1_weight, ln1_bias)
            qkv = (ln1 @ qkv_weight.T).reshape(S, B, N_KV, (Q_PER_KV + 2) * HEAD_DIM)
            q_dim = Q_PER_KV * HEAD_DIM
            q = qkv[..., :q_dim].reshape(S, B, N_HEADS, HEAD_DIM)
            k = jnp.repeat(qkv[..., q_dim:q_dim + HEAD_DIM], Q_PER_KV, axis=2)
            v = jnp.repeat(qkv[..., q_dim + HEAD_DIM:], Q_PER_KV, axis=2)
            scores = jnp.einsum('sbhd,tbhd->bhst', q, k) / jnp.sqrt(jnp.float32(HEAD_DIM))
            causal = jnp.tril(jnp.ones((S, S), bool))
            attn = jax.nn.softmax(jnp.where(causal[None, None], scores, NEG), axis=-1)
            attn_out = jnp.einsum('bhst,tbhd->sbhd', attn, v).reshape(S, B, H)
            hidden_after_attn = hidden_states + attn_out @ proj_weight.T
            x = _ln(hidden_after_attn, ln2_weight, ln2_bias).reshape(-1, H)
            N = S * B
            probs = jax.nn.softmax(x.astype(jnp.float32) @ router_weight, axis=-1)
            top_p, top_i = jax.lax.top_k(probs, TOP_K)
            top_p = top_p / jnp.sum(top_p, -1, keepdims=True)
            flat_exp = top_i.reshape(-1)
            order = jnp.argsort(flat_exp)
            sorted_exp = flat_exp[order]
            counts = jnp.bincount(sorted_exp, length=N_EXP)
            offsets = jnp.concatenate([jnp.zeros((1,), counts.dtype), jnp.cumsum(counts)])
            within = jnp.arange(N * TOP_K) - offsets[sorted_exp]
            cap = int(np.ceil(N * TOP_K / N_EXP * CAP_F))
            keep = within < cap
            slot = jnp.where(keep, sorted_exp * cap + within, N_EXP * cap)
            tok_id = order // TOP_K
            padded_tokens = jnp.zeros((N_EXP * cap + 1, H), x.dtype).at[slot].set(x[tok_id])[:-1]
            padded_probs = jnp.zeros((N_EXP * cap + 1,), jnp.float32).at[slot].set(top_p.reshape(-1)[order])[:-1]
            padded_ids = jnp.zeros((N_EXP * cap + 1,), jnp.int32).at[slot].set(tok_id.astype(jnp.int32))[:-1]
            exp_in = padded_tokens.reshape(N_EXP, cap, H)
            act = jax.nn.gelu(jnp.einsum('ech,ehf->ecf', exp_in, moe_w1), approximate=False)
            exp_out = jnp.einsum('ecf,efh->ech', act, moe_w2).reshape(N_EXP * cap, H)
            weighted = exp_out * padded_probs[:, None].astype(exp_out.dtype)
            moe = jnp.zeros((N, H), exp_out.dtype).at[padded_ids].add(weighted)
            return hidden_after_attn + moe.reshape(S, B, H)
        ks = jax.random.split(jax.random.key(seed), 6)
        qkv_out = N_KV * (Q_PER_KV + 2) * HEAD_DIM
        sc = 0.02
        return {'hidden_states': jax.random.normal(ks[0], (S_LEN, BATCH, HIDDEN), jnp.float32), 'ln1_weight': jnp.ones((HIDDEN,), jnp.float32), 'ln1_bias': jnp.zeros((HIDDEN,), jnp.float32), 'ln2_weight': jnp.ones((HIDDEN,), jnp.float32), 'ln2_bias': jnp.zeros((HIDDEN,), jnp.float32), 'qkv_weight': jax.random.normal(ks[1], (qkv_out, HIDDEN), jnp.float32) * sc, 'proj_weight': jax.random.normal(ks[2], (HIDDEN, HIDDEN), jnp.float32) * sc, 'router_weight': jax.random.normal(ks[3], (HIDDEN, N_EXP), jnp.float32) * sc, 'moe_w1': jax.random.normal(ks[4], (N_EXP, HIDDEN, FFN), jnp.float32) * sc, 'moe_w2': jax.random.normal(ks[5], (N_EXP, FFN, HIDDEN), jnp.float32) * sc}
    _L1_ffn_all = _L1_ffn_setup()
    _L1_ffn_in = {k: v for k, v in _L1_ffn_all.items() if k in ('ln1_weight', 'ln1_bias', 'ln2_weight', 'ln2_bias', 'qkv_weight', 'proj_weight', 'router_weight', 'moe_w1', 'moe_w2')}
    del _L1_ffn_all

    def _L2_xattn_setup():
        import jax, jax.numpy as jnp
        import numpy as np
        B, S, D, H = (4, 256, 128, 16)
        DK = D // H

        def _split_heads(x):
            b, s, _ = x.shape
            return x.reshape(b, s, H, DK).transpose(0, 2, 1, 3)
        key = jax.random.key(seed)
        ks = jax.random.split(key, 11)
        inp = {'query': jax.random.normal(ks[0], (B, S, D), dtype=jnp.float32), 'key': jax.random.normal(ks[1], (B, S, D), dtype=jnp.float32), 'value': jax.random.normal(ks[2], (B, S, D), dtype=jnp.float32), 'mask': jnp.triu(jnp.ones((S, S), dtype=jnp.float32), k=1)[None, None, :, :]}
        scale = 0.02
        inp['Wq'] = jax.random.normal(ks[3], (D, D), dtype=jnp.float32) * scale
        inp['bq'] = jnp.zeros((D,), dtype=jnp.float32)
        inp['Wk'] = jax.random.normal(ks[4], (D, D), dtype=jnp.float32) * scale
        inp['bk'] = jnp.zeros((D,), dtype=jnp.float32)
        inp['Wv'] = jax.random.normal(ks[5], (D, D), dtype=jnp.float32) * scale
        inp['bv'] = jnp.zeros((D,), dtype=jnp.float32)
        inp['Wo'] = jax.random.normal(ks[6], (D, D), dtype=jnp.float32) * scale
        inp['bo'] = jnp.zeros((D,), dtype=jnp.float32)
        return inp
    _L2_xattn_all = _L2_xattn_setup()
    _L2_xattn_in = {k: v for k, v in _L2_xattn_all.items() if k in ('Wq', 'bq', 'Wk', 'bk', 'Wv', 'bv', 'Wo', 'bo')}
    del _L2_xattn_all

    def _L2_ffn_setup():
        import jax, jax.numpy as jnp
        import numpy as np
        DIM = 128
        DEPTH = 6
        HEADS = 16
        DIM_HEAD = 64
        WINDOW = 32
        INNER = HEADS * DIM_HEAD
        DIM_INNER = int(DIM * 4 * 2 / 3)
        QK_SCALE = 8.0

        def shift_tokens(t):
            a, s = jnp.split(t, 2, -1)
            s = jnp.pad(s, ((0, 0), (1, 0), (0, 0)))[:, :-1]
            return jnp.concatenate([a, s], -1)

        def l2norm(t):
            return t / jnp.maximum(jnp.linalg.norm(t, axis=-1, keepdims=True), 1e-12)

        def rotate_half(x):
            x1, x2 = jnp.split(x, 2, -1)
            return jnp.concatenate([-x2, x1], -1)

        def rotary_tables(n):
            half = jnp.arange(0, DIM_HEAD, 2, dtype=jnp.float32)
            inv_freq = 1.0 / 10000.0 ** (half / DIM_HEAD)
            t = jnp.arange(n, dtype=jnp.float32)
            freqs = t[:, None] * inv_freq[None, :]
            freqs = jnp.concatenate([freqs, freqs], -1)
            base_scale = (half + 0.4 * DIM_HEAD) / (1.4 * DIM_HEAD)
            power = (t - n // 2) / (WINDOW // 2)
            scale = base_scale[None, :] ** power[:, None]
            scale = jnp.concatenate([scale, scale], -1)
            return (freqs, scale)

        def local_attention(q, k, v):
            b, h, n, d = q.shape
            w = WINDOW
            nw = n // w
            bq = q.reshape(b, h, nw, w, d)
            bk = k.reshape(b, h, nw, w, d)
            bv = v.reshape(b, h, nw, w, d)

            def look(t):
                p = jnp.pad(t, ((0, 0), (0, 0), (1, 0), (0, 0), (0, 0)))
                return jnp.concatenate([p[:, :, :nw], p[:, :, 1:]], axis=3)
            bk2, bv2 = (look(bk), look(bv))
            seq = jnp.arange(n).reshape(nw, w)
            seq_p = jnp.pad(seq, ((1, 0), (0, 0)), constant_values=-1)
            jt = jnp.concatenate([seq_p[:nw], seq_p[1:]], axis=1)
            it = seq[:, :, None]
            jb = jt[:, None, :]
            mask = (it < jb) | (it > jb + w) | (jb == -1)
            sim = jnp.einsum('bhwie,bhwje->bhwij', bq, bk2) * QK_SCALE
            sim = jnp.where(mask, -jnp.finfo(sim.dtype).max, sim)
            attn = jax.nn.softmax(sim, -1)
            out = jnp.einsum('bhwij,bhwje->bhwie', attn, bv2)
            return out.reshape(b, h, n, d)

        def attn_layer(x, Wqkv, qs, ksc, Wo):
            b, n, _ = x.shape
            qkv = x @ Wqkv
            q, k, v = jnp.split(qkv, 3, -1)
            sh = lambda t: t.reshape(b, n, HEADS, DIM_HEAD).transpose(0, 2, 1, 3)
            q, k, v = (sh(q), sh(k), sh(v))
            q = l2norm(q) * qs
            k = l2norm(k) * ksc
            freqs, scale = rotary_tables(n)
            cos, sin = (jnp.cos(freqs), jnp.sin(freqs))
            q = q * cos * scale + rotate_half(q) * sin * scale
            inv = 1.0 / scale
            k = k * cos * inv + rotate_half(k) * sin * inv
            out = local_attention(q, k, v)
            out = out.transpose(0, 2, 1, 3).reshape(b, n, INNER)
            return out @ Wo

        def ffn_layer(x, g, bln, W1, b1, W2, b2):
            mu = x.mean(-1, keepdims=True)
            var = ((x - mu) ** 2).mean(-1, keepdims=True)
            xn = (x - mu) / jnp.sqrt(var + 1e-05) * g + bln
            hg = xn @ W1 + b1
            a, gate = jnp.split(hg, 2, -1)
            return a * jax.nn.gelu(gate, approximate=False) @ W2 + b2
        key = jax.random.key(seed)
        ks = jax.random.split(key, 8)
        B, N = (2, 256)
        init = lambda k, shape: jax.random.normal(k, shape, jnp.float32) * 0.02
        return {'x': jax.random.normal(ks[0], (B, N, DIM), jnp.float32), 'Wqkv': init(ks[1], (DEPTH, DIM, 3 * INNER)), 'q_scale': jnp.ones((DEPTH, DIM_HEAD), jnp.float32), 'k_scale': jnp.ones((DEPTH, DIM_HEAD), jnp.float32), 'Wo': init(ks[2], (DEPTH, INNER, DIM)), 'ln_g': jnp.ones((DEPTH, DIM), jnp.float32), 'ln_b': jnp.zeros((DEPTH, DIM), jnp.float32), 'W1': init(ks[3], (DEPTH, DIM, 2 * DIM_INNER)), 'b1': jnp.zeros((DEPTH, 2 * DIM_INNER), jnp.float32), 'W2': init(ks[4], (DEPTH, DIM_INNER, DIM)), 'b2': jnp.zeros((DEPTH, DIM), jnp.float32)}
    _L2_ffn_all = _L2_ffn_setup()
    _L2_ffn_in = {k: v for k, v in _L2_ffn_all.items() if k in ('Wqkv', 'q_scale', 'k_scale', 'Wo', 'ln_g', 'ln_b', 'W1', 'b1', 'W2', 'b2')}
    del _L2_ffn_all

    def _L3_xattn_setup():
        import jax, jax.numpy as jnp
        import numpy as np
        EPS = 1e-05

        def layer_norm(x, g, b):
            mu = jnp.mean(x, axis=-1, keepdims=True)
            var = jnp.mean((x - mu) ** 2, axis=-1, keepdims=True)
            return (x - mu) * jax.lax.rsqrt(var + EPS) * g + b
        key = jax.random.key(seed)
        ks = jax.random.split(key, 8)
        b, n, l, D = (8, 512, 64, 128)
        heads, dim_head = (16, 64)
        inner = heads * dim_head
        x = jax.random.normal(ks[0], (b, n, D), dtype=jnp.float32)
        latents = jax.random.normal(ks[1], (b, l, D), dtype=jnp.float32)
        mask = jax.random.randint(ks[2], (b, n), 0, 2) > 0
        Wq = jax.random.normal(ks[3], (D, inner), dtype=jnp.float32) * D ** (-0.5)
        Wkv = jax.random.normal(ks[4], (D, 2 * inner), dtype=jnp.float32) * D ** (-0.5)
        Wout = jax.random.normal(ks[5], (inner, D), dtype=jnp.float32) * inner ** (-0.5)
        g1 = jnp.ones((D,), jnp.float32)
        b1 = jnp.zeros((D,), jnp.float32)
        g2 = jnp.ones((D,), jnp.float32)
        b2 = jnp.zeros((D,), jnp.float32)
        return {'x': x, 'latents': latents, 'mask': mask, 'g1': g1, 'b1': b1, 'g2': g2, 'b2': b2, 'Wq': Wq, 'Wkv': Wkv, 'Wout': Wout}
    _L3_xattn_all = _L3_xattn_setup()
    _L3_xattn_in = {k: v for k, v in _L3_xattn_all.items() if k in ('g1', 'b1', 'g2', 'b2', 'Wq', 'Wkv', 'Wout')}
    del _L3_xattn_all

    def _L3_ffn_setup():
        import jax, jax.numpy as jnp
        import numpy as np
        E = 8
        K = 2
        D = 128
        H = 4 * D
        EPS = 1e-05
        TEMP = 1.5
        key = jax.random.key(seed)
        ks = jax.random.split(key, 6)
        B, T = (2, 256)
        x = jax.random.normal(ks[0], (B, T, D), dtype=jnp.float32)
        gamma = jnp.ones((D,), dtype=jnp.float32)
        beta = jnp.zeros((D,), dtype=jnp.float32)
        router_w = jax.random.normal(ks[1], (E, D), dtype=jnp.float32) * 0.02
        W1 = jax.random.normal(ks[2], (E, D, H), dtype=jnp.float32) * 0.02
        W2 = jax.random.normal(ks[3], (E, H, D), dtype=jnp.float32) * 0.02
        return {'x': x, 'gamma': gamma, 'beta': beta, 'router_w': router_w, 'W1': W1, 'W2': W2}
    _L3_ffn_all = _L3_ffn_setup()
    _L3_ffn_in = {k: v for k, v in _L3_ffn_all.items() if k in ('gamma', 'beta', 'router_w', 'W1', 'W2')}
    del _L3_ffn_all
    return {'x': x, 'ctx_1024': ctx_1024, 'mask_1x1xSxS2_ik0': mask_1x1xSxS2_ik0, 'mask_1x1xSxS2_fk1': mask_1x1xSxS2_fk1, 'mask_BxS2_bk0': mask_BxS2_bk0, 'L0_ffn_w_gate': _L0_ffn_in['w_gate'], 'L0_ffn_w_up': _L0_ffn_in['w_up'], 'L0_ffn_w_down': _L0_ffn_in['w_down'], 'L1_xattn_Wq': _L1_xattn_in['Wq'], 'L1_xattn_bq': _L1_xattn_in['bq'], 'L1_xattn_Wk': _L1_xattn_in['Wk'], 'L1_xattn_bk': _L1_xattn_in['bk'], 'L1_xattn_Wv': _L1_xattn_in['Wv'], 'L1_xattn_bv': _L1_xattn_in['bv'], 'L1_xattn_Wo': _L1_xattn_in['Wo'], 'L1_xattn_bo': _L1_xattn_in['bo'], 'L1_ffn_ln1_weight': _L1_ffn_in['ln1_weight'], 'L1_ffn_ln1_bias': _L1_ffn_in['ln1_bias'], 'L1_ffn_ln2_weight': _L1_ffn_in['ln2_weight'], 'L1_ffn_ln2_bias': _L1_ffn_in['ln2_bias'], 'L1_ffn_qkv_weight': _L1_ffn_in['qkv_weight'], 'L1_ffn_proj_weight': _L1_ffn_in['proj_weight'], 'L1_ffn_router_weight': _L1_ffn_in['router_weight'], 'L1_ffn_moe_w1': _L1_ffn_in['moe_w1'], 'L1_ffn_moe_w2': _L1_ffn_in['moe_w2'], 'L2_xattn_Wq': _L2_xattn_in['Wq'], 'L2_xattn_bq': _L2_xattn_in['bq'], 'L2_xattn_Wk': _L2_xattn_in['Wk'], 'L2_xattn_bk': _L2_xattn_in['bk'], 'L2_xattn_Wv': _L2_xattn_in['Wv'], 'L2_xattn_bv': _L2_xattn_in['bv'], 'L2_xattn_Wo': _L2_xattn_in['Wo'], 'L2_xattn_bo': _L2_xattn_in['bo'], 'L2_ffn_Wqkv': _L2_ffn_in['Wqkv'], 'L2_ffn_q_scale': _L2_ffn_in['q_scale'], 'L2_ffn_k_scale': _L2_ffn_in['k_scale'], 'L2_ffn_Wo': _L2_ffn_in['Wo'], 'L2_ffn_ln_g': _L2_ffn_in['ln_g'], 'L2_ffn_ln_b': _L2_ffn_in['ln_b'], 'L2_ffn_W1': _L2_ffn_in['W1'], 'L2_ffn_b1': _L2_ffn_in['b1'], 'L2_ffn_W2': _L2_ffn_in['W2'], 'L2_ffn_b2': _L2_ffn_in['b2'], 'L3_xattn_g1': _L3_xattn_in['g1'], 'L3_xattn_b1': _L3_xattn_in['b1'], 'L3_xattn_g2': _L3_xattn_in['g2'], 'L3_xattn_b2': _L3_xattn_in['b2'], 'L3_xattn_Wq': _L3_xattn_in['Wq'], 'L3_xattn_Wkv': _L3_xattn_in['Wkv'], 'L3_xattn_Wout': _L3_xattn_in['Wout'], 'L3_ffn_gamma': _L3_ffn_in['gamma'], 'L3_ffn_beta': _L3_ffn_in['beta'], 'L3_ffn_router_w': _L3_ffn_in['router_w'], 'L3_ffn_W1': _L3_ffn_in['W1'], 'L3_ffn_W2': _L3_ffn_in['W2']}

def reference(x, ctx_1024, mask_1x1xSxS2_ik0, mask_1x1xSxS2_fk1, mask_BxS2_bk0, L0_ffn_w_gate, L0_ffn_w_up, L0_ffn_w_down, L1_xattn_Wq, L1_xattn_bq, L1_xattn_Wk, L1_xattn_bk, L1_xattn_Wv, L1_xattn_bv, L1_xattn_Wo, L1_xattn_bo, L1_ffn_ln1_weight, L1_ffn_ln1_bias, L1_ffn_ln2_weight, L1_ffn_ln2_bias, L1_ffn_qkv_weight, L1_ffn_proj_weight, L1_ffn_router_weight, L1_ffn_moe_w1, L1_ffn_moe_w2, L2_xattn_Wq, L2_xattn_bq, L2_xattn_Wk, L2_xattn_bk, L2_xattn_Wv, L2_xattn_bv, L2_xattn_Wo, L2_xattn_bo, L2_ffn_Wqkv, L2_ffn_q_scale, L2_ffn_k_scale, L2_ffn_Wo, L2_ffn_ln_g, L2_ffn_ln_b, L2_ffn_W1, L2_ffn_b1, L2_ffn_W2, L2_ffn_b2, L3_xattn_g1, L3_xattn_b1, L3_xattn_g2, L3_xattn_b2, L3_xattn_Wq, L3_xattn_Wkv, L3_xattn_Wout, L3_ffn_gamma, L3_ffn_beta, L3_ffn_router_w, L3_ffn_W1, L3_ffn_W2):
    import jax
    import jax.numpy as jnp

    def _L0_xattn_ref(teacher_features, student_features):
        import jax, jax.numpy as jnp
        import numpy as np
        from jax import lax
        BIG = jnp.float32(1e+30)

        def _pairwise_euclidean(a, b):
            aa = jnp.sum(a * a, axis=-1)[:, None]
            bb = jnp.sum(b * b, axis=-1)[None, :]
            ab = a @ b.T
            return jnp.sqrt(jnp.maximum(aa + bb - 2.0 * ab, 0.0))

        def _dtw_cost(D):
            row0 = jnp.cumsum(D[0])

            def row_step(prev_row, d_row):
                first = d_row[0] + prev_row[0]

                def col_step(left, inp):
                    d_ij, up, diag = inp
                    r = d_ij + jnp.minimum(jnp.minimum(up, left), diag)
                    return (r, r)
                _, rest = lax.scan(col_step, first, (d_row[1:], prev_row[1:], prev_row[:-1]))
                row = jnp.concatenate([first[None], rest])
                return (row, row)
            _, rows = lax.scan(row_step, row0, D[1:])
            return jnp.concatenate([row0[None], rows], axis=0)

        def _backtrack(R, T1, T2):
            L = T1 + T2 - 1

            def step(carry, _):
                i, j, done = carry
                valid = jnp.logical_not(done)
                cd = jnp.where((i > 0) & (j > 0), R[jnp.maximum(i - 1, 0), jnp.maximum(j - 1, 0)], BIG)
                cu = jnp.where(i > 0, R[jnp.maximum(i - 1, 0), j], BIG)
                cl = jnp.where(j > 0, R[i, jnp.maximum(j - 1, 0)], BIG)
                choice = jnp.argmin(jnp.stack([cd, cu, cl]))
                ni = jnp.where(choice <= 1, i - 1, i)
                nj = jnp.where((choice == 0) | (choice == 2), j - 1, j)
                at_origin = (i == 0) & (j == 0)
                ni = jnp.where(at_origin, 0, ni)
                nj = jnp.where(at_origin, 0, nj)
                return ((ni, nj, done | at_origin), (i, j, valid))
            init = (jnp.int32(T1 - 1), jnp.int32(T2 - 1), jnp.bool_(False))
            _, (i_idx, j_idx, valid) = lax.scan(step, init, None, length=L)
            return (i_idx, j_idx, valid)

        def _align_one(small, large):
            T_small, d = small.shape
            T_large = large.shape[0]
            D = _pairwise_euclidean(small, large)
            R = _dtw_cost(D)
            i_idx, j_idx, valid = _backtrack(R, T_small, T_large)
            contrib = small[i_idx] * valid[:, None].astype(small.dtype)
            expanded = jnp.zeros((T_large, d), dtype=small.dtype).at[j_idx].add(contrib)
            return expanded
        return jax.vmap(_align_one)(teacher_features, student_features)

    def _L0_ffn_ref(x, w_gate, w_up, w_down):
        import jax, jax.numpy as jnp
        import numpy as np
        BLOCK = 32
        W_BITS = 4
        ACT_BITS = 16

        def act_qdq(x):
            qmax = 2.0 ** (ACT_BITS - 1) - 1.0
            scale = jnp.maximum(jnp.max(jnp.abs(x)) / qmax, 1e-12)
            return jnp.clip(jnp.round(x / scale), -qmax - 1.0, qmax) * scale

        def fixed_qdq_u16(x):
            scale = 1.0 / 65536.0
            return jnp.clip(jnp.round(x / scale), 0.0, 65535.0) * scale

        def lpbq_dequant(w):
            O, I = w.shape
            qmax = 2.0 ** (W_BITS - 1) - 1.0
            wb = w.reshape(O, I // BLOCK, BLOCK)
            s = jnp.maximum(jnp.max(jnp.abs(wb), axis=-1, keepdims=True) / qmax, 1e-12)
            wq = jnp.clip(jnp.round(wb / s), -qmax - 1.0, qmax) * s
            return wq.reshape(O, I)
        x = act_qdq(x)
        up = act_qdq(x @ lpbq_dequant(w_up).T)
        gate = act_qdq(x @ lpbq_dequant(w_gate).T)
        sig = fixed_qdq_u16(jax.nn.sigmoid(gate))
        gate = act_qdq(gate * sig)
        o = act_qdq(gate * up)
        return o @ lpbq_dequant(w_down).T

    def _L1_xattn_ref(query, key, value, mask, Wq, bq, Wk, bk, Wv, bv, Wo, bo):
        import jax, jax.numpy as jnp
        import numpy as np
        D_MODEL = 128
        NUM_HEADS = 16
        D_K = D_MODEL // NUM_HEADS
        B, S = (4, 256)
        b = query.shape[0]
        Q = query @ Wq.T + bq
        K = key @ Wk.T + bk
        V = value @ Wv.T + bv

        def split_heads(x):
            return x.reshape(b, -1, NUM_HEADS, D_K).transpose(0, 2, 1, 3)
        Q, K, V = (split_heads(Q), split_heads(K), split_heads(V))
        scores = jnp.einsum('bhqd,bhkd->bhqk', Q, K) / jnp.sqrt(jnp.float32(D_K))
        scores = jnp.where(mask == 0, jnp.float32(-jnp.inf), scores)
        attn = jax.nn.softmax(scores, axis=-1)
        x = jnp.einsum('bhqk,bhkd->bhqd', attn, V)
        x = x.transpose(0, 2, 1, 3).reshape(b, -1, D_MODEL)
        return x @ Wo.T + bo

    def _L1_ffn_ref(hidden_states, ln1_weight, ln1_bias, ln2_weight, ln2_bias, qkv_weight, proj_weight, router_weight, moe_w1, moe_w2):
        import jax, jax.numpy as jnp
        import numpy as np
        S_LEN, BATCH, HIDDEN = (256, 2, 128)
        N_HEADS, N_KV = (16, 8)
        N_EXP, TOP_K, CAP_F = (8, 2, 1.25)
        FFN = 512
        HEAD_DIM = HIDDEN // N_HEADS
        Q_PER_KV = N_HEADS // N_KV
        EPS = 1e-05
        NEG = -1000000000.0

        def _ln(x, w, b):
            mu = jnp.mean(x, -1, keepdims=True)
            var = jnp.var(x, -1, keepdims=True)
            return (x - mu) * jax.lax.rsqrt(var + EPS) * w + b

        def _forward(hidden_states, ln1_weight, ln1_bias, ln2_weight, ln2_bias, qkv_weight, proj_weight, router_weight, moe_w1, moe_w2):
            S, B, H = hidden_states.shape
            ln1 = _ln(hidden_states, ln1_weight, ln1_bias)
            qkv = (ln1 @ qkv_weight.T).reshape(S, B, N_KV, (Q_PER_KV + 2) * HEAD_DIM)
            q_dim = Q_PER_KV * HEAD_DIM
            q = qkv[..., :q_dim].reshape(S, B, N_HEADS, HEAD_DIM)
            k = jnp.repeat(qkv[..., q_dim:q_dim + HEAD_DIM], Q_PER_KV, axis=2)
            v = jnp.repeat(qkv[..., q_dim + HEAD_DIM:], Q_PER_KV, axis=2)
            scores = jnp.einsum('sbhd,tbhd->bhst', q, k) / jnp.sqrt(jnp.float32(HEAD_DIM))
            causal = jnp.tril(jnp.ones((S, S), bool))
            attn = jax.nn.softmax(jnp.where(causal[None, None], scores, NEG), axis=-1)
            attn_out = jnp.einsum('bhst,tbhd->sbhd', attn, v).reshape(S, B, H)
            hidden_after_attn = hidden_states + attn_out @ proj_weight.T
            x = _ln(hidden_after_attn, ln2_weight, ln2_bias).reshape(-1, H)
            N = S * B
            probs = jax.nn.softmax(x.astype(jnp.float32) @ router_weight, axis=-1)
            top_p, top_i = jax.lax.top_k(probs, TOP_K)
            top_p = top_p / jnp.sum(top_p, -1, keepdims=True)
            flat_exp = top_i.reshape(-1)
            order = jnp.argsort(flat_exp)
            sorted_exp = flat_exp[order]
            counts = jnp.bincount(sorted_exp, length=N_EXP)
            offsets = jnp.concatenate([jnp.zeros((1,), counts.dtype), jnp.cumsum(counts)])
            within = jnp.arange(N * TOP_K) - offsets[sorted_exp]
            cap = int(np.ceil(N * TOP_K / N_EXP * CAP_F))
            keep = within < cap
            slot = jnp.where(keep, sorted_exp * cap + within, N_EXP * cap)
            tok_id = order // TOP_K
            padded_tokens = jnp.zeros((N_EXP * cap + 1, H), x.dtype).at[slot].set(x[tok_id])[:-1]
            padded_probs = jnp.zeros((N_EXP * cap + 1,), jnp.float32).at[slot].set(top_p.reshape(-1)[order])[:-1]
            padded_ids = jnp.zeros((N_EXP * cap + 1,), jnp.int32).at[slot].set(tok_id.astype(jnp.int32))[:-1]
            exp_in = padded_tokens.reshape(N_EXP, cap, H)
            act = jax.nn.gelu(jnp.einsum('ech,ehf->ecf', exp_in, moe_w1), approximate=False)
            exp_out = jnp.einsum('ecf,efh->ech', act, moe_w2).reshape(N_EXP * cap, H)
            weighted = exp_out * padded_probs[:, None].astype(exp_out.dtype)
            moe = jnp.zeros((N, H), exp_out.dtype).at[padded_ids].add(weighted)
            return hidden_after_attn + moe.reshape(S, B, H)
        return _forward(hidden_states, ln1_weight, ln1_bias, ln2_weight, ln2_bias, qkv_weight, proj_weight, router_weight, moe_w1, moe_w2)

    def _L2_xattn_ref(query, key, value, mask, Wq, bq, Wk, bk, Wv, bv, Wo, bo):
        import jax, jax.numpy as jnp
        import numpy as np
        B, S, D, H = (4, 256, 128, 16)
        DK = D // H

        def _split_heads(x):
            b, s, _ = x.shape
            return x.reshape(b, s, H, DK).transpose(0, 2, 1, 3)
        q = _split_heads(query @ Wq + bq)
        k = _split_heads(key @ Wk + bk)
        v = _split_heads(value @ Wv + bv)
        scale = 1.0 / jnp.sqrt(jnp.asarray(DK, dtype=q.dtype))
        scores = jnp.einsum('bhqd,bhkd->bhqk', q, k) * scale
        scores = scores + mask * -1000000000.0
        attn = jax.nn.softmax(scores, axis=-1)
        x = jnp.einsum('bhqk,bhkd->bhqd', attn, v)
        x = x.transpose(0, 2, 1, 3).reshape(query.shape[0], -1, D)
        return x @ Wo + bo

    def _L2_ffn_ref(x, Wqkv, q_scale, k_scale, Wo, ln_g, ln_b, W1, b1, W2, b2):
        import jax, jax.numpy as jnp
        import numpy as np
        DIM = 128
        DEPTH = 6
        HEADS = 16
        DIM_HEAD = 64
        WINDOW = 32
        INNER = HEADS * DIM_HEAD
        DIM_INNER = int(DIM * 4 * 2 / 3)
        QK_SCALE = 8.0

        def shift_tokens(t):
            a, s = jnp.split(t, 2, -1)
            s = jnp.pad(s, ((0, 0), (1, 0), (0, 0)))[:, :-1]
            return jnp.concatenate([a, s], -1)

        def l2norm(t):
            return t / jnp.maximum(jnp.linalg.norm(t, axis=-1, keepdims=True), 1e-12)

        def rotate_half(x):
            x1, x2 = jnp.split(x, 2, -1)
            return jnp.concatenate([-x2, x1], -1)

        def rotary_tables(n):
            half = jnp.arange(0, DIM_HEAD, 2, dtype=jnp.float32)
            inv_freq = 1.0 / 10000.0 ** (half / DIM_HEAD)
            t = jnp.arange(n, dtype=jnp.float32)
            freqs = t[:, None] * inv_freq[None, :]
            freqs = jnp.concatenate([freqs, freqs], -1)
            base_scale = (half + 0.4 * DIM_HEAD) / (1.4 * DIM_HEAD)
            power = (t - n // 2) / (WINDOW // 2)
            scale = base_scale[None, :] ** power[:, None]
            scale = jnp.concatenate([scale, scale], -1)
            return (freqs, scale)

        def local_attention(q, k, v):
            b, h, n, d = q.shape
            w = WINDOW
            nw = n // w
            bq = q.reshape(b, h, nw, w, d)
            bk = k.reshape(b, h, nw, w, d)
            bv = v.reshape(b, h, nw, w, d)

            def look(t):
                p = jnp.pad(t, ((0, 0), (0, 0), (1, 0), (0, 0), (0, 0)))
                return jnp.concatenate([p[:, :, :nw], p[:, :, 1:]], axis=3)
            bk2, bv2 = (look(bk), look(bv))
            seq = jnp.arange(n).reshape(nw, w)
            seq_p = jnp.pad(seq, ((1, 0), (0, 0)), constant_values=-1)
            jt = jnp.concatenate([seq_p[:nw], seq_p[1:]], axis=1)
            it = seq[:, :, None]
            jb = jt[:, None, :]
            mask = (it < jb) | (it > jb + w) | (jb == -1)
            sim = jnp.einsum('bhwie,bhwje->bhwij', bq, bk2) * QK_SCALE
            sim = jnp.where(mask, -jnp.finfo(sim.dtype).max, sim)
            attn = jax.nn.softmax(sim, -1)
            out = jnp.einsum('bhwij,bhwje->bhwie', attn, bv2)
            return out.reshape(b, h, n, d)

        def attn_layer(x, Wqkv, qs, ksc, Wo):
            b, n, _ = x.shape
            qkv = x @ Wqkv
            q, k, v = jnp.split(qkv, 3, -1)
            sh = lambda t: t.reshape(b, n, HEADS, DIM_HEAD).transpose(0, 2, 1, 3)
            q, k, v = (sh(q), sh(k), sh(v))
            q = l2norm(q) * qs
            k = l2norm(k) * ksc
            freqs, scale = rotary_tables(n)
            cos, sin = (jnp.cos(freqs), jnp.sin(freqs))
            q = q * cos * scale + rotate_half(q) * sin * scale
            inv = 1.0 / scale
            k = k * cos * inv + rotate_half(k) * sin * inv
            out = local_attention(q, k, v)
            out = out.transpose(0, 2, 1, 3).reshape(b, n, INNER)
            return out @ Wo

        def ffn_layer(x, g, bln, W1, b1, W2, b2):
            mu = x.mean(-1, keepdims=True)
            var = ((x - mu) ** 2).mean(-1, keepdims=True)
            xn = (x - mu) / jnp.sqrt(var + 1e-05) * g + bln
            hg = xn @ W1 + b1
            a, gate = jnp.split(hg, 2, -1)
            return a * jax.nn.gelu(gate, approximate=False) @ W2 + b2
        for i in range(DEPTH):
            x = attn_layer(shift_tokens(x), Wqkv[i], q_scale[i], k_scale[i], Wo[i]) + x
            x = ffn_layer(shift_tokens(x), ln_g[i], ln_b[i], W1[i], b1[i], W2[i], b2[i]) + x
        return x

    def _L3_xattn_ref(x, latents, mask, g1, b1, g2, b2, Wq, Wkv, Wout):
        import jax, jax.numpy as jnp
        import numpy as np
        EPS = 1e-05

        def layer_norm(x, g, b):
            mu = jnp.mean(x, axis=-1, keepdims=True)
            var = jnp.mean((x - mu) ** 2, axis=-1, keepdims=True)
            return (x - mu) * jax.lax.rsqrt(var + EPS) * g + b
        heads, dim_head = (16, 64)
        b, n, D = x.shape
        l = latents.shape[1]
        xn = layer_norm(x, g1, b1)
        ln_lat = layer_norm(latents, g2, b2)
        q = ln_lat @ Wq
        kv = jnp.concatenate([xn, ln_lat], axis=1) @ Wkv
        k, v = jnp.split(kv, 2, axis=-1)

        def to_heads(t):
            return t.reshape(t.shape[0], t.shape[1], heads, dim_head).transpose(0, 2, 1, 3)
        q, k, v = (to_heads(q), to_heads(k), to_heads(v))
        scale = 1.0 / np.sqrt(np.sqrt(dim_head)).astype(np.float32)
        weight = jnp.einsum('bhld,bhnd->bhln', q * scale, k * scale)
        full_mask = jnp.concatenate([mask, jnp.ones((b, l), dtype=bool)], axis=1)
        neg = -jnp.finfo(weight.dtype).max
        weight = jnp.where(full_mask[:, None, None, :], weight, neg)
        weight = jax.nn.softmax(weight.astype(jnp.float32), axis=-1).astype(q.dtype)
        out = jnp.einsum('bhln,bhnd->bhld', weight, v)
        out = out.transpose(0, 2, 1, 3).reshape(b, l, heads * dim_head)
        return out @ Wout

    def _L3_ffn_ref(x, gamma, beta, router_w, W1, W2):
        import jax, jax.numpy as jnp
        import numpy as np
        E = 8
        K = 2
        D = 128
        H = 4 * D
        EPS = 1e-05
        TEMP = 1.5
        res = x
        mu = jnp.mean(x, axis=-1, keepdims=True)
        var = jnp.mean(jnp.square(x - mu), axis=-1, keepdims=True)
        xn = (x - mu) * jax.lax.rsqrt(var + EPS) * gamma + beta
        logits = jnp.einsum('btd,ed->bte', xn, router_w)
        probs = jax.nn.softmax(logits / TEMP, axis=-1)
        w, idx = jax.lax.top_k(probs, K)
        wdense = jnp.sum(jax.nn.one_hot(idx, E, dtype=w.dtype) * w[..., None], axis=-2)
        h = jax.nn.silu(jnp.einsum('btd,edf->betf', xn, W1))
        y = jnp.einsum('betf,efd->betd', h, W2)
        out = jnp.einsum('bte,betd->btd', wdense, y)
        return out + res
    x = x + _L0_xattn_ref(ctx_1024, _layernorm(x, axis=-1))
    x = x + _L0_ffn_ref(_layernorm(x, axis=-1), L0_ffn_w_gate, L0_ffn_w_up, L0_ffn_w_down)
    x = x + _L1_xattn_ref(_layernorm(x, axis=-1), ctx_1024, ctx_1024, mask_1x1xSxS2_ik0, L1_xattn_Wq, L1_xattn_bq, L1_xattn_Wk, L1_xattn_bk, L1_xattn_Wv, L1_xattn_bv, L1_xattn_Wo, L1_xattn_bo)
    x = x + _L1_ffn_ref(_layernorm(x, axis=-1), L1_ffn_ln1_weight, L1_ffn_ln1_bias, L1_ffn_ln2_weight, L1_ffn_ln2_bias, L1_ffn_qkv_weight, L1_ffn_proj_weight, L1_ffn_router_weight, L1_ffn_moe_w1, L1_ffn_moe_w2)
    x = x + _L2_xattn_ref(_layernorm(x, axis=-1), ctx_1024, ctx_1024, mask_1x1xSxS2_fk1, L2_xattn_Wq, L2_xattn_bq, L2_xattn_Wk, L2_xattn_bk, L2_xattn_Wv, L2_xattn_bv, L2_xattn_Wo, L2_xattn_bo)
    x = x + _L2_ffn_ref(_layernorm(x, axis=-1), L2_ffn_Wqkv, L2_ffn_q_scale, L2_ffn_k_scale, L2_ffn_Wo, L2_ffn_ln_g, L2_ffn_ln_b, L2_ffn_W1, L2_ffn_b1, L2_ffn_W2, L2_ffn_b2)
    x = x + _L3_xattn_ref(ctx_1024, _layernorm(x, axis=-1), mask_BxS2_bk0, L3_xattn_g1, L3_xattn_b1, L3_xattn_g2, L3_xattn_b2, L3_xattn_Wq, L3_xattn_Wkv, L3_xattn_Wout)
    x = x + _L3_ffn_ref(_layernorm(x, axis=-1), L3_ffn_gamma, L3_ffn_beta, L3_ffn_router_w, L3_ffn_W1, L3_ffn_W2)
    return x

_drawn_inputs = setup_inputs


def setup_inputs(seed=0):
    import zlib

    import numpy as np

    out = dict(_drawn_inputs(seed))
    spreads = {'L1_xattn_bq': (0.0, 0.449),
     'L1_xattn_bk': (0.0, 2.0),
     'L1_xattn_bv': (0.0, 0.1),
     'L1_xattn_bo': (0.0, 0.1),
     'L1_ffn_ln1_weight': (1.0, 0.6),
     'L1_ffn_ln1_bias': (0.0, 0.8),
     'L1_ffn_ln2_weight': (1.0, 0.6),
     'L1_ffn_ln2_bias': (0.0, 0.8),
     'L2_xattn_bq': (0.0, 2.0),
     'L2_xattn_bk': (0.0, 2.0),
     'L2_xattn_bv': (0.0, 0.793),
     'L2_xattn_bo': (0.0, 0.1),
     'L2_ffn_q_scale': (1.0, 0.6),
     'L2_ffn_k_scale': (1.0, 0.6),
     'L2_ffn_ln_g': (1.0, 0.6),
     'L2_ffn_ln_b': (0.0, 0.8),
     'L2_ffn_b1': (0.0, 0.8),
     'L2_ffn_b2': (0.0, 0.442),
     'L3_xattn_g1': (1.0, 0.6),
     'L3_xattn_b1': (0.0, 2.0),
     'L3_xattn_g2': (1.0, 0.6),
     'L3_xattn_b2': (0.0, 1.886),
     'L3_ffn_gamma': (1.0, 0.6),
     'L3_ffn_beta': (0.0, 0.8)}
    factors = {'L0_ffn_w_gate': 7.281,
     'L0_ffn_w_up': 6.887,
     'L0_ffn_w_down': 6.772,
     'L1_ffn_qkv_weight': 2.922,
     'L1_ffn_proj_weight': 2.906,
     'L1_ffn_router_weight': 4.38,
     'L1_ffn_moe_w1': 3.828,
     'L1_ffn_moe_w2': 3.828,
     'L2_xattn_Wq': 8.0,
     'L2_xattn_Wk': 8.0,
     'L2_xattn_Wv': 3.561,
     'L2_xattn_Wo': 2.722,
     'L2_ffn_W1': 6.301,
     'L2_ffn_W2': 6.359,
     'L3_ffn_router_w': 8.0,
     'L3_ffn_W1': 8.0,
     'L3_ffn_W2': 8.0,
     'L3_xattn_Wq': 6.557}
    for name, (base, spread) in spreads.items():
        noise = np.random.default_rng([zlib.crc32(name.encode()), seed]).standard_normal(out[name].shape)
        drawn = base * np.exp(spread * noise) if base else spread * noise
        out[name] = jnp.asarray(drawn.astype(out[name].dtype))
    for name, factor in factors.items():
        out[name] = (out[name] * factor).astype(out[name].dtype)
    return out
```

```python
from contextlib import ExitStack

import numpy as np

import concourse.bass as bass
from concourse import mybir

F32 = mybir.dt.float32
F16 = mybir.dt.float16
BF16 = mybir.dt.bfloat16
I32 = mybir.dt.int32
U8 = mybir.dt.uint8
ALU = mybir.AluOpType
ACT = mybir.ActivationFunctionType
X = mybir.AxisListType.X

PARTS = 8
P = 128
B = 2
S = 512
T = B * S
NT = T // P
KC = 77
H = 16
EPS = 1e-5
BIG = 1e30
NEG = -1e30

SEG = 8
SC = S // SEG
STEPS = KC + SEG - 1
ROWS = SEG + KC + SEG
RING = 12
COPY = 4
assert STEPS % RING == 0 and RING % COPY == 0

DH = P // H
HK = H * KC
HKC = -(-HK // P)
HKP = HKC * P
HGROUPS = ((0, 6), (6, 6), (12, 4))

E = 8
FF = 512
CAP = -(-T * 2 * 5 // (E * 4))
assert CAP == 320

DEPTH = 6
D2 = 64
WIN = 32
INNER = H * D2
FFI = 341
GUESS = float(0x5f3759df - 2 ** 30 - 2 ** 22)


QW = 384
QMAX = 32767.0
MAGIC = 1.5 * 2.0 ** 23


class Tally:

    def __init__(self):
        self.seen = {}

    def __call__(self, who, sem):
        key = (who, sem.name)
        self.seen[key] = self.seen.get(key, 0) + 1
        return self.seen[key]


def build(nc, io):
    ctx = ExitStack()
    n = Tally()

    def sem(name):
        return ctx.enter_context(nc.semaphore(name))

    def sb(name, shape, dt=F32, at=None):
        return (at or ctx).enter_context(nc.sbuf_tensor(name, shape, dt))

    def dram(name, shape, dt=F32):
        return nc.dram_tensor(name, shape, dt, kind="Internal").ap()

    def view(ap, offset, dims):
        return bass.AP(tensor=ap.tensor, offset=offset, ap=dims)

    PS = ctx.enter_context(nc.psum_tensor("PS", [P, 8, 512], F32))

    x = sb("x", [P, B, S])
    xn = sb("xn", [P, B, S])
    xc = sb("xc", [P, B, S])
    sq = sb("sq", [P, B, S])
    rstd = sb("rstd", [16, 2, 64])
    cst = sb("cst", [P, C_ALL])
    vec = sb("vec", [P, V_ALL])
    row = sb("row", [1, R_ALL])
    ctxT = sb("ctxT", [P, B * KC])
    ctxN = sb("ctxN", [KC, B, P])

    def const(name):
        a, w = C_AT[name]
        return cst[:, a:a + w]

    def column(name):
        a = V_AT[name][0]
        return vec[:, a:a + 1]

    ident = const("ident")

    loaded = sem("loaded")
    x_ready = sem("x_ready")
    vec_step = sem("vec_step")
    LOADS = 6

    class Chain:

        def __init__(self, s, who="dve"):
            self.s, self.who = s, who

        def step(self, ins):
            ins.then_inc(self.s, 1)
            self.at = n(self.who, self.s)

        def link(self, eng, ins):
            ins.then_inc(self.s, 1)
            eng.wait_ge(self.s, n(self.who, self.s))

    order = Chain(vec_step)

    class Norm:

        def __init__(self, tag, parts=(0, 1), banks=(6, 7), chain=None):
            self.parts, self.banks, self.chain = parts, banks, chain or order
            self.mean_ready = sem(tag + "_mean_ready")
            self.centred = sem(tag + "_centred")
            self.squared = sem(tag + "_squared")
            self.var_ready = sem(tag + "_var_ready")
            self.std_ready = sem(tag + "_std_ready")
            self.rstd_ready = sem(tag + "_rstd_ready")
            self.spread_ready = sem(tag + "_spread_ready")
            self.normed = sem(tag + "_normed")
            self.uses = {}

        def wait(self, eng, who, halves=2):
            eng.wait_ge(self.normed, 2 * (self.uses[who] - 1) + halves)

        def rows(self, b):
            at = 8 * self.parts.index(b)
            return at, 8 * len(self.parts)

        def pe(self, pe, src, src_ready):
            self.uses["pe"] = self.uses.get("pe", 0) + 1
            for b in self.parts:
                if src_ready is not None:
                    pe.wait_ge(src_ready, n("pe", src_ready))
                pe.matmul(PS[:, self.banks[b], :], const("mean"), src[:, b, :], start=True, stop=True)\
                  .then_inc(self.mean_ready, 1)
            for b in self.parts:
                at, rows = self.rows(b)
                pe.wait_ge(self.squared, n("pe", self.squared))
                for j in range(8):
                    mm = pe.matmul(PS[0:rows, self.banks[self.parts[0]], 0:64],
                                   const("slide")[:, 15 - at - j:15 - at - j + rows],
                                   sq[:, b, 64 * j:64 * j + 64],
                                   start=(at + j == 0), stop=(at + j == rows - 1))
            mm.then_inc(self.var_ready, 1)
            pe.wait_ge(self.rstd_ready, n("pe", self.rstd_ready))
            for b in self.parts:
                at, rows = self.rows(b)
                for j in range(8):
                    mm = pe.matmul(PS[:, self.banks[b], 64 * j:64 * j + 64],
                                   cst[0:rows, at + j:at + j + 1].broadcast_to([rows, P]),
                                   rstd[0:rows, 1, :], start=(j == 0), stop=(j == 7))
                mm.then_inc(self.spread_ready, 1)

        def act(self, act):
            self.uses["act"] = self.uses.get("act", 0) + 1
            for b in self.parts:
                act.wait_ge(self.centred, n("act", self.centred))
                act.activation(sq[:, b, :], xc[:, b, :], ACT.Square).then_inc(self.squared, 1)
            _, rows = self.rows(self.parts[0])
            act.wait_ge(self.var_ready, n("act", self.var_ready))
            act.activation(rstd[0:rows, 0, :], PS[0:rows, self.banks[self.parts[0]], 0:64], ACT.Sqrt,
                           bias=cst[0:rows, C_AT["eps"][0]:C_AT["eps"][0] + 1]).then_inc(self.std_ready, 1)

        def dve(self, dve, src, dst, gamma=None, beta=None):
            self.uses["dve"] = self.uses.get("dve", 0) + 1
            c = self.chain
            for b in self.parts:
                dve.wait_ge(self.mean_ready, n("dve", self.mean_ready))
                dve.tensor_tensor(xc[:, b, :], src[:, b, :], PS[:, self.banks[b], :], ALU.subtract)\
                   .then_inc(self.centred, 1)
            _, rows = self.rows(self.parts[0])
            dve.wait_ge(self.std_ready, n("dve", self.std_ready))
            dve.reciprocal(rstd[0:rows, 1, :], rstd[0:rows, 0, :]).then_inc(self.rstd_ready, 1)
            for b in self.parts:
                dve.wait_ge(self.spread_ready, n("dve", self.spread_ready))
                if gamma is None:
                    dve.tensor_tensor(dst[:, b, :], xc[:, b, :], PS[:, self.banks[b], :], ALU.mult)\
                       .then_inc(self.normed, 1)
                else:
                    c.link(dve, dve.tensor_tensor(xc[:, b, :], xc[:, b, :], PS[:, self.banks[b], :],
                                                  ALU.mult))
                    dve.tensor_scalar(dst[:, b, :], xc[:, b, :], gamma, beta, ALU.mult, ALU.add)\
                       .then_inc(self.normed, 1)

    norm = Norm("ln")

    class Align:
        def __init__(self):
            at = self.stack = ExitStack()
            self.aa = sb("al_aa", [KC, B], at=at)
            self.ctxm2 = sb("al_ctxm2", [P, B * KC], at=at)
            self.dist = sb("al_dist", [KC, B, S], at=at)
            self.big = sb("al_big", [KC, B, S + 1], at=at)
            self.skew = sb("al_skew", [32, STEPS, SC], at=at)
            self.hist = sb("al_hist", [32, STEPS, SC], at=at)
            self.ring = sb("al_ring", [32, RING, SC + 1], at=at)
            self.low = sb("al_low", [32, SC], at=at)
            self.cur = sb("al_cur", [KC, B, S + 1], at=at)
            self.t0 = sb("al_t0", [KC, B, S], at=at)
            self.t1 = sb("al_t1", [KC, B, S], at=at)
            self.keep = sb("al_keep", [KC, B, S], at=at)
            self.enter = sb("al_enter", [KC, B, S], F16, at=at)
            self.left = sb("al_left", [KC, B, S], at=at)
            self.path = sb("al_path", [B, KC, S], F16, at=at)
            self.ent = sb("al_ent", [B, KC], at=at)
            self.entT = sb("al_entT", [KC, B], at=at)
            self.exT = sb("al_exT", [KC, B], at=at)
            self.pick = sb("al_pick", [B, 2, S], at=at)
            self.plane = dram("al_plane", [B, ROWS, S])
            self.costs = dram("al_costs", [B, ROWS, S])
            self.big_set = sem("al_big_set")
            self.pads_out = sem("al_pads_out")
            self.aa_ready = sem("al_aa_ready")
            self.xsq = sem("al_xsq")
            self.prod_ready = sem("al_prod_ready")
            self.d2_ready = sem("al_d2_ready")
            self.dist_ready = sem("al_dist_ready")
            self.plane_out = sem("al_plane_out")
            self.skew_in = sem("al_skew_in")
            self.scan_done = sem("al_scan_done")
            self.shifted = sem("al_shifted")
            self.ctxm2_ready = sem("al_ctxm2_ready")
            self.ring_free = sem("al_ring_free")
            self.costs_out = sem("al_costs_out")
            self.rows_in = sem("al_rows_in")
            self.enter_ready = sem("al_enter_ready")
            self.path_in = sem("al_path_in")
            self.walked = sem("al_walked")
            self.ent_ready = sem("al_ent_ready")
            self.entT_ready = sem("al_entT_ready")
            self.on_ready = sem("al_on_ready")
            self.sum_ready = sem("al_sum_ready")

        def strip(self, plane, b, row0):
            return view(plane, (b * ROWS + 1 + row0) * S + (SEG - 1) * SC,
                        [[S - SC, SEG], [S, STEPS], [1, SC]])

        def pool(self, pool):
            pool.memset(self.big[:, :, :], BIG).then_inc(self.big_set, 1)
            pool.memset(self.skew[:, :, :], BIG).then_inc(self.big_set, 1)
            pool.memset(self.cur[:, :, :], BIG).then_inc(self.big_set, 1)
            pool.memset(self.path[:, :, :], 0.0).then_inc(self.big_set, 1)

        def sp(self, sp):
            sp.wait_ge(self.big_set, 1)
            for b in range(B):
                for r in (0, SEG + KC):
                    sp.dma_start(self.plane[b, r:r + SEG, :], self.big[0:SEG, b, 0:S]).then_inc(self.pads_out, 16)
            for b in range(B):
                sp.wait_ge(self.dist_ready, b + 1)
                sp.dma_start(self.plane[b, SEG:SEG + KC, :], self.dist[:, b, :]).then_inc(self.plane_out, 16)
            sp.wait_ge(self.pads_out, 64)
            sp.wait_ge(self.plane_out, 32)
            sp.wait_ge(self.big_set, 3)
            for b in range(B):
                sp.dma_start(self.skew[SEG * b:SEG * b + SEG, :, :], self.strip(self.plane, b, 0))\
                  .then_inc(self.skew_in, 16)
            sp.wait_ge(self.ring_free, STEPS // COPY + RING // COPY)
            for b in range(B):
                sp.dma_start(self.strip(self.costs, b, 0), self.hist[SEG * b:SEG * b + SEG, :, :])\
                  .then_inc(self.costs_out, 16)
            sp.wait_ge(self.costs_out, 32)
            for b in range(B):
                sp.dma_start(self.cur[:, b, 1:], self.costs[b, SEG:SEG + KC, :]).then_inc(self.rows_in, 16)
                sp.dma_start(self.big[1:KC, b, 1:], self.costs[b, SEG:SEG + KC - 1, :]).then_inc(self.rows_in, 16)
            sp.wait_ge(self.enter_ready, 1)
            sp.wait_ge(self.big_set, 4)
            for b in range(B):
                sp.dma_start(self.path[b:b + 1, :, :], self.enter[:, b, :]).then_inc(self.path_in, 16)

        def act(self, act):
            act.wait_ge(loaded, 16 * LOADS)
            for b in range(B):
                act.activation(self.dist[:, b, 0:P], ctxN[:, b, :], ACT.Square,
                               accum_out=self.aa[:, b:b + 1]).then_inc(self.aa_ready, 1)
            norm.wait(act, "act")
            for b in range(B):
                act.activation(sq[:, b, :], xn[:, b, :], ACT.Square).then_inc(self.xsq, 1)
            for b in range(B):
                act.wait_ge(self.d2_ready, b + 1)
                act.activation(self.dist[:, b, :], self.t0[:, b, :], ACT.Sqrt).then_inc(self.dist_ready, 1)
            act.sem_inc(self.ring_free, RING // COPY)
            with act.Fori(0, STEPS // RING) as i:
                for k in range(RING // COPY):
                    act.wait_ge(self.scan_done, i * RING + COPY * (k + 1) + 1)
                    act.activation(self.hist[:, bass.ds(i * RING + COPY * k, COPY), :],
                                   self.ring[:, COPY * k:COPY * k + COPY, 1:], ACT.Copy)\
                       .then_inc(self.ring_free, 1)

        def pe(self, pe):
            for b in range(B):
                if b == 0:
                    pe.wait_ge(self.ctxm2_ready, 1)
                pe.wait_ge(self.xsq, b + 1)
                pe.matmul(PS[0:KC, b, :], const("one")[:, 0:KC], sq[:, b, :], start=True, stop=False)
                pe.matmul(PS[0:KC, b, :], self.ctxm2[:, KC * b:KC * b + KC], xn[:, b, :],
                          start=False, stop=True).then_inc(self.prod_ready, 1)
            pe.wait_ge(self.ent_ready, 1)
            pe.transpose(PS[0:KC, 2, 0:B], self.ent[:, :], ident[0:B, 0:B]).then_inc(self.entT_ready, 1)
            for b in range(B):
                pe.wait_ge(self.on_ready, b + 1)
                pe.matmul(PS[:, b, :], ctxN[:, b, :], self.t1[:, b, :], start=True, stop=True)\
                  .then_inc(self.sum_ready, 1)

        def dve(self, dve):
            iota = const("iota")
            dve.tensor_scalar(self.ctxm2[:, :], ctxT[:, :], -2.0, None, ALU.mult).then_inc(self.ctxm2_ready, 1)
            dve.wait_ge(self.aa_ready, 2)
            for b in range(B):
                dve.wait_ge(self.prod_ready, b + 1)
                dve.tensor_scalar(self.t0[:, b, :], PS[0:KC, b, :], self.aa[:, b:b + 1], 0.0, ALU.add, ALU.max)\
                   .then_inc(self.d2_ready, 1)
            a = C_AT["rinit"][0]
            dve.wait_ge(self.skew_in, 32)
            dve.tensor_copy(self.ring[:, RING - 1, :], cst[0:32, a:a + SC + 1]).then_inc(self.scan_done, 1)
            shift = [p + 1 if p < 16 and p % SEG < SEG - 1 else 31 for p in range(32)]
            with dve.Fori(0, STEPS // RING) as i:
                for k in range(RING):
                    now, last = self.ring[:, k, :], self.ring[:, (k - 1) % RING, :]
                    if k % COPY == 0:
                        dve.wait_ge(self.ring_free, i * (RING // COPY) + k // COPY + 1)
                    dve.wait_ge(self.scan_done, i * RING + k + 1)
                    dve.tensor_tensor(self.low[:, :], last[:, 1:], last[:, 0:SC], ALU.min)
                    dve.stream_shuffle(now[:, 0:1], last[:, SC:SC + 1], shift).then_inc(self.shifted, 1)
                    dve.wait_ge(self.shifted, i * RING + k + 1)
                    dve.tensor_tensor_scan(now[:, 1:], self.low[:, :],
                                           self.skew[:, bass.ds(i * RING + k, 1), :].rearrange("p a b -> p (a b)"),
                                           now[:, 0:1], ALU.min, ALU.add).then_inc(self.scan_done, 1)
            dve.wait_ge(self.rows_in, 64)
            above, diag, left = self.big[:, :, 1:], self.big[:, :, 0:S], self.cur[:, :, 0:S]
            cols = iota[0:KC, :].unsqueeze(1).broadcast_to([KC, B, S])
            order.step(dve.tensor_tensor(self.t1[:, :, :], diag, above, ALU.is_le))
            order.link(dve, dve.tensor_tensor(self.t0[:, :, :], diag, above, ALU.min))
            order.link(dve, dve.tensor_tensor(self.keep[:, :, :], left, self.t0[:, :, :], ALU.is_ge))
            order.link(dve, dve.tensor_tensor(self.t1[:, :, :], cols, self.t1[:, :, :], ALU.subtract))
            order.step(dve.tensor_tensor(self.t1[:, :, :], self.t1[:, :, :], self.keep[:, :, :], ALU.mult))
            order.link(dve, dve.tensor_tensor(self.t0[:, :, :], cols, self.keep[:, :, :], ALU.mult))
            for b in range(B):
                order.step(dve.tensor_tensor_scan(self.enter[:, b, :], self.t1[:, b, :], self.t1[:, b, :], 0.0,
                                                  ALU.max, ALU.max))
            dve.tensor_tensor_scan(self.left[:, 0, :], self.t0[:, 0, :], self.t0[:, 0, :], 0.0,
                                   ALU.max, ALU.max).then_inc(self.enter_ready, 1)
            dve.tensor_tensor_scan(self.left[:, 1, :], self.t0[:, 1, :], self.t0[:, 1, :], 0.0,
                                   ALU.max, ALU.max).then_inc(self.enter_ready, 1)
            dve.wait_ge(self.path_in, 32)
            dve.memset(self.ent[:, KC - 1:KC], float(S - 1)).then_inc(self.walked, 1)
            with dve.Fori(0, (KC - 1) // 4) as i:
                for k in range(4):
                    at = dve.snap(i * -4 + (KC - 1 - k))
                    dve.wait_ge(self.walked, i * 4 + k + 1)
                    dve.scalar_tensor_tensor(
                        self.pick[:, k % 2, :], iota[0:B, :], self.ent[:, bass.ds(at, 1)],
                        self.path[:, bass.ds(at, 1), :].rearrange("p a b -> p (a b)"), ALU.is_equal, ALU.mult,
                        accum_out=self.ent[:, bass.ds(at - 1, 1)]).then_inc(self.walked, 1)
            dve.wait_ge(self.walked, KC)
            dve.sem_inc(self.ent_ready, 1)
            dve.wait_ge(self.entT_ready, 1)
            order.link(dve, dve.tensor_copy(self.entT[:, :], PS[0:KC, 2, 0:B]))
            for b in range(B):
                order.link(dve, dve.scalar_tensor_tensor(
                    self.keep[:, b, :], iota[0:KC, :], self.entT[:, b:b + 1], self.left[:, b, :],
                    ALU.is_equal, ALU.mult, accum_out=self.exT[:, b:b + 1]))
                order.link(dve, dve.tensor_scalar(self.t0[:, b, :], iota[0:KC, :], self.entT[:, b:b + 1], None,
                                                  ALU.is_le))
                dve.scalar_tensor_tensor(self.t1[:, b, :], iota[0:KC, :], self.exT[:, b:b + 1], self.t0[:, b, :],
                                         ALU.is_ge, ALU.mult).then_inc(self.on_ready, 1)
            for b in range(B):
                dve.wait_ge(self.sum_ready, b + 1)
                dve.tensor_tensor(x[:, b, :], x[:, b, :], PS[:, b, :], ALU.add).then_inc(x_ready, 1)

    class Quantised:
        QF = 384
        CH = QF // P

        def __init__(self):
            CH = self.CH
            at = self.stack = ExitStack()
            self.wraw = sb("q_wraw", [P, 3, QW], at=at)
            self.wmax = sb("q_wmax", [P, 3, QW // 32], at=at)
            self.winv = sb("q_winv", [P, 3, QW // 32], at=at)
            self.wT = sb("q_wT", [P, 3, CH, P], at=at)
            self.h = sb("q_h", [P, 4, CH, T], at=at)
            self.mx = sb("q_mx", [P, 8], at=at)
            self.sc = sb("q_sc", [P, 8], at=at)
            self.inv = sb("q_inv", [P, 8], at=at)
            self.top = sb("q_top", [1, 8], at=at)
            self.w_in = sem("q_w_in")
            self.w_ready = sem("q_w_ready")
            self.wT_ready = sem("q_wT_ready")
            self.wT_copied = sem("q_wT_copied")
            self.mx_ready = sem("q_mx_ready")
            self.mxT_ready = sem("q_mxT_ready")
            self.top_ready = sem("q_top_ready")
            self.spread = sem("q_spread")
            self.x_quant = sem("q_x_quant")
            self.prod = sem("q_prod")
            self.evac = sem("q_evac")
            self.gate_quant = sem("q_gate_quant")
            self.sig_ready = sem("q_sig_ready")
            self.o_quant = sem("q_o_quant")
            self.down = sem("q_down")

        def sp(self, sp):
            for k, w in enumerate(("wg", "wu", "wd")):
                sp.dma_start(self.wraw[:, k, :], io["q_" + w]).then_inc(self.w_in, 16)

        def weights_dve(self, dve):
            dve.wait_ge(self.w_in, 48)
            blocks = self.wraw[:, :, :].rearrange("p k (g i) -> p (k g) i", i=32)
            G = 3 * QW // 32
            mx, inv = self.wmax[:, :, :].rearrange("p k g -> p (k g)"), self.winv[:, :, :].rearrange("p k g -> p (k g)")
            order.link(dve, dve.tensor_reduce(mx, blocks, X, ALU.max, apply_absolute_value=True))
            order.link(dve, dve.tensor_scalar(mx, mx, 1.0 / 7.0, 1e-12, ALU.mult, ALU.max))
            order.link(dve, dve.reciprocal(inv, mx))
            order.link(dve, dve.tensor_tensor(blocks, blocks, inv.unsqueeze(2).broadcast_to([P, G, 32]), ALU.mult))
            flat = self.wraw[:, :, :].rearrange("p k i -> p (k i)")
            order.link(dve, dve.tensor_scalar(flat, flat, MAGIC, -MAGIC, ALU.add, ALU.add))
            order.link(dve, dve.tensor_scalar(flat, flat, -8.0, 7.0, ALU.max, ALU.min))
            dve.tensor_tensor(blocks, blocks, mx.unsqueeze(2).broadcast_to([P, G, 32]), ALU.mult)\
               .then_inc(self.w_ready, 1)

        def weights_pe(self, pe):
            pe.wait_ge(self.w_ready, 1)
            for k in range(3):
                for c in range(self.CH):
                    mm = pe.transpose(PS[:, 3 + k, P * c:P * c + P], self.wraw[:, k, P * c:P * c + P], ident)
                mm.then_inc(self.wT_ready, 1)

        def weights_act(self, act):
            for k in range(3):
                act.wait_ge(self.wT_ready, k + 1)
                act.activation(self.wT[:, k, :, :].rearrange("p c i -> p (c i)"), PS[:, 3 + k, 0:QW], ACT.Copy)\
                   .then_inc(self.wT_copied, 1)

        def scale_dve(self, dve, j, src):
            dve.tensor_reduce(self.mx[:, j:j + 1], src, X, ALU.max, apply_absolute_value=True)\
               .then_inc(self.mx_ready, 1)
            dve.wait_ge(self.mxT_ready, n("dve", self.mxT_ready))
            dve.tensor_reduce(self.top[:, j:j + 1], PS[0:1, 7, 0:P], X, ALU.max).then_inc(self.top_ready, 1)
            dve.wait_ge(self.spread, n("dve", self.spread))
            order.link(dve, dve.tensor_scalar(self.sc[:, j:j + 1], PS[:, 7, P:P + 1], 1.0 / QMAX, 1e-12,
                                              ALU.mult, ALU.max))
            order.link(dve, dve.reciprocal(self.inv[:, j:j + 1], self.sc[:, j:j + 1]))

        def scale_pe(self, pe, j):
            pe.wait_ge(self.mx_ready, n("pe", self.mx_ready))
            pe.transpose(PS[0:1, 7, 0:P], self.mx[:, j:j + 1], ident).then_inc(self.mxT_ready, 1)
            pe.wait_ge(self.top_ready, n("pe", self.top_ready))
            pe.matmul(PS[:, 7, P:P + 1], const("one")[0:1, :], self.top[:, j:j + 1], start=True, stop=True)\
              .then_inc(self.spread, 1)

        def quant_dve(self, dve, j, a):
            order.link(dve, dve.tensor_scalar(a, a, self.inv[:, j:j + 1], MAGIC, ALU.mult, ALU.add))
            order.link(dve, dve.tensor_scalar(a, a, -MAGIC, QMAX, ALU.add, ALU.min))
            return dve.tensor_scalar(a, a, -QMAX - 1.0, self.sc[:, j:j + 1], ALU.max, ALU.mult)

        def dve(self, dve):
            up, gate, sig, o = [self.h[:, k, :, :].rearrange("p c t -> p (c t)") for k in range(4)]
            norm.wait(dve, "dve")
            flat = xn[:, :, :].rearrange("p b t -> p (b t)")
            self.scale_dve(dve, 0, flat)
            self.quant_dve(dve, 0, flat).then_inc(self.x_quant, 1)
            dve.wait_ge(self.evac, 6)
            self.scale_dve(dve, 1, gate)
            self.quant_dve(dve, 1, gate).then_inc(self.gate_quant, 1)
            dve.wait_ge(self.evac, 12)
            self.scale_dve(dve, 2, up)
            order.link(dve, self.quant_dve(dve, 2, up))
            dve.wait_ge(self.sig_ready, 1)
            order.link(dve, dve.tensor_scalar(sig, sig, 65536.0, MAGIC, ALU.mult, ALU.add))
            order.link(dve, dve.tensor_scalar(sig, sig, -MAGIC, 65535.0, ALU.add, ALU.min))
            order.link(dve, dve.tensor_scalar(sig, sig, 0.0, 1.0 / 65536.0, ALU.max, ALU.mult))
            order.link(dve, dve.tensor_tensor(gate, gate, sig, ALU.mult))
            self.scale_dve(dve, 3, gate)
            order.link(dve, self.quant_dve(dve, 3, gate))
            order.link(dve, dve.tensor_tensor(o, gate, up, ALU.mult))
            self.scale_dve(dve, 4, o)
            self.quant_dve(dve, 4, o).then_inc(self.o_quant, 1)
            for b in range(B):
                dve.wait_ge(self.down, b + 1)
                dve.tensor_tensor(x[:, b, :], x[:, b, :], PS[:, b, :], ALU.add).then_inc(x_ready, 1)

        def pe(self, pe):
            self.scale_pe(pe, 0)
            pe.wait_ge(self.x_quant, 1)
            pe.wait_ge(self.wT_copied, 3)
            k = 0
            for w, j in ((0, 1), (1, 2)):
                for c in range(self.CH):
                    for b in range(B):
                        if k >= 6:
                            pe.wait_ge(self.evac, k - 5)
                        pe.matmul(PS[:, k % 6, :], self.wT[:, w, c, :], xn[:, b, :],
                                  start=True, stop=True).then_inc(self.prod, 1)
                        k += 1
                self.scale_pe(pe, j)
            self.scale_pe(pe, 3)
            self.scale_pe(pe, 4)
            pe.wait_ge(self.o_quant, 1)
            for b in range(B):
                for c in range(self.CH):
                    mm = pe.matmul(PS[:, b, :], self.wT[:, 2, c, :], self.h[:, 3, c, S * b:S * b + S],
                                   start=(c == 0), stop=(c == self.CH - 1))
                mm.then_inc(self.down, 1)

        def act(self, act):
            k = 0
            for dst in (1, 0):
                for c in range(self.CH):
                    for b in range(B):
                        act.wait_ge(self.prod, k + 1)
                        act.activation(self.h[:, dst, c, S * b:S * b + S], PS[:, k % 6, :], ACT.Copy)\
                           .then_inc(self.evac, 1)
                        k += 1
            act.wait_ge(self.gate_quant, 1)
            act.activation(self.h[:, 2, :, :], self.h[:, 1, :, :], ACT.Sigmoid).then_inc(self.sig_ready, 1)

    class ContextAttention:

        COUNTS = dict(w_in=64, mask_ready=1, pads=1, kv_prod=3, kv_ready=3, kb_ready=2, vb_prod=6, vb_ready=6, q_prod=2,
                      q_ready=2, scores=NT, scores_read=NT, centred=NT, exps=NT, rden_ready=NT, probs=NT,
                      turned=3 * NT, pT_ready=3 * NT, mixed=NT, o_ready=2, out_prod=2)
        sems = {}

        def __init__(self, tag, mask_is_int, use):
            self.tag, self.mask_is_int = tag, mask_is_int
            self.past = {k: use * v for k, v in self.COUNTS.items()}
            at = self.stack = ExitStack()
            name = lambda a: tag + "_" + a
            self.w = sb(name("w"), [P, 4, P], at=at)
            self.mraw = sb(name("mraw"), [P, NT // B, KC], I32 if mask_is_int else F32, at=at)
            self.mask = sb(name("mask"), [P, NT // B, KC], at=at)
            self.sel = sb(name("sel"), [KC, HKP], at=at)
            self.hmask = sb(name("hmask"), [P, HKC, P], at=at)
            self.k = sb(name("k"), [P, B, KC], at=at)
            self.v = sb(name("v"), [KC, B, P], at=at)
            self.kb = sb(name("kb"), [P, B, H, KC], at=at)
            self.vb = sb(name("vb"), [P, B, HKC, P], at=at)
            self.q = sb(name("q"), [P, B, S], at=at)
            self.s = sb(name("s"), [P, 2, HKP], at=at)
            self.pT = sb(name("pT"), [P, 2, HKC, P], at=at)
            self.o = sb(name("o"), [P, B, S], at=at)
            self.mx = sb(name("mx"), [P, 2, H], at=at)
            self.den = sb(name("den"), [P, 2, H], at=at)
            self.rden = sb(name("rden"), [P, 2, H], at=at)
            if not use:
                self.sems.update({k: sem("ca_" + k) for k in self.COUNTS})
            (self.w_in, self.mask_ready, self.pads, self.kv_prod, self.kv_ready, self.kb_ready, self.vb_prod,
             self.vb_ready, self.q_prod, self.q_ready, self.scores, self.scores_read, self.centred, self.exps,
             self.rden_ready, self.probs, self.turned, self.pT_ready, self.mixed, self.o_ready, self.out_prod) = [self.sems[what] for what in self.COUNTS]

        def sp(self, sp):
            t = self.tag
            sp.dma_start(self.w[:, :, :], io[t + "_w"]).then_inc(self.w_in, 16)
            sp.dma_start(self.mraw[:, :, :], io[t + "_mask"]).then_inc(self.w_in, 16)
            sp.dma_start(self.sel[:, :], io["sel"]).then_inc(self.w_in, 16)
            sp.dma_start(self.hmask[:, :, :], io["hmask"]).then_inc(self.w_in, 16)

        def pe_prepare(self, pe):
            pe.wait_ge(self.w_in, self.past["w_in"] + 64)
            pe.matmul(PS[:, 0, 0:B * KC], self.w[:, 1, :], ctxT[:, :], start=True, stop=True).then_inc(self.kv_prod, 1)
            a = R_AT[self.tag + "_bv"][0]
            for b in range(B):
                pe.matmul(PS[0:KC, 1 + b, 0:P], ctxT[:, KC * b:KC * b + KC], self.w[:, 2, :], start=True, stop=False)
                pe.matmul(PS[0:KC, 1 + b, 0:P], const("one")[0:1, 0:KC], row[:, a:a + P],
                          start=False, stop=True).then_inc(self.kv_prod, 1)
            pe.wait_ge(self.kv_ready, self.past["kv_ready"] + 3)
            for b in range(B):
                for c in range(HKC):
                    bank, at = 3 * b + c // 4, P * (c % 4)
                    mm = pe.matmul(PS[:, bank, at:at + P], self.sel[:, P * c:P * c + P], self.v[:, b, :],
                                   start=True, stop=True)
                    if c % 4 == 3 or c == HKC - 1:
                        mm.then_inc(self.vb_prod, 1)

        def act_prepare(self, act):
            act.wait_ge(self.kv_prod, self.past["kv_prod"] + 1)
            act.activation(self.k[:, :, :].rearrange("p b k -> p (b k)"), PS[:, 0, 0:B * KC], ACT.Identity,
                           bias=column(self.tag + "_bk")).then_inc(self.kv_ready, 1)
            for b in range(B):
                act.wait_ge(self.kv_prod, self.past["kv_prod"] + 2 + b)
                act.activation(self.v[:, b, :], PS[0:KC, 1 + b, 0:P], ACT.Copy).then_inc(self.kv_ready, 1)

        def pool(self, pool):
            pool.memset(self.s[:, :, HK:], 0.0).then_inc(self.pads, 1)
            pool.wait_ge(self.w_in, self.past["w_in"] + 64)
            pool.wait_ge(self.kv_ready, self.past["kv_ready"] + 1)
            for b in range(B):
                pool.tensor_tensor(self.kb[:, b, :, :], self.k[:, b, :].unsqueeze(1).broadcast_to([P, H, KC]),
                                   const("hm").unsqueeze(2).broadcast_to([P, H, KC]), ALU.mult)\
                    .then_inc(self.kb_ready, 1)
            for t in range(NT):
                pool.wait_ge(self.rden_ready, self.past["rden_ready"] + t + 1)
                s = self.s[:, t % 2, 0:HK].rearrange("p (h k) -> p h k", h=H)
                pool.tensor_tensor(s, s, self.rden[:, t % 2, :].unsqueeze(2).broadcast_to([P, H, KC]), ALU.mult)\
                    .then_inc(self.probs, 1)

        def dve_prepare(self, dve):
            dve.wait_ge(self.w_in, self.past["w_in"] + 64)
            if self.mask_is_int:
                dve.tensor_scalar(self.mask[:, :, :], self.mraw[:, :, :], 0, NEG, ALU.is_equal, ALU.mult)\
                   .then_inc(self.mask_ready, 1)
            else:
                dve.tensor_scalar(self.mask[:, :, :], self.mraw[:, :, :], -1e9, None, ALU.mult)\
                   .then_inc(self.mask_ready, 1)
            for b in range(B):
                for g in range(3):
                    dve.wait_ge(self.vb_prod, self.past["vb_prod"] + 3 * b + g + 1)
                    c0, c1 = 4 * g, min(4 * g + 4, HKC)
                    dve.tensor_tensor(self.vb[:, b, c0:c1, :].rearrange("p c f -> p (c f)"),
                                      PS[:, 3 * b + g, 0:P * (c1 - c0)],
                                      self.hmask[:, c0:c1, :].rearrange("p c f -> p (c f)"), ALU.mult)\
                       .then_inc(self.vb_ready, 1)

        def pe(self, pe):
            pe.wait_ge(self.vb_ready, self.past["vb_ready"] + 6)
            norm.wait(pe, "pe")
            for b in range(B):
                pe.matmul(PS[:, 6 + b, :], self.w[:, 0, :], xn[:, b, :], start=True, stop=True)\
                  .then_inc(self.q_prod, 1)
            pe.wait_ge(self.kb_ready, self.past["kb_ready"] + 2)
            for t in range(NT + 1):
                if t < NT:
                    b, j = divmod(t, NT // B)
                    if j == 0:
                        pe.wait_ge(self.q_ready, self.past["q_ready"] + b + 1)
                    if t >= 1:
                        pe.wait_ge(self.scores_read, self.past["scores_read"] + t)
                    for g, (h0, nh) in enumerate(HGROUPS):
                        mm = pe.matmul(PS[:, g, 0:nh * KC], self.q[:, b, P * j:P * j + P],
                                       self.kb[:, b, h0:h0 + nh, :].rearrange("p h k -> p (h k)"), start=True, stop=True)
                    mm.then_inc(self.scores, 1)
                if t >= 1:
                    u = t - 1
                    b, j = divmod(u, NT // B)
                    pe.wait_ge(self.probs, self.past["probs"] + u + 1)
                    for c in range(HKC):
                        if u >= 1 and c % 4 == 0:
                            pe.wait_ge(self.pT_ready, self.past["pT_ready"] + 3 * (u - 1) + c // 4 + 1)
                        mm = pe.transpose(PS[:, 3 + c // 4, P * (c % 4):P * (c % 4) + P],
                                          self.s[:, u % 2, P * c:P * c + P], ident)
                        if c % 4 == 3 or c == HKC - 1:
                            mm.then_inc(self.turned, 1)
                    if j == 0 and b == 1:
                        pe.wait_ge(self.o_ready, self.past["o_ready"] + 1)
                    for c in range(HKC):
                        if c % 4 == 0:
                            pe.wait_ge(self.pT_ready, self.past["pT_ready"] + 3 * u + c // 4 + 1)
                        mm = pe.matmul(PS[:, 6, P * j:P * j + P], self.vb[:, b, c, :], self.pT[:, u % 2, c, :],
                                       start=(c == 0), stop=(c == HKC - 1))
                    mm.then_inc(self.mixed, 1)
                    if j == NT // B - 1:
                        pe.wait_ge(self.o_ready, self.past["o_ready"] + b + 1)
                        if b == 1:
                            pe.wait_ge(self.scores_read, self.past["scores_read"] + NT)
                        pe.matmul(PS[:, 7 - 7 * b, :], self.w[:, 3, :], self.o[:, b, :], start=True, stop=True)\
                          .then_inc(self.out_prod, 1)

        def act(self, act):
            for b in range(B):
                act.wait_ge(self.q_prod, self.past["q_prod"] + b + 1)
                act.activation(self.q[:, b, :], PS[:, 6 + b, :], ACT.Identity, bias=column(self.tag + "_bq"))\
                   .then_inc(self.q_ready, 1)
            for t in range(NT + 1):
                if t < NT:
                    act.wait_ge(self.centred, self.past["centred"] + t + 1)
                    s = self.s[:, t % 2, 0:HK]
                    act.activation(s, s, ACT.Exp).then_inc(self.exps, 1)
                if t >= 1:
                    u = t - 1
                    b, j = divmod(u, NT // B)
                    for g in range(3):
                        act.wait_ge(self.turned, self.past["turned"] + 3 * u + g + 1)
                        if u >= 2 and g == 0:
                            act.wait_ge(self.mixed, self.past["mixed"] + u - 1)
                        c0, c1 = 4 * g, min(4 * g + 4, HKC)
                        act.activation(self.pT[:, u % 2, c0:c1, :].rearrange("p c f -> p (c f)"),
                                       PS[:, 3 + g, 0:P * (c1 - c0)], ACT.Copy).then_inc(self.pT_ready, 1)
                    if j == NT // B - 1:
                        act.wait_ge(self.mixed, self.past["mixed"] + u + 1)
                        act.activation(self.o[:, b, :], PS[:, 6, :], ACT.Copy).then_inc(self.o_ready, 1)

        def dve(self, dve):
            scale = float(1.0 / np.sqrt(np.float32(DH)))
            dve.wait_ge(self.mask_ready, self.past["mask_ready"] + 1)
            dve.wait_ge(self.pads, self.past["pads"] + 1)
            for t in range(NT + 1):
                if t < NT:
                    j = t % (NT // B)
                    s = self.s[:, t % 2, 0:HK].rearrange("p (h k) -> p h k", h=H)
                    dve.wait_ge(self.scores, self.past["scores"] + t + 1)
                    if t >= 2:
                        dve.wait_ge(self.turned, self.past["turned"] + 3 * (t - 1))
                    for g, (h0, nh) in enumerate(HGROUPS):
                        ins = dve.scalar_tensor_tensor(
                            s[:, h0:h0 + nh, :], PS[:, g, 0:nh * KC].rearrange("p (h k) -> p h k", h=nh), scale,
                            self.mask[:, j, :].unsqueeze(1).broadcast_to([P, nh, KC]), ALU.mult, ALU.add)
                    ins.then_inc(self.scores_read, 1)
                    dve.wait_ge(self.scores_read, self.past["scores_read"] + t + 1)
                    order.link(dve, dve.tensor_reduce(self.mx[:, t % 2, :], s, X, ALU.max))
                    dve.tensor_tensor(s, s, self.mx[:, t % 2, :].unsqueeze(2).broadcast_to([P, H, KC]), ALU.subtract)\
                       .then_inc(self.centred, 1)
                if t >= 1:
                    u = t - 1
                    su = self.s[:, u % 2, 0:HK].rearrange("p (h k) -> p h k", h=H)
                    dve.wait_ge(self.exps, self.past["exps"] + u + 1)
                    order.link(dve, dve.tensor_reduce(self.den[:, u % 2, :], su, X, ALU.add))
                    if u >= 2:
                        dve.wait_ge(self.probs, self.past["probs"] + u - 1)
                    dve.reciprocal(self.rden[:, u % 2, :], self.den[:, u % 2, :]).then_inc(self.rden_ready, 1)
            for b in range(B):
                dve.wait_ge(self.out_prod, self.past["out_prod"] + b + 1)
                dve.scalar_tensor_tensor(x[:, b, :], PS[:, 7 - 7 * b, :], column(self.tag + "_bo"), x[:, b, :],
                                         ALU.add, ALU.add).then_inc(x_ready, 1)

    class PairAttention:

        def __init__(self):
            at = self.stack = ExitStack()
            self.w = sb("pa_w", [P, 4, P], at=at)
            self.h0 = sb("pa_h0", [P, B, S], at=at)
            self.h2 = sb("pa_h2", [P, B, S], at=at)
            self.q = sb("pa_q", [P, S], at=at)
            self.v = sb("pa_v", [P, B, S], at=at)
            self.qk = sb("pa_qk", [P, B, S], at=at)
            self.s = sb("pa_s", [P, B, S], at=at)
            self.m = sb("pa_m", [P, S], at=at)
            (self.w_in, self.prod, self.q_ready, self.v_ready, self.qk_ready, self.scores, self.s1_ready,
             self.centred, self.exps, self.mixed, self.out_prod, self.h2_ready) = [
                sem("pa_" + what) for what in (
                "w_in prod q_ready v_ready qk_ready scores s1_ready centred exps mixed out_prod h2_ready").split()]

        def sp(self, sp):
            sp.dma_start(self.w[:, :, :], io["pa_w"]).then_inc(self.w_in, 16)

        def pe(self, pe):
            norm.wait(pe, "pe")
            norm.pe(pe, self.h0, None)
            norm.wait(pe, "pe")
            pe.wait_ge(self.w_in, 16)
            for bank, (w, b) in enumerate(((0, 1), (1, 0), (1, 1), (2, 0), (2, 1))):
                pe.matmul(PS[:, bank, :], self.w[:, w, :], xn[:, b, :], start=True, stop=True).then_inc(self.prod, 1)
            for b in range(B):
                pe.wait_ge(self.qk_ready, b + 1)
                pe.matmul(PS[:, 5 + b, :], const("blk8"), self.qk[:, b, :], start=True, stop=True)\
                  .then_inc(self.scores, 1)
            pe.wait_ge(self.v_ready, 2)
            pe.matmul(PS[:, 0, :], self.w[:, 3, :], self.v[:, 0, :], start=True, stop=True).then_inc(self.out_prod, 1)
            pe.wait_ge(self.mixed, 1)
            pe.matmul(PS[:, 1, :], self.w[:, 3, :], self.qk[:, 0, :], start=True, stop=True).then_inc(self.out_prod, 1)
            norm.pe(pe, self.h2, self.h2_ready)

        def act(self, act):
            norm.act(act)
            act.wait_ge(self.prod, 1)
            act.activation(self.q[:, :], PS[:, 0, :], ACT.Copy).then_inc(self.q_ready, 1)
            for b in range(B):
                act.wait_ge(self.prod, 4 + b)
                act.activation(self.v[:, b, :], PS[:, 3 + b, :], ACT.Copy).then_inc(self.v_ready, 1)
            act.wait_ge(self.scores, 2)
            act.activation(self.s[:, 1, :], PS[:, 6, :], ACT.Copy).then_inc(self.s1_ready, 1)
            act.wait_ge(self.centred, 1)
            act.activation(self.s[:, :, :], self.s[:, :, :], ACT.Exp, scale=float(1.0 / np.sqrt(np.float32(DH))))\
               .then_inc(self.exps, 1)
            norm.act(act)

        def dve(self, dve):
            norm.wait(dve, "dve")
            norm.dve(dve, self.h0, xn, column("pa_ln1w"), column("pa_ln1b"))
            dve.wait_ge(self.q_ready, 1)
            for b in range(B):
                dve.wait_ge(self.prod, 2 + b)
                dve.tensor_tensor(self.qk[:, b, :], PS[:, 1 + b, :], self.q[:, :], ALU.mult).then_inc(self.qk_ready, 1)
            dve.wait_ge(self.s1_ready, 1)
            order.link(dve, dve.tensor_tensor(self.m[:, :], PS[:, 5, :], self.s[:, 1, :], ALU.max))
            order.step(dve.tensor_tensor(self.s[:, 0, :], PS[:, 5, :], self.m[:, :], ALU.subtract))
            dve.tensor_tensor(self.s[:, 1, :], self.s[:, 1, :], self.m[:, :], ALU.subtract).then_inc(self.centred, 1)
            dve.wait_ge(self.exps, 1)
            order.link(dve, dve.tensor_tensor(self.m[:, :], self.s[:, 0, :], self.s[:, 1, :], ALU.add))
            order.link(dve, dve.reciprocal(self.m[:, :], self.m[:, :]))
            for b in range(B):
                order.link(dve, dve.tensor_tensor(self.s[:, b, :], self.s[:, b, :], self.m[:, :], ALU.mult))
            dve.wait_ge(self.v_ready, 2)
            for b in range(B):
                order.link(dve, dve.tensor_tensor(self.s[:, b, :], self.s[:, b, :], self.v[:, b, :], ALU.mult))
            dve.tensor_tensor(self.qk[:, 0, :], self.s[:, 0, :], self.s[:, 1, :], ALU.add).then_inc(self.mixed, 1)
            for b in range(B):
                dve.wait_ge(self.out_prod, b + 1)
                dve.tensor_tensor(self.h2[:, b, :], self.h0[:, b, :], PS[:, b, :], ALU.add).then_inc(self.h2_ready, 1)
            dve.wait_ge(self.h2_ready, 2)
            norm.dve(dve, self.h2, xn, column("pa_ln2w"), column("pa_ln2b"))

    class Experts:

        COUNTS = dict(router_in=16, ones_set=1, logits=1, g_centred=1, g_exps=1, g_ready=1, g_turned=4, wT_ready=2,
                      wb_prod=E * B, wb_ready=E * B, w_in0=16 * E, w_in1=16 * E, h_prod=E * B * FF // P,
                      h_ready=4 + E * B * FF // P, y_prod=2 + E * B, y_used=2 + E * B, y_step=E * B)
        sems = {}

        def __init__(self, tag, act_fn, temperature, capped, use):
            self.tag, self.fn, self.temperature, self.capped = tag, act_fn, temperature, capped
            self.past = {k: use * v for k, v in self.COUNTS.items()}
            at = self.stack = ExitStack()
            name = lambda a: tag + "_" + a
            self.router = sb(name("router"), [P, E], at=at)
            self.w1 = sb(name("w1"), [P, 2, FF], at=at)
            self.w2 = sb(name("w2"), [P, 2, FF // P, P], at=at)
            self.g = sb(name("g"), [P, 4, NT, E], at=at)
            self.r = sb(name("r"), [P, 2, NT], at=at)
            self.wT = sb(name("wT"), [E, T], at=at)
            self.rank = sb(name("rank"), [E, T], at=at)
            self.ones = sb(name("ones"), [E, T], at=at)
            self.wb = sb(name("wb"), [P, E, B, S], at=at)
            self.h = sb(name("h"), [P, 2, FF // P, S], at=at)
            self.y = sb(name("y"), [P, 2, S], at=at)
            if not use:
                self.sems.update({k: sem("ex_" + k) for k in self.COUNTS})
            (self.router_in, self.ones_set, self.logits, self.g_centred, self.g_exps, self.g_ready, self.g_turned,
             self.wT_ready, self.wb_prod, self.wb_ready, self.w_in0, self.w_in1, self.h_prod, self.h_ready,
             self.y_prod, self.y_used, self.y_step) = [self.sems[what] for what in self.COUNTS]
            self.w_in = (self.w_in0, self.w_in1)

        def load(self, sp, e, slot):
            sp.dma_start(self.w1[:, slot, :], io[self.tag + "_w1"][e]).then_inc(self.w_in[slot], 16)
            sp.dma_start(self.w2[:, slot, :, :], io[self.tag + "_w2"][e].rearrange("(c p) d -> p c d", p=P))\
              .then_inc(self.w_in[slot], 16)

        def sp(self, sp):
            sp.dma_start(self.router[:, :], io[self.tag + "_router"]).then_inc(self.router_in, 16)
            for e in range(2):
                self.load(sp, e, e)
            with sp.Fori(0, E // 2 - 1) as i:
                for slot in range(2):
                    sp.wait_ge(self.y_prod, self.past["y_prod"] + i * 4 + 2 * slot + 4)
                    e = i * 2 + 2 + slot
                    sp.dma_start(self.w1[:, slot, :], io[self.tag + "_w1"][bass.ds(e, 1)].rearrange("a p f -> p (a f)"))\
                      .then_inc(self.w_in[slot], 16)
                    sp.dma_start(self.w2[:, slot, :, :],
                                 io[self.tag + "_w2"][bass.ds(e, 1)].rearrange("a (c p) d -> p (a c) d", p=P))\
                      .then_inc(self.w_in[slot], 16)

        def pool(self, pool):
            pool.memset(self.ones[:, :], 1.0).then_inc(self.ones_set, 1)

        def gate_pe(self, pe):
            norm.wait(pe, "pe")
            pe.wait_ge(self.router_in, self.past["router_in"] + 16)
            for t in range(NT):
                mm = pe.matmul(PS[:, 0, E * t:E * t + E], xn[:, t * P // S, P * (t % (S // P)):P * (t % (S // P)) + P],
                               self.router[:, :], start=True, stop=True)
            mm.then_inc(self.logits, 1)
            pe.wait_ge(self.g_ready, self.past["g_ready"] + 1)
            for k in range(2 if self.capped else 1):
                for t in range(NT):
                    mm = pe.transpose(PS[0:E, 1 + 2 * k + t // 4, P * (t % 4):P * (t % 4) + P], self.g[:, k, t, :], ident)
                    if t % 4 == 3:
                        mm.then_inc(self.g_turned, 1)
            for b in range(B):
                pe.wait_ge(self.wT_ready, self.past["wT_ready"] + b + 1)
            for u in range(E * B):
                e, b = divmod(u, B)
                if u >= 3:
                    pe.wait_ge(self.wb_ready, self.past["wb_ready"] + u - 2)
                pe.matmul(PS[:, 5 + u % 3, :], cst[0:E, e:e + 1].broadcast_to([E, P]), self.wT[:, S * b:S * b + S],
                          start=True, stop=True).then_inc(self.wb_prod, 1)

        def gate_act(self, act):
            act.wait_ge(self.g_centred, self.past["g_centred"] + 1)
            g = self.g[:, 3, :, :]
            act.activation(g, g, ACT.Exp, scale=1.0 / self.temperature).then_inc(self.g_exps, 1)
            for u in range(E * B):
                e, b = divmod(u, B)
                act.wait_ge(self.wb_prod, self.past["wb_prod"] + u + 1)
                act.activation(self.wb[:, e, b, :], PS[:, 5 + u % 3, :], ACT.Copy).then_inc(self.wb_ready, 1)

        def gate_dve(self, dve):
            logits = PS[:, 0, 0:NT * E].rearrange("p (t e) -> p t e", e=E)
            w, sel, t2, ex = [self.g[:, k, :, :] for k in range(4)]
            r0, r1 = self.r[:, 0, :], self.r[:, 1, :]
            wide = lambda r: r.unsqueeze(2).broadcast_to([P, NT, E])
            kidx = const("kidx").unsqueeze(1).broadcast_to([P, NT, E])

            def pick(src, dst):
                order.link(dve, dve.tensor_reduce(r0, src, X, ALU.max))
                order.link(dve, dve.tensor_tensor(dst, src, wide(r0), ALU.is_equal))
                order.link(dve, dve.tensor_tensor(dst, dst, kidx, ALU.mult))
                order.link(dve, dve.tensor_reduce(r0, dst, X, ALU.max))
                order.link(dve, dve.tensor_tensor(dst, dst, wide(r0), ALU.is_equal))

            dve.wait_ge(self.logits, self.past["logits"] + 1)
            order.link(dve, dve.tensor_reduce(r0, logits, X, ALU.max))
            dve.tensor_tensor(ex, logits, wide(r0), ALU.subtract).then_inc(self.g_centred, 1)
            dve.wait_ge(self.g_exps, self.past["g_exps"] + 1)
            pick(ex, sel)
            order.link(dve, dve.scalar_tensor_tensor(w, sel, -2.0, ex, ALU.mult, ALU.add))
            pick(w, t2)
            order.link(dve, dve.tensor_tensor(sel, sel, t2, ALU.add))
            order.link(dve, dve.tensor_tensor(w, ex, sel, ALU.mult))
            order.link(dve, dve.tensor_reduce(r1, w if self.capped else ex, X, ALU.add))
            order.link(dve, dve.reciprocal(r1, r1))
            dve.tensor_tensor(w, w, wide(r1), ALU.mult).then_inc(self.g_ready, 1)
            if not self.capped:
                for b in range(B):
                    dve.wait_ge(self.g_turned, self.past["g_turned"] + b + 1)
                    dve.tensor_copy(self.wT[:, S * b:S * b + S], PS[0:E, 1 + b, :]).then_inc(self.wT_ready, 1)
                return
            dve.wait_ge(self.ones_set, self.past["ones_set"] + 1)
            for b in range(B):
                dve.wait_ge(self.g_turned, self.past["g_turned"] + 3 + b)
                init = self.rank[:, S - 1:S] if b else 0.0
                order.link(dve, dve.tensor_tensor_scan(self.rank[:, S * b:S * b + S], self.ones[:, S * b:S * b + S],
                                                       PS[0:E, 3 + b, :], init, ALU.mult, ALU.add))
            for b in range(B):
                dve.scalar_tensor_tensor(self.wT[:, S * b:S * b + S], self.rank[:, S * b:S * b + S], float(CAP),
                                         PS[0:E, 1 + b, :], ALU.is_le, ALU.mult).then_inc(self.wT_ready, 1)

        def pe(self, pe):
            C = FF // P

            def hidden(i, u):
                slot, b = divmod(u, B)
                if b == 0:
                    pe.wait_ge(self.w_in[slot], self.past["w_in0"] + i * 32 + 32)
                for c in range(C):
                    pe.wait_ge(self.h_ready, self.past["h_ready"] + i * 16 + 4 * u + c + 1)
                    pe.matmul(PS[:, c, :], self.w1[:, slot, P * c:P * c + P], xn[:, b, :], start=True, stop=True)\
                      .then_inc(self.h_prod, 1)

            def outward(i, u):
                slot, b = divmod(u, B)
                pe.wait_ge(self.h_ready, self.past["h_ready"] + i * 16 + 4 * u + 4 + 4)
                pe.wait_ge(self.y_used, self.past["y_used"] + i * 4 + u + 1)
                for c in range(C):
                    mm = pe.matmul(PS[:, 4 + u % 2, :], self.w2[:, slot, c, :], self.h[:, u % 2, c, :],
                                   start=(c == 0), stop=(c == C - 1))
                mm.then_inc(self.y_prod, 1)

            pe.sem_inc(self.y_prod, 2)
            with pe.Fori(0, E // 2) as i:
                hidden(i, 0)
                for u in range(1, 4):
                    hidden(i, u)
                    outward(i, u - 1)
                outward(i, 3)

        def act(self, act):
            act.sem_inc(self.h_ready, 4)
            with act.Fori(0, E // 2) as i:
                for u in range(4):
                    for c in range(FF // P):
                        act.wait_ge(self.h_prod, self.past["h_prod"] + i * 16 + 4 * u + c + 1)
                        if c == 0:
                            act.wait_ge(self.y_prod, self.past["y_prod"] + i * 4 + u + 1)
                        act.activation(self.h[:, u % 2, c, :], PS[:, c, :], self.fn).then_inc(self.h_ready, 1)

        def dve(self, dve, base):
            for b in range(B):
                order.link(dve, dve.tensor_tensor(x[:, b, :], x[:, b, :], base[:, b, :], ALU.add))
            dve.wait_ge(self.wb_ready, self.past["wb_ready"] + E * B)
            dve.sem_inc(self.y_used, 2)
            with dve.Fori(0, E // 2) as i:
                for u in range(4):
                    slot, b = divmod(u, B)
                    dve.wait_ge(self.y_prod, self.past["y_prod"] + i * 4 + u + 3)
                    dve.tensor_tensor(self.y[:, u % 2, :], PS[:, 4 + u % 2, :],
                                      self.wb[:, bass.ds(i * 2 + slot, 1), b, :].rearrange("p a s -> p (a s)"),
                                      ALU.mult).then_inc(self.y_used, 1)
                    dve.wait_ge(self.y_used, self.past["y_used"] + i * 4 + u + 3)
                    dve.tensor_tensor(x[:, b, :], x[:, b, :], self.y[:, u % 2, :], ALU.add).then_inc(self.y_step, 1)
            dve.wait_ge(self.y_step, self.past["y_step"] + 2 * E)
            dve.sem_inc(x_ready, 2)

    class Stack:

        TILES = S // P
        CHUNKS = ((0, 128), (128, 128), (256, FFI - 256))

        def __init__(self):
            at = self.stack = ExitStack()
            s = lambda name, shape, dt=F32: sb("st_" + name, shape, dt, at=at)
            self.wqkv = s("wqkv", [P, 3, INNER])
            self.wo = s("wo", [P, INNER // P, P])
            self.w1 = s("w1", [P, 2 * FFI])
            self.w2 = s("w2", [P, 3, P])
            self.sv = s("sv", [P, 9])
            self.qks = s("qks", [P, 2, 2, D2])
            self.base = s("base", [P, 2, 2, 4, D2])
            self.rot = s("rot", [P, 2, 2, 4, D2])
            self.wmask = s("wmask", [P, 2, 2 * WIN], BF16)
            self.identb = s("identb", [P, P], BF16)
            self.xs = s("xs", [P, B, S])
            self.xf = s("xf", [P, S])
            self.xfn = s("xfn", [P, S])
            self.y0 = s("y0", [P, B, S])
            self.sqh = s("sqh", [P, 2, 512])
            self.t2 = s("t2", [P, 2, 512])
            self.r = s("r", [P, 2, 4, 512])
            self.ss = s("ss", [P, 2, 32])
            self.gy = s("gy", [P, 2, 32])
            self.gt = s("gt", [P, 2, 32])
            self.qT = s("qT", [P, 8, S])
            self.kT = s("kT", [P, 8, WIN + S])
            self.v = s("v", [P, 4, INNER])
            self.vs = s("vs", [P, 4, INNER])
            self.e = s("e", [P, 16, 2 * WIN])
            self.pT = s("pT", [P, 16, 2, WIN])
            self.mx = s("mx", [P, 16])
            self.den = s("den", [P, 16])
            self.rden = s("rden", [P, 2, 16])
            self.on = s("on", [P, 8, 2, D2])
            self.oT = s("oT", [P, 8, S])
            self.gel = s("gel", [P, 2, S])
            self.hid = s("hid", [P, 3, S])
            (self.c_in, self.wv_in, self.wq_in, self.wk_in, self.wf_in, self.qks_in, self.set_up, self.rot_ready,
             self.xs_ready, self.proj, self.v_evac, self.squares, self.ss_done, self.qk_used, self.added,
             self.v_ready, self.guess, self.newton, self.r_ready, self.turned, self.evac, self.scores, self.mx_ready,
             self.sub_done, self.exps, self.den_ready, self.rden_ready, self.pt_ready, self.pv_done, self.on_ready,
             self.wo_done, self.xu_ready, self.xf_ready, self.mean, self.centred, self.lnsq, self.var, self.std,
             self.rstd, self.spread, self.ln_tmp, self.ffn_in, self.up, self.gelu, self.act_ready, self.down) = [
                sem("st_" + what) for what in (
                "c_in wv_in wq_in wk_in wf_in qks_in set_up rot_ready xs_ready proj v_evac squares ss_done "
                "qk_used added v_ready guess newton r_ready turned evac scores mx_ready sub_done exps "
                "den_ready rden_ready pt_ready pv_done on_ready wo_done xu_ready xf_ready mean centred lnsq "
                "var std rstd spread ln_tmp ffn_in up gelu act_ready down").split()]
            self.mix_begun = sem("st_mix_begun")
            self.load_begun = sem("st_load_begun")
            self.vshift = [sem("st_vshift%d" % t) for t in range(4)]

        def load_a(self, sp, l):
            for k, s in enumerate((self.wq_in, self.wk_in, self.wv_in)):
                src = io["st_wqkv"][bass.ds(l, 1), :, INNER * k:INNER * k + INNER].rearrange("a p n -> p (a n)")
                sp.dma_start(self.wqkv[:, k, :], src).then_inc(s, 16)
            sp.dma_start(self.qks[:, :, :, :], io["st_qks"][bass.ds(l, 1)].rearrange("a q k d -> a (q k d)")
                         .broadcast_to([P, 4 * D2])).then_inc(self.qks_in, 16)

        def load_f(self, sp, l):
            one = lambda name: io[name][bass.ds(l, 1)]
            sp.dma_start(self.wo[:, :, :], one("st_wo").rearrange("a (c p) d -> p (a c) d", p=P)).then_inc(self.wf_in, 16)
            sp.dma_start(self.w1[:, :], one("st_w1").rearrange("a p n -> p (a n)")).then_inc(self.wf_in, 16)
            sp.dma_start(self.w2[:, 0:2, :], one("st_w2")[:, 0:256, :].rearrange("a (c p) d -> p (a c) d", p=P))\
              .then_inc(self.wf_in, 16)
            sp.dma_start(self.w2[0:FFI - 256, 2, :], one("st_w2")[:, 256:, :].rearrange("a p d -> p (a d)"))\
              .then_inc(self.wf_in, 16)
            sp.dma_start(self.sv[:, :], one("st_sv").rearrange("a p n -> p (a n)")).then_inc(self.wf_in, 16)

        WF = 5 * 16

        def sp_shift(self, sp, u):
            for t in range(4):
                T = 4 * u + t
                sp.wait_ge(self.pv_done, T + 1)
                sp.wait_ge(self.v_evac, T * 2 + 2)
                sp.dma_start(self.vs[WIN:P, t, :], self.v[0:P - WIN, t, :]).then_inc(self.vshift[t], 16)
                if t < 3:
                    sp.wait_ge(self.pv_done, T + 2)
                    sp.dma_start(self.vs[0:WIN, t + 1, :], self.v[P - WIN:P, t, :]).then_inc(self.vshift[t + 1], 16)

        def sp(self, sp):
            sp.dma_start(self.base[:, :, :, :, :], io["st_base"]).then_inc(self.c_in, 16)
            sp.dma_start(self.wmask[:, :, :], io["st_wmask"]).then_inc(self.c_in, 16)
            sp.dma_start(self.identb[:, :], io["identb"]).then_inc(self.c_in, 16)
            self.load_a(sp, 0)
            self.load_f(sp, 0)
            self.sp_shift(sp, 0)
            with sp.Fori(0, DEPTH - 1) as i:
                self.sp_shift(sp, i * 2 + 1)
                sp.wait_ge(self.rot_ready, i + 1)
                sp.wait_ge(self.proj, (i * 2 + 2) * 24)
                sp.sem_inc(self.load_begun, 1)
                self.load_a(sp, i + 1)
                self.sp_shift(sp, i * 2 + 2)
                sp.wait_ge(self.xs_ready, i * 2 + 4)
                sp.sem_inc(self.load_begun, 1)
                self.load_f(sp, i + 1)
            self.sp_shift(sp, 2 * DEPTH - 1)

        def pe_proj(self, pe, u, t, ms):
            T = 4 * u + t
            b = self.b_of(u)
            l = self.l_of(u)
            for m in ms:
                if m == 0 and t == 0:
                    pe.wait_ge(self.xs_ready, u + 1)
                if m % 2 == 0 and t == 0:
                    pe.wait_ge((self.wv_in, self.wq_in, self.wk_in)[m // 2], l * 16 + 16)
                if m < 3:
                    if self.later(T):
                        pe.wait_ge(self.qk_used, T * 4 - 2 + m)
                elif m < 5:
                    pe.wait_ge(self.v_evac, T * 2 + m - 2)
                else:
                    pe.wait_ge(self.qk_used, T * 4 + 1)
                k, half = ((2, 0), (2, 1), (0, 0), (0, 1), (1, 0), (1, 1))[m]
                pe.matmul(PS[:, 4 + m % 3, :], self.xs[:, b, P * t:P * t + P],
                          self.wqkv[:, k, 512 * half:512 * half + 512], start=True, stop=True).then_inc(self.proj, 1)

        def later(self, T):
            return not isinstance(T, int) or T > 0

        def b_of(self, u):
            return self.now[0]

        def l_of(self, u):
            return self.now[1]

        def group(self, u, k):
            return u * 24 + 12 + k

        def pe_turn(self, pe, u, t, g, number):
            pe.wait_ge(self.r_ready, (4 * u + t) * 4 + g + 1)
            if not isinstance(number, int) or number > 0:
                pe.wait_ge(self.evac, number)
            for j in range(4):
                mm = pe.transpose(PS[:, 7, P * j:P * j + P], self.r[:, t % 2, g, P * j:P * j + P], ident)
            mm.then_inc(self.turned, 1)

        def act_turn(self, act, u, t, g, number):
            act.wait_ge(self.turned, number + 1)
            src = PS[:, 7, :].rearrange("p (c n) -> p c n", c=4)
            c = 4 * (g % 2)
            dst = self.qT[:, c:c + 4, P * t:P * t + P] if g < 2 else self.kT[:, c:c + 4, WIN + P * t:WIN + P * t + P]
            act.activation(dst, src, ACT.Copy).then_inc(self.evac, 1)

        def act_proj(self, act, u, t, ms):
            T = 4 * u + t
            for m in ms:
                act.wait_ge(self.proj, T * 6 + m + 1)
                if m < 2:
                    if m == 0 and t < 3 and self.later(u):
                        act.wait_ge(self.vshift[t + 1], u * 32)
                    act.activation(self.v[:, t, 512 * m:512 * m + 512], PS[:, 4 + m % 3, :], ACT.Copy)\
                       .then_inc(self.v_evac, 1)
                else:
                    c = m - 2
                    if c >= 2 or self.later(T):
                        act.wait_ge(self.ss_done, T * 4 + c - 1)
                    act.activation(self.sqh[:, c % 2, :], PS[:, 4 + m % 3, :], ACT.Square).then_inc(self.squares, 1)

        def dve_proj(self, dve, u, t, cs):
            T = 4 * u + t
            for c in cs:
                m, k = c + 2, c // 2
                ps = PS[:, 4 + m % 3, :]
                dve.wait_ge(self.squares, T * 4 + c + 1)
                if c == 0 and (t >= 2 or self.later(u)):
                    dve.wait_ge(self.turned, self.turned_by(u, t))
                if c == 0 and t == 0:
                    dve.wait_ge(self.rot_ready, self.l_of(u) + 1)
                h3 = lambda a: a.rearrange("p (h d) -> p h d", h=8)
                h4 = lambda a: a.rearrange("p (h s d) -> p h s d", h=8, s=2)
                table = lambda j: self.rot[:, k, j, t, :].unsqueeze(1).broadcast_to([P, 8, D2])
                dve.tensor_tensor(h3(self.r[:, t % 2, c, :]), h3(ps), table(0), ALU.mult)
                if c >= 2 or self.later(T):
                    dve.wait_ge(self.added, T * 4 + c - 1)
                for s in range(2):
                    ins = dve.tensor_tensor(h4(self.t2[:, c % 2, :])[:, :, s, :], h4(ps)[:, :, 1 - s, :],
                                            self.rot[:, k, 1, t, 32 * s:32 * s + 32].unsqueeze(1)
                                            .broadcast_to([P, 8, 32]), ALU.mult)
                ins.then_inc(self.qk_used, 1)
                if c == 0 and (t >= 2 or self.later(u)):
                    dve.wait_ge(self.r_ready, T * 4 - 4)
                dve.tensor_reduce(self.ss[:, t % 2, 8 * c:8 * c + 8], h3(self.sqh[:, c % 2, :]), X, ALU.add)\
                   .then_inc(self.ss_done, 1)
                if c == 3:
                    ss, y = self.ss[:, t % 2, :], self.gy[:, t % 2, :]
                    dve.wait_ge(self.ss_done, T * 4 + 4)
                    dve.tensor_scalar(ss, ss, 1e-24, -0.5, ALU.max, ALU.mult).then_inc(self.v_ready, 1)
                    dve.wait_ge(self.v_ready, T + 1)
                    dve.tensor_scalar(y.bitcast(I32), ss.bitcast(I32), -0.5, GUESS, ALU.mult, ALU.add)\
                       .then_inc(self.guess, 1)

        def turned_by(self, u, t):
            if t >= 2:
                if isinstance(u, int) and u == 0:
                    return 4 * (t - 1)
                return (u - 1) * 24 + 12 + (10, 16)[t - 2]
            if t == 0:
                return (u - 1) * 24 + 12 if not (isinstance(u, int) and u == 0) else 0
            return (u - 1) * 24 + 12 + 4

        def pool_proj(self, pool, u, t):
            T = 4 * u + t
            for c in range(4):
                pool.wait_ge(self.qk_used, T * 4 + c + 1)
                r = self.r[:, t % 2, c, :]
                pool.tensor_tensor(r, r, self.t2[:, c % 2, :], ALU.add).then_inc(self.added, 1)
            pool.wait_ge(self.guess, T + 1)
            ss, y, g = self.ss[:, t % 2, :], self.gy[:, t % 2, :], self.gt[:, t % 2, :]
            k = 0
            for _ in range(3):
                for f in (lambda: pool.tensor_tensor(g, y, y, ALU.mult),
                          lambda: pool.tensor_tensor(g, g, ss, ALU.mult),
                          lambda: pool.tensor_tensor(g, g, const("threehalves").broadcast_to([P, 32]), ALU.add),
                          lambda: pool.tensor_tensor(y, y, g, ALU.mult)):
                    f().then_inc(self.newton, 1)
                    k += 1
                    pool.wait_ge(self.newton, T * 12 + k)
            pool.wait_ge(self.added, T * 4 + 4)
            for c in range(4):
                r = self.r[:, t % 2, c, :].rearrange("p (h d) -> p h d", h=8)
                pool.tensor_tensor(r, r, y[:, 8 * c:8 * c + 8].unsqueeze(2).broadcast_to([P, 8, D2]), ALU.mult)\
                    .then_inc(self.r_ready, 1)

        def pe_scores(self, pe, u, t):
            T = 4 * u + t
            pe.wait_ge(self.evac, self.group(u, 4 if t == 3 else 0))
            pe.wait_ge(self.sub_done, T + 1)
            for e in range(2):
                pe.matmul(PS[:, e, :], self.identb[:, :],
                          self.wmask[:, min(t, 1), :].unsqueeze(1).broadcast_to([P, 8, 2 * WIN]),
                          start=True, stop=False, skip_group_check=True)
            for e in range(2):
                for c in range(8):
                    for w in range(4):
                        q = P * t + WIN * w
                        mm = pe.matmul(PS[WIN * w:WIN * w + WIN, e, D2 * c:D2 * c + D2],
                                       self.qT[64 * e:64 * e + 64, c, q:q + WIN],
                                       self.kT[64 * e:64 * e + 64, c, q:q + 2 * WIN],
                                       start=False, stop=(c == 7), skip_group_check=True,
                                       tile_position=(64 * e, WIN * w))
            mm.then_inc(self.scores, 1)

        def pe_mix(self, pe, u, t):
            T = 4 * u + t
            pe.wait_ge(self.pt_ready, T + 2)
            pe.wait_ge(self.vshift[t], (u + 1) * (32 if t else 16))
            pe.wait_ge(self.on_ready, T + 1)
            pe.sem_inc(self.mix_begun, 1)
            for c in range(8):
                for e in range(2):
                    for k, v in ((0, self.vs), (1, self.v)):
                        for w in range(4):
                            g = slice(WIN * w, WIN * w + WIN)
                            h = D2 * (2 * c + e)
                            mm = pe.matmul(PS[g, 2 + e, D2 * c:D2 * c + D2], self.pT[g, 8 * e + c, k, :],
                                           v[g, t, h:h + D2], start=(k == 0), stop=(k == 1),
                                           tile_position=(WIN * w, WIN * w), skip_group_check=True)
            mm.then_inc(self.pv_done, 1)

        def pe_turn_o(self, pe, u, t, half, number):
            pe.wait_ge(self.on_ready, 4 * u + t + 2)
            pe.wait_ge(self.evac, number)
            for j in range(4):
                c = 4 * half + j
                mm = pe.transpose(PS[:, 7, P * j:P * j + P], self.on[:, c, :, :].rearrange("p e d -> p (e d)"), ident)
            mm.then_inc(self.turned, 1)

        def act_turn_o(self, act, u, t, half, number):
            act.wait_ge(self.turned, number + 1)
            act.activation(self.oT[:, 4 * half:4 * half + 4, P * t:P * t + P],
                           PS[:, 7, :].rearrange("p (c n) -> p c n", c=4), ACT.Copy).then_inc(self.evac, 1)

        def act_exp(self, act, u, t):
            act.wait_ge(self.sub_done, 4 * u + t + 2)
            act.activation(self.e[:, :, :], self.e[:, :, :], ACT.Exp, scale=8.0).then_inc(self.exps, 1)

        def dve_max(self, dve, u, t):
            T = 4 * u + t
            dve.wait_ge(self.scores, T + 1)
            ps = PS[:, 0:2, :].rearrange("p e (c k) -> p (e c) k", c=8)
            dve.tensor_reduce(self.mx[:, :], ps, X, ALU.max).then_inc(self.mx_ready, 1)
            dve.wait_ge(self.mx_ready, T + 1)
            dve.wait_ge(self.pt_ready, T + 1)
            dve.tensor_tensor(self.e[:, :, :], ps, self.mx[:, :].unsqueeze(2).broadcast_to([P, 16, 2 * WIN]),
                              ALU.subtract).then_inc(self.sub_done, 1)

        def dve_sum(self, dve, u, t):
            T = 4 * u + t
            dve.wait_ge(self.exps, T + 1)
            dve.tensor_reduce(self.den[:, :], self.e[:, :, :], X, ALU.add).then_inc(self.den_ready, 1)
            dve.wait_ge(self.den_ready, T + 1)
            dve.reciprocal(self.rden[:, t % 2, :], self.den[:, :]).then_inc(self.rden_ready, 1)
            dve.transpose(self.pT[:, :, :, :].rearrange("p h k q -> p (h k q)"),
                          self.e[:, :, :].rearrange("p h k -> p (h k)")).then_inc(self.pt_ready, 1)

        def dve_out(self, dve, u, t, number):
            T = 4 * u + t
            dve.wait_ge(self.pv_done, T + 1 + 4)
            dve.wait_ge(self.rden_ready, T + 1)
            dve.wait_ge(self.turned, number)
            dve.tensor_tensor(self.on[:, :, :, :].rearrange("p c e d -> p e c d"),
                              PS[:, 2:4, :].rearrange("p e (c d) -> p e c d", c=8),
                              self.rden[:, t % 2, :].rearrange("p (e c) -> p e c", e=2).unsqueeze(3)
                              .broadcast_to([P, 2, 8, D2]), ALU.mult).then_inc(self.on_ready, 1)

        def pe_wo(self, pe, u):
            pe.wait_ge(self.wf_in, self.l_of(u) * self.WF + self.WF)
            pe.wait_ge(self.evac, self.group(u, 21))
            for c in range(8):
                mm = pe.matmul(PS[:, 2, :], self.wo[:, c, :], self.oT[:, c, :], start=(c == 0), stop=(c == 7))
            mm.then_inc(self.wo_done, 1)

        def pe_mean(self, pe, u):
            pe.wait_ge(self.xf_ready, u + 1)
            pe.matmul(PS[:, 3, :], const("mean"), self.xf[:, :], start=True, stop=True).then_inc(self.mean, 1)

        def pe_var(self, pe, u):
            pe.wait_ge(self.lnsq, u + 1)
            for j in range(8):
                mm = pe.matmul(PS[0:8, 3, 0:64], const("slide")[:, 15 - j:23 - j], sq[:, 0, 64 * j:64 * j + 64],
                               start=(j == 0), stop=(j == 7))
            mm.then_inc(self.var, 1)

        def pe_spread(self, pe, u):
            pe.wait_ge(self.rstd, u + 1)
            for j in range(8):
                mm = pe.matmul(PS[:, 3, 64 * j:64 * j + 64], cst[0:8, j:j + 1].broadcast_to([8, P]), rstd[0:8, 1, :],
                               start=(j == 0), stop=(j == 7))
            mm.then_inc(self.spread, 1)

        def pe_ffn(self, pe, u):
            pe.wait_ge(self.ffn_in, u + 1)
            for j, (a, w) in enumerate(self.CHUNKS):
                bank = 2 * (j % 2)
                if j == 2:
                    pe.wait_ge(self.act_ready, u * 3 + 1)
                pe.matmul(PS[0:w, bank + 1, :], self.w1[:, FFI + a:FFI + a + w], self.xfn[:, :], start=True, stop=True)
                pe.matmul(PS[0:w, bank, :], self.w1[:, a:a + w], self.xfn[:, :], start=True, stop=True)\
                  .then_inc(self.up, 1)
            for j, (a, w) in enumerate(self.CHUNKS):
                if j != 0:
                    pe.wait_ge(self.act_ready, u * 3 + j + 1)
                else:
                    pe.wait_ge(self.act_ready, u * 3 + 2)
                mm = pe.matmul(PS[:, 3, :], self.w2[0:w, j, :], self.hid[0:w, j, :], start=(j == 0), stop=(j == 2))
            mm.then_inc(self.down, 1)

        def act_ln_square(self, act, u):
            act.wait_ge(self.centred, u + 1)
            act.activation(sq[:, 0, :], xc[:, 0, :], ACT.Square).then_inc(self.lnsq, 1)

        def act_ln_root(self, act, u):
            act.wait_ge(self.var, u + 1)
            a = C_AT["eps"][0]
            act.activation(rstd[0:8, 0, :], PS[0:8, 3, 0:64], ACT.Sqrt, bias=cst[0:8, a:a + 1]).then_inc(self.std, 1)

        def act_ffn(self, act, u):
            for j, (a, w) in enumerate(self.CHUNKS):
                act.wait_ge(self.up, u * 3 + j + 1)
                if j == 2:
                    act.wait_ge(self.act_ready, u * 3 + 1)
                act.activation(self.gel[0:w, j % 2, :], PS[0:w, 2 * (j % 2) + 1, :], ACT.Gelu,
                               bias=self.sv[0:w, 6 + j:7 + j]).then_inc(self.gelu, 1)

        def shift(self, dve, b, dst, signal):
            dve.tensor_copy(dst[0:64, :], x[0:64, b, :])
            dve.tensor_copy(dst[64:P, 1:], x[64:P, b, 0:S - 1]).then_inc(signal, 1)

        def dve_wo(self, dve, u):
            b = self.b_of(u)
            dve.wait_ge(self.wo_done, u + 1)
            dve.tensor_tensor(x[:, b, :], x[:, b, :], PS[:, 2, :], ALU.add).then_inc(self.xu_ready, 1)
            dve.wait_ge(self.xu_ready, u * 2 + 1)
            self.shift(dve, b, self.xf, self.xf_ready)

        def dve_ln_centre(self, dve, u):
            dve.wait_ge(self.mean, u + 1)
            dve.wait_ge(self.xf_ready, u + 1)
            dve.tensor_tensor(xc[:, 0, :], self.xf[:, :], PS[:, 3, :], ALU.subtract).then_inc(self.centred, 1)

        def dve_ln_root(self, dve, u):
            dve.wait_ge(self.std, u + 1)
            dve.reciprocal(rstd[0:8, 1, :], rstd[0:8, 0, :]).then_inc(self.rstd, 1)

        def dve_ln_out(self, dve, u):
            dve.wait_ge(self.spread, u + 1)
            dve.wait_ge(self.centred, u + 1)
            dve.tensor_tensor(xc[:, 0, :], xc[:, 0, :], PS[:, 3, :], ALU.mult).then_inc(self.ln_tmp, 1)
            dve.wait_ge(self.ln_tmp, u + 1)
            dve.tensor_scalar(self.xfn[:, :], xc[:, 0, :], self.sv[:, 0:1], self.sv[:, 1:2], ALU.mult, ALU.add)\
               .then_inc(self.ffn_in, 1)

        def dve_ffn(self, dve, u):
            b = self.b_of(u)
            for j, (a, w) in enumerate(self.CHUNKS):
                dve.wait_ge(self.gelu, u * 3 + j + 1)
                dve.scalar_tensor_tensor(self.hid[0:w, j, :], PS[0:w, 2 * (j % 2), :], self.sv[0:w, 3 + j:4 + j],
                                         self.gel[0:w, j % 2, :], ALU.add, ALU.mult).then_inc(self.act_ready, 1)
            dve.wait_ge(self.down, u + 1)
            dve.scalar_tensor_tensor(x[:, b, :], PS[:, 3, :], self.sv[:, 2:3], x[:, b, :], ALU.add, ALU.add)\
               .then_inc(self.xu_ready, 1)
            dve.wait_ge(self.xu_ready, u * 2 + 2)
            self.shift(dve, b, self.xs[:, b, :], self.xs_ready)

        def dve_tables(self, dve, l, u):
            dve.wait_ge(self.qks_in, l * 16 + 16)
            if self.later(u):
                dve.wait_ge(self.qk_used, u * 16)
            for k in range(2):
                for j in range(2):
                    ins = dve.tensor_tensor(self.rot[:, k, j, :, :], self.base[:, k, j, :, :],
                                            self.qks[:, k, j, :].unsqueeze(1).broadcast_to([P, 4, D2]), ALU.mult)
            ins.then_inc(self.rot_ready, 1)

        def at(self, slot):
            self.now = slot[1:]
            return slot[0]

        def pe_slot(self, pe, slot, nxt):
            u = self.at(slot)
            g = lambda k: self.group(u, k)
            self.pe_scores(pe, u, 0)
            for k in range(4):
                self.pe_turn(pe, u, 3, k, g(k))
            self.pe_scores(pe, u, 1)
            self.pe_mix(pe, u, 0)
            if nxt:
                self.pe_proj(pe, self.at(nxt), 0, range(6))
            self.pe_scores(pe, self.at(slot), 2)
            self.pe_mix(pe, u, 1)
            for half in range(2):
                self.pe_turn_o(pe, u, 0, half, g(4 + half))
            if nxt:
                self.pe_proj_turn(pe, self.at(nxt), 1, g(6))
            self.pe_scores(pe, self.at(slot), 3)
            self.pe_mix(pe, u, 2)
            for half in range(2):
                self.pe_turn_o(pe, u, 1, half, self.with_next(nxt, g(10 + half), g(6 + half)))
            if nxt:
                self.pe_proj_turn(pe, self.at(nxt), 2, g(12))
            self.at(slot)
            self.pe_mix(pe, u, 3)
            for half in range(2):
                self.pe_turn_o(pe, u, 2, half, self.with_next(nxt, g(16 + half), g(8 + half)))
            if nxt:
                v = self.at(nxt)
                self.pe_proj(pe, v, 3, (0, 1, 2))
                self.pe_turn(pe, v, 2, 0, g(18))
            self.at(slot)
            for half in range(2):
                self.pe_turn_o(pe, u, 3, half, self.with_next(nxt, g(19 + half), g(10 + half)))
            if nxt:
                self.pe_wo(pe, u)
            else:
                self.pe_wo_last(pe, u)
            self.pe_mean(pe, u)
            if nxt:
                v = self.at(nxt)
                self.pe_proj(pe, v, 3, (3,))
                self.pe_turn(pe, v, 2, 1, g(21))
                self.pe_proj(pe, v, 3, (4,))
            self.at(slot)
            self.pe_var(pe, u)
            if nxt:
                v = self.at(nxt)
                self.pe_turn(pe, v, 2, 2, g(22))
                self.pe_proj(pe, v, 3, (5,))
                self.pe_turn(pe, v, 2, 3, g(23))
            self.at(slot)
            self.pe_spread(pe, u)
            self.pe_ffn(pe, u)

        def with_next(self, nxt, a, b):
            return a if nxt else b

        def pe_wo_last(self, pe, u):
            pe.wait_ge(self.wf_in, self.l_of(u) * self.WF + self.WF)
            pe.wait_ge(self.evac, self.group(u, 12))
            for c in range(8):
                mm = pe.matmul(PS[:, 2, :], self.wo[:, c, :], self.oT[:, c, :], start=(c == 0), stop=(c == 7))
            mm.then_inc(self.wo_done, 1)

        def pe_proj_turn(self, pe, v, t, number):
            self.pe_proj(pe, v, t, (0, 1))
            for k in range(4):
                self.pe_turn(pe, v, t - 1, k, number + k)
                self.pe_proj(pe, v, t, (2 + k,))

        def act_proj_turn(self, act, v, t, number):
            self.act_proj(act, v, t, (0, 1))
            for k in range(4):
                self.act_turn(act, v, t - 1, k, number + k)
                self.act_proj(act, v, t, (2 + k,))

        def act_slot(self, act, slot, nxt):
            u = self.at(slot)
            g = lambda k: self.group(u, k)
            self.act_exp(act, u, 0)
            for k in range(4):
                self.act_turn(act, u, 3, k, g(k))
            self.act_exp(act, u, 1)
            if nxt:
                self.act_proj(act, self.at(nxt), 0, range(6))
            self.act_exp(act, self.at(slot), 2)
            for half in range(2):
                self.act_turn_o(act, u, 0, half, g(4 + half))
            if nxt:
                self.act_proj_turn(act, self.at(nxt), 1, g(6))
            self.act_exp(act, self.at(slot), 3)
            for half in range(2):
                self.act_turn_o(act, u, 1, half, self.with_next(nxt, g(10 + half), g(6 + half)))
            if nxt:
                self.act_proj_turn(act, self.at(nxt), 2, g(12))
            self.at(slot)
            for half in range(2):
                self.act_turn_o(act, u, 2, half, self.with_next(nxt, g(16 + half), g(8 + half)))
            if nxt:
                v = self.at(nxt)
                self.act_proj(act, v, 3, (0, 1, 2))
                self.act_turn(act, v, 2, 0, g(18))
            self.at(slot)
            for half in range(2):
                self.act_turn_o(act, u, 3, half, self.with_next(nxt, g(19 + half), g(10 + half)))
            self.act_ln_square(act, u)
            if nxt:
                v = self.at(nxt)
                self.act_proj(act, v, 3, (3,))
                self.act_turn(act, v, 2, 1, g(21))
                self.act_proj(act, v, 3, (4,))
            self.at(slot)
            self.act_ln_root(act, u)
            if nxt:
                v = self.at(nxt)
                self.act_turn(act, v, 2, 2, g(22))
                self.act_proj(act, v, 3, (5,))
                self.act_turn(act, v, 2, 3, g(23))
            self.at(slot)
            self.act_ffn(act, u)

        def dve_slot(self, dve, slot, nxt, tables=None):
            u = self.at(slot)
            g = lambda k: self.group(u, k)
            self.dve_max(dve, u, 0)
            self.dve_sum(dve, u, 0)
            self.dve_max(dve, u, 1)
            self.dve_out(dve, u, 0, g(0) if isinstance(u, int) else g(0))
            self.dve_sum(dve, u, 1)
            if nxt:
                v = self.at(nxt)
                if tables is not None:
                    self.dve_tables(dve, tables, v)
                self.dve_proj(dve, v, 0, range(4))
            self.dve_max(dve, self.at(slot), 2)
            self.dve_out(dve, u, 1, g(6))
            self.dve_sum(dve, u, 2)
            if nxt:
                self.dve_proj(dve, self.at(nxt), 1, range(4))
            self.dve_max(dve, self.at(slot), 3)
            self.dve_out(dve, u, 2, self.with_next(nxt, g(12), g(8)))
            self.dve_sum(dve, u, 3)
            if nxt:
                self.dve_proj(dve, self.at(nxt), 2, range(4))
            self.at(slot)
            self.dve_out(dve, u, 3, self.with_next(nxt, g(18), g(10)))
            if nxt:
                self.dve_proj(dve, self.at(nxt), 3, (0,))
            self.at(slot)
            self.dve_wo(dve, u)
            self.dve_ln_centre(dve, u)
            if nxt:
                self.dve_proj(dve, self.at(nxt), 3, (1, 2))
            self.at(slot)
            self.dve_ln_root(dve, u)
            if nxt:
                self.dve_proj(dve, self.at(nxt), 3, (3,))
            self.at(slot)
            self.dve_ln_out(dve, u)
            self.dve_ffn(dve, u)

        def rounds(self, eng, body, last):
            with eng.Fori(0, DEPTH - 1) as i:
                body((i * 2, 0, i), (i * 2 + 1, 1, i), None)
                body((i * 2 + 1, 1, i), (i * 2 + 2, 0, i + 1), i + 1)
            L = DEPTH - 1
            body((2 * L, 0, L), (2 * L + 1, 1, L), None)
            last((2 * L + 1, 1, L))

        def pe(self, pe):
            pe.wait_ge(self.c_in, 48)
            pe.wait_ge(self.set_up, 4)
            pe.sem_inc(self.pv_done, 4)
            u = self.at((0, 0, 0))
            self.pe_proj(pe, u, 0, range(6))
            for t in range(1, 4):
                self.pe_proj_turn(pe, u, t, 4 * (t - 1))
            self.rounds(pe, lambda a, b, l: self.pe_slot(pe, a, b), lambda a: self.pe_slot(pe, a, None))

        def act(self, act):
            u = self.at((0, 0, 0))
            self.act_proj(act, u, 0, range(6))
            for t in range(1, 4):
                self.act_proj_turn(act, u, t, 4 * (t - 1))
            self.rounds(act, lambda a, b, l: self.act_slot(act, a, b), lambda a: self.act_slot(act, a, None))

        def dve(self, dve):
            for b in range(B):
                order.link(dve, dve.tensor_copy(xn[:, b, :], x[:, b, :]))
                order.link(dve, dve.tensor_copy(x[:, b, :], self.y0[:, b, :]))
            dve.wait_ge(self.set_up, 4)
            for b in range(B):
                self.shift(dve, b, self.xs[:, b, :], self.xs_ready)
            self.dve_tables(dve, 0, 0)
            dve.sem_inc(self.sub_done, 1)
            dve.sem_inc(self.pt_ready, 1)
            dve.sem_inc(self.on_ready, 1)
            u = self.at((0, 0, 0))
            for t in range(4):
                self.dve_proj(dve, u, t, range(4))
            self.rounds(dve, lambda a, b, l: self.dve_slot(dve, a, b, l), lambda a: self.dve_slot(dve, a, None))
            dve.wait_ge(self.xs_ready, 2 * DEPTH + 2)
            for b in range(B):
                dve.tensor_tensor(x[:, b, :], x[:, b, :], xn[:, b, :], ALU.add).then_inc(x_ready, 1)

        def pool(self, pool):
            for k, what in enumerate((self.xs[64:P, :, 0:1], self.xf[64:P, 0:1], self.kT[:, :, 0:WIN],
                                      self.vs[0:WIN, 0, :])):
                pool.memset(what, 0.0).then_inc(self.set_up, 1)
                pool.wait_ge(self.set_up, k + 1)
            for t in range(4):
                self.pool_proj(pool, 0, t)
            with pool.Fori(1, 2 * DEPTH) as u:
                for t in range(4):
                    self.pool_proj(pool, u, t)

    class LatentAttention:

        KEYS = S + KC
        TK = S // P + 1
        PIECES = B * (S // P + 1) * 2
        UNITS, GROUPS = 16, 8
        WAS = dict(w_in=16, proj=5, act_took=1, dve_took=2, scores=2, maxed=1, exps=1, mixed=1, out_prod=2,
                   turned=2, pT_ready=1, o_ready=2)
        FREE = dict(scores=1, exps=2, turned=2, pT_ready=1, mixed=2, o_ready=1, o_turned=2, oT_ready=1)

        def __init__(self):
            at = self.stack = ExitStack()
            s = lambda name, shape, dt=F32: sb("la_" + name, shape, dt, at=at)
            self.h0 = s("h0", [P, B, S])
            self.wv = s("wv", [P, INNER])
            self.wo = s("wo", [P, INNER // P, P])
            self.wc = s("wc", [P, 2, P])
            self.mraw = s("mraw", [1, B * KC], U8)
            self.mneg = s("mneg", [1, B * KC])
            self.cc = s("cc", [P, 3, B * KC])
            self.cn = s("cn", [P, B * KC])
            self.v = s("v", [P, B, self.TK, INNER])
            self.q = s("q", [P, B, S])
            self.k = s("k", [P, B, self.KEYS])
            self.p = s("p", [P, 2, self.KEYS])
            self.pT = s("pT", [P, 2, self.TK * P])
            self.nmx = s("nmx", [P, 4])
            self.den = s("den", [P, 4])
            self.rden = s("rden", [P, 2, 2])
            self.o = s("o", [P, 2, P])
            self.oT = s("oT", [P, INNER // P, B, S])
            self.w_in, self.proj, self.act_took, self.dve_took = pair.w_in, pair.prod, pair.q_ready, pair.v_ready
            self.scores, self.maxed, self.exps, self.mixed = pair.scores, pair.centred, pair.exps, pair.mixed
            self.out_prod, self.turned, self.pT_ready = pair.out_prod, pair.qk_ready, pair.s1_ready
            self.o_ready = pair.h2_ready
            self.wc_in, self.o_turned, self.oT_ready, self.rdens = [
                sem("la_" + what) for what in ("wc_in", "o_turned", "oT_ready", "rdens")]
            self.valued = dict(proj=self.PIECES, act_took=self.PIECES // 2, dve_took=self.PIECES // 2)

        def c(self, what, k):
            return self.WAS.get(what, 0) + self.valued.get(what, 0) + self.FREE.get(what, 0) + k

        def sp(self, sp):
            for dst, name in ((self.wv[:, :], "la_wv"), (self.wo[:, :, :], "la_wo"), (self.mraw[:, :], "la_mask")):
                sp.dma_start(dst, io[name]).then_inc(self.w_in, 16)
            with sp.Fori(0, INNER // P) as i:
                sp.wait_ge(self.proj, i * 5 + self.c("proj", 0))
                sp.dma_start(self.wc[:, :, :], io["la_wc"][bass.ds(i, 1)].rearrange("a p k n -> p (a k) n"))\
                  .then_inc(self.wc_in, 16)

        def ctx_pe(self, pe):
            pe.matmul(PS[:, 5, 0:B * KC], const("mean"), ctxT[:, :], start=True, stop=True).then_inc(norm.mean_ready, 1)
            pe.wait_ge(norm.squared, n("pe", norm.squared))
            pe.matmul(PS[:, 5, 0:B * KC], const("mean"), self.cc[:, 1, :], start=True, stop=True)\
              .then_inc(norm.var_ready, 1)
            pe.wait_ge(norm.rstd_ready, n("pe", norm.rstd_ready))

        def ctx_act(self, act):
            act.wait_ge(norm.centred, n("act", norm.centred))
            act.activation(self.cc[:, 1, :], self.cc[:, 0, :], ACT.Square).then_inc(norm.squared, 1)
            act.wait_ge(norm.var_ready, n("act", norm.var_ready))
            act.activation(self.cc[:, 2, :], PS[:, 5, 0:B * KC], ACT.Sqrt, bias=const("eps")).then_inc(norm.std_ready, 1)

        def ctx_dve(self, dve):
            dve.wait_ge(norm.mean_ready, n("dve", norm.mean_ready))
            dve.tensor_tensor(self.cc[:, 0, :], ctxT[:, :], PS[:, 5, 0:B * KC], ALU.subtract).then_inc(norm.centred, 1)
            dve.wait_ge(norm.std_ready, n("dve", norm.std_ready))
            order.link(dve, dve.reciprocal(self.cc[:, 2, :], self.cc[:, 2, :]))
            order.link(dve, dve.tensor_tensor(self.cc[:, 0, :], self.cc[:, 0, :], self.cc[:, 2, :], ALU.mult))
            dve.tensor_scalar(self.cn[:, :], self.cc[:, 0, :], column("la_g1"), column("la_b1"), ALU.mult, ALU.add)\
               .then_inc(norm.rstd_ready, 1)
            dve.wait_ge(self.w_in, self.WAS["w_in"] + 48)
            order.link(dve, dve.tensor_copy(self.mneg[:, :], self.mraw[:, :]))
            order.link(dve, dve.tensor_scalar(self.mneg[:, :], self.mneg[:, :], -NEG, NEG, ALU.mult, ALU.add))

        def pieces(self):
            for k in range(self.PIECES):
                b, rest = divmod(k, 2 * self.TK)
                t, half = divmod(rest, 2)
                rows = P if t < self.TK - 1 else KC
                yield k, b, t, half, rows, PS[0:rows, k % 4, :], self.v[0:rows, b, t, 512 * half:512 * half + 512]

        def values_pe(self, pe):
            norm.wait(pe, "pe")
            pe.wait_ge(self.w_in, self.WAS["w_in"] + 48)
            for k, b, t, half, rows, ps, _ in self.pieces():
                if k >= 4:
                    if k % 2 == 0:
                        pe.wait_ge(self.act_took, self.WAS["act_took"] + (k - 4) // 2 + 1)
                    else:
                        pe.wait_ge(self.dve_took, self.WAS["dve_took"] + (k - 4) // 2 + 1)
                lhsT = xn[:, b, P * t:P * t + P] if rows == P else self.cn[:, KC * b:KC * b + KC]
                pe.matmul(ps, lhsT, self.wv[:, 512 * half:512 * half + 512], start=True, stop=True).then_inc(self.proj, 1)
            pe.wait_ge(self.act_took, self.WAS["act_took"] + self.PIECES // 2)
            pe.wait_ge(self.dve_took, self.WAS["dve_took"] + self.PIECES // 2)

        def values_act(self, act):
            for k, b, t, half, rows, ps, dst in self.pieces():
                if k % 2 == 0:
                    act.wait_ge(self.proj, self.WAS["proj"] + k + 1)
                    act.activation(dst, ps, ACT.Copy).then_inc(self.act_took, 1)

        def values_dve(self, dve):
            for k, b, t, half, rows, ps, dst in self.pieces():
                if k % 2 == 1:
                    dve.wait_ge(self.proj, self.WAS["proj"] + k + 1)
                    dve.tensor_copy(dst, ps).then_inc(self.dve_took, 1)

        def unit(self, u):
            return u // 8, (u // 2) % 4, u % 2

        def pe_scores(self, pe, i, u):
            b, t, e = self.unit(u)
            at, h = 2 * (u % 2), slice(64 * e, 64 * e + 64)
            pe.wait_ge(self.exps, i * self.UNITS + self.c("exps", u - 1))
            pe.matmul(PS[:, at, :], self.q[h, b, P * t:P * t + P], self.k[h, b, 0:S], start=True, stop=True)
            pe.matmul(PS[:, at + 1, 0:KC], self.q[h, b, P * t:P * t + P], self.k[h, b, S:], start=True, stop=False)
            pe.matmul(PS[:, at + 1, 0:KC], const("one")[0:1, :], self.mneg[:, KC * b:KC * b + KC],
                      start=False, stop=True).then_inc(self.scores, 1)

        def pe(self, pe):
            pe.sem_inc(self.turned, self.FREE["turned"])
            pe.sem_inc(self.mixed, self.FREE["mixed"])
            pe.sem_inc(self.scores, self.FREE["scores"])
            pe.sem_inc(self.o_turned, self.FREE["o_turned"])
            with pe.Fori(0, INNER // P) as i:
                pe.wait_ge(self.wc_in, i * 16 + 16)
                pe.wait_ge(self.pT_ready, i * self.UNITS + self.c("pT_ready", 0))
                wq, wk = self.wc[:, 0, :], self.wc[:, 1, :]
                pe.matmul(PS[:, 4, :], wq, xn[:, 0, :], start=True, stop=True).then_inc(self.proj, 1)
                pe.matmul(PS[:, 5, :], wk, xn[:, 0, :], start=True, stop=True).then_inc(self.proj, 1)
                pe.wait_ge(self.o_ready, i * self.GROUPS + self.c("o_ready", 0))
                pe.matmul(PS[:, 6, 0:B * KC], wk, self.cn[:, :], start=True, stop=True).then_inc(self.proj, 1)
                pe.wait_ge(self.oT_ready, i * B + self.c("oT_ready", 0))
                pe.matmul(PS[:, 7, :], wq, xn[:, 1, :], start=True, stop=True).then_inc(self.proj, 1)
                pe.wait_ge(self.act_took, i * 3 + self.c("act_took", 1))
                pe.matmul(PS[:, 4, :], wk, xn[:, 1, :], start=True, stop=True).then_inc(self.proj, 1)
                pe.wait_ge(self.act_took, i * 3 + self.c("act_took", 2))
                pe.wait_ge(self.dve_took, i * 2 + self.c("dve_took", 1))
                for u in range(2):
                    self.pe_scores(pe, i, u)
                pe.wait_ge(self.act_took, i * 3 + self.c("act_took", 3))
                pe.wait_ge(self.dve_took, i * 2 + self.c("dve_took", 2))
                for u in range(self.UNITS):
                    b, t, e = self.unit(u)
                    g = u // 2
                    pe.wait_ge(self.pT_ready, i * self.UNITS + self.c("pT_ready", u))
                    pe.wait_ge(self.exps, i * self.UNITS + self.c("exps", u + 1))
                    for k in range(self.TK):
                        w = P if k < self.TK - 1 else KC
                        mm = pe.transpose(PS[0:w, 4 + k // 4, P * (k % 4):P * (k % 4) + P],
                                          self.p[:, u % 2, P * k:P * k + w], ident)
                    mm.then_inc(self.turned, 1)
                    if u + 2 < self.UNITS:
                        self.pe_scores(pe, i, u + 2)
                    if e == 0:
                        pe.wait_ge(self.o_ready, i * self.GROUPS + self.c("o_ready", g))
                        if g:
                            self.pe_turn_o(pe, i, g - 1)
                    pe.wait_ge(self.pT_ready, i * self.UNITS + self.c("pT_ready", u + 1))
                    for k in range(self.TK):
                        w = P if k < self.TK - 1 else KC
                        mm = pe.matmul(PS[:, 6, 64 * e:64 * e + 64], self.pT[0:w, u % 2, P * k:P * k + P],
                                       self.v[0:w, b, k, bass.ds(i * P + 64 * e, 64)],
                                       start=(k == 0), stop=(k == self.TK - 1))
                    mm.then_inc(self.mixed, 1)
                self.pe_turn_o(pe, i, self.GROUPS - 1)
            pe.wait_ge(self.oT_ready, self.c("oT_ready", INNER // P * B))
            for b in range(B):
                for c in range(INNER // P):
                    mm = pe.matmul(PS[:, b, :], self.wo[:, c, :], self.oT[:, c, b, :],
                                   start=(c == 0), stop=(c == INNER // P - 1))
                mm.then_inc(self.out_prod, 1)

        def pe_turn_o(self, pe, i, g):
            if g == 4:
                pe.wait_ge(self.oT_ready, i * B + self.c("oT_ready", 1))
            pe.wait_ge(self.o_ready, i * self.GROUPS + self.c("o_ready", g + 1))
            pe.transpose(PS[:, 7, P * (g % 4):P * (g % 4) + P], self.o[:, g % 2, :], ident).then_inc(self.o_turned, 1)

        def act(self, act):
            act.sem_inc(self.exps, self.FREE["exps"])
            act.sem_inc(self.oT_ready, self.FREE["oT_ready"])
            with act.Fori(0, INNER // P) as i:
                act.wait_ge(self.scores, i * self.UNITS + self.c("scores", 0))
                act.wait_ge(self.proj, i * 5 + self.c("proj", 1))
                act.activation(self.q[:, 0, :], PS[:, 4, :], ACT.Copy, scale=0.125).then_inc(self.act_took, 1)
                act.wait_ge(self.proj, i * 5 + self.c("proj", 3))
                act.activation(self.k[:, :, S:], PS[:, 6, 0:B * KC].rearrange("p (b k) -> p b k", b=B), ACT.Copy)\
                   .then_inc(self.act_took, 1)
                act.wait_ge(self.proj, i * 5 + self.c("proj", 4))
                act.activation(self.q[:, 1, :], PS[:, 7, :], ACT.Copy, scale=0.125).then_inc(self.act_took, 1)
                for u in range(self.UNITS):
                    act.wait_ge(self.maxed, i * self.UNITS + self.c("maxed", u + 1))
                    act.wait_ge(self.turned, i * self.UNITS + self.c("turned", u - 1))
                    if u % 2 == 0:
                        act.wait_ge(self.o_ready, i * self.GROUPS + self.c("o_ready", u // 2 - 1))
                    act.activation(self.p[:, u % 2, :], self.span(u), ACT.Exp, bias=self.nmx[:, u % 4:u % 4 + 1],
                                   accum_out=self.den[:, u % 4:u % 4 + 1]).then_inc(self.exps, 1)
                    if u == 9:
                        self.act_oT(act, i, 0)
                self.act_oT(act, i, 1)

        def act_oT(self, act, i, b):
            act.wait_ge(self.o_turned, i * self.GROUPS + self.c("o_turned", 4 * b + 4))
            act.activation(self.oT[:, bass.ds(i, 1), b, :].rearrange("p a s -> p (a s)"), PS[:, 7, :], ACT.Copy)\
               .then_inc(self.oT_ready, 1)

        def span(self, u):
            return PS[:, 2 * (u % 2):2 * (u % 2) + 2, :].rearrange("p b n -> p (b n)")[:, 0:self.KEYS]

        def dve(self, dve):
            dve.sem_inc(self.pT_ready, self.FREE["pT_ready"])
            dve.sem_inc(self.o_ready, self.FREE["o_ready"])
            with dve.Fori(0, INNER // P) as i:
                dve.wait_ge(self.scores, i * self.UNITS + self.c("scores", 0))
                for b in range(B):
                    dve.wait_ge(self.proj, i * 5 + self.c("proj", 3 * b + 2))
                    dve.tensor_copy(self.k[:, b, 0:S], PS[:, 5 - b, :]).then_inc(self.dve_took, 1)
                for u in range(2):
                    self.dve_max(dve, i, u)
                for u in range(self.UNITS):
                    dve.wait_ge(self.turned, i * self.UNITS + self.c("turned", u + 1))
                    dve.wait_ge(self.mixed, i * self.UNITS + self.c("mixed", u - 1))
                    dve.tensor_copy(self.pT[:, u % 2, 0:512], PS[:, 4, :])
                    dve.tensor_copy(self.pT[0:KC, u % 2, 512:], PS[0:KC, 5, 0:P]).then_inc(self.pT_ready, 1)
                    if u + 2 < self.UNITS:
                        self.dve_max(dve, i, u + 2)
                    if u % 2 == 1:
                        g = u // 2
                        dve.wait_ge(self.mixed, i * self.UNITS + self.c("mixed", u + 1))
                        dve.wait_ge(self.o_turned, i * self.GROUPS + self.c("o_turned", g - 1))
                        dve.reciprocal(self.rden[:, g % 2, :], self.den[:, 2 * (g % 2):2 * (g % 2) + 2])\
                           .then_inc(self.rdens, 1)
                        dve.wait_ge(self.rdens, i * self.GROUPS + g + 1)
                        dve.tensor_tensor(self.o[:, g % 2, :].rearrange("p (e d) -> p e d", e=2),
                                          PS[:, 6, 0:P].rearrange("p (e d) -> p e d", e=2),
                                          self.rden[:, g % 2, :].unsqueeze(2).broadcast_to([P, 2, D2]), ALU.mult)\
                           .then_inc(self.o_ready, 1)
            for b in range(B):
                dve.wait_ge(self.out_prod, self.WAS["out_prod"] + b + 1)
                dve.tensor_tensor(x[:, b, :], x[:, b, :], PS[:, b, :], ALU.add).then_inc(x_ready, 1)

        def dve_max(self, dve, i, u):
            dve.wait_ge(self.scores, i * self.UNITS + self.c("scores", u + 1))
            dve.tensor_reduce(self.nmx[:, u % 4:u % 4 + 1], self.span(u), X, ALU.max, negate=True)\
               .then_inc(self.maxed, 1)

    align = Align()
    align.stack.close()
    quantised = Quantised()
    quantised.stack.close()
    attend1 = ContextAttention("l1", True, 0)
    attend1.stack.close()
    pair = PairAttention()
    experts1 = Experts("m1", ACT.Gelu, 1.0, True, 0)
    experts1.stack.close()
    pair.stack.close()
    attend2 = ContextAttention("l2", False, 1)
    attend2.stack.close()
    stack = Stack()
    stack.stack.close()
    latents = LatentAttention()
    latents.stack.close()
    experts3 = Experts("m3", ACT.Silu, 1.5, False, 1)
    h7 = sb("h7", [P, B, S], at=experts3.stack)
    experts3.stack.close()
    final = sem("final")
    out = io["out"]
    block = ctx.enter_context(nc.Block())

    @block.sync
    def _(sp):
        sp.dma_start(x[:, :, :], io["xT"]).then_inc(loaded, 16)
        sp.dma_start(cst[:, :], io["cst"]).then_inc(loaded, 16)
        sp.dma_start(ctxT[:, :], io["ctxT"]).then_inc(loaded, 16)
        sp.dma_start(ctxN[:, :, :], io["ctxN"]).then_inc(loaded, 16)
        sp.dma_start(vec[:, :], io["vec"]).then_inc(loaded, 16)
        sp.dma_start(row[:, :], io["row"]).then_inc(loaded, 16)
        align.sp(sp)
        sp.wait_ge(x_ready, 2)
        quantised.sp(sp)
        sp.wait_ge(x_ready, 4)
        attend1.sp(sp)
        sp.wait_ge(x_ready, 6)
        pair.sp(sp)
        experts1.sp(sp)
        sp.wait_ge(x_ready, 8)
        attend2.sp(sp)
        sp.wait_ge(x_ready, 10)
        stack.sp(sp)
        sp.wait_ge(x_ready, 12)
        latents.sp(sp)
        sp.wait_ge(x_ready, 14)
        experts3.sp(sp)
        sp.wait_ge(x_ready, 2 * PARTS)
        sp.dma_start(out, x[:, :, :]).then_inc(final, 16)
        sp.wait_ge(final, 16)

    @block.gpsimd
    def _(pool):
        align.pool(pool)
        pool.wait_ge(x_ready, 4)
        attend1.pool(pool)
        pool.wait_ge(x_ready, 6)
        experts1.pool(pool)
        pool.wait_ge(x_ready, 8)
        attend2.pool(pool)
        pool.wait_ge(x_ready, 10)
        stack.pool(pool)

    @block.scalar
    def _(act):
        act.wait_ge(loaded, 16 * LOADS)
        norm.act(act)
        align.act(act)
        norm.act(act)
        quantised.weights_act(act)
        quantised.act(act)
        attend1.act_prepare(act)
        norm.act(act)
        attend1.act(act)
        norm.act(act)
        pair.act(act)
        experts1.gate_act(act)
        experts1.act(act)
        attend2.act_prepare(act)
        norm.act(act)
        attend2.act(act)
        norm.act(act)
        stack.act(act)
        norm.act(act)
        latents.ctx_act(act)
        norm.act(act)
        latents.values_act(act)
        latents.act(act)
        norm.act(act)
        norm.act(act)
        experts3.gate_act(act)
        experts3.act(act)

    @block.tensor
    def _(pe):
        pe.wait_ge(loaded, 16 * LOADS)
        norm.pe(pe, x, None)
        align.pe(pe)
        norm.pe(pe, x, x_ready)
        quantised.weights_pe(pe)
        quantised.pe(pe)
        attend1.pe_prepare(pe)
        norm.pe(pe, x, x_ready)
        attend1.pe(pe)
        norm.pe(pe, x, x_ready)
        pair.pe(pe)
        experts1.gate_pe(pe)
        experts1.pe(pe)
        attend2.pe_prepare(pe)
        norm.pe(pe, x, x_ready)
        attend2.pe(pe)
        norm.pe(pe, x, x_ready)
        stack.pe(pe)
        norm.pe(pe, x, x_ready)
        latents.ctx_pe(pe)
        norm.wait(pe, "pe")
        norm.pe(pe, latents.h0, None)
        latents.values_pe(pe)
        latents.pe(pe)
        norm.pe(pe, x, x_ready)
        norm.wait(pe, "pe")
        norm.pe(pe, h7, None)
        experts3.gate_pe(pe)
        experts3.pe(pe)

    @block.vector
    def _(dve):
        dve.wait_ge(loaded, 16 * LOADS)
        norm.dve(dve, x, xn)
        align.dve(dve)
        norm.dve(dve, x, xn)
        quantised.weights_dve(dve)
        quantised.dve(dve)
        attend1.dve_prepare(dve)
        norm.dve(dve, x, xn)
        attend1.dve(dve)
        norm.dve(dve, x, pair.h0)
        pair.dve(dve)
        experts1.gate_dve(dve)
        experts1.dve(dve, pair.h2)
        attend2.dve_prepare(dve)
        norm.dve(dve, x, xn)
        attend2.dve(dve)
        norm.dve(dve, x, stack.y0)
        stack.dve(dve)
        norm.dve(dve, x, latents.h0)
        latents.ctx_dve(dve)
        norm.wait(dve, "dve")
        norm.dve(dve, latents.h0, xn, column("la_g2"), column("la_b2"))
        latents.values_dve(dve)
        latents.dve(dve)
        norm.dve(dve, x, h7)
        norm.wait(dve, "dve")
        norm.dve(dve, h7, xn, column("m3_g"), column("m3_b"))
        experts3.gate_dve(dve)
        experts3.dve(dve, h7)

    ctx.close()


def spans(parts):
    at, out = 0, {}
    for name, width in parts:
        out[name] = (at, width)
        at += width
    return out, at


C_AT, C_ALL = spans([("ident", P), ("mean", P), ("one", P), ("slide", 31), ("eps", 1), ("rinit", SC + 1),
                     ("iota", S), ("blk8", P), ("hm", H), ("kidx", E), ("threehalves", 1)])
VECTORS = {"l1_bq": "L1_xattn_bq", "l1_bk": "L1_xattn_bk", "l1_bo": "L1_xattn_bo",
           "pa_ln1w": "L1_ffn_ln1_weight", "pa_ln1b": "L1_ffn_ln1_bias",
           "pa_ln2w": "L1_ffn_ln2_weight", "pa_ln2b": "L1_ffn_ln2_bias",
           "l2_bq": "L2_xattn_bq", "l2_bk": "L2_xattn_bk", "l2_bo": "L2_xattn_bo",
           "la_g1": "L3_xattn_g1", "la_b1": "L3_xattn_b1", "la_g2": "L3_xattn_g2", "la_b2": "L3_xattn_b2",
           "m3_g": "L3_ffn_gamma", "m3_b": "L3_ffn_beta"}
V_AT, V_ALL = spans([(k, 1) for k in VECTORS])
R_AT, R_ALL = spans([("l1_bv", P), ("l2_bv", P)])


def constants():
    c = np.zeros((P, C_ALL), np.float32)

    def put(name, a):
        at, w = C_AT[name]
        c[:, at:at + w] = a
    put("ident", np.eye(P))
    put("mean", 1.0 / P)
    put("one", 1.0)
    s = np.zeros((P, 31)); s[:, 15] = 1.0 / P
    put("slide", s)
    put("eps", EPS)
    put("threehalves", 1.5)
    r = np.full((P, SC + 1), BIG); r[SEG - 1, 0] = 0; r[2 * SEG - 1, 0] = 0
    put("rinit", r)
    put("iota", np.arange(S)[None])
    head = np.arange(P) // DH
    put("blk8", head[:, None] == head[None])
    put("hm", head[:, None] == np.arange(H)[None])
    put("kidx", (E - np.arange(E))[None])
    r = np.arange(HKP)
    sel = (r[None] % KC == np.arange(KC)[:, None]) & (r[None] < HK)
    r = r.reshape(HKC, P).T
    hmask = (r[:, :, None] // KC == head[None, None]) & (r[:, :, None] < HK)
    half = np.arange(0, D2, 2, dtype=np.float32)
    token = np.arange(S, dtype=np.float32)
    freqs = token[:, None] * (1.0 / np.float32(10000.0) ** (half / D2)).astype(np.float32)[None]
    scale = ((half + 0.4 * D2) / (1.4 * D2)).astype(np.float32)[None] ** ((token - S // 2) / (WIN // 2))[:, None]
    sign = np.where(np.arange(D2) < D2 // 2, -1.0, 1.0)[None]
    both = lambda m: np.concatenate([m, m], axis=1)
    base = np.stack([np.stack([both(np.cos(freqs) * s), both(np.sin(freqs) * s) * sign])
                     for s in (scale, 1.0 / scale)])
    base = base.reshape(2, 2, 4, P, D2).transpose(3, 0, 1, 2, 4)
    i, jj = np.arange(P)[:, None] % WIN, np.arange(2 * WIN)[None]
    seen = (jj >= i) & (jj <= i + WIN)
    first = seen & ~((np.arange(P)[:, None] < WIN) & (jj < WIN))
    wmask = np.where(np.stack([first, seen], axis=1), 0.0, NEG)
    bf16 = mybir.dt.np(BF16)
    return {"st_base": np.ascontiguousarray(base, np.float32), "st_wmask": wmask.astype(bf16),
            "identb": np.eye(P).astype(bf16), "cst": c, "sel": sel.astype(np.float32), "hmask": hmask.astype(np.float32)}


def lay(inputs):
    f = lambda k: np.asarray(inputs[k])
    a = dict(constants())
    a["xT"] = np.ascontiguousarray(f("x").reshape(T, P).T.reshape(P, B, S))
    a["ctxT"] = np.ascontiguousarray(f("ctx_1024").reshape(B * KC, P).T)
    a["ctxN"] = np.ascontiguousarray(f("ctx_1024").transpose(1, 0, 2))
    for k, w in (("wg", "gate"), ("wu", "up")):
        a["q_" + k] = np.ascontiguousarray(f("L0_ffn_w_" + w).reshape(QW // P, P, P).transpose(1, 0, 2)).reshape(P, QW)
    a["q_wd"] = f("L0_ffn_w_down")
    a["vec"] = np.stack([f(k) for k in VECTORS.values()], axis=1)
    a["row"] = np.concatenate([f("L1_xattn_bv"), f("L2_xattn_bv")])[None]
    a["l1_w"] = np.stack([f("L1_xattn_W" + k).T for k in "qkvo"], axis=1)
    a["l2_w"] = np.stack([f("L2_xattn_W" + k) for k in "qkvo"], axis=1)
    for t, k in (("l1", "mask_1x1xSxS2_ik0"), ("l2", "mask_1x1xSxS2_fk1")):
        a[t + "_mask"] = np.ascontiguousarray(f(k)[0, 0].reshape(NT // B, P, KC).transpose(1, 0, 2))
    g = f("L1_ffn_qkv_weight").reshape(H // 2, 4, DH, P)
    twice = lambda k: np.repeat(g[:, k:k + 1], 2, axis=1)
    a["pa_w"] = np.stack([np.ascontiguousarray(w.reshape(P, P).T) for w in
                          (g[:, 0:2], twice(2), twice(3), f("L1_ffn_proj_weight"))], axis=1)
    a["m1_router"] = f("L1_ffn_router_weight")
    a["st_wqkv"], a["st_wo"] = f("L2_ffn_Wqkv"), f("L2_ffn_Wo")
    a["st_w1"], a["st_w2"] = f("L2_ffn_W1"), f("L2_ffn_W2")
    scales = np.stack([f("L2_ffn_q_scale"), f("L2_ffn_k_scale")], axis=1)
    a["st_qks"] = np.stack([scales, np.roll(scales, D2 // 2, axis=2)], axis=2)
    b1 = np.zeros((DEPTH, 2, 3 * P), np.float32)
    b1[:, :, 0:FFI] = f("L2_ffn_b1").reshape(DEPTH, 2, FFI)
    a["st_sv"] = np.concatenate([np.stack([f("L2_ffn_ln_g"), f("L2_ffn_ln_b"), f("L2_ffn_b2")], axis=2),
                                 b1.reshape(DEPTH, 6, P).transpose(0, 2, 1)], axis=2)
    wkv = f("L3_xattn_Wkv")
    a["la_wc"] = np.ascontiguousarray(np.stack([f("L3_xattn_Wq"), wkv[:, 0:INNER]]).reshape(2, P, INNER // P, P)
                                      .transpose(2, 1, 0, 3))
    a["la_wv"] = np.ascontiguousarray(wkv[:, INNER:])
    a["la_wo"] = np.ascontiguousarray(f("L3_xattn_Wout").reshape(INNER // P, P, P).transpose(1, 0, 2))
    a["la_mask"] = f("mask_BxS2_bk0").reshape(1, B * KC)
    a["m3_router"] = np.ascontiguousarray(f("L3_ffn_router_w").T)
    a["m3_w1"], a["m3_w2"] = f("L3_ffn_W1"), f("L3_ffn_W2")
    a["m1_w1"], a["m1_w2"] = f("L1_ffn_moe_w1"), f("L1_ffn_moe_w2")
    return a


def kernel(**inputs):
    import concourse.bacc as bacc
    from concourse.bass_utils import run_bass_kernel_spmd

    nc = bacc.Bacc("TRN2", target_bir_lowering=False, num_devices=1)
    arrays = lay(inputs)
    io = {k: nc.dram_tensor("in_" + k, a.shape, mybir.dt.from_np(a.dtype), kind="ExternalInput").ap()
          for k, a in arrays.items()}
    io["out"] = nc.dram_tensor("out_x", (P, B, S), F32, kind="ExternalOutput").ap()
    build(nc, io)
    r = run_bass_kernel_spmd(nc, [{"in_" + k: a for k, a in arrays.items()}], core_ids=[0])
    got = r.results[0]["out_x"]
    return np.ascontiguousarray(got.reshape(P, T).T.reshape(B, S, P))
```

```python
from contextlib import ExitStack

import numpy as np

import concourse.bass as bass
from concourse import mybir

F32 = mybir.dt.float32
F16 = mybir.dt.float16
BF16 = mybir.dt.bfloat16
I32 = mybir.dt.int32
U8 = mybir.dt.uint8
ALU = mybir.AluOpType
ACT = mybir.ActivationFunctionType
X = mybir.AxisListType.X

PARTS = 8
P = 128
B = 2
S = 512
T = B * S
NT = T // P
KC = 77
H = 16
EPS = 1e-5
BIG = 1e30
NEG = -1e30

SEG = 8
SC = S // SEG
STEPS = KC + SEG - 1
ROWS = SEG + KC + SEG
RING = 12
COPY = 4
assert STEPS % RING == 0 and RING % COPY == 0

DH = P // H
HK = H * KC
HKC = -(-HK // P)
HKP = HKC * P
HGROUPS = ((0, 6), (6, 6), (12, 4))

E = 8
FF = 512
CAP = -(-T * 2 * 5 // (E * 4))
assert CAP == 320

DEPTH = 6
D2 = 64
WIN = 32
INNER = H * D2
FFI = 341
GUESS = float(0x5f3759df - 2 ** 30 - 2 ** 22)


QW = 384
QMAX = 32767.0
MAGIC = 1.5 * 2.0 ** 23


class Tally:

    def __init__(self):
        self.seen = {}

    def __call__(self, who, sem):
        key = (who, sem.name)
        self.seen[key] = self.seen.get(key, 0) + 1
        return self.seen[key]


def build(nc, io):
    ctx = ExitStack()
    n = Tally()

    def sem(name):
        return ctx.enter_context(nc.semaphore(name))

    def sb(name, shape, dt=F32, at=None):
        return (at or ctx).enter_context(nc.sbuf_tensor(name, shape, dt))

    def dram(name, shape, dt=F32):
        return nc.dram_tensor(name, shape, dt, kind="Internal").ap()

    def view(ap, offset, dims):
        return bass.AP(tensor=ap.tensor, offset=offset, ap=dims)

    PS = ctx.enter_context(nc.psum_tensor("PS", [P, 8, 512], F32))

    x = sb("x", [P, B, S])
    xn = sb("xn", [P, B, S])
    xc = sb("xc", [P, B, S])
    sq = sb("sq", [P, B, S])
    rstd = sb("rstd", [16, 2, 64])
    cst = sb("cst", [P, C_ALL])
    vec = sb("vec", [P, V_ALL])
    row = sb("row", [1, R_ALL])
    ctxT = sb("ctxT", [P, B * KC])
    ctxN = sb("ctxN", [KC, B, P])

    def const(name):
        a, w = C_AT[name]
        return cst[:, a:a + w]

    def column(name):
        a = V_AT[name][0]
        return vec[:, a:a + 1]

    ident = const("ident")

    loaded = sem("loaded")
    x_ready = sem("x_ready")
    vec_step = sem("vec_step")
    LOADS = 6

    class Chain:

        def __init__(self, s, who="dve"):
            self.s, self.who = s, who

        def step(self, ins):
            ins.then_inc(self.s, 1)
            self.at = n(self.who, self.s)

        def link(self, eng, ins):
            ins.then_inc(self.s, 1)
            eng.wait_ge(self.s, n(self.who, self.s))

    order = Chain(vec_step)

    class Norm:

        def __init__(self, tag, parts=(0, 1), banks=(6, 7), chain=None):
            self.parts, self.banks, self.chain = parts, banks, chain or order
            self.mean_ready = sem(tag + "_mean_ready")
            self.centred = sem(tag + "_centred")
            self.squared = sem(tag + "_squared")
            self.var_ready = sem(tag + "_var_ready")
            self.std_ready = sem(tag + "_std_ready")
            self.rstd_ready = sem(tag + "_rstd_ready")
            self.spread_ready = sem(tag + "_spread_ready")
            self.normed = sem(tag + "_normed")
            self.uses = {}

        def wait(self, eng, who, halves=2):
            eng.wait_ge(self.normed, 2 * (self.uses[who] - 1) + halves)

        def rows(self, b):
            at = 8 * self.parts.index(b)
            return at, 8 * len(self.parts)

        def pe(self, pe, src, src_ready):
            self.uses["pe"] = self.uses.get("pe", 0) + 1
            for b in self.parts:
                if src_ready is not None:
                    pe.wait_ge(src_ready, n("pe", src_ready))
                pe.matmul(PS[:, self.banks[b], :], const("mean"), src[:, b, :], start=True, stop=True)\
                  .then_inc(self.mean_ready, 1)
            for b in self.parts:
                at, rows = self.rows(b)
                pe.wait_ge(self.squared, n("pe", self.squared))
                for j in range(8):
                    mm = pe.matmul(PS[0:rows, self.banks[self.parts[0]], 0:64],
                                   const("slide")[:, 15 - at - j:15 - at - j + rows],
                                   sq[:, b, 64 * j:64 * j + 64],
                                   start=(at + j == 0), stop=(at + j == rows - 1))
            mm.then_inc(self.var_ready, 1)
            pe.wait_ge(self.rstd_ready, n("pe", self.rstd_ready))
            for b in self.parts:
                at, rows = self.rows(b)
                for j in range(8):
                    mm = pe.matmul(PS[:, self.banks[b], 64 * j:64 * j + 64],
                                   cst[0:rows, at + j:at + j + 1].broadcast_to([rows, P]),
                                   rstd[0:rows, 1, :], start=(j == 0), stop=(j == 7))
                mm.then_inc(self.spread_ready, 1)

        def act(self, act):
            self.uses["act"] = self.uses.get("act", 0) + 1
            for b in self.parts:
                act.wait_ge(self.centred, n("act", self.centred))
                act.activation(sq[:, b, :], xc[:, b, :], ACT.Square).then_inc(self.squared, 1)
            _, rows = self.rows(self.parts[0])
            act.wait_ge(self.var_ready, n("act", self.var_ready))
            act.activation(rstd[0:rows, 0, :], PS[0:rows, self.banks[self.parts[0]], 0:64], ACT.Sqrt,
                           bias=cst[0:rows, C_AT["eps"][0]:C_AT["eps"][0] + 1]).then_inc(self.std_ready, 1)

        def dve(self, dve, src, dst, gamma=None, beta=None):
            self.uses["dve"] = self.uses.get("dve", 0) + 1
            c = self.chain
            for b in self.parts:
                dve.wait_ge(self.mean_ready, n("dve", self.mean_ready))
                dve.tensor_tensor(xc[:, b, :], src[:, b, :], PS[:, self.banks[b], :], ALU.subtract)\
                   .then_inc(self.centred, 1)
            _, rows = self.rows(self.parts[0])
            dve.wait_ge(self.std_ready, n("dve", self.std_ready))
            dve.reciprocal(rstd[0:rows, 1, :], rstd[0:rows, 0, :]).then_inc(self.rstd_ready, 1)
            for b in self.parts:
                dve.wait_ge(self.spread_ready, n("dve", self.spread_ready))
                if gamma is None:
                    dve.tensor_tensor(dst[:, b, :], xc[:, b, :], PS[:, self.banks[b], :], ALU.mult)\
                       .then_inc(self.normed, 1)
                else:
                    c.link(dve, dve.tensor_tensor(xc[:, b, :], xc[:, b, :], PS[:, self.banks[b], :],
                                                  ALU.mult))
                    dve.tensor_scalar(dst[:, b, :], xc[:, b, :], gamma, beta, ALU.mult, ALU.add)\
                       .then_inc(self.normed, 1)

    norm = Norm("ln")

    class Align:
        def __init__(self):
            at = self.stack = ExitStack()
            self.aa = sb("al_aa", [KC, B], at=at)
            self.ctxm2 = sb("al_ctxm2", [P, B * KC], at=at)
            self.dist = sb("al_dist", [KC, B, S], at=at)
            self.big = sb("al_big", [KC, B, S + 1], at=at)
            self.skew = sb("al_skew", [32, STEPS, SC], at=at)
            self.hist = sb("al_hist", [32, STEPS, SC], at=at)
            self.ring = sb("al_ring", [32, RING, SC + 1], at=at)
            self.low = sb("al_low", [32, SC], at=at)
            self.cur = sb("al_cur", [KC, B, S + 1], at=at)
            self.t0 = sb("al_t0", [KC, B, S], at=at)
            self.t1 = sb("al_t1", [KC, B, S], at=at)
            self.keep = sb("al_keep", [KC, B, S], at=at)
            self.enter = sb("al_enter", [KC, B, S], F16, at=at)
            self.left = sb("al_left", [KC, B, S], at=at)
            self.path = sb("al_path", [B, KC, S], F16, at=at)
            self.ent = sb("al_ent", [B, KC], at=at)
            self.entT = sb("al_entT", [KC, B], at=at)
            self.exT = sb("al_exT", [KC, B], at=at)
            self.pick = sb("al_pick", [B, 2, S], at=at)
            self.plane = dram("al_plane", [B, ROWS, S])
            self.costs = dram("al_costs", [B, ROWS, S])
            self.big_set = sem("al_big_set")
            self.pads_out = sem("al_pads_out")
            self.aa_ready = sem("al_aa_ready")
            self.xsq = sem("al_xsq")
            self.prod_ready = sem("al_prod_ready")
            self.d2_ready = sem("al_d2_ready")
            self.dist_ready = sem("al_dist_ready")
            self.plane_out = sem("al_plane_out")
            self.skew_in = sem("al_skew_in")
            self.scan_done = sem("al_scan_done")
            self.shifted = sem("al_shifted")
            self.ctxm2_ready = sem("al_ctxm2_ready")
            self.ring_free = sem("al_ring_free")
            self.costs_out = sem("al_costs_out")
            self.rows_in = sem("al_rows_in")
            self.enter_ready = sem("al_enter_ready")
            self.path_in = sem("al_path_in")
            self.walked = sem("al_walked")
            self.ent_ready = sem("al_ent_ready")
            self.entT_ready = sem("al_entT_ready")
            self.on_ready = sem("al_on_ready")
            self.sum_ready = sem("al_sum_ready")

        def strip(self, plane, b, row0):
            return view(plane, (b * ROWS + 1 + row0) * S + (SEG - 1) * SC,
                        [[S - SC, SEG], [S, STEPS], [1, SC]])

        def pool(self, pool):
            pool.memset(self.big[:, :, :], BIG).then_inc(self.big_set, 1)
            pool.memset(self.skew[:, :, :], BIG).then_inc(self.big_set, 1)
            pool.memset(self.cur[:, :, :], BIG).then_inc(self.big_set, 1)
            pool.memset(self.path[:, :, :], 0.0).then_inc(self.big_set, 1)

        def sp(self, sp):
            sp.wait_ge(self.big_set, 1)
            for b in range(B):
                for r in (0, SEG + KC):
                    sp.dma_start(self.plane[b, r:r + SEG, :], self.big[0:SEG, b, 0:S]).then_inc(self.pads_out, 16)
            for b in range(B):
                sp.wait_ge(self.dist_ready, b + 1)
                sp.dma_start(self.plane[b, SEG:SEG + KC, :], self.dist[:, b, :]).then_inc(self.plane_out, 16)
            sp.wait_ge(self.pads_out, 64)
            sp.wait_ge(self.plane_out, 32)
            sp.wait_ge(self.big_set, 3)
            for b in range(B):
                sp.dma_start(self.skew[SEG * b:SEG * b + SEG, :, :], self.strip(self.plane, b, 0))\
                  .then_inc(self.skew_in, 16)
            sp.wait_ge(self.ring_free, STEPS // COPY + RING // COPY)
            for b in range(B):
                sp.dma_start(self.strip(self.costs, b, 0), self.hist[SEG * b:SEG * b + SEG, :, :])\
                  .then_inc(self.costs_out, 16)
            sp.wait_ge(self.costs_out, 32)
            for b in range(B):
                sp.dma_start(self.cur[:, b, 1:], self.costs[b, SEG:SEG + KC, :]).then_inc(self.rows_in, 16)
                sp.dma_start(self.big[1:KC, b, 1:], self.costs[b, SEG:SEG + KC - 1, :]).then_inc(self.rows_in, 16)
            sp.wait_ge(self.enter_ready, 1)
            sp.wait_ge(self.big_set, 4)
            for b in range(B):
                sp.dma_start(self.path[b:b + 1, :, :], self.enter[:, b, :]).then_inc(self.path_in, 16)

        def act(self, act):
            act.wait_ge(loaded, 16 * LOADS)
            for b in range(B):
                act.activation(self.dist[:, b, 0:P], ctxN[:, b, :], ACT.Square,
                               accum_out=self.aa[:, b:b + 1]).then_inc(self.aa_ready, 1)
            norm.wait(act, "act")
            for b in range(B):
                act.activation(sq[:, b, :], xn[:, b, :], ACT.Square).then_inc(self.xsq, 1)
            for b in range(B):
                act.wait_ge(self.d2_ready, b + 1)
                act.activation(self.dist[:, b, :], self.t0[:, b, :], ACT.Sqrt).then_inc(self.dist_ready, 1)
            act.sem_inc(self.ring_free, RING // COPY)
            with act.Fori(0, STEPS // RING) as i:
                for k in range(RING // COPY):
                    act.wait_ge(self.scan_done, i * RING + COPY * (k + 1) + 1)
                    act.activation(self.hist[:, bass.ds(i * RING + COPY * k, COPY), :],
                                   self.ring[:, COPY * k:COPY * k + COPY, 1:], ACT.Copy)\
                       .then_inc(self.ring_free, 1)

        def pe(self, pe):
            for b in range(B):
                if b == 0:
                    pe.wait_ge(self.ctxm2_ready, 1)
                pe.wait_ge(self.xsq, b + 1)
                pe.matmul(PS[0:KC, b, :], const("one")[:, 0:KC], sq[:, b, :], start=True, stop=False)
                pe.matmul(PS[0:KC, b, :], self.ctxm2[:, KC * b:KC * b + KC], xn[:, b, :],
                          start=False, stop=True).then_inc(self.prod_ready, 1)
            pe.wait_ge(self.ent_ready, 1)
            pe.transpose(PS[0:KC, 2, 0:B], self.ent[:, :], ident[0:B, 0:B]).then_inc(self.entT_ready, 1)
            for b in range(B):
                pe.wait_ge(self.on_ready, b + 1)
                pe.matmul(PS[:, b, :], ctxN[:, b, :], self.t1[:, b, :], start=True, stop=True)\
                  .then_inc(self.sum_ready, 1)

        def dve(self, dve):
            iota = const("iota")
            dve.tensor_scalar(self.ctxm2[:, :], ctxT[:, :], -2.0, None, ALU.mult).then_inc(self.ctxm2_ready, 1)
            dve.wait_ge(self.aa_ready, 2)
            for b in range(B):
                dve.wait_ge(self.prod_ready, b + 1)
                dve.tensor_scalar(self.t0[:, b, :], PS[0:KC, b, :], self.aa[:, b:b + 1], 0.0, ALU.add, ALU.max)\
                   .then_inc(self.d2_ready, 1)
            a = C_AT["rinit"][0]
            dve.wait_ge(self.skew_in, 32)
            dve.tensor_copy(self.ring[:, RING - 1, :], cst[0:32, a:a + SC + 1]).then_inc(self.scan_done, 1)
            shift = [p + 1 if p < 16 and p % SEG < SEG - 1 else 31 for p in range(32)]
            with dve.Fori(0, STEPS // RING) as i:
                for k in range(RING):
                    now, last = self.ring[:, k, :], self.ring[:, (k - 1) % RING, :]
                    if k % COPY == 0:
                        dve.wait_ge(self.ring_free, i * (RING // COPY) + k // COPY + 1)
                    dve.wait_ge(self.scan_done, i * RING + k + 1)
                    dve.tensor_tensor(self.low[:, :], last[:, 1:], last[:, 0:SC], ALU.min)
                    dve.stream_shuffle(now[:, 0:1], last[:, SC:SC + 1], shift).then_inc(self.shifted, 1)
                    dve.wait_ge(self.shifted, i * RING + k + 1)
                    dve.tensor_tensor_scan(now[:, 1:], self.low[:, :],
                                           self.skew[:, bass.ds(i * RING + k, 1), :].rearrange("p a b -> p (a b)"),
                                           now[:, 0:1], ALU.min, ALU.add).then_inc(self.scan_done, 1)
            dve.wait_ge(self.rows_in, 64)
            above, diag, left = self.big[:, :, 1:], self.big[:, :, 0:S], self.cur[:, :, 0:S]
            cols = iota[0:KC, :].unsqueeze(1).broadcast_to([KC, B, S])
            order.step(dve.tensor_tensor(self.t1[:, :, :], diag, above, ALU.is_le))
            order.link(dve, dve.tensor_tensor(self.t0[:, :, :], diag, above, ALU.min))
            order.link(dve, dve.tensor_tensor(self.keep[:, :, :], left, self.t0[:, :, :], ALU.is_ge))
            order.link(dve, dve.tensor_tensor(self.t1[:, :, :], cols, self.t1[:, :, :], ALU.subtract))
            order.step(dve.tensor_tensor(self.t1[:, :, :], self.t1[:, :, :], self.keep[:, :, :], ALU.mult))
            order.link(dve, dve.tensor_tensor(self.t0[:, :, :], cols, self.keep[:, :, :], ALU.mult))
            for b in range(B):
                order.step(dve.tensor_tensor_scan(self.enter[:, b, :], self.t1[:, b, :], self.t1[:, b, :], 0.0,
                                                  ALU.max, ALU.max))
            dve.tensor_tensor_scan(self.left[:, 0, :], self.t0[:, 0, :], self.t0[:, 0, :], 0.0,
                                   ALU.max, ALU.max).then_inc(self.enter_ready, 1)
            dve.tensor_tensor_scan(self.left[:, 1, :], self.t0[:, 1, :], self.t0[:, 1, :], 0.0,
                                   ALU.max, ALU.max).then_inc(self.enter_ready, 1)
            dve.wait_ge(self.path_in, 32)
            dve.memset(self.ent[:, KC - 1:KC], float(S - 1)).then_inc(self.walked, 1)
            with dve.Fori(0, (KC - 1) // 4) as i:
                for k in range(4):
                    at = dve.snap(i * -4 + (KC - 1 - k))
                    dve.wait_ge(self.walked, i * 4 + k + 1)
                    dve.scalar_tensor_tensor(
                        self.pick[:, k % 2, :], iota[0:B, :], self.ent[:, bass.ds(at, 1)],
                        self.path[:, bass.ds(at, 1), :].rearrange("p a b -> p (a b)"), ALU.is_equal, ALU.mult,
                        accum_out=self.ent[:, bass.ds(at - 1, 1)]).then_inc(self.walked, 1)
            dve.wait_ge(self.walked, KC)
            dve.sem_inc(self.ent_ready, 1)
            dve.wait_ge(self.entT_ready, 1)
            order.link(dve, dve.tensor_copy(self.entT[:, :], PS[0:KC, 2, 0:B]))
            for b in range(B):
                order.link(dve, dve.scalar_tensor_tensor(
                    self.keep[:, b, :], iota[0:KC, :], self.entT[:, b:b + 1], self.left[:, b, :],
                    ALU.is_equal, ALU.mult, accum_out=self.exT[:, b:b + 1]))
                order.link(dve, dve.tensor_scalar(self.t0[:, b, :], iota[0:KC, :], self.entT[:, b:b + 1], None,
                                                  ALU.is_le))
                dve.scalar_tensor_tensor(self.t1[:, b, :], iota[0:KC, :], self.exT[:, b:b + 1], self.t0[:, b, :],
                                         ALU.is_ge, ALU.mult).then_inc(self.on_ready, 1)
            for b in range(B):
                dve.wait_ge(self.sum_ready, b + 1)
                dve.tensor_tensor(x[:, b, :], x[:, b, :], PS[:, b, :], ALU.add).then_inc(x_ready, 1)

    class Quantised:
        QF = 384
        CH = QF // P

        def __init__(self):
            CH = self.CH
            at = self.stack = ExitStack()
            self.wraw = sb("q_wraw", [P, 3, QW], at=at)
            self.wmax = sb("q_wmax", [P, 3, QW // 32], at=at)
            self.winv = sb("q_winv", [P, 3, QW // 32], at=at)
            self.wT = sb("q_wT", [P, 3, CH, P], at=at)
            self.h = sb("q_h", [P, 4, CH, T], at=at)
            self.mx = sb("q_mx", [P, 8], at=at)
            self.sc = sb("q_sc", [P, 8], at=at)
            self.inv = sb("q_inv", [P, 8], at=at)
            self.top = sb("q_top", [1, 8], at=at)
            self.w_in = sem("q_w_in")
            self.w_ready = sem("q_w_ready")
            self.wT_ready = sem("q_wT_ready")
            self.wT_copied = sem("q_wT_copied")
            self.mx_ready = sem("q_mx_ready")
            self.mxT_ready = sem("q_mxT_ready")
            self.top_ready = sem("q_top_ready")
            self.spread = sem("q_spread")
            self.x_quant = sem("q_x_quant")
            self.prod = sem("q_prod")
            self.evac = sem("q_evac")
            self.gate_quant = sem("q_gate_quant")
            self.sig_ready = sem("q_sig_ready")
            self.o_quant = sem("q_o_quant")
            self.down = sem("q_down")

        def sp(self, sp):
            for k, w in enumerate(("wg", "wu", "wd")):
                sp.dma_start(self.wraw[:, k, :], io["q_" + w]).then_inc(self.w_in, 16)

        def weights_dve(self, dve):
            dve.wait_ge(self.w_in, 48)
            blocks = self.wraw[:, :, :].rearrange("p k (g i) -> p (k g) i", i=32)
            G = 3 * QW // 32
            mx, inv = self.wmax[:, :, :].rearrange("p k g -> p (k g)"), self.winv[:, :, :].rearrange("p k g -> p (k g)")
            order.link(dve, dve.tensor_reduce(mx, blocks, X, ALU.max, apply_absolute_value=True))
            order.link(dve, dve.tensor_scalar(mx, mx, 1.0 / 7.0, 1e-12, ALU.mult, ALU.max))
            order.link(dve, dve.reciprocal(inv, mx))
            order.link(dve, dve.tensor_tensor(blocks, blocks, inv.unsqueeze(2).broadcast_to([P, G, 32]), ALU.mult))
            flat = self.wraw[:, :, :].rearrange("p k i -> p (k i)")
            order.link(dve, dve.tensor_scalar(flat, flat, MAGIC, -MAGIC, ALU.add, ALU.add))
            order.link(dve, dve.tensor_scalar(flat, flat, -8.0, 7.0, ALU.max, ALU.min))
            dve.tensor_tensor(blocks, blocks, mx.unsqueeze(2).broadcast_to([P, G, 32]), ALU.mult)\
               .then_inc(self.w_ready, 1)

        def weights_pe(self, pe):
            pe.wait_ge(self.w_ready, 1)
            for k in range(3):
                for c in range(self.CH):
                    mm = pe.transpose(PS[:, 3 + k, P * c:P * c + P], self.wraw[:, k, P * c:P * c + P], ident)
                mm.then_inc(self.wT_ready, 1)

        def weights_act(self, act):
            for k in range(3):
                act.wait_ge(self.wT_ready, k + 1)
                act.activation(self.wT[:, k, :, :].rearrange("p c i -> p (c i)"), PS[:, 3 + k, 0:QW], ACT.Copy)\
                   .then_inc(self.wT_copied, 1)

        def scale_dve(self, dve, j, src):
            dve.tensor_reduce(self.mx[:, j:j + 1], src, X, ALU.max, apply_absolute_value=True)\
               .then_inc(self.mx_ready, 1)
            dve.wait_ge(self.mxT_ready, n("dve", self.mxT_ready))
            dve.tensor_reduce(self.top[:, j:j + 1], PS[0:1, 7, 0:P], X, ALU.max).then_inc(self.top_ready, 1)
            dve.wait_ge(self.spread, n("dve", self.spread))
            order.link(dve, dve.tensor_scalar(self.sc[:, j:j + 1], PS[:, 7, P:P + 1], 1.0 / QMAX, 1e-12,
                                              ALU.mult, ALU.max))
            order.link(dve, dve.reciprocal(self.inv[:, j:j + 1], self.sc[:, j:j + 1]))

        def scale_pe(self, pe, j):
            pe.wait_ge(self.mx_ready, n("pe", self.mx_ready))
            pe.transpose(PS[0:1, 7, 0:P], self.mx[:, j:j + 1], ident).then_inc(self.mxT_ready, 1)
            pe.wait_ge(self.top_ready, n("pe", self.top_ready))
            pe.matmul(PS[:, 7, P:P + 1], const("one")[0:1, :], self.top[:, j:j + 1], start=True, stop=True)\
              .then_inc(self.spread, 1)

        def quant_dve(self, dve, j, a):
            order.link(dve, dve.tensor_scalar(a, a, self.inv[:, j:j + 1], MAGIC, ALU.mult, ALU.add))
            order.link(dve, dve.tensor_scalar(a, a, -MAGIC, QMAX, ALU.add, ALU.min))
            return dve.tensor_scalar(a, a, -QMAX - 1.0, self.sc[:, j:j + 1], ALU.max, ALU.mult)

        def dve(self, dve):
            up, gate, sig, o = [self.h[:, k, :, :].rearrange("p c t -> p (c t)") for k in range(4)]
            norm.wait(dve, "dve")
            flat = xn[:, :, :].rearrange("p b t -> p (b t)")
            self.scale_dve(dve, 0, flat)
            self.quant_dve(dve, 0, flat).then_inc(self.x_quant, 1)
            dve.wait_ge(self.evac, 6)
            self.scale_dve(dve, 1, gate)
            self.quant_dve(dve, 1, gate).then_inc(self.gate_quant, 1)
            dve.wait_ge(self.evac, 12)
            self.scale_dve(dve, 2, up)
            order.link(dve, self.quant_dve(dve, 2, up))
            dve.wait_ge(self.sig_ready, 1)
            order.link(dve, dve.tensor_scalar(sig, sig, 65536.0, MAGIC, ALU.mult, ALU.add))
            order.link(dve, dve.tensor_scalar(sig, sig, -MAGIC, 65535.0, ALU.add, ALU.min))
            order.link(dve, dve.tensor_scalar(sig, sig, 0.0, 1.0 / 65536.0, ALU.max, ALU.mult))
            order.link(dve, dve.tensor_tensor(gate, gate, sig, ALU.mult))
            self.scale_dve(dve, 3, gate)
            order.link(dve, self.quant_dve(dve, 3, gate))
            order.link(dve, dve.tensor_tensor(o, gate, up, ALU.mult))
            self.scale_dve(dve, 4, o)
            self.quant_dve(dve, 4, o).then_inc(self.o_quant, 1)
            for b in range(B):
                dve.wait_ge(self.down, b + 1)
                dve.tensor_tensor(x[:, b, :], x[:, b, :], PS[:, b, :], ALU.add).then_inc(x_ready, 1)

        def pe(self, pe):
            self.scale_pe(pe, 0)
            pe.wait_ge(self.x_quant, 1)
            pe.wait_ge(self.wT_copied, 3)
            k = 0
            for w, j in ((0, 1), (1, 2)):
                for c in range(self.CH):
                    for b in range(B):
                        if k >= 6:
                            pe.wait_ge(self.evac, k - 5)
                        pe.matmul(PS[:, k % 6, :], self.wT[:, w, c, :], xn[:, b, :],
                                  start=True, stop=True).then_inc(self.prod, 1)
                        k += 1
                self.scale_pe(pe, j)
            self.scale_pe(pe, 3)
            self.scale_pe(pe, 4)
            pe.wait_ge(self.o_quant, 1)
            for b in range(B):
                for c in range(self.CH):
                    mm = pe.matmul(PS[:, b, :], self.wT[:, 2, c, :], self.h[:, 3, c, S * b:S * b + S],
                                   start=(c == 0), stop=(c == self.CH - 1))
                mm.then_inc(self.down, 1)

        def act(self, act):
            k = 0
            for dst in (1, 0):
                for c in range(self.CH):
                    for b in range(B):
                        act.wait_ge(self.prod, k + 1)
                        act.activation(self.h[:, dst, c, S * b:S * b + S], PS[:, k % 6, :], ACT.Copy)\
                           .then_inc(self.evac, 1)
                        k += 1
            act.wait_ge(self.gate_quant, 1)
            act.activation(self.h[:, 2, :, :], self.h[:, 1, :, :], ACT.Sigmoid).then_inc(self.sig_ready, 1)

    class ContextAttention:

        COUNTS = dict(w_in=64, mask_ready=1, pads=1, kv_prod=3, kv_ready=3, kb_ready=2, vb_prod=6, vb_ready=6, q_prod=2,
                      q_ready=2, scores=NT, scores_read=NT, centred=NT, exps=NT, rden_ready=NT, probs=NT,
                      turned=3 * NT, pT_ready=3 * NT, mixed=NT, o_ready=2, out_prod=2)
        sems = {}

        def __init__(self, tag, mask_is_int, use):
            self.tag, self.mask_is_int = tag, mask_is_int
            self.past = {k: use * v for k, v in self.COUNTS.items()}
            at = self.stack = ExitStack()
            name = lambda a: tag + "_" + a
            self.w = sb(name("w"), [P, 4, P], at=at)
            self.mraw = sb(name("mraw"), [P, NT // B, KC], I32 if mask_is_int else F32, at=at)
            self.mask = sb(name("mask"), [P, NT // B, KC], at=at)
            self.sel = sb(name("sel"), [KC, HKP], at=at)
            self.hmask = sb(name("hmask"), [P, HKC, P], at=at)
            self.k = sb(name("k"), [P, B, KC], at=at)
            self.v = sb(name("v"), [KC, B, P], at=at)
            self.kb = sb(name("kb"), [P, B, H, KC], at=at)
            self.vb = sb(name("vb"), [P, B, HKC, P], at=at)
            self.q = sb(name("q"), [P, B, S], at=at)
            self.s = sb(name("s"), [P, 3, HKP], at=at)
            self.pT = sb(name("pT"), [P, 2, HKC, P], at=at)
            self.o = sb(name("o"), [P, B, S], at=at)
            self.mx = sb(name("mx"), [P, 2, H], at=at)
            self.den = sb(name("den"), [P, 2, H], at=at)
            self.rden = sb(name("rden"), [P, 2, H], at=at)
            if not use:
                self.sems.update({k: sem("ca_" + k) for k in self.COUNTS})
            (self.w_in, self.mask_ready, self.pads, self.kv_prod, self.kv_ready, self.kb_ready, self.vb_prod,
             self.vb_ready, self.q_prod, self.q_ready, self.scores, self.scores_read, self.centred, self.exps,
             self.rden_ready, self.probs, self.turned, self.pT_ready, self.mixed, self.o_ready, self.out_prod) = [self.sems[what] for what in self.COUNTS]

        def sp(self, sp):
            t = self.tag
            sp.dma_start(self.w[:, :, :], io[t + "_w"]).then_inc(self.w_in, 16)
            sp.dma_start(self.mraw[:, :, :], io[t + "_mask"]).then_inc(self.w_in, 16)
            sp.dma_start(self.sel[:, :], io["sel"]).then_inc(self.w_in, 16)
            sp.dma_start(self.hmask[:, :, :], io["hmask"]).then_inc(self.w_in, 16)

        def pe_prepare(self, pe):
            pe.wait_ge(self.w_in, self.past["w_in"] + 64)
            pe.matmul(PS[:, 0, 0:B * KC], self.w[:, 1, :], ctxT[:, :], start=True, stop=True).then_inc(self.kv_prod, 1)
            a = R_AT[self.tag + "_bv"][0]
            for b in range(B):
                pe.matmul(PS[0:KC, 1 + b, 0:P], ctxT[:, KC * b:KC * b + KC], self.w[:, 2, :], start=True, stop=False)
                pe.matmul(PS[0:KC, 1 + b, 0:P], const("one")[0:1, 0:KC], row[:, a:a + P],
                          start=False, stop=True).then_inc(self.kv_prod, 1)
            pe.wait_ge(self.kv_ready, self.past["kv_ready"] + 3)
            for b in range(B):
                for c in range(HKC):
                    bank, at = 3 * b + c // 4, P * (c % 4)
                    mm = pe.matmul(PS[:, bank, at:at + P], self.sel[:, P * c:P * c + P], self.v[:, b, :],
                                   start=True, stop=True)
                    if c % 4 == 3 or c == HKC - 1:
                        mm.then_inc(self.vb_prod, 1)

        def act_prepare(self, act):
            act.wait_ge(self.kv_prod, self.past["kv_prod"] + 1)
            act.activation(self.k[:, :, :].rearrange("p b k -> p (b k)"), PS[:, 0, 0:B * KC], ACT.Identity,
                           bias=column(self.tag + "_bk")).then_inc(self.kv_ready, 1)
            for b in range(B):
                act.wait_ge(self.kv_prod, self.past["kv_prod"] + 2 + b)
                act.activation(self.v[:, b, :], PS[0:KC, 1 + b, 0:P], ACT.Copy).then_inc(self.kv_ready, 1)

        def pool(self, pool):
            pool.memset(self.s[:, :, HK:], 0.0).then_inc(self.pads, 1)
            pool.wait_ge(self.w_in, self.past["w_in"] + 64)
            pool.wait_ge(self.kv_ready, self.past["kv_ready"] + 1)
            for b in range(B):
                pool.tensor_tensor(self.kb[:, b, :, :], self.k[:, b, :].unsqueeze(1).broadcast_to([P, H, KC]),
                                   const("hm").unsqueeze(2).broadcast_to([P, H, KC]), ALU.mult)\
                    .then_inc(self.kb_ready, 1)
            for t in range(NT):
                pool.wait_ge(self.rden_ready, self.past["rden_ready"] + t + 1)
                s = self.s[:, t % 3, 0:HK].rearrange("p (h k) -> p h k", h=H)
                pool.tensor_tensor(s, s, self.rden[:, t % 2, :].unsqueeze(2).broadcast_to([P, H, KC]), ALU.mult)\
                    .then_inc(self.probs, 1)

        def dve_prepare(self, dve):
            dve.wait_ge(self.w_in, self.past["w_in"] + 64)
            if self.mask_is_int:
                dve.tensor_scalar(self.mask[:, :, :], self.mraw[:, :, :], 0, NEG, ALU.is_equal, ALU.mult)\
                   .then_inc(self.mask_ready, 1)
            else:
                dve.tensor_scalar(self.mask[:, :, :], self.mraw[:, :, :], -1e9, None, ALU.mult)\
                   .then_inc(self.mask_ready, 1)
            for b in range(B):
                for g in range(3):
                    dve.wait_ge(self.vb_prod, self.past["vb_prod"] + 3 * b + g + 1)
                    c0, c1 = 4 * g, min(4 * g + 4, HKC)
                    dve.tensor_tensor(self.vb[:, b, c0:c1, :].rearrange("p c f -> p (c f)"),
                                      PS[:, 3 * b + g, 0:P * (c1 - c0)],
                                      self.hmask[:, c0:c1, :].rearrange("p c f -> p (c f)"), ALU.mult)\
                       .then_inc(self.vb_ready, 1)

        def pe(self, pe):
            pe.wait_ge(self.vb_ready, self.past["vb_ready"] + 6)
            norm.wait(pe, "pe")
            for b in range(B):
                pe.matmul(PS[:, 6 + b, :], self.w[:, 0, :], xn[:, b, :], start=True, stop=True)\
                  .then_inc(self.q_prod, 1)
            pe.wait_ge(self.kb_ready, self.past["kb_ready"] + 2)
            for t in range(NT + 2):
                if t < NT:
                    b, j = divmod(t, NT // B)
                    if j == 0:
                        pe.wait_ge(self.q_ready, self.past["q_ready"] + b + 1)
                    if t >= 1:
                        pe.wait_ge(self.scores_read, self.past["scores_read"] + t)
                    for g, (h0, nh) in enumerate(HGROUPS):
                        mm = pe.matmul(PS[:, g, 0:nh * KC], self.q[:, b, P * j:P * j + P],
                                       self.kb[:, b, h0:h0 + nh, :].rearrange("p h k -> p (h k)"), start=True, stop=True)
                    mm.then_inc(self.scores, 1)
                if t >= 2:
                    u = t - 2
                    b, j = divmod(u, NT // B)
                    pe.wait_ge(self.probs, self.past["probs"] + u + 1)
                    for c in range(HKC):
                        if u >= 1 and c % 4 == 0:
                            pe.wait_ge(self.pT_ready, self.past["pT_ready"] + 3 * (u - 1) + c // 4 + 1)
                        mm = pe.transpose(PS[:, 3 + c // 4, P * (c % 4):P * (c % 4) + P],
                                          self.s[:, u % 3, P * c:P * c + P], ident)
                        if c % 4 == 3 or c == HKC - 1:
                            mm.then_inc(self.turned, 1)
                    if j == 0 and b == 1:
                        pe.wait_ge(self.o_ready, self.past["o_ready"] + 1)
                    for c in range(HKC):
                        if c % 4 == 0:
                            pe.wait_ge(self.pT_ready, self.past["pT_ready"] + 3 * u + c // 4 + 1)
                        mm = pe.matmul(PS[:, 6, P * j:P * j + P], self.vb[:, b, c, :], self.pT[:, u % 2, c, :],
                                       start=(c == 0), stop=(c == HKC - 1))
                    mm.then_inc(self.mixed, 1)
                    if j == NT // B - 1:
                        pe.wait_ge(self.o_ready, self.past["o_ready"] + b + 1)
                        if b == 1:
                            pe.wait_ge(self.scores_read, self.past["scores_read"] + NT)
                        pe.matmul(PS[:, 7 - 7 * b, :], self.w[:, 3, :], self.o[:, b, :], start=True, stop=True)\
                          .then_inc(self.out_prod, 1)

        def act(self, act):
            for b in range(B):
                act.wait_ge(self.q_prod, self.past["q_prod"] + b + 1)
                act.activation(self.q[:, b, :], PS[:, 6 + b, :], ACT.Identity, bias=column(self.tag + "_bq"))\
                   .then_inc(self.q_ready, 1)
            for t in range(NT + 2):
                if t >= 2:
                    u = t - 2
                    b, j = divmod(u, NT // B)
                    for g in range(3):
                        act.wait_ge(self.turned, self.past["turned"] + 3 * u + g + 1)
                        if u >= 2 and g == 0:
                            act.wait_ge(self.mixed, self.past["mixed"] + u - 1)
                        c0, c1 = 4 * g, min(4 * g + 4, HKC)
                        act.activation(self.pT[:, u % 2, c0:c1, :].rearrange("p c f -> p (c f)"),
                                       PS[:, 3 + g, 0:P * (c1 - c0)], ACT.Copy).then_inc(self.pT_ready, 1)
                if t < NT:
                    act.wait_ge(self.centred, self.past["centred"] + t + 1)
                    s = self.s[:, t % 3, 0:HK]
                    act.activation(s, s, ACT.Exp).then_inc(self.exps, 1)
                if t >= 2 and j == NT // B - 1:
                    act.wait_ge(self.mixed, self.past["mixed"] + u + 1)
                    act.activation(self.o[:, b, :], PS[:, 6, :], ACT.Copy).then_inc(self.o_ready, 1)

        def dve(self, dve):
            scale = float(1.0 / np.sqrt(np.float32(DH)))
            dve.wait_ge(self.mask_ready, self.past["mask_ready"] + 1)
            dve.wait_ge(self.pads, self.past["pads"] + 1)
            for t in range(NT + 1):
                if t < NT:
                    j = t % (NT // B)
                    s = self.s[:, t % 3, 0:HK].rearrange("p (h k) -> p h k", h=H)
                    dve.wait_ge(self.scores, self.past["scores"] + t + 1)
                    if t >= 3:
                        dve.wait_ge(self.turned, self.past["turned"] + 3 * (t - 2))
                    for g, (h0, nh) in enumerate(HGROUPS):
                        ins = dve.scalar_tensor_tensor(
                            s[:, h0:h0 + nh, :], PS[:, g, 0:nh * KC].rearrange("p (h k) -> p h k", h=nh), scale,
                            self.mask[:, j, :].unsqueeze(1).broadcast_to([P, nh, KC]), ALU.mult, ALU.add)
                    ins.then_inc(self.scores_read, 1)
                if t >= 1:
                    u = t - 1
                    su = self.s[:, u % 3, 0:HK].rearrange("p (h k) -> p h k", h=H)
                    dve.wait_ge(self.exps, self.past["exps"] + u + 1)
                    order.link(dve, dve.tensor_reduce(self.den[:, u % 2, :], su, X, ALU.add))
                    if u >= 2:
                        dve.wait_ge(self.probs, self.past["probs"] + u - 1)
                    dve.reciprocal(self.rden[:, u % 2, :], self.den[:, u % 2, :]).then_inc(self.rden_ready, 1)
                if t < NT:
                    dve.wait_ge(self.scores_read, self.past["scores_read"] + t + 1)
                    order.link(dve, dve.tensor_reduce(self.mx[:, t % 2, :], s, X, ALU.max))
                    dve.tensor_tensor(s, s, self.mx[:, t % 2, :].unsqueeze(2).broadcast_to([P, H, KC]), ALU.subtract)\
                       .then_inc(self.centred, 1)
            for b in range(B):
                dve.wait_ge(self.out_prod, self.past["out_prod"] + b + 1)
                dve.scalar_tensor_tensor(x[:, b, :], PS[:, 7 - 7 * b, :], column(self.tag + "_bo"), x[:, b, :],
                                         ALU.add, ALU.add).then_inc(x_ready, 1)

    class PairAttention:

        def __init__(self):
            at = self.stack = ExitStack()
            self.w = sb("pa_w", [P, 4, P], at=at)
            self.h0 = sb("pa_h0", [P, B, S], at=at)
            self.h2 = sb("pa_h2", [P, B, S], at=at)
            self.q = sb("pa_q", [P, S], at=at)
            self.v = sb("pa_v", [P, B, S], at=at)
            self.qk = sb("pa_qk", [P, B, S], at=at)
            self.s = sb("pa_s", [P, B, S], at=at)
            self.m = sb("pa_m", [P, S], at=at)
            (self.w_in, self.prod, self.q_ready, self.v_ready, self.qk_ready, self.scores, self.s1_ready,
             self.centred, self.exps, self.mixed, self.out_prod, self.h2_ready) = [
                sem("pa_" + what) for what in (
                "w_in prod q_ready v_ready qk_ready scores s1_ready centred exps mixed out_prod h2_ready").split()]

        def sp(self, sp):
            sp.dma_start(self.w[:, :, :], io["pa_w"]).then_inc(self.w_in, 16)

        def pe(self, pe):
            norm.wait(pe, "pe")
            norm.pe(pe, self.h0, None)
            norm.wait(pe, "pe")
            pe.wait_ge(self.w_in, 16)
            for bank, (w, b) in enumerate(((0, 1), (1, 0), (1, 1), (2, 0), (2, 1))):
                pe.matmul(PS[:, bank, :], self.w[:, w, :], xn[:, b, :], start=True, stop=True).then_inc(self.prod, 1)
            for b in range(B):
                pe.wait_ge(self.qk_ready, b + 1)
                pe.matmul(PS[:, 5 + b, :], const("blk8"), self.qk[:, b, :], start=True, stop=True)\
                  .then_inc(self.scores, 1)
            pe.wait_ge(self.v_ready, 2)
            pe.matmul(PS[:, 0, :], self.w[:, 3, :], self.v[:, 0, :], start=True, stop=True).then_inc(self.out_prod, 1)
            pe.wait_ge(self.mixed, 1)
            pe.matmul(PS[:, 1, :], self.w[:, 3, :], self.qk[:, 0, :], start=True, stop=True).then_inc(self.out_prod, 1)
            norm.pe(pe, self.h2, self.h2_ready)

        def act(self, act):
            norm.act(act)
            act.wait_ge(self.prod, 1)
            act.activation(self.q[:, :], PS[:, 0, :], ACT.Copy).then_inc(self.q_ready, 1)
            for b in range(B):
                act.wait_ge(self.prod, 4 + b)
                act.activation(self.v[:, b, :], PS[:, 3 + b, :], ACT.Copy).then_inc(self.v_ready, 1)
            act.wait_ge(self.scores, 2)
            act.activation(self.s[:, 1, :], PS[:, 6, :], ACT.Copy).then_inc(self.s1_ready, 1)
            act.wait_ge(self.centred, 1)
            act.activation(self.s[:, :, :], self.s[:, :, :], ACT.Exp, scale=float(1.0 / np.sqrt(np.float32(DH))))\
               .then_inc(self.exps, 1)
            norm.act(act)

        def dve(self, dve):
            norm.wait(dve, "dve")
            norm.dve(dve, self.h0, xn, column("pa_ln1w"), column("pa_ln1b"))
            dve.wait_ge(self.q_ready, 1)
            for b in range(B):
                dve.wait_ge(self.prod, 2 + b)
                dve.tensor_tensor(self.qk[:, b, :], PS[:, 1 + b, :], self.q[:, :], ALU.mult).then_inc(self.qk_ready, 1)
            dve.wait_ge(self.s1_ready, 1)
            order.link(dve, dve.tensor_tensor(self.m[:, :], PS[:, 5, :], self.s[:, 1, :], ALU.max))
            order.step(dve.tensor_tensor(self.s[:, 0, :], PS[:, 5, :], self.m[:, :], ALU.subtract))
            dve.tensor_tensor(self.s[:, 1, :], self.s[:, 1, :], self.m[:, :], ALU.subtract).then_inc(self.centred, 1)
            dve.wait_ge(self.exps, 1)
            order.link(dve, dve.tensor_tensor(self.m[:, :], self.s[:, 0, :], self.s[:, 1, :], ALU.add))
            order.link(dve, dve.reciprocal(self.m[:, :], self.m[:, :]))
            for b in range(B):
                order.link(dve, dve.tensor_tensor(self.s[:, b, :], self.s[:, b, :], self.m[:, :], ALU.mult))
            dve.wait_ge(self.v_ready, 2)
            for b in range(B):
                order.link(dve, dve.tensor_tensor(self.s[:, b, :], self.s[:, b, :], self.v[:, b, :], ALU.mult))
            dve.tensor_tensor(self.qk[:, 0, :], self.s[:, 0, :], self.s[:, 1, :], ALU.add).then_inc(self.mixed, 1)
            for b in range(B):
                dve.wait_ge(self.out_prod, b + 1)
                dve.tensor_tensor(self.h2[:, b, :], self.h0[:, b, :], PS[:, b, :], ALU.add).then_inc(self.h2_ready, 1)
            dve.wait_ge(self.h2_ready, 2)
            norm.dve(dve, self.h2, xn, column("pa_ln2w"), column("pa_ln2b"))

    class Experts:

        COUNTS = dict(router_in=16, ones_set=1, logits=1, g_centred=1, g_exps=1, g_ready=1, g_turned=4, wT_ready=2,
                      wb_prod=E * B, wb_ready=E * B, w_in0=16 * E, w_in1=16 * E, h_prod=E * B * FF // P,
                      h_ready=4 + E * B * FF // P, y_prod=2 + E * B, y_used=2 + E * B, y_step=E * B)
        sems = {}

        def __init__(self, tag, act_fn, temperature, capped, use):
            self.tag, self.fn, self.temperature, self.capped = tag, act_fn, temperature, capped
            self.past = {k: use * v for k, v in self.COUNTS.items()}
            at = self.stack = ExitStack()
            name = lambda a: tag + "_" + a
            self.router = sb(name("router"), [P, E], at=at)
            self.w1 = sb(name("w1"), [P, 2, FF], at=at)
            self.w2 = sb(name("w2"), [P, 2, FF // P, P], at=at)
            self.g = sb(name("g"), [P, 4, NT, E], at=at)
            self.r = sb(name("r"), [P, 2, NT], at=at)
            self.wT = sb(name("wT"), [E, T], at=at)
            self.rank = sb(name("rank"), [E, T], at=at)
            self.ones = sb(name("ones"), [E, T], at=at)
            self.wb = sb(name("wb"), [P, E, B, S], at=at)
            self.h = sb(name("h"), [P, 2, FF // P, S], at=at)
            self.y = sb(name("y"), [P, 2, S], at=at)
            if not use:
                self.sems.update({k: sem("ex_" + k) for k in self.COUNTS})
            (self.router_in, self.ones_set, self.logits, self.g_centred, self.g_exps, self.g_ready, self.g_turned,
             self.wT_ready, self.wb_prod, self.wb_ready, self.w_in0, self.w_in1, self.h_prod, self.h_ready,
             self.y_prod, self.y_used, self.y_step) = [self.sems[what] for what in self.COUNTS]
            self.w_in = (self.w_in0, self.w_in1)

        def load(self, sp, e, slot):
            sp.dma_start(self.w1[:, slot, :], io[self.tag + "_w1"][e]).then_inc(self.w_in[slot], 16)
            sp.dma_start(self.w2[:, slot, :, :], io[self.tag + "_w2"][e].rearrange("(c p) d -> p c d", p=P))\
              .then_inc(self.w_in[slot], 16)

        def sp(self, sp):
            sp.dma_start(self.router[:, :], io[self.tag + "_router"]).then_inc(self.router_in, 16)
            for e in range(2):
                self.load(sp, e, e)
            with sp.Fori(0, E // 2 - 1) as i:
                for slot in range(2):
                    sp.wait_ge(self.y_prod, self.past["y_prod"] + i * 4 + 2 * slot + 4)
                    e = i * 2 + 2 + slot
                    sp.dma_start(self.w1[:, slot, :], io[self.tag + "_w1"][bass.ds(e, 1)].rearrange("a p f -> p (a f)"))\
                      .then_inc(self.w_in[slot], 16)
                    sp.dma_start(self.w2[:, slot, :, :],
                                 io[self.tag + "_w2"][bass.ds(e, 1)].rearrange("a (c p) d -> p (a c) d", p=P))\
                      .then_inc(self.w_in[slot], 16)

        def pool(self, pool):
            pool.memset(self.ones[:, :], 1.0).then_inc(self.ones_set, 1)

        def gate_pe(self, pe):
            norm.wait(pe, "pe")
            pe.wait_ge(self.router_in, self.past["router_in"] + 16)
            for t in range(NT):
                mm = pe.matmul(PS[:, 0, E * t:E * t + E], xn[:, t * P // S, P * (t % (S // P)):P * (t % (S // P)) + P],
                               self.router[:, :], start=True, stop=True)
            mm.then_inc(self.logits, 1)
            pe.wait_ge(self.g_ready, self.past["g_ready"] + 1)
            for k in range(2 if self.capped else 1):
                for t in range(NT):
                    mm = pe.transpose(PS[0:E, 1 + 2 * k + t // 4, P * (t % 4):P * (t % 4) + P], self.g[:, k, t, :], ident)
                    if t % 4 == 3:
                        mm.then_inc(self.g_turned, 1)
            for b in range(B):
                pe.wait_ge(self.wT_ready, self.past["wT_ready"] + b + 1)
            for u in range(E * B):
                e, b = divmod(u, B)
                if u >= 3:
                    pe.wait_ge(self.wb_ready, self.past["wb_ready"] + u - 2)
                pe.matmul(PS[:, 5 + u % 3, :], cst[0:E, e:e + 1].broadcast_to([E, P]), self.wT[:, S * b:S * b + S],
                          start=True, stop=True).then_inc(self.wb_prod, 1)

        def gate_act(self, act):
            act.wait_ge(self.g_centred, self.past["g_centred"] + 1)
            g = self.g[:, 3, :, :]
            act.activation(g, g, ACT.Exp, scale=1.0 / self.temperature).then_inc(self.g_exps, 1)
            for u in range(E * B):
                e, b = divmod(u, B)
                act.wait_ge(self.wb_prod, self.past["wb_prod"] + u + 1)
                act.activation(self.wb[:, e, b, :], PS[:, 5 + u % 3, :], ACT.Copy).then_inc(self.wb_ready, 1)

        def gate_dve(self, dve):
            logits = PS[:, 0, 0:NT * E].rearrange("p (t e) -> p t e", e=E)
            w, sel, t2, ex = [self.g[:, k, :, :] for k in range(4)]
            r0, r1 = self.r[:, 0, :], self.r[:, 1, :]
            wide = lambda r: r.unsqueeze(2).broadcast_to([P, NT, E])
            kidx = const("kidx").unsqueeze(1).broadcast_to([P, NT, E])

            def pick(src, dst):
                order.link(dve, dve.tensor_reduce(r0, src, X, ALU.max))
                order.link(dve, dve.tensor_tensor(dst, src, wide(r0), ALU.is_equal))
                order.link(dve, dve.tensor_tensor(dst, dst, kidx, ALU.mult))
                order.link(dve, dve.tensor_reduce(r0, dst, X, ALU.max))
                order.link(dve, dve.tensor_tensor(dst, dst, wide(r0), ALU.is_equal))

            dve.wait_ge(self.logits, self.past["logits"] + 1)
            order.link(dve, dve.tensor_reduce(r0, logits, X, ALU.max))
            dve.tensor_tensor(ex, logits, wide(r0), ALU.subtract).then_inc(self.g_centred, 1)
            dve.wait_ge(self.g_exps, self.past["g_exps"] + 1)
            pick(ex, sel)
            order.link(dve, dve.scalar_tensor_tensor(w, sel, -2.0, ex, ALU.mult, ALU.add))
            pick(w, t2)
            order.link(dve, dve.tensor_tensor(sel, sel, t2, ALU.add))
            order.link(dve, dve.tensor_tensor(w, ex, sel, ALU.mult))
            order.link(dve, dve.tensor_reduce(r1, w if self.capped else ex, X, ALU.add))
            order.link(dve, dve.reciprocal(r1, r1))
            dve.tensor_tensor(w, w, wide(r1), ALU.mult).then_inc(self.g_ready, 1)
            if not self.capped:
                for b in range(B):
                    dve.wait_ge(self.g_turned, self.past["g_turned"] + b + 1)
                    dve.tensor_copy(self.wT[:, S * b:S * b + S], PS[0:E, 1 + b, :]).then_inc(self.wT_ready, 1)
                return
            dve.wait_ge(self.ones_set, self.past["ones_set"] + 1)
            for b in range(B):
                dve.wait_ge(self.g_turned, self.past["g_turned"] + 3 + b)
                init = self.rank[:, S - 1:S] if b else 0.0
                order.link(dve, dve.tensor_tensor_scan(self.rank[:, S * b:S * b + S], self.ones[:, S * b:S * b + S],
                                                       PS[0:E, 3 + b, :], init, ALU.mult, ALU.add))
            for b in range(B):
                dve.scalar_tensor_tensor(self.wT[:, S * b:S * b + S], self.rank[:, S * b:S * b + S], float(CAP),
                                         PS[0:E, 1 + b, :], ALU.is_le, ALU.mult).then_inc(self.wT_ready, 1)

        def pe(self, pe):
            C = FF // P

            def hidden(i, u):
                slot, b = divmod(u, B)
                if b == 0:
                    pe.wait_ge(self.w_in[slot], self.past["w_in0"] + i * 32 + 32)
                for c in range(C):
                    pe.wait_ge(self.h_ready, self.past["h_ready"] + i * 16 + 4 * u + c + 1)
                    pe.matmul(PS[:, c, :], self.w1[:, slot, P * c:P * c + P], xn[:, b, :], start=True, stop=True)\
                      .then_inc(self.h_prod, 1)

            def outward(i, u):
                slot, b = divmod(u, B)
                pe.wait_ge(self.h_ready, self.past["h_ready"] + i * 16 + 4 * u + 4 + 4)
                pe.wait_ge(self.y_used, self.past["y_used"] + i * 4 + u + 1)
                for c in range(C):
                    mm = pe.matmul(PS[:, 4 + u % 2, :], self.w2[:, slot, c, :], self.h[:, u % 2, c, :],
                                   start=(c == 0), stop=(c == C - 1))
                mm.then_inc(self.y_prod, 1)

            pe.sem_inc(self.y_prod, 2)
            with pe.Fori(0, E // 2) as i:
                hidden(i, 0)
                for u in range(1, 4):
                    hidden(i, u)
                    outward(i, u - 1)
                outward(i, 3)

        def act(self, act):
            act.sem_inc(self.h_ready, 4)
            with act.Fori(0, E // 2) as i:
                for u in range(4):
                    for c in range(FF // P):
                        act.wait_ge(self.h_prod, self.past["h_prod"] + i * 16 + 4 * u + c + 1)
                        if c == 0:
                            act.wait_ge(self.y_prod, self.past["y_prod"] + i * 4 + u + 1)
                        act.activation(self.h[:, u % 2, c, :], PS[:, c, :], self.fn).then_inc(self.h_ready, 1)

        def dve(self, dve, base):
            for b in range(B):
                order.link(dve, dve.tensor_tensor(x[:, b, :], x[:, b, :], base[:, b, :], ALU.add))
            dve.wait_ge(self.wb_ready, self.past["wb_ready"] + E * B)
            dve.sem_inc(self.y_used, 2)
            with dve.Fori(0, E // 2) as i:
                for u in range(4):
                    slot, b = divmod(u, B)
                    dve.wait_ge(self.y_prod, self.past["y_prod"] + i * 4 + u + 3)
                    dve.tensor_tensor(self.y[:, u % 2, :], PS[:, 4 + u % 2, :],
                                      self.wb[:, bass.ds(i * 2 + slot, 1), b, :].rearrange("p a s -> p (a s)"),
                                      ALU.mult).then_inc(self.y_used, 1)
                    dve.wait_ge(self.y_used, self.past["y_used"] + i * 4 + u + 3)
                    dve.tensor_tensor(x[:, b, :], x[:, b, :], self.y[:, u % 2, :], ALU.add).then_inc(self.y_step, 1)
            dve.wait_ge(self.y_step, self.past["y_step"] + 2 * E)
            dve.sem_inc(x_ready, 2)

    class Stack:

        TILES = S // P
        CHUNKS = ((0, 128), (128, 128), (256, FFI - 256))

        def __init__(self):
            at = self.stack = ExitStack()
            s = lambda name, shape, dt=F32: sb("st_" + name, shape, dt, at=at)
            self.wqkv = s("wqkv", [P, 3, INNER])
            self.wo = s("wo", [P, INNER // P, P])
            self.w1 = s("w1", [P, 2 * FFI])
            self.w2 = s("w2", [P, 3, P])
            self.sv = s("sv", [P, 9])
            self.qks = s("qks", [P, 2, 2, D2])
            self.base = s("base", [P, 2, 2, 4, D2])
            self.rot = s("rot", [P, 2, 2, 4, D2])
            self.wmask = s("wmask", [P, 2, 2 * WIN], BF16)
            self.identb = s("identb", [P, P], BF16)
            self.xs = s("xs", [P, B, S])
            self.xf = s("xf", [P, S])
            self.xfn = s("xfn", [P, S])
            self.y0 = s("y0", [P, B, S])
            self.sqh = s("sqh", [P, 2, 512])
            self.t2 = s("t2", [P, 2, 512])
            self.r = s("r", [P, 2, 4, 512])
            self.ss = s("ss", [P, 2, 32])
            self.gy = s("gy", [P, 2, 32])
            self.gt = s("gt", [P, 2, 32])
            self.qT = s("qT", [P, 8, S])
            self.kT = s("kT", [P, 8, WIN + S])
            self.v = s("v", [P, 2, INNER])
            self.v_out = dram("st_v_out", (4, P, INNER))
            self.vv = s("vv", [P, S // WIN, INNER // 2])
            self.e = s("e", [P, 8, 2, 2 * WIN])
            self.pT = s("pT", [P, 8, P])
            self.mx = s("mx", [P, 16])
            self.den = s("den", [P, 16])
            self.rden = s("rden", [P, 2, 16])
            self.on = s("on", [P, 8, 2, D2])
            self.oT = s("oT", [P, 8, S])
            self.gel = s("gel", [P, 2, S])
            self.hid = s("hid", [P, 3, S])
            (self.c_in, self.wv_in, self.wq_in, self.wk_in, self.wf_in, self.qks_in, self.set_up, self.rot_ready,
             self.xs_ready, self.proj, self.v_evac, self.squares, self.ss_done, self.qk_used, self.added,
             self.v_ready, self.guess, self.newton, self.r_ready, self.turned, self.evac, self.scores, self.mx_ready,
             self.sub_done, self.exps, self.den_ready, self.rden_ready, self.v_stored, self.pv_done, self.on_ready,
             self.wo_done, self.xu_ready, self.xf_ready, self.mean, self.centred, self.lnsq, self.var, self.std,
             self.rstd, self.spread, self.ln_tmp, self.ffn_in, self.up, self.gelu, self.act_ready, self.down) = [
                sem("st_" + what) for what in (
                "c_in wv_in wq_in wk_in wf_in qks_in set_up rot_ready xs_ready proj v_evac squares ss_done "
                "qk_used added v_ready guess newton r_ready turned evac scores mx_ready sub_done exps "
                "den_ready rden_ready v_stored pv_done on_ready wo_done xu_ready xf_ready mean centred lnsq "
                "var std rstd spread ln_tmp ffn_in up gelu act_ready down").split()]
            self.mix_begun = sem("st_mix_begun")
            self.load_begun = sem("st_load_begun")
            self.vshift = [sem("st_vshift%d" % t) for t in range(4)]

        def load_a(self, sp, l):
            for k in (2, 0, 1):
                self.load_w(sp, l, k)
            sp.dma_start(self.qks[:, :, :, :], io["st_qks"][bass.ds(l, 1)].rearrange("a q k d -> a (q k d)")
                         .broadcast_to([P, 4 * D2])).then_inc(self.qks_in, 16)

        def load_w(self, sp, l, k):
            src = io["st_wqkv"][bass.ds(l, 1), :, INNER * k:INNER * k + INNER].rearrange("a p n -> p (a n)")
            sp.dma_start(self.wqkv[:, k, :], src).then_inc((self.wq_in, self.wk_in, self.wv_in)[k], 16)

        def load_f(self, sp, l):
            one = lambda name: io[name][bass.ds(l, 1)]
            sp.dma_start(self.wo[:, :, :], one("st_wo").rearrange("a (c p) d -> p (a c) d", p=P)).then_inc(self.wf_in, 16)
            sp.dma_start(self.w1[:, :], one("st_w1").rearrange("a p n -> p (a n)")).then_inc(self.wf_in, 16)
            sp.dma_start(self.w2[:, 0:2, :], one("st_w2")[:, 0:256, :].rearrange("a (c p) d -> p (a c) d", p=P))\
              .then_inc(self.wf_in, 16)
            sp.dma_start(self.w2[0:FFI - 256, 2, :], one("st_w2")[:, 256:, :].rearrange("a p d -> p (a d)"))\
              .then_inc(self.wf_in, 16)
            sp.dma_start(self.sv[:, :], one("st_sv").rearrange("a p n -> p (a n)")).then_inc(self.wf_in, 16)

        WF = 5 * 16

        def sp_shift(self, sp, u):
            for t in range(4):
                T = 4 * u + t
                sp.wait_ge(self.pv_done, T + 1)
                sp.wait_ge(self.v_evac, T * 2 + 2)
                sp.dma_start(self.v_out[t], self.v[:, t % 2, :]).then_inc(self.v_stored, 16)
                if t < 3:
                    sp.wait_ge(self.pv_done, T + 2)
                sp.wait_ge(self.v_stored, T * 16 + 16)
                for e in range(2):
                    for h in range(2):
                        first, count = 4 * t + 1 - h, 4 - (t == 3 and h == 0)
                        rows = slice(64 * e + WIN * h, 64 * e + WIN * h + WIN)
                        src = view(self.v_out, t * P * INNER + 512 * e, [[INNER, WIN], [WIN * INNER, count], [1, 512]])
                        sp.dma_start(self.vv[rows, first:first + count, :], src).then_inc(self.vshift[t], 16)

        def sp(self, sp):
            sp.dma_start(self.base[:, :, :, :, :], io["st_base"]).then_inc(self.c_in, 16)
            sp.dma_start(self.wmask[:, :, :], io["st_wmask"]).then_inc(self.c_in, 16)
            sp.dma_start(self.identb[:, :], io["identb"]).then_inc(self.c_in, 16)
            self.load_a(sp, 0)
            self.load_f(sp, 0)
            self.sp_shift(sp, 0)
            with sp.Fori(0, DEPTH - 1) as i:
                self.sp_shift(sp, i * 2 + 1)
                sp.wait_ge(self.rot_ready, i + 1)
                sp.sem_inc(self.load_begun, 1)
                sp.dma_start(self.qks[:, :, :, :], io["st_qks"][bass.ds(i + 1, 1)].rearrange("a q k d -> a (q k d)")
                             .broadcast_to([P, 4 * D2])).then_inc(self.qks_in, 16)
                for k, done in ((2, 20), (0, 22), (1, 24)):
                    sp.wait_ge(self.proj, (i * 2 + 1) * 24 + done)
                    sp.sem_inc(self.load_begun, 1)
                    self.load_w(sp, i + 1, k)
                self.sp_shift(sp, i * 2 + 2)
                sp.wait_ge(self.xs_ready, i * 2 + 4)
                sp.sem_inc(self.load_begun, 1)
                self.load_f(sp, i + 1)
            self.sp_shift(sp, 2 * DEPTH - 1)

        def pe_proj(self, pe, u, t, ms):
            T = 4 * u + t
            b = self.b_of(u)
            l = self.l_of(u)
            for m in ms:
                if m == 0 and t == 0:
                    pe.wait_ge(self.xs_ready, u + 1)
                if m % 2 == 0 and t == 0:
                    pe.wait_ge((self.wv_in, self.wq_in, self.wk_in)[m // 2], l * 16 + 16)
                if m < 3:
                    if self.later(T):
                        pe.wait_ge(self.qk_used, T * 4 - 2 + m)
                elif m < 5:
                    pe.wait_ge(self.v_evac, T * 2 + m - 2)
                else:
                    pe.wait_ge(self.qk_used, T * 4 + 1)
                k, half = ((2, 0), (2, 1), (0, 0), (0, 1), (1, 0), (1, 1))[m]
                pe.matmul(PS[:, 4 + m % 3, :], self.xs[:, b, P * t:P * t + P],
                          self.wqkv[:, k, 512 * half:512 * half + 512], start=True, stop=True).then_inc(self.proj, 1)

        def later(self, T):
            return not isinstance(T, int) or T > 0

        def b_of(self, u):
            return self.now[0]

        def l_of(self, u):
            return self.now[1]

        def group(self, u, k):
            return u * 32 + 12 + k

        def pe_turn(self, pe, u, t, g, number):
            pe.wait_ge(self.r_ready, (4 * u + t) * 4 + g + 1)
            if not isinstance(number, int) or number > 0:
                pe.wait_ge(self.evac, number)
            for j in range(4):
                mm = pe.transpose(PS[:, 7, P * j:P * j + P], self.r[:, t % 2, g, P * j:P * j + P], ident)
            mm.then_inc(self.turned, 1)

        def act_turn(self, act, u, t, g, number):
            act.wait_ge(self.turned, number + 1)
            src = PS[:, 7, :].rearrange("p (c n) -> p c n", c=4)
            c = 4 * (g % 2)
            dst = self.qT[:, c:c + 4, P * t:P * t + P] if g < 2 else self.kT[:, c:c + 4, WIN + P * t:WIN + P * t + P]
            act.activation(dst, src, ACT.Copy).then_inc(self.evac, 1)

        def act_proj(self, act, u, t, ms):
            T = 4 * u + t
            for m in ms:
                act.wait_ge(self.proj, T * 6 + m + 1)
                if m < 2:
                    if m == 0 and (t >= 2 or self.later(u)):
                        act.wait_ge(self.v_stored, T * 16 - 16)
                    act.activation(self.v[:, t % 2, 512 * m:512 * m + 512], PS[:, 4 + m % 3, :], ACT.Copy)\
                       .then_inc(self.v_evac, 1)
                else:
                    c = m - 2
                    if c >= 2 or self.later(T):
                        act.wait_ge(self.ss_done, T * 4 + c - 1)
                    act.activation(self.sqh[:, c % 2, :], PS[:, 4 + m % 3, :], ACT.Square).then_inc(self.squares, 1)

        def dve_proj(self, dve, u, t, cs):
            T = 4 * u + t
            for c in cs:
                m, k = c + 2, c // 2
                ps = PS[:, 4 + m % 3, :]
                dve.wait_ge(self.squares, T * 4 + c + 1)
                if c == 0 and (t >= 2 or self.later(u)):
                    dve.wait_ge(self.turned, self.turned_by(u, t))
                if c == 0 and t == 0:
                    dve.wait_ge(self.rot_ready, self.l_of(u) + 1)
                h3 = lambda a: a.rearrange("p (h d) -> p h d", h=8)
                h4 = lambda a: a.rearrange("p (h s d) -> p h s d", h=8, s=2)
                table = lambda j: self.rot[:, k, j, t, :].unsqueeze(1).broadcast_to([P, 8, D2])
                dve.tensor_tensor(h3(self.r[:, t % 2, c, :]), h3(ps), table(0), ALU.mult)
                if c >= 2 or self.later(T):
                    dve.wait_ge(self.added, T * 4 + c - 1)
                for s in range(2):
                    ins = dve.tensor_tensor(h4(self.t2[:, c % 2, :])[:, :, s, :], h4(ps)[:, :, 1 - s, :],
                                            self.rot[:, k, 1, t, 32 * s:32 * s + 32].unsqueeze(1)
                                            .broadcast_to([P, 8, 32]), ALU.mult)
                ins.then_inc(self.qk_used, 1)
                if c == 0 and (t >= 2 or self.later(u)):
                    dve.wait_ge(self.r_ready, T * 4 - 4)
                dve.tensor_reduce(self.ss[:, t % 2, 8 * c:8 * c + 8], h3(self.sqh[:, c % 2, :]), X, ALU.add)\
                   .then_inc(self.ss_done, 1)
                if c == 3:
                    ss, y = self.ss[:, t % 2, :], self.gy[:, t % 2, :]
                    dve.wait_ge(self.ss_done, T * 4 + 4)
                    dve.tensor_scalar(ss, ss, 1e-24, -0.5, ALU.max, ALU.mult).then_inc(self.v_ready, 1)
                    dve.wait_ge(self.v_ready, T + 1)
                    dve.tensor_scalar(y.bitcast(I32), ss.bitcast(I32), -0.5, GUESS, ALU.mult, ALU.add)\
                       .then_inc(self.guess, 1)

        def turned_by(self, u, t):
            if t >= 2:
                if isinstance(u, int) and u == 0:
                    return 4 * (t - 1)
                return (u - 1) * 32 + 12 + (14, 22)[t - 2]
            if t == 0:
                return (u - 1) * 32 + 12 if not (isinstance(u, int) and u == 0) else 0
            return (u - 1) * 32 + 12 + 4

        def pool_proj(self, pool, u, t):
            T = 4 * u + t
            for c in range(4):
                pool.wait_ge(self.qk_used, T * 4 + c + 1)
                r = self.r[:, t % 2, c, :]
                pool.tensor_tensor(r, r, self.t2[:, c % 2, :], ALU.add).then_inc(self.added, 1)
            pool.wait_ge(self.guess, T + 1)
            ss, y, g = self.ss[:, t % 2, :], self.gy[:, t % 2, :], self.gt[:, t % 2, :]
            k = 0
            for _ in range(3):
                for f in (lambda: pool.tensor_tensor(g, y, y, ALU.mult),
                          lambda: pool.tensor_tensor(g, g, ss, ALU.mult),
                          lambda: pool.tensor_tensor(g, g, const("threehalves").broadcast_to([P, 32]), ALU.add),
                          lambda: pool.tensor_tensor(y, y, g, ALU.mult)):
                    f().then_inc(self.newton, 1)
                    k += 1
                    pool.wait_ge(self.newton, T * 12 + k)
            pool.wait_ge(self.added, T * 4 + 4)
            for c in range(4):
                r = self.r[:, t % 2, c, :].rearrange("p (h d) -> p h d", h=8)
                pool.tensor_tensor(r, r, y[:, 8 * c:8 * c + 8].unsqueeze(2).broadcast_to([P, 8, D2]), ALU.mult)\
                    .then_inc(self.r_ready, 1)

        def pe_scores(self, pe, u, t):
            T = 4 * u + t
            pe.wait_ge(self.evac, self.group(u, 4 if t == 3 else 0))
            pe.wait_ge(self.sub_done, T + 1)
            for e in range(2):
                pe.matmul(PS[:, e, :], self.identb[:, :],
                          self.wmask[:, min(t, 1), :].unsqueeze(1).broadcast_to([P, 8, 2 * WIN]),
                          start=True, stop=False, skip_group_check=True)
            for e in range(2):
                for c in range(8):
                    for w in range(4):
                        q = P * t + WIN * w
                        mm = pe.matmul(PS[WIN * w:WIN * w + WIN, e, D2 * c:D2 * c + D2],
                                       self.qT[64 * e:64 * e + 64, c, q:q + WIN],
                                       self.kT[64 * e:64 * e + 64, c, q:q + 2 * WIN],
                                       start=False, stop=(c == 7), skip_group_check=True,
                                       tile_position=(64 * e, WIN * w))
            mm.then_inc(self.scores, 1)

        def pe_turn_p(self, pe, u, t, number):
            for half in range(2):
                if half == 0:
                    pe.wait_ge(self.exps, 4 * u + t + 1)
                pe.wait_ge(self.evac, number + half)
                for j in range(4):
                    mm = pe.transpose(PS[:, 7, P * j:P * j + P],
                                      self.e[:, 4 * half + j, :, :].rearrange("p e k -> p (e k)"), ident)
                mm.then_inc(self.turned, 1)

        def act_turn_p(self, act, u, t, number):
            for half in range(2):
                act.wait_ge(self.turned, number + half + 1)
                if half == 0:
                    act.wait_ge(self.pv_done, 4 * u + t + 4)
                act.activation(self.pT[:, 4 * half:4 * half + 4, :], PS[:, 7, :].rearrange("p (c n) -> p c n", c=4),
                               ACT.Copy).then_inc(self.evac, 1)

        def pe_mix(self, pe, u, t, number):
            T = 4 * u + t
            pe.wait_ge(self.evac, number)
            pe.wait_ge(self.vshift[t], (u + 1) * 64)
            pe.wait_ge(self.on_ready, T + 1)
            pe.sem_inc(self.mix_begun, 1)
            for e in range(2):
                rows = slice(64 * e, 64 * e + 64)
                for c in range(8):
                    for w in range(4):
                        g = slice(WIN * w, WIN * w + WIN)
                        mm = pe.matmul(PS[g, 2 + e, D2 * c:D2 * c + D2], self.pT[rows, c, g],
                                       self.vv[rows, 4 * t + w, D2 * c:D2 * c + D2], start=True, stop=True,
                                       tile_position=(64 * e, WIN * w), skip_group_check=True)
            mm.then_inc(self.pv_done, 1)

        def pe_turn_o(self, pe, u, t, half, number):
            pe.wait_ge(self.on_ready, 4 * u + t + 2)
            pe.wait_ge(self.evac, number)
            for j in range(4):
                c = 4 * half + j
                mm = pe.transpose(PS[:, 7, P * j:P * j + P], self.on[:, c, :, :].rearrange("p e d -> p (e d)"), ident)
            mm.then_inc(self.turned, 1)

        def act_turn_o(self, act, u, t, half, number):
            act.wait_ge(self.turned, number + 1)
            act.activation(self.oT[:, 4 * half:4 * half + 4, P * t:P * t + P],
                           PS[:, 7, :].rearrange("p (c n) -> p c n", c=4), ACT.Copy).then_inc(self.evac, 1)

        def act_exp(self, act, u, t):
            act.wait_ge(self.sub_done, 4 * u + t + 2)
            act.activation(self.e[:, :, :, :], self.e[:, :, :, :], ACT.Exp, scale=8.0).then_inc(self.exps, 1)

        def dve_max(self, dve, u, t, number):
            T = 4 * u + t
            heads = lambda a: a.rearrange("p (e c) -> p e c", e=2)
            dve.wait_ge(self.scores, T + 1)
            ps = PS[:, 0:2, :].rearrange("p e (c k) -> p e c k", c=8)
            dve.tensor_reduce(heads(self.mx[:, :]), ps, X, ALU.max).then_inc(self.mx_ready, 1)
            dve.wait_ge(self.mx_ready, T + 1)
            dve.wait_ge(self.turned, number)
            dve.wait_ge(self.den_ready, T + 1)
            dve.tensor_tensor(self.e[:, :, :, :].rearrange("p c e k -> p e c k"), ps,
                              heads(self.mx[:, :]).unsqueeze(3).broadcast_to([P, 2, 8, 2 * WIN]),
                              ALU.subtract).then_inc(self.sub_done, 1)

        def dve_sum(self, dve, u, t):
            T = 4 * u + t
            dve.wait_ge(self.exps, T + 1)
            dve.tensor_reduce(self.den[:, :].rearrange("p (e c) -> p e c", e=2),
                              self.e[:, :, :, :].rearrange("p c e k -> p e c k"), X, ALU.add)\
               .then_inc(self.den_ready, 1)
            dve.wait_ge(self.den_ready, T + 2)
            dve.reciprocal(self.rden[:, t % 2, :], self.den[:, :]).then_inc(self.rden_ready, 1)

        def dve_out(self, dve, u, t, number):
            T = 4 * u + t
            dve.wait_ge(self.pv_done, T + 1 + 4)
            dve.wait_ge(self.rden_ready, T + 1)
            dve.wait_ge(self.turned, number)
            dve.tensor_tensor(self.on[:, :, :, :].rearrange("p c e d -> p e c d"),
                              PS[:, 2:4, :].rearrange("p e (c d) -> p e c d", c=8),
                              self.rden[:, t % 2, :].rearrange("p (e c) -> p e c", e=2).unsqueeze(3)
                              .broadcast_to([P, 2, 8, D2]), ALU.mult).then_inc(self.on_ready, 1)

        def pe_wo(self, pe, u):
            pe.wait_ge(self.wf_in, self.l_of(u) * self.WF + self.WF)
            pe.wait_ge(self.evac, self.group(u, 29))
            for c in range(8):
                mm = pe.matmul(PS[:, 2, :], self.wo[:, c, :], self.oT[:, c, :], start=(c == 0), stop=(c == 7))
            mm.then_inc(self.wo_done, 1)

        def pe_mean(self, pe, u):
            pe.wait_ge(self.xf_ready, u + 1)
            pe.matmul(PS[:, 3, :], const("mean"), self.xf[:, :], start=True, stop=True).then_inc(self.mean, 1)

        def pe_var(self, pe, u):
            pe.wait_ge(self.lnsq, u + 1)
            for j in range(8):
                mm = pe.matmul(PS[0:8, 3, 0:64], const("slide")[:, 15 - j:23 - j], sq[:, 0, 64 * j:64 * j + 64],
                               start=(j == 0), stop=(j == 7))
            mm.then_inc(self.var, 1)

        def pe_spread(self, pe, u):
            pe.wait_ge(self.rstd, u + 1)
            for j in range(8):
                mm = pe.matmul(PS[:, 3, 64 * j:64 * j + 64], cst[0:8, j:j + 1].broadcast_to([8, P]), rstd[0:8, 1, :],
                               start=(j == 0), stop=(j == 7))
            mm.then_inc(self.spread, 1)

        def pe_ffn(self, pe, u):
            pe.wait_ge(self.ffn_in, u + 1)
            for j, (a, w) in enumerate(self.CHUNKS):
                bank = 2 * (j % 2)
                if j == 2:
                    pe.wait_ge(self.act_ready, u * 3 + 1)
                pe.matmul(PS[0:w, bank + 1, :], self.w1[:, FFI + a:FFI + a + w], self.xfn[:, :], start=True, stop=True)
                pe.matmul(PS[0:w, bank, :], self.w1[:, a:a + w], self.xfn[:, :], start=True, stop=True)\
                  .then_inc(self.up, 1)
            for j, (a, w) in enumerate(self.CHUNKS):
                if j != 0:
                    pe.wait_ge(self.act_ready, u * 3 + j + 1)
                else:
                    pe.wait_ge(self.act_ready, u * 3 + 2)
                mm = pe.matmul(PS[:, 3, :], self.w2[0:w, j, :], self.hid[0:w, j, :], start=(j == 0), stop=(j == 2))
            mm.then_inc(self.down, 1)

        def act_ln_square(self, act, u):
            act.wait_ge(self.centred, u + 1)
            act.activation(sq[:, 0, :], xc[:, 0, :], ACT.Square).then_inc(self.lnsq, 1)

        def act_ln_root(self, act, u):
            act.wait_ge(self.var, u + 1)
            a = C_AT["eps"][0]
            act.activation(rstd[0:8, 0, :], PS[0:8, 3, 0:64], ACT.Sqrt, bias=cst[0:8, a:a + 1]).then_inc(self.std, 1)

        def act_ffn(self, act, u):
            for j, (a, w) in enumerate(self.CHUNKS):
                act.wait_ge(self.up, u * 3 + j + 1)
                if j == 2:
                    act.wait_ge(self.act_ready, u * 3 + 1)
                act.activation(self.gel[0:w, j % 2, :], PS[0:w, 2 * (j % 2) + 1, :], ACT.Gelu,
                               bias=self.sv[0:w, 6 + j:7 + j]).then_inc(self.gelu, 1)

        def shift(self, dve, b, dst, signal):
            dve.tensor_copy(dst[0:64, :], x[0:64, b, :])
            dve.tensor_copy(dst[64:P, 1:], x[64:P, b, 0:S - 1]).then_inc(signal, 1)

        def dve_wo(self, dve, u):
            b = self.b_of(u)
            dve.wait_ge(self.wo_done, u + 1)
            dve.tensor_tensor(x[:, b, :], x[:, b, :], PS[:, 2, :], ALU.add).then_inc(self.xu_ready, 1)
            dve.wait_ge(self.xu_ready, u * 2 + 1)
            self.shift(dve, b, self.xf, self.xf_ready)

        def dve_ln_centre(self, dve, u):
            dve.wait_ge(self.mean, u + 1)
            dve.wait_ge(self.xf_ready, u + 1)
            dve.tensor_tensor(xc[:, 0, :], self.xf[:, :], PS[:, 3, :], ALU.subtract).then_inc(self.centred, 1)

        def dve_ln_root(self, dve, u):
            dve.wait_ge(self.std, u + 1)
            dve.reciprocal(rstd[0:8, 1, :], rstd[0:8, 0, :]).then_inc(self.rstd, 1)

        def dve_ln_out(self, dve, u):
            dve.wait_ge(self.spread, u + 1)
            dve.wait_ge(self.centred, u + 1)
            dve.tensor_tensor(xc[:, 0, :], xc[:, 0, :], PS[:, 3, :], ALU.mult).then_inc(self.ln_tmp, 1)
            dve.wait_ge(self.ln_tmp, u + 1)
            dve.tensor_scalar(self.xfn[:, :], xc[:, 0, :], self.sv[:, 0:1], self.sv[:, 1:2], ALU.mult, ALU.add)\
               .then_inc(self.ffn_in, 1)

        def dve_ffn(self, dve, u):
            b = self.b_of(u)
            for j, (a, w) in enumerate(self.CHUNKS):
                dve.wait_ge(self.gelu, u * 3 + j + 1)
                dve.scalar_tensor_tensor(self.hid[0:w, j, :], PS[0:w, 2 * (j % 2), :], self.sv[0:w, 3 + j:4 + j],
                                         self.gel[0:w, j % 2, :], ALU.add, ALU.mult).then_inc(self.act_ready, 1)
            dve.wait_ge(self.down, u + 1)
            dve.scalar_tensor_tensor(x[:, b, :], PS[:, 3, :], self.sv[:, 2:3], x[:, b, :], ALU.add, ALU.add)\
               .then_inc(self.xu_ready, 1)
            dve.wait_ge(self.xu_ready, u * 2 + 2)
            self.shift(dve, b, self.xs[:, b, :], self.xs_ready)

        def dve_tables(self, dve, l, u):
            dve.wait_ge(self.qks_in, l * 16 + 16)
            if self.later(u):
                dve.wait_ge(self.qk_used, u * 16)
            for k in range(2):
                for j in range(2):
                    ins = dve.tensor_tensor(self.rot[:, k, j, :, :], self.base[:, k, j, :, :],
                                            self.qks[:, k, j, :].unsqueeze(1).broadcast_to([P, 4, D2]), ALU.mult)
            ins.then_inc(self.rot_ready, 1)

        def at(self, slot):
            self.now = slot[1:]
            return slot[0]

        def pe_slot(self, pe, slot, nxt):
            u = self.at(slot)
            g = lambda with_next, last=None: self.group(u, with_next if nxt or last is None else last)
            self.pe_scores(pe, u, 0)
            if nxt:
                self.pe_proj(pe, self.at(nxt), 0, (0, 1))
            for k in range(4):
                self.at(slot)
                self.pe_turn(pe, u, 3, k, g(k))
                if nxt:
                    self.pe_proj(pe, self.at(nxt), 0, (2 + k,))
            self.at(slot)
            self.pe_turn_p(pe, u, 0, g(4))
            self.pe_scores(pe, u, 1)
            self.pe_mix(pe, u, 0, g(6))
            self.pe_turn_p(pe, u, 1, g(6))
            self.pe_scores(pe, u, 2)
            self.pe_mix(pe, u, 1, g(8))
            for half in range(2):
                self.pe_turn_o(pe, u, 0, half, g(8 + half))
            if nxt:
                self.pe_proj_turn(pe, self.at(nxt), 1, g(10))
            self.at(slot)
            self.pe_turn_p(pe, u, 2, g(14, 10))
            self.pe_scores(pe, u, 3)
            self.pe_mix(pe, u, 2, g(16, 12))
            for half in range(2):
                self.pe_turn_o(pe, u, 1, half, g(16 + half, 12 + half))
            if nxt:
                self.pe_proj_turn(pe, self.at(nxt), 2, g(18))
            self.at(slot)
            self.pe_turn_p(pe, u, 3, g(22, 14))
            for half in range(2):
                self.pe_turn_o(pe, u, 2, half, g(24 + half, 16 + half))
            self.pe_mix(pe, u, 3, g(24, 16))
            if nxt:
                v = self.at(nxt)
                self.pe_proj(pe, v, 3, (0, 1, 2))
                self.pe_turn(pe, v, 2, 0, g(26))
            self.at(slot)
            for half in range(2):
                self.pe_turn_o(pe, u, 3, half, g(27 + half, 18 + half))
            if nxt:
                self.pe_wo(pe, u)
            else:
                self.pe_wo_last(pe, u)
            self.pe_mean(pe, u)
            if nxt:
                v = self.at(nxt)
                self.pe_proj(pe, v, 3, (3,))
                self.pe_turn(pe, v, 2, 1, g(29))
                self.pe_proj(pe, v, 3, (4,))
            self.at(slot)
            self.pe_var(pe, u)
            if nxt:
                v = self.at(nxt)
                self.pe_turn(pe, v, 2, 2, g(30))
                self.pe_proj(pe, v, 3, (5,))
                self.pe_turn(pe, v, 2, 3, g(31))
            self.at(slot)
            self.pe_spread(pe, u)
            self.pe_ffn(pe, u)

        def pe_wo_last(self, pe, u):
            pe.wait_ge(self.wf_in, self.l_of(u) * self.WF + self.WF)
            pe.wait_ge(self.evac, self.group(u, 20))
            for c in range(8):
                mm = pe.matmul(PS[:, 2, :], self.wo[:, c, :], self.oT[:, c, :], start=(c == 0), stop=(c == 7))
            mm.then_inc(self.wo_done, 1)

        def pe_proj_turn(self, pe, v, t, number):
            self.pe_proj(pe, v, t, (0, 1))
            for k in range(4):
                self.pe_turn(pe, v, t - 1, k, number + k)
                self.pe_proj(pe, v, t, (2 + k,))

        def act_proj_turn(self, act, v, t, number):
            self.act_proj(act, v, t, (0, 1))
            for k in range(4):
                self.act_turn(act, v, t - 1, k, number + k)
                self.act_proj(act, v, t, (2 + k,))

        def act_slot(self, act, slot, nxt):
            u = self.at(slot)
            g = lambda with_next, last=None: self.group(u, with_next if nxt or last is None else last)
            if nxt:
                self.act_proj(act, self.at(nxt), 0, (0, 1))
            for k in range(4):
                self.at(slot)
                self.act_turn(act, u, 3, k, g(k))
                if k == 1:
                    self.act_exp(act, u, 0)
                if nxt:
                    self.act_proj(act, self.at(nxt), 0, (2 + k,))
            self.at(slot)
            self.act_turn_p(act, u, 0, g(4))
            self.act_exp(act, u, 1)
            self.act_turn_p(act, u, 1, g(6))
            self.act_exp(act, u, 2)
            for half in range(2):
                self.act_turn_o(act, u, 0, half, g(8 + half))
            if nxt:
                self.act_proj_turn(act, self.at(nxt), 1, g(10))
            self.at(slot)
            self.act_turn_p(act, u, 2, g(14, 10))
            self.act_exp(act, u, 3)
            for half in range(2):
                self.act_turn_o(act, u, 1, half, g(16 + half, 12 + half))
            if nxt:
                self.act_proj_turn(act, self.at(nxt), 2, g(18))
            self.at(slot)
            self.act_turn_p(act, u, 3, g(22, 14))
            for half in range(2):
                self.act_turn_o(act, u, 2, half, g(24 + half, 16 + half))
            if nxt:
                v = self.at(nxt)
                self.act_proj(act, v, 3, (0, 1, 2))
                self.act_turn(act, v, 2, 0, g(26))
            self.at(slot)
            for half in range(2):
                self.act_turn_o(act, u, 3, half, g(27 + half, 18 + half))
            self.act_ln_square(act, u)
            if nxt:
                v = self.at(nxt)
                self.act_proj(act, v, 3, (3,))
                self.act_turn(act, v, 2, 1, g(29))
                self.act_proj(act, v, 3, (4,))
            self.at(slot)
            self.act_ln_root(act, u)
            if nxt:
                v = self.at(nxt)
                self.act_turn(act, v, 2, 2, g(30))
                self.act_proj(act, v, 3, (5,))
                self.act_turn(act, v, 2, 3, g(31))
            self.at(slot)
            self.act_ffn(act, u)

        def dve_slot(self, dve, slot, nxt, tables=None):
            u = self.at(slot)
            g = lambda with_next, last=None: self.group(u, with_next if nxt or last is None else last)
            self.dve_max(dve, u, 0, g(0))
            if nxt:
                v = self.at(nxt)
                if tables is not None:
                    self.dve_tables(dve, tables, v)
                self.dve_proj(dve, v, 0, (0, 1))
            self.at(slot)
            self.dve_sum(dve, u, 0)
            if nxt:
                self.dve_proj(dve, self.at(nxt), 0, (2, 3))
            self.at(slot)
            self.dve_max(dve, u, 1, g(6))
            self.dve_out(dve, u, 0, g(0))
            self.dve_sum(dve, u, 1)
            self.dve_max(dve, u, 2, g(8))
            self.dve_out(dve, u, 1, g(10))
            self.dve_sum(dve, u, 2)
            if nxt:
                self.dve_proj(dve, self.at(nxt), 1, range(4))
            self.at(slot)
            self.dve_max(dve, u, 3, g(16, 12))
            self.dve_out(dve, u, 2, g(18, 14))
            self.dve_sum(dve, u, 3)
            if nxt:
                self.dve_proj(dve, self.at(nxt), 2, range(4))
            self.at(slot)
            self.dve_out(dve, u, 3, g(26, 18))
            if nxt:
                self.dve_proj(dve, self.at(nxt), 3, (0,))
            self.at(slot)
            self.dve_wo(dve, u)
            self.dve_ln_centre(dve, u)
            if nxt:
                self.dve_proj(dve, self.at(nxt), 3, (1, 2))
            self.at(slot)
            self.dve_ln_root(dve, u)
            if nxt:
                self.dve_proj(dve, self.at(nxt), 3, (3,))
            self.at(slot)
            self.dve_ln_out(dve, u)
            self.dve_ffn(dve, u)

        def rounds(self, eng, body, last):
            with eng.Fori(0, DEPTH - 1) as i:
                body((i * 2, 0, i), (i * 2 + 1, 1, i), None)
                body((i * 2 + 1, 1, i), (i * 2 + 2, 0, i + 1), i + 1)
            L = DEPTH - 1
            body((2 * L, 0, L), (2 * L + 1, 1, L), None)
            last((2 * L + 1, 1, L))

        def pe(self, pe):
            pe.wait_ge(self.c_in, 48)
            pe.wait_ge(self.set_up, 5)
            pe.sem_inc(self.pv_done, 4)
            u = self.at((0, 0, 0))
            self.pe_proj(pe, u, 0, range(6))
            for t in range(1, 4):
                self.pe_proj_turn(pe, u, t, 4 * (t - 1))
            self.rounds(pe, lambda a, b, l: self.pe_slot(pe, a, b), lambda a: self.pe_slot(pe, a, None))

        def act(self, act):
            u = self.at((0, 0, 0))
            self.act_proj(act, u, 0, range(6))
            for t in range(1, 4):
                self.act_proj_turn(act, u, t, 4 * (t - 1))
            self.rounds(act, lambda a, b, l: self.act_slot(act, a, b), lambda a: self.act_slot(act, a, None))

        def dve(self, dve):
            for b in range(B):
                order.link(dve, dve.tensor_copy(xn[:, b, :], x[:, b, :]))
                order.link(dve, dve.tensor_copy(x[:, b, :], self.y0[:, b, :]))
            dve.wait_ge(self.set_up, 5)
            for b in range(B):
                self.shift(dve, b, self.xs[:, b, :], self.xs_ready)
            self.dve_tables(dve, 0, 0)
            dve.sem_inc(self.sub_done, 1)
            dve.sem_inc(self.den_ready, 1)
            dve.sem_inc(self.on_ready, 1)
            u = self.at((0, 0, 0))
            for t in range(4):
                self.dve_proj(dve, u, t, range(4))
            self.rounds(dve, lambda a, b, l: self.dve_slot(dve, a, b, l), lambda a: self.dve_slot(dve, a, None))
            dve.wait_ge(self.xs_ready, 2 * DEPTH + 2)
            for b in range(B):
                dve.tensor_tensor(x[:, b, :], x[:, b, :], xn[:, b, :], ALU.add).then_inc(x_ready, 1)

        def pool(self, pool):
            for k, what in enumerate((self.xs[64:P, :, 0:1], self.xf[64:P, 0:1], self.kT[:, :, 0:WIN],
                                      self.vv[0:WIN, 0, :], self.vv[64:64 + WIN, 0, :])):
                pool.memset(what, 0.0).then_inc(self.set_up, 1)
                pool.wait_ge(self.set_up, k + 1)
            for t in range(4):
                self.pool_proj(pool, 0, t)
            with pool.Fori(1, 2 * DEPTH) as u:
                for t in range(4):
                    self.pool_proj(pool, u, t)

    class LatentAttention:

        KEYS = S + KC
        TK = S // P + 1
        UNITS, GROUPS, PIECES = 16, 4, 8
        WAS = dict(w_in=16, proj=5, act_took=1, dve_took=2, scores=2, maxed=1, exps=1, mixed=1, out_prod=2,
                   turned=2, pT_ready=1)
        FREE = dict(exps=2, turned=2, pT_ready=1, mixed=2, oT_ready=1)

        def __init__(self):
            at = self.stack = ExitStack()
            s = lambda name, shape, dt=F32: sb("la_" + name, shape, dt, at=at)
            self.h0 = s("h0", [P, B, S])
            self.wo = s("wo", [P, INNER // P, P])
            self.wc = s("wc", [P, 3, P])
            self.mraw = s("mraw", [1, B * KC], U8)
            self.mneg = s("mneg", [1, B * KC])
            self.cc = s("cc", [P, 3, B * KC])
            self.cn = s("cn", [P, B * KC])
            self.q = s("q", [P, B, S])
            self.k = s("k", [P, B, self.KEYS])
            self.v = s("v", [P, B, self.TK, P])
            self.p = s("p", [P, 2, self.KEYS])
            self.pT = s("pT", [P, 2, 2, self.TK, 2 * P])
            self.nmx = s("nmx", [P, self.UNITS])
            self.den = s("den", [P, self.UNITS])
            self.rden = s("rden", [P, self.UNITS])
            self.oT = s("oT", [P, INNER // P, B, S])
            self.w_in, self.proj, self.act_took, self.dve_took = pair.w_in, pair.prod, pair.q_ready, pair.v_ready
            self.scores, self.maxed, self.exps, self.mixed = pair.scores, pair.centred, pair.exps, pair.mixed
            self.out_prod, self.turned, self.pT_ready = pair.out_prod, pair.qk_ready, pair.s1_ready
            self.wc_in, self.oT_ready, self.rdens, self.sums_ready = [
                sem("la_" + what) for what in ("wc_in", "oT_ready", "rdens", "sums_ready")]

        def c(self, what, k):
            return self.WAS.get(what, 0) + self.FREE.get(what, 0) + k

        def sp(self, sp):
            sp.dma_start(self.wo[:, :, :], io["la_wo"]).then_inc(self.w_in, 16)
            sp.dma_start(self.mraw[:, :], io["la_mask"]).then_inc(self.w_in, 16)
            sp.dma_start(self.wc[:, :, :], io["la_wc"][0]).then_inc(self.wc_in, 16)
            with sp.Fori(0, INNER // P - 1) as i:
                sp.wait_ge(self.proj, i * self.PIECES + self.c("proj", self.PIECES))
                sp.dma_start(self.wc[:, :, :], io["la_wc"][bass.ds(i + 1, 1)].rearrange("a p k n -> p (a k) n"))\
                  .then_inc(self.wc_in, 16)

        def ctx_pe(self, pe):
            pe.matmul(PS[:, 5, 0:B * KC], const("mean"), ctxT[:, :], start=True, stop=True).then_inc(norm.mean_ready, 1)
            pe.wait_ge(norm.squared, n("pe", norm.squared))
            pe.matmul(PS[:, 5, 0:B * KC], const("mean"), self.cc[:, 1, :], start=True, stop=True)\
              .then_inc(norm.var_ready, 1)
            pe.wait_ge(norm.rstd_ready, n("pe", norm.rstd_ready))

        def ctx_act(self, act):
            act.wait_ge(norm.centred, n("act", norm.centred))
            act.activation(self.cc[:, 1, :], self.cc[:, 0, :], ACT.Square).then_inc(norm.squared, 1)
            act.wait_ge(norm.var_ready, n("act", norm.var_ready))
            act.activation(self.cc[:, 2, :], PS[:, 5, 0:B * KC], ACT.Sqrt, bias=const("eps")).then_inc(norm.std_ready, 1)

        def ctx_dve(self, dve):
            dve.wait_ge(norm.mean_ready, n("dve", norm.mean_ready))
            dve.tensor_tensor(self.cc[:, 0, :], ctxT[:, :], PS[:, 5, 0:B * KC], ALU.subtract).then_inc(norm.centred, 1)
            dve.wait_ge(norm.std_ready, n("dve", norm.std_ready))
            order.link(dve, dve.reciprocal(self.cc[:, 2, :], self.cc[:, 2, :]))
            order.link(dve, dve.tensor_tensor(self.cc[:, 0, :], self.cc[:, 0, :], self.cc[:, 2, :], ALU.mult))
            dve.tensor_scalar(self.cn[:, :], self.cc[:, 0, :], column("la_g1"), column("la_b1"), ALU.mult, ALU.add)\
               .then_inc(norm.rstd_ready, 1)
            dve.wait_ge(self.w_in, self.WAS["w_in"] + 32)
            order.link(dve, dve.tensor_copy(self.mneg[:, :], self.mraw[:, :]))
            order.link(dve, dve.tensor_scalar(self.mneg[:, :], self.mneg[:, :], -NEG, NEG, ALU.mult, ALU.add))

        def unit(self, u):
            return u // 8, (u // 2) % 4, u % 2

        def span(self, u):
            return PS[:, 2 * (u % 2):2 * (u % 2) + 2, :].rearrange("p b n -> p (b n)")[:, 0:self.KEYS]

        def piece(self, i, k):
            bank = 4 + k % 4
            b = k // 4
            if k in (0, 4):
                return self.q[:, b, :], PS[:, bank, :], 0.125
            if k in (1, 5):
                return self.k[:, b, 0:S], PS[:, bank, :], 1.0
            if k == 2:
                return self.k[:, :, S:], PS[:, bank, 0:B * KC].rearrange("p (b k) -> p b k", b=B), 1.0
            if k in (3, 6):
                b = (k - 3) // 3
                return self.v[:, b, 0:4, :], PS[:, bank, :].rearrange("p (t n) -> p t n", t=4), 1.0
            return self.v[0:KC, :, 4, :], PS[0:KC, bank, 0:B * P].rearrange("p (b n) -> p b n", b=B), 1.0

        def pe_piece(self, pe, i, k):
            wq, wk, wv = [self.wc[:, j, :] for j in range(3)]
            bank, b = 4 + k % 4, k // 4
            if k in (0, 4):
                mm = pe.matmul(PS[:, bank, :], wq, xn[:, b, :], start=True, stop=True)
            elif k in (1, 5):
                mm = pe.matmul(PS[:, bank, :], wk, xn[:, b, :], start=True, stop=True)
            elif k == 2:
                mm = pe.matmul(PS[:, bank, 0:B * KC], wk, self.cn[:, :], start=True, stop=True)
            elif k in (3, 6):
                for t in range(4):
                    mm = pe.matmul(PS[:, bank, P * t:P * t + P], xn[:, (k - 3) // 3, P * t:P * t + P], wv,
                                   start=True, stop=True)
            else:
                for b in range(B):
                    mm = pe.matmul(PS[0:KC, bank, P * b:P * b + P], self.cn[:, KC * b:KC * b + KC], wv,
                                   start=True, stop=True)
            mm.then_inc(self.proj, 1)

        def pe_scores(self, pe, i, u):
            b, t, e = self.unit(u)
            at, h = 2 * (u % 2), slice(64 * e, 64 * e + 64)
            pe.wait_ge(self.exps, i * self.UNITS + self.c("exps", u - 1))
            pe.matmul(PS[:, at, :], self.q[h, b, P * t:P * t + P], self.k[h, b, 0:S], start=True, stop=True)
            pe.matmul(PS[:, at + 1, 0:KC], self.q[h, b, P * t:P * t + P], self.k[h, b, S:], start=True, stop=False)
            pe.matmul(PS[:, at + 1, 0:KC], const("one")[0:1, :], self.mneg[:, KC * b:KC * b + KC],
                      start=False, stop=True).then_inc(self.scores, 1)

        def pe_mix(self, pe, i, g):
            b, half = divmod(g, 2)
            at = 2 * P * half
            pe.wait_ge(self.rdens, i * (self.UNITS // 2) + 2 * g + 2)
            if g == 2:
                pe.wait_ge(self.oT_ready, i * B + self.c("oT_ready", 1))
            pe.wait_ge(self.pT_ready, i * self.UNITS + self.c("pT_ready", 4 * g + 4))
            for k in range(2):
                for e in range(2):
                    u = 4 * g + 2 * k + e
                    pe.matmul(PS[64 * e:64 * e + 64, 7, at + P * k:at + P * k + P],
                              self.rden[:, u:u + 1].broadcast_to([P, D2]), ident, start=True, stop=True,
                              skip_group_check=True, tile_position=(0, 64 * e))
            for k in range(self.TK):
                w = P if k < self.TK - 1 else KC
                for e in range(2):
                    mm = pe.matmul(PS[64 * e:64 * e + 64, 6, at:at + 2 * P], self.v[0:w, b, k, 64 * e:64 * e + 64],
                                   self.pT[0:w, g % 2, e, k, :], start=(k == 0), stop=(k == self.TK - 1),
                                   skip_group_check=True, tile_position=(0, 64 * e))
            mm.then_inc(self.mixed, 1)

        def pe(self, pe):
            norm.wait(pe, "pe")
            pe.wait_ge(self.w_in, self.WAS["w_in"] + 32)
            pe.sem_inc(self.turned, self.FREE["turned"])
            pe.sem_inc(self.mixed, self.FREE["mixed"])
            with pe.Fori(0, INNER // P) as i:
                pe.wait_ge(self.wc_in, i * 16 + 16)
                pe.wait_ge(self.pT_ready, i * self.UNITS + self.c("pT_ready", 0))
                self.pe_piece(pe, i, 0)
                self.pe_piece(pe, i, 1)
                pe.wait_ge(self.oT_ready, i * B + self.c("oT_ready", 0))
                self.pe_piece(pe, i, 2)
                self.pe_piece(pe, i, 3)
                pe.wait_ge(self.act_took, i * 4 + self.c("act_took", 1))
                self.pe_piece(pe, i, 4)
                pe.wait_ge(self.dve_took, i * 4 + self.c("dve_took", 1))
                self.pe_piece(pe, i, 5)
                pe.wait_ge(self.act_took, i * 4 + self.c("act_took", 2))
                for u in range(2):
                    self.pe_scores(pe, i, u)
                self.pe_piece(pe, i, 6)
                pe.wait_ge(self.dve_took, i * 4 + self.c("dve_took", 2))
                self.pe_piece(pe, i, 7)
                pe.wait_ge(self.act_took, i * 4 + self.c("act_took", 4))
                pe.wait_ge(self.dve_took, i * 4 + self.c("dve_took", 4))
                for u in range(self.UNITS):
                    pe.wait_ge(self.pT_ready, i * self.UNITS + self.c("pT_ready", u))
                    pe.wait_ge(self.exps, i * self.UNITS + self.c("exps", u + 1))
                    for k in range(self.TK):
                        w = P if k < self.TK - 1 else KC
                        mm = pe.transpose(PS[0:w, 4 + k // 4, P * (k % 4):P * (k % 4) + P],
                                          self.p[:, u % 2, P * k:P * k + w], ident)
                    mm.then_inc(self.turned, 1)
                    if u + 2 < self.UNITS:
                        self.pe_scores(pe, i, u + 2)
                    if u % 4 == 0 and u:
                        self.pe_mix(pe, i, u // 4 - 1)
                self.pe_mix(pe, i, self.GROUPS - 1)
            pe.wait_ge(self.oT_ready, self.c("oT_ready", INNER // P * B))
            for b in range(B):
                for c in range(INNER // P):
                    mm = pe.matmul(PS[:, b, :], self.wo[:, c, :], self.oT[:, c, b, :],
                                   start=(c == 0), stop=(c == INNER // P - 1))
                mm.then_inc(self.out_prod, 1)

        def act(self, act):
            act.sem_inc(self.exps, self.FREE["exps"])
            with act.Fori(0, INNER // P) as i:
                for k in range(0, self.PIECES, 2):
                    act.wait_ge(self.proj, i * self.PIECES + self.c("proj", k + 1))
                    dst, src, scale = self.piece(i, k)
                    act.activation(dst, src, ACT.Copy, scale=scale).then_inc(self.act_took, 1)
                for u in range(self.UNITS):
                    act.wait_ge(self.maxed, i * self.UNITS + self.c("maxed", u + 1))
                    act.wait_ge(self.turned, i * self.UNITS + self.c("turned", u - 1))
                    act.activation(self.p[:, u % 2, :], self.span(u), ACT.Exp, bias=self.nmx[:, u:u + 1],
                                   accum_out=self.den[:, u:u + 1]).then_inc(self.exps, 1)
                    if u == 9:
                        self.act_sums(act, i, 0)
                self.act_sums(act, i, 1)

        def act_sums(self, act, i, b):
            act.wait_ge(self.mixed, i * self.GROUPS + self.c("mixed", 2 * b + 2))
            act.activation(sq[:, b, :], PS[:, 7, :], ACT.Copy).then_inc(self.sums_ready, 1)

        def dve(self, dve):
            dve.sem_inc(self.pT_ready, self.FREE["pT_ready"])
            dve.sem_inc(self.oT_ready, self.FREE["oT_ready"])
            with dve.Fori(0, INNER // P) as i:
                for k in range(1, self.PIECES, 2):
                    dve.wait_ge(self.proj, i * self.PIECES + self.c("proj", k + 1))
                    dst, src, scale = self.piece(i, k)
                    dve.tensor_copy(dst, src).then_inc(self.dve_took, 1)
                    if k == 5:
                        for u in range(2):
                            self.dve_max(dve, i, u)
                for u in range(self.UNITS):
                    g, e = u // 4, u % 2
                    dve.wait_ge(self.turned, i * self.UNITS + self.c("turned", u + 1))
                    if u % 4 == 0:
                        dve.wait_ge(self.mixed, i * self.GROUPS + self.c("mixed", g - 1))
                    at = P * ((u // 2) % 2)
                    dve.tensor_copy(self.pT[:, g % 2, e, 0:4, at:at + P], PS[:, 4, :].rearrange("p (k q) -> p k q", k=4))
                    dve.tensor_copy(self.pT[0:KC, g % 2, e, 4, at:at + P], PS[0:KC, 5, 0:P]).then_inc(self.pT_ready, 1)
                    if u + 2 < self.UNITS:
                        self.dve_max(dve, i, u + 2)
                    if e == 1:
                        dve.reciprocal(self.rden[:, u - 1:u + 1], self.den[:, u - 1:u + 1]).then_inc(self.rdens, 1)
                    if u == 9:
                        self.dve_out(dve, i, 0)
                self.dve_out(dve, i, 1)
            for b in range(B):
                dve.wait_ge(self.out_prod, self.WAS["out_prod"] + b + 1)
                dve.tensor_tensor(x[:, b, :], x[:, b, :], PS[:, b, :], ALU.add).then_inc(x_ready, 1)

        def dve_out(self, dve, i, b):
            dve.wait_ge(self.sums_ready, i * B + b + 1)
            dve.tensor_tensor(self.oT[:, bass.ds(i, 1), b, :].rearrange("p a s -> p (a s)"), PS[:, 6, :],
                              sq[:, b, :], ALU.mult).then_inc(self.oT_ready, 1)

        def dve_max(self, dve, i, u):
            dve.wait_ge(self.scores, i * self.UNITS + self.c("scores", u + 1))
            dve.tensor_reduce(self.nmx[:, u:u + 1], self.span(u), X, ALU.max, negate=True).then_inc(self.maxed, 1)

    align = Align()
    align.stack.close()
    quantised = Quantised()
    quantised.stack.close()
    attend1 = ContextAttention("l1", True, 0)
    attend1.stack.close()
    pair = PairAttention()
    experts1 = Experts("m1", ACT.Gelu, 1.0, True, 0)
    experts1.stack.close()
    pair.stack.close()
    attend2 = ContextAttention("l2", False, 1)
    attend2.stack.close()
    stack = Stack()
    stack.stack.close()
    latents = LatentAttention()
    latents.stack.close()
    experts3 = Experts("m3", ACT.Silu, 1.5, False, 1)
    h7 = sb("h7", [P, B, S], at=experts3.stack)
    experts3.stack.close()
    final = sem("final")
    out = io["out"]
    block = ctx.enter_context(nc.Block())

    @block.sync
    def _(sp):
        sp.dma_start(x[:, :, :], io["xT"]).then_inc(loaded, 16)
        sp.dma_start(cst[:, :], io["cst"]).then_inc(loaded, 16)
        sp.dma_start(ctxT[:, :], io["ctxT"]).then_inc(loaded, 16)
        sp.dma_start(ctxN[:, :, :], io["ctxN"]).then_inc(loaded, 16)
        sp.dma_start(vec[:, :], io["vec"]).then_inc(loaded, 16)
        sp.dma_start(row[:, :], io["row"]).then_inc(loaded, 16)
        align.sp(sp)
        sp.wait_ge(x_ready, 2)
        quantised.sp(sp)
        sp.wait_ge(x_ready, 4)
        attend1.sp(sp)
        sp.wait_ge(x_ready, 6)
        pair.sp(sp)
        experts1.sp(sp)
        sp.wait_ge(x_ready, 8)
        attend2.sp(sp)
        sp.wait_ge(x_ready, 10)
        stack.sp(sp)
        sp.wait_ge(x_ready, 12)
        latents.sp(sp)
        sp.wait_ge(x_ready, 14)
        experts3.sp(sp)
        sp.wait_ge(x_ready, 2 * PARTS)
        sp.dma_start(out, x[:, :, :]).then_inc(final, 16)
        sp.wait_ge(final, 16)

    @block.gpsimd
    def _(pool):
        align.pool(pool)
        pool.wait_ge(x_ready, 4)
        attend1.pool(pool)
        pool.wait_ge(x_ready, 6)
        experts1.pool(pool)
        pool.wait_ge(x_ready, 8)
        attend2.pool(pool)
        pool.wait_ge(x_ready, 10)
        stack.pool(pool)

    @block.scalar
    def _(act):
        act.wait_ge(loaded, 16 * LOADS)
        norm.act(act)
        align.act(act)
        norm.act(act)
        quantised.weights_act(act)
        quantised.act(act)
        attend1.act_prepare(act)
        norm.act(act)
        attend1.act(act)
        norm.act(act)
        pair.act(act)
        experts1.gate_act(act)
        experts1.act(act)
        attend2.act_prepare(act)
        norm.act(act)
        attend2.act(act)
        norm.act(act)
        stack.act(act)
        norm.act(act)
        latents.ctx_act(act)
        norm.act(act)
        latents.act(act)
        norm.act(act)
        norm.act(act)
        experts3.gate_act(act)
        experts3.act(act)

    @block.tensor
    def _(pe):
        pe.wait_ge(loaded, 16 * LOADS)
        norm.pe(pe, x, None)
        align.pe(pe)
        norm.pe(pe, x, x_ready)
        quantised.weights_pe(pe)
        quantised.pe(pe)
        attend1.pe_prepare(pe)
        norm.pe(pe, x, x_ready)
        attend1.pe(pe)
        norm.pe(pe, x, x_ready)
        pair.pe(pe)
        experts1.gate_pe(pe)
        experts1.pe(pe)
        attend2.pe_prepare(pe)
        norm.pe(pe, x, x_ready)
        attend2.pe(pe)
        norm.pe(pe, x, x_ready)
        stack.pe(pe)
        norm.pe(pe, x, x_ready)
        latents.ctx_pe(pe)
        norm.wait(pe, "pe")
        norm.pe(pe, latents.h0, None)
        latents.pe(pe)
        norm.pe(pe, x, x_ready)
        norm.wait(pe, "pe")
        norm.pe(pe, h7, None)
        experts3.gate_pe(pe)
        experts3.pe(pe)

    @block.vector
    def _(dve):
        dve.wait_ge(loaded, 16 * LOADS)
        norm.dve(dve, x, xn)
        align.dve(dve)
        norm.dve(dve, x, xn)
        quantised.weights_dve(dve)
        quantised.dve(dve)
        attend1.dve_prepare(dve)
        norm.dve(dve, x, xn)
        attend1.dve(dve)
        norm.dve(dve, x, pair.h0)
        pair.dve(dve)
        experts1.gate_dve(dve)
        experts1.dve(dve, pair.h2)
        attend2.dve_prepare(dve)
        norm.dve(dve, x, xn)
        attend2.dve(dve)
        norm.dve(dve, x, stack.y0)
        stack.dve(dve)
        norm.dve(dve, x, latents.h0)
        latents.ctx_dve(dve)
        norm.wait(dve, "dve")
        norm.dve(dve, latents.h0, xn, column("la_g2"), column("la_b2"))
        latents.dve(dve)
        norm.dve(dve, x, h7)
        norm.wait(dve, "dve")
        norm.dve(dve, h7, xn, column("m3_g"), column("m3_b"))
        experts3.gate_dve(dve)
        experts3.dve(dve, h7)

    ctx.close()


def spans(parts):
    at, out = 0, {}
    for name, width in parts:
        out[name] = (at, width)
        at += width
    return out, at


C_AT, C_ALL = spans([("ident", P), ("mean", P), ("one", P), ("slide", 31), ("eps", 1), ("rinit", SC + 1),
                     ("iota", S), ("blk8", P), ("hm", H), ("kidx", E), ("threehalves", 1)])
VECTORS = {"l1_bq": "L1_xattn_bq", "l1_bk": "L1_xattn_bk", "l1_bo": "L1_xattn_bo",
           "pa_ln1w": "L1_ffn_ln1_weight", "pa_ln1b": "L1_ffn_ln1_bias",
           "pa_ln2w": "L1_ffn_ln2_weight", "pa_ln2b": "L1_ffn_ln2_bias",
           "l2_bq": "L2_xattn_bq", "l2_bk": "L2_xattn_bk", "l2_bo": "L2_xattn_bo",
           "la_g1": "L3_xattn_g1", "la_b1": "L3_xattn_b1", "la_g2": "L3_xattn_g2", "la_b2": "L3_xattn_b2",
           "m3_g": "L3_ffn_gamma", "m3_b": "L3_ffn_beta"}
V_AT, V_ALL = spans([(k, 1) for k in VECTORS])
R_AT, R_ALL = spans([("l1_bv", P), ("l2_bv", P)])


def constants():
    c = np.zeros((P, C_ALL), np.float32)

    def put(name, a):
        at, w = C_AT[name]
        c[:, at:at + w] = a
    put("ident", np.eye(P))
    put("mean", 1.0 / P)
    put("one", 1.0)
    s = np.zeros((P, 31)); s[:, 15] = 1.0 / P
    put("slide", s)
    put("eps", EPS)
    put("threehalves", 1.5)
    r = np.full((P, SC + 1), BIG); r[SEG - 1, 0] = 0; r[2 * SEG - 1, 0] = 0
    put("rinit", r)
    put("iota", np.arange(S)[None])
    head = np.arange(P) // DH
    put("blk8", head[:, None] == head[None])
    put("hm", head[:, None] == np.arange(H)[None])
    put("kidx", (E - np.arange(E))[None])
    r = np.arange(HKP)
    sel = (r[None] % KC == np.arange(KC)[:, None]) & (r[None] < HK)
    r = r.reshape(HKC, P).T
    hmask = (r[:, :, None] // KC == head[None, None]) & (r[:, :, None] < HK)
    half = np.arange(0, D2, 2, dtype=np.float32)
    token = np.arange(S, dtype=np.float32)
    freqs = token[:, None] * (1.0 / np.float32(10000.0) ** (half / D2)).astype(np.float32)[None]
    scale = ((half + 0.4 * D2) / (1.4 * D2)).astype(np.float32)[None] ** ((token - S // 2) / (WIN // 2))[:, None]
    sign = np.where(np.arange(D2) < D2 // 2, -1.0, 1.0)[None]
    both = lambda m: np.concatenate([m, m], axis=1)
    base = np.stack([np.stack([both(np.cos(freqs) * s), both(np.sin(freqs) * s) * sign])
                     for s in (scale, 1.0 / scale)])
    base = base.reshape(2, 2, 4, P, D2).transpose(3, 0, 1, 2, 4)
    i, jj = np.arange(P)[:, None] % WIN, np.arange(2 * WIN)[None]
    seen = (jj >= i) & (jj <= i + WIN)
    first = seen & ~((np.arange(P)[:, None] < WIN) & (jj < WIN))
    wmask = np.where(np.stack([first, seen], axis=1), 0.0, NEG)
    bf16 = mybir.dt.np(BF16)
    return {"st_base": np.ascontiguousarray(base, np.float32), "st_wmask": wmask.astype(bf16),
            "identb": np.eye(P).astype(bf16), "cst": c, "sel": sel.astype(np.float32), "hmask": hmask.astype(np.float32)}


def lay(inputs):
    f = lambda k: np.asarray(inputs[k])
    a = dict(constants())
    a["xT"] = np.ascontiguousarray(f("x").reshape(T, P).T.reshape(P, B, S))
    a["ctxT"] = np.ascontiguousarray(f("ctx_1024").reshape(B * KC, P).T)
    a["ctxN"] = np.ascontiguousarray(f("ctx_1024").transpose(1, 0, 2))
    for k, w in (("wg", "gate"), ("wu", "up")):
        a["q_" + k] = np.ascontiguousarray(f("L0_ffn_w_" + w).reshape(QW // P, P, P).transpose(1, 0, 2)).reshape(P, QW)
    a["q_wd"] = f("L0_ffn_w_down")
    a["vec"] = np.stack([f(k) for k in VECTORS.values()], axis=1)
    a["row"] = np.concatenate([f("L1_xattn_bv"), f("L2_xattn_bv")])[None]
    a["l1_w"] = np.stack([f("L1_xattn_W" + k).T for k in "qkvo"], axis=1)
    a["l2_w"] = np.stack([f("L2_xattn_W" + k) for k in "qkvo"], axis=1)
    for t, k in (("l1", "mask_1x1xSxS2_ik0"), ("l2", "mask_1x1xSxS2_fk1")):
        a[t + "_mask"] = np.ascontiguousarray(f(k)[0, 0].reshape(NT // B, P, KC).transpose(1, 0, 2))
    g = f("L1_ffn_qkv_weight").reshape(H // 2, 4, DH, P)
    twice = lambda k: np.repeat(g[:, k:k + 1], 2, axis=1)
    a["pa_w"] = np.stack([np.ascontiguousarray(w.reshape(P, P).T) for w in
                          (g[:, 0:2], twice(2), twice(3), f("L1_ffn_proj_weight"))], axis=1)
    a["m1_router"] = f("L1_ffn_router_weight")
    w = f("L2_ffn_Wqkv")
    wv = w[:, :, 2 * INNER:].reshape(DEPTH, P, H // 2, 2, D2).transpose(0, 1, 3, 2, 4).reshape(DEPTH, P, INNER)
    a["st_wqkv"], a["st_wo"] = np.concatenate([w[:, :, :2 * INNER], wv], axis=2), f("L2_ffn_Wo")
    a["st_w1"], a["st_w2"] = f("L2_ffn_W1"), f("L2_ffn_W2")
    scales = np.stack([f("L2_ffn_q_scale"), f("L2_ffn_k_scale")], axis=1)
    a["st_qks"] = np.stack([scales, np.roll(scales, D2 // 2, axis=2)], axis=2)
    b1 = np.zeros((DEPTH, 2, 3 * P), np.float32)
    b1[:, :, 0:FFI] = f("L2_ffn_b1").reshape(DEPTH, 2, FFI)
    a["st_sv"] = np.concatenate([np.stack([f("L2_ffn_ln_g"), f("L2_ffn_ln_b"), f("L2_ffn_b2")], axis=2),
                                 b1.reshape(DEPTH, 6, P).transpose(0, 2, 1)], axis=2)
    wkv = f("L3_xattn_Wkv")
    a["la_wc"] = np.ascontiguousarray(np.stack([f("L3_xattn_Wq"), wkv[:, 0:INNER], wkv[:, INNER:]])
                                      .reshape(3, P, INNER // P, P).transpose(2, 1, 0, 3))
    a["la_wo"] = np.ascontiguousarray(f("L3_xattn_Wout").reshape(INNER // P, P, P).transpose(1, 0, 2))
    a["la_mask"] = f("mask_BxS2_bk0").reshape(1, B * KC)
    a["m3_router"] = np.ascontiguousarray(f("L3_ffn_router_w").T)
    a["m3_w1"], a["m3_w2"] = f("L3_ffn_W1"), f("L3_ffn_W2")
    a["m1_w1"], a["m1_w2"] = f("L1_ffn_moe_w1"), f("L1_ffn_moe_w2")
    return a


def kernel(**inputs):
    import concourse.bacc as bacc
    from concourse.bass_utils import run_bass_kernel_spmd

    nc = bacc.Bacc("TRN2", target_bir_lowering=False, num_devices=1)
    arrays = lay(inputs)
    io = {k: nc.dram_tensor("in_" + k, a.shape, mybir.dt.from_np(a.dtype), kind="ExternalInput").ap()
          for k, a in arrays.items()}
    io["out"] = nc.dram_tensor("out_x", (P, B, S), F32, kind="ExternalOutput").ap()
    build(nc, io)
    r = run_bass_kernel_spmd(nc, [{"in_" + k: a for k, a in arrays.items()}], core_ids=[0])
    got = r.results[0]["out_x"]
    return np.ascontiguousarray(got.reshape(P, T).T.reshape(B, S, P))
```

```python
from contextlib import ExitStack

import numpy as np

import concourse.bass as bass
from concourse import mybir

F32 = mybir.dt.float32
F16 = mybir.dt.float16
BF16 = mybir.dt.bfloat16
I32 = mybir.dt.int32
U8 = mybir.dt.uint8
ALU = mybir.AluOpType
ACT = mybir.ActivationFunctionType
X = mybir.AxisListType.X

PARTS = 8
P = 128
B = 2
S = 512
T = B * S
NT = T // P
KC = 77
H = 16
EPS = 1e-5
BIG = 1e30
NEG = -1e30

SEG = 8
SC = S // SEG
STEPS = KC + SEG - 1
ROWS = SEG + KC + SEG
RING = 12
COPY = 4
assert STEPS % RING == 0 and RING % COPY == 0

DH = P // H
HK = H * KC
HKC = -(-HK // P)
HKP = HKC * P
HGROUPS = ((0, 6), (6, 6), (12, 4))

E = 8
FF = 512
CAP = -(-T * 2 * 5 // (E * 4))
assert CAP == 320

DEPTH = 6
D2 = 64
WIN = 32
INNER = H * D2
FFI = 341
GUESS = float(0x5f3759df - 2 ** 30 - 2 ** 22)


QW = 384
QMAX = 32767.0
MAGIC = 1.5 * 2.0 ** 23


class Tally:

    def __init__(self):
        self.seen = {}

    def __call__(self, who, sem):
        key = (who, sem.name)
        self.seen[key] = self.seen.get(key, 0) + 1
        return self.seen[key]


def build(nc, io):
    ctx = ExitStack()
    n = Tally()

    def sem(name):
        return ctx.enter_context(nc.semaphore(name))

    def sb(name, shape, dt=F32, at=None):
        return (at or ctx).enter_context(nc.sbuf_tensor(name, shape, dt))

    def dram(name, shape, dt=F32):
        return nc.dram_tensor(name, shape, dt, kind="Internal").ap()

    def view(ap, offset, dims):
        return bass.AP(tensor=ap.tensor, offset=offset, ap=dims)

    PS = ctx.enter_context(nc.psum_tensor("PS", [P, 8, 512], F32))

    x = sb("x", [P, B, S])
    xn = sb("xn", [P, B, S])
    xc = sb("xc", [P, B, S])
    sq = sb("sq", [P, B, S])
    rstd = sb("rstd", [16, 2, 64])
    cst = sb("cst", [P, C_ALL])
    vec = sb("vec", [P, V_ALL])
    row = sb("row", [1, R_ALL])
    ctxT = sb("ctxT", [P, B * KC])
    ctxN = sb("ctxN", [KC, B, P])

    def const(name):
        a, w = C_AT[name]
        return cst[:, a:a + w]

    def column(name):
        a = V_AT[name][0]
        return vec[:, a:a + 1]

    ident = const("ident")

    loaded = sem("loaded")
    x_ready = sem("x_ready")
    vec_step = sem("vec_step")
    LOADS = 6

    class Chain:

        def __init__(self, s, who="dve"):
            self.s, self.who = s, who

        def step(self, ins):
            ins.then_inc(self.s, 1)
            self.at = n(self.who, self.s)

        def link(self, eng, ins):
            ins.then_inc(self.s, 1)
            eng.wait_ge(self.s, n(self.who, self.s))

    order = Chain(vec_step)

    class Norm:

        def __init__(self, tag, parts=(0, 1), banks=(6, 7), chain=None):
            self.parts, self.banks, self.chain = parts, banks, chain or order
            self.mean_ready = sem(tag + "_mean_ready")
            self.centred = sem(tag + "_centred")
            self.squared = sem(tag + "_squared")
            self.var_ready = sem(tag + "_var_ready")
            self.std_ready = sem(tag + "_std_ready")
            self.rstd_ready = sem(tag + "_rstd_ready")
            self.spread_ready = sem(tag + "_spread_ready")
            self.normed = sem(tag + "_normed")
            self.uses = {}

        def wait(self, eng, who, halves=2):
            eng.wait_ge(self.normed, 2 * (self.uses[who] - 1) + halves)

        def rows(self, b):
            at = 8 * self.parts.index(b)
            return at, 8 * len(self.parts)

        def pe(self, pe, src, src_ready):
            self.uses["pe"] = self.uses.get("pe", 0) + 1
            for b in self.parts:
                if src_ready is not None:
                    pe.wait_ge(src_ready, n("pe", src_ready))
                pe.matmul(PS[:, self.banks[b], :], const("mean"), src[:, b, :], start=True, stop=True)\
                  .then_inc(self.mean_ready, 1)
            for b in self.parts:
                at, rows = self.rows(b)
                pe.wait_ge(self.squared, n("pe", self.squared))
                for j in range(8):
                    mm = pe.matmul(PS[0:rows, self.banks[self.parts[0]], 0:64],
                                   const("slide")[:, 15 - at - j:15 - at - j + rows],
                                   sq[:, b, 64 * j:64 * j + 64],
                                   start=(at + j == 0), stop=(at + j == rows - 1))
            mm.then_inc(self.var_ready, 1)
            pe.wait_ge(self.rstd_ready, n("pe", self.rstd_ready))
            for b in self.parts:
                at, rows = self.rows(b)
                for j in range(8):
                    mm = pe.matmul(PS[:, self.banks[b], 64 * j:64 * j + 64],
                                   cst[0:rows, at + j:at + j + 1].broadcast_to([rows, P]),
                                   rstd[0:rows, 1, :], start=(j == 0), stop=(j == 7))
                mm.then_inc(self.spread_ready, 1)

        def act(self, act):
            self.uses["act"] = self.uses.get("act", 0) + 1
            for b in self.parts:
                act.wait_ge(self.centred, n("act", self.centred))
                act.activation(sq[:, b, :], xc[:, b, :], ACT.Square).then_inc(self.squared, 1)
            _, rows = self.rows(self.parts[0])
            act.wait_ge(self.var_ready, n("act", self.var_ready))
            act.activation(rstd[0:rows, 0, :], PS[0:rows, self.banks[self.parts[0]], 0:64], ACT.Sqrt,
                           bias=cst[0:rows, C_AT["eps"][0]:C_AT["eps"][0] + 1]).then_inc(self.std_ready, 1)

        def dve(self, dve, src, dst, gamma=None, beta=None):
            self.uses["dve"] = self.uses.get("dve", 0) + 1
            c = self.chain
            for b in self.parts:
                dve.wait_ge(self.mean_ready, n("dve", self.mean_ready))
                dve.tensor_tensor(xc[:, b, :], src[:, b, :], PS[:, self.banks[b], :], ALU.subtract)\
                   .then_inc(self.centred, 1)
            _, rows = self.rows(self.parts[0])
            dve.wait_ge(self.std_ready, n("dve", self.std_ready))
            dve.reciprocal(rstd[0:rows, 1, :], rstd[0:rows, 0, :]).then_inc(self.rstd_ready, 1)
            for b in self.parts:
                dve.wait_ge(self.spread_ready, n("dve", self.spread_ready))
                if gamma is None:
                    dve.tensor_tensor(dst[:, b, :], xc[:, b, :], PS[:, self.banks[b], :], ALU.mult)\
                       .then_inc(self.normed, 1)
                else:
                    c.link(dve, dve.tensor_tensor(xc[:, b, :], xc[:, b, :], PS[:, self.banks[b], :],
                                                  ALU.mult))
                    dve.tensor_scalar(dst[:, b, :], xc[:, b, :], gamma, beta, ALU.mult, ALU.add)\
                       .then_inc(self.normed, 1)

    norm = Norm("ln")

    class Align:
        def __init__(self):
            at = self.stack = ExitStack()
            self.aa = sb("al_aa", [KC, B], at=at)
            self.ctxm2 = sb("al_ctxm2", [P, B * KC], at=at)
            self.dist = sb("al_dist", [KC, B, S], at=at)
            self.big = sb("al_big", [KC, B, S + 1], at=at)
            self.skew = sb("al_skew", [32, STEPS, SC], at=at)
            self.hist = sb("al_hist", [32, STEPS, SC], at=at)
            self.ring = sb("al_ring", [32, RING, SC + 1], at=at)
            self.low = sb("al_low", [32, SC], at=at)
            self.cur = sb("al_cur", [KC, B, S + 1], at=at)
            self.t0 = sb("al_t0", [KC, B, S], at=at)
            self.t1 = sb("al_t1", [KC, B, S], at=at)
            self.keep = sb("al_keep", [KC, B, S], at=at)
            self.enter = sb("al_enter", [KC, B, S], F16, at=at)
            self.left = sb("al_left", [KC, B, S], at=at)
            self.path = sb("al_path", [B, KC, S], F16, at=at)
            self.ent = sb("al_ent", [B, KC], at=at)
            self.entT = sb("al_entT", [KC, B], at=at)
            self.exT = sb("al_exT", [KC, B], at=at)
            self.pick = sb("al_pick", [B, 2, S], at=at)
            self.plane = dram("al_plane", [B, ROWS, S])
            self.costs = dram("al_costs", [B, ROWS, S])
            self.big_set = sem("al_big_set")
            self.pads_out = sem("al_pads_out")
            self.aa_ready = sem("al_aa_ready")
            self.xsq = sem("al_xsq")
            self.prod_ready = sem("al_prod_ready")
            self.d2_ready = sem("al_d2_ready")
            self.dist_ready = sem("al_dist_ready")
            self.plane_out = sem("al_plane_out")
            self.skew_in = sem("al_skew_in")
            self.scan_done = sem("al_scan_done")
            self.shifted = sem("al_shifted")
            self.ctxm2_ready = sem("al_ctxm2_ready")
            self.ring_free = sem("al_ring_free")
            self.costs_out = sem("al_costs_out")
            self.rows_in = sem("al_rows_in")
            self.enter_ready = sem("al_enter_ready")
            self.path_in = sem("al_path_in")
            self.walked = sem("al_walked")
            self.ent_ready = sem("al_ent_ready")
            self.entT_ready = sem("al_entT_ready")
            self.on_ready = sem("al_on_ready")
            self.sum_ready = sem("al_sum_ready")

        def strip(self, plane, b, row0):
            return view(plane, (b * ROWS + 1 + row0) * S + (SEG - 1) * SC,
                        [[S - SC, SEG], [S, STEPS], [1, SC]])

        def pool(self, pool):
            pool.memset(self.big[:, :, :], BIG).then_inc(self.big_set, 1)
            pool.memset(self.cur[:, :, 0:1], BIG).then_inc(self.big_set, 1)

        def sp(self, sp):
            sp.wait_ge(self.big_set, 3)
            for b in range(B):
                for r in (0, SEG + KC):
                    sp.dma_start(self.plane[b, r:r + SEG, :], self.big[0:SEG, b, 0:S]).then_inc(self.pads_out, 16)
            for b in range(B):
                sp.wait_ge(self.dist_ready, b + 1)
                sp.dma_start(self.plane[b, SEG:SEG + KC, :], self.dist[:, b, :]).then_inc(self.plane_out, 16)
            sp.wait_ge(self.pads_out, 64)
            sp.wait_ge(self.plane_out, 32)
            for b in range(B):
                sp.dma_start(self.skew[SEG * b:SEG * b + SEG, :, :], self.strip(self.plane, b, 0))\
                  .then_inc(self.skew_in, 16)
            sp.wait_ge(self.ring_free, STEPS // COPY + RING // COPY)
            for b in range(B):
                sp.dma_start(self.strip(self.costs, b, 0), self.hist[SEG * b:SEG * b + SEG, :, :])\
                  .then_inc(self.costs_out, 16)
            sp.wait_ge(self.costs_out, 32)
            for b in range(B):
                sp.dma_start(self.cur[:, b, 1:], self.costs[b, SEG:SEG + KC, :]).then_inc(self.rows_in, 16)
                sp.dma_start(self.big[1:KC, b, 1:], self.costs[b, SEG:SEG + KC - 1, :]).then_inc(self.rows_in, 16)
            sp.wait_ge(self.enter_ready, 1)
            for b in range(B):
                sp.dma_start(self.path[b:b + 1, :, :], self.enter[:, b, :]).then_inc(self.path_in, 16)

        def act(self, act):
            act.wait_ge(loaded, 16 * LOADS)
            for b in range(B):
                act.activation(self.dist[:, b, 0:P], ctxN[:, b, :], ACT.Square,
                               accum_out=self.aa[:, b:b + 1]).then_inc(self.aa_ready, 1)
            norm.wait(act, "act")
            for b in range(B):
                act.activation(sq[:, b, :], xn[:, b, :], ACT.Square).then_inc(self.xsq, 1)
            for b in range(B):
                act.wait_ge(self.d2_ready, b + 1)
                act.activation(self.dist[:, b, :], self.t0[:, b, :], ACT.Sqrt).then_inc(self.dist_ready, 1)
            act.sem_inc(self.ring_free, RING // COPY)
            with act.Fori(0, STEPS // RING) as i:
                for k in range(RING // COPY):
                    act.wait_ge(self.scan_done, i * RING + COPY * (k + 1) + 1)
                    act.activation(self.hist[:, bass.ds(i * RING + COPY * k, COPY), :],
                                   self.ring[:, COPY * k:COPY * k + COPY, 1:], ACT.Copy)\
                       .then_inc(self.ring_free, 1)

        def pe(self, pe):
            for b in range(B):
                if b == 0:
                    pe.wait_ge(self.ctxm2_ready, 1)
                pe.wait_ge(self.xsq, b + 1)
                pe.matmul(PS[0:KC, b, :], const("one")[:, 0:KC], sq[:, b, :], start=True, stop=False)
                pe.matmul(PS[0:KC, b, :], self.ctxm2[:, KC * b:KC * b + KC], xn[:, b, :],
                          start=False, stop=True).then_inc(self.prod_ready, 1)
            pe.wait_ge(self.ent_ready, 1)
            pe.transpose(PS[0:KC, 2, 0:B], self.ent[:, :], ident[0:B, 0:B]).then_inc(self.entT_ready, 1)
            for b in range(B):
                pe.wait_ge(self.on_ready, b + 1)
                pe.matmul(PS[:, b, :], ctxN[:, b, :], self.t1[:, b, :], start=True, stop=True)\
                  .then_inc(self.sum_ready, 1)

        def strips_dve(self, dve):
            dve.memset(self.skew[:, :, :], BIG).then_inc(self.big_set, 1)

        def dve(self, dve):
            iota = const("iota")
            dve.tensor_scalar(self.ctxm2[:, :], ctxT[:, :], -2.0, None, ALU.mult).then_inc(self.ctxm2_ready, 1)
            dve.wait_ge(self.aa_ready, 2)
            for b in range(B):
                dve.wait_ge(self.prod_ready, b + 1)
                dve.tensor_scalar(self.t0[:, b, :], PS[0:KC, b, :], self.aa[:, b:b + 1], 0.0, ALU.add, ALU.max)\
                   .then_inc(self.d2_ready, 1)
            a = C_AT["rinit"][0]
            dve.wait_ge(self.skew_in, 32)
            dve.tensor_copy(self.ring[:, RING - 1, :], cst[0:32, a:a + SC + 1]).then_inc(self.scan_done, 1)
            shift = [p + 1 if p < 16 and p % SEG < SEG - 1 else 31 for p in range(32)]
            with dve.Fori(0, STEPS // RING) as i:
                for k in range(RING):
                    now, last = self.ring[:, k, :], self.ring[:, (k - 1) % RING, :]
                    if k % COPY == 0:
                        dve.wait_ge(self.ring_free, i * (RING // COPY) + k // COPY + 1)
                    dve.wait_ge(self.scan_done, i * RING + k + 1)
                    dve.tensor_tensor(self.low[:, :], last[:, 1:], last[:, 0:SC], ALU.min)
                    dve.stream_shuffle(now[:, 0:1], last[:, SC:SC + 1], shift).then_inc(self.shifted, 1)
                    dve.wait_ge(self.shifted, i * RING + k + 1)
                    dve.tensor_tensor_scan(now[:, 1:], self.low[:, :],
                                           self.skew[:, bass.ds(i * RING + k, 1), :].rearrange("p a b -> p (a b)"),
                                           now[:, 0:1], ALU.min, ALU.add).then_inc(self.scan_done, 1)
            dve.wait_ge(self.rows_in, 64)
            above, diag, left = self.big[:, :, 1:], self.big[:, :, 0:S], self.cur[:, :, 0:S]
            cols = iota[0:KC, :].unsqueeze(1).broadcast_to([KC, B, S])
            order.step(dve.tensor_tensor(self.t1[:, :, :], diag, above, ALU.is_le))
            order.link(dve, dve.tensor_tensor(self.t0[:, :, :], diag, above, ALU.min))
            order.link(dve, dve.tensor_tensor(self.keep[:, :, :], left, self.t0[:, :, :], ALU.is_ge))
            order.link(dve, dve.tensor_tensor(self.t1[:, :, :], cols, self.t1[:, :, :], ALU.subtract))
            order.step(dve.tensor_tensor(self.t1[:, :, :], self.t1[:, :, :], self.keep[:, :, :], ALU.mult))
            order.link(dve, dve.tensor_tensor(self.t0[:, :, :], cols, self.keep[:, :, :], ALU.mult))
            for b in range(B):
                order.step(dve.tensor_tensor_scan(self.enter[:, b, :], self.t1[:, b, :], self.t1[:, b, :], 0.0,
                                                  ALU.max, ALU.max))
            dve.tensor_tensor_scan(self.left[:, 0, :], self.t0[:, 0, :], self.t0[:, 0, :], 0.0,
                                   ALU.max, ALU.max).then_inc(self.enter_ready, 1)
            dve.tensor_tensor_scan(self.left[:, 1, :], self.t0[:, 1, :], self.t0[:, 1, :], 0.0,
                                   ALU.max, ALU.max).then_inc(self.enter_ready, 1)
            dve.wait_ge(self.path_in, 32)
            dve.memset(self.ent[:, KC - 1:KC], float(S - 1)).then_inc(self.walked, 1)
            with dve.Fori(0, (KC - 1) // 4) as i:
                for k in range(4):
                    at = dve.snap(i * -4 + (KC - 1 - k))
                    dve.wait_ge(self.walked, i * 4 + k + 1)
                    dve.scalar_tensor_tensor(
                        self.pick[:, k % 2, :], iota[0:B, :], self.ent[:, bass.ds(at, 1)],
                        self.path[:, bass.ds(at, 1), :].rearrange("p a b -> p (a b)"), ALU.is_equal, ALU.mult,
                        accum_out=self.ent[:, bass.ds(at - 1, 1)]).then_inc(self.walked, 1)
            dve.wait_ge(self.walked, KC)
            dve.sem_inc(self.ent_ready, 1)
            dve.wait_ge(self.entT_ready, 1)
            order.link(dve, dve.tensor_copy(self.entT[:, :], PS[0:KC, 2, 0:B]))
            for b in range(B):
                order.link(dve, dve.scalar_tensor_tensor(
                    self.keep[:, b, :], iota[0:KC, :], self.entT[:, b:b + 1], self.left[:, b, :],
                    ALU.is_equal, ALU.mult, accum_out=self.exT[:, b:b + 1]))
                order.link(dve, dve.tensor_scalar(self.t0[:, b, :], iota[0:KC, :], self.entT[:, b:b + 1], None,
                                                  ALU.is_le))
                dve.scalar_tensor_tensor(self.t1[:, b, :], iota[0:KC, :], self.exT[:, b:b + 1], self.t0[:, b, :],
                                         ALU.is_ge, ALU.mult).then_inc(self.on_ready, 1)
            for b in range(B):
                dve.wait_ge(self.sum_ready, b + 1)
                dve.tensor_tensor(x[:, b, :], x[:, b, :], PS[:, b, :], ALU.add).then_inc(x_ready, 1)

    class Quantised:
        QF = 384
        CH = QF // P

        def __init__(self):
            CH = self.CH
            at = self.stack = ExitStack()
            self.wraw = sb("q_wraw", [P, 3, QW], at=at)
            self.wmax = sb("q_wmax", [P, 3, QW // 32], at=at)
            self.winv = sb("q_winv", [P, 3, QW // 32], at=at)
            self.wT = sb("q_wT", [P, 3, CH, P], at=at)
            self.h = sb("q_h", [P, 4, CH, T], at=at)
            self.mx = sb("q_mx", [P, 8], at=at)
            self.sc = sb("q_sc", [P, 8], at=at)
            self.inv = sb("q_inv", [P, 8], at=at)
            self.top = sb("q_top", [1, 8], at=at)
            self.w_in = sem("q_w_in")
            self.w_ready = sem("q_w_ready")
            self.wT_ready = sem("q_wT_ready")
            self.wT_copied = sem("q_wT_copied")
            self.mx_ready = sem("q_mx_ready")
            self.mxT_ready = sem("q_mxT_ready")
            self.top_ready = sem("q_top_ready")
            self.spread = sem("q_spread")
            self.x_quant = sem("q_x_quant")
            self.prod = sem("q_prod")
            self.evac = sem("q_evac")
            self.gate_quant = sem("q_gate_quant")
            self.sig_ready = sem("q_sig_ready")
            self.o_quant = sem("q_o_quant")
            self.down = sem("q_down")

        def sp(self, sp):
            for k, w in enumerate(("wg", "wu", "wd")):
                sp.dma_start(self.wraw[:, k, :], io["q_" + w]).then_inc(self.w_in, 16)

        def weights_dve(self, dve):
            dve.wait_ge(self.w_in, 48)
            blocks = self.wraw[:, :, :].rearrange("p k (g i) -> p (k g) i", i=32)
            G = 3 * QW // 32
            mx, inv = self.wmax[:, :, :].rearrange("p k g -> p (k g)"), self.winv[:, :, :].rearrange("p k g -> p (k g)")
            order.link(dve, dve.tensor_reduce(mx, blocks, X, ALU.max, apply_absolute_value=True))
            order.link(dve, dve.tensor_scalar(mx, mx, 1.0 / 7.0, 1e-12, ALU.mult, ALU.max))
            order.link(dve, dve.reciprocal(inv, mx))
            order.link(dve, dve.tensor_tensor(blocks, blocks, inv.unsqueeze(2).broadcast_to([P, G, 32]), ALU.mult))
            flat = self.wraw[:, :, :].rearrange("p k i -> p (k i)")
            order.link(dve, dve.tensor_scalar(flat, flat, MAGIC, -MAGIC, ALU.add, ALU.add))
            order.link(dve, dve.tensor_scalar(flat, flat, -8.0, 7.0, ALU.max, ALU.min))
            dve.tensor_tensor(blocks, blocks, mx.unsqueeze(2).broadcast_to([P, G, 32]), ALU.mult)\
               .then_inc(self.w_ready, 1)

        def weights_pe(self, pe):
            pe.wait_ge(self.w_ready, 1)
            for k in range(3):
                for c in range(self.CH):
                    mm = pe.transpose(PS[:, 3 + k, P * c:P * c + P], self.wraw[:, k, P * c:P * c + P], ident)
                mm.then_inc(self.wT_ready, 1)

        def weights_act(self, act):
            for k in range(3):
                act.wait_ge(self.wT_ready, k + 1)
                act.activation(self.wT[:, k, :, :].rearrange("p c i -> p (c i)"), PS[:, 3 + k, 0:QW], ACT.Copy)\
                   .then_inc(self.wT_copied, 1)

        def scale_dve(self, dve, j, src):
            dve.tensor_reduce(self.mx[:, j:j + 1], src, X, ALU.max, apply_absolute_value=True)\
               .then_inc(self.mx_ready, 1)
            dve.wait_ge(self.mxT_ready, n("dve", self.mxT_ready))
            dve.tensor_reduce(self.top[:, j:j + 1], PS[0:1, 7, 0:P], X, ALU.max).then_inc(self.top_ready, 1)
            dve.wait_ge(self.spread, n("dve", self.spread))
            order.link(dve, dve.tensor_scalar(self.sc[:, j:j + 1], PS[:, 7, P:P + 1], 1.0 / QMAX, 1e-12,
                                              ALU.mult, ALU.max))
            order.link(dve, dve.reciprocal(self.inv[:, j:j + 1], self.sc[:, j:j + 1]))

        def scale_pe(self, pe, j):
            pe.wait_ge(self.mx_ready, n("pe", self.mx_ready))
            pe.transpose(PS[0:1, 7, 0:P], self.mx[:, j:j + 1], ident).then_inc(self.mxT_ready, 1)
            pe.wait_ge(self.top_ready, n("pe", self.top_ready))
            pe.matmul(PS[:, 7, P:P + 1], const("one")[0:1, :], self.top[:, j:j + 1], start=True, stop=True)\
              .then_inc(self.spread, 1)

        def quant_dve(self, dve, j, a):
            order.link(dve, dve.tensor_scalar(a, a, self.inv[:, j:j + 1], MAGIC, ALU.mult, ALU.add))
            order.link(dve, dve.tensor_scalar(a, a, -MAGIC, QMAX, ALU.add, ALU.min))
            return dve.tensor_scalar(a, a, -QMAX - 1.0, self.sc[:, j:j + 1], ALU.max, ALU.mult)

        def dve(self, dve):
            up, gate, sig, o = [self.h[:, k, :, :].rearrange("p c t -> p (c t)") for k in range(4)]
            norm.wait(dve, "dve")
            flat = xn[:, :, :].rearrange("p b t -> p (b t)")
            self.scale_dve(dve, 0, flat)
            self.quant_dve(dve, 0, flat).then_inc(self.x_quant, 1)
            dve.wait_ge(self.evac, 6)
            self.scale_dve(dve, 1, gate)
            self.quant_dve(dve, 1, gate).then_inc(self.gate_quant, 1)
            dve.wait_ge(self.evac, 12)
            self.scale_dve(dve, 2, up)
            order.link(dve, self.quant_dve(dve, 2, up))
            dve.wait_ge(self.sig_ready, 1)
            order.link(dve, dve.tensor_scalar(sig, sig, 65536.0, MAGIC, ALU.mult, ALU.add))
            order.link(dve, dve.tensor_scalar(sig, sig, -MAGIC, 65535.0, ALU.add, ALU.min))
            order.link(dve, dve.tensor_scalar(sig, sig, 0.0, 1.0 / 65536.0, ALU.max, ALU.mult))
            order.link(dve, dve.tensor_tensor(gate, gate, sig, ALU.mult))
            self.scale_dve(dve, 3, gate)
            order.link(dve, self.quant_dve(dve, 3, gate))
            order.link(dve, dve.tensor_tensor(o, gate, up, ALU.mult))
            self.scale_dve(dve, 4, o)
            self.quant_dve(dve, 4, o).then_inc(self.o_quant, 1)
            for b in range(B):
                dve.wait_ge(self.down, b + 1)
                dve.tensor_tensor(x[:, b, :], x[:, b, :], PS[:, b, :], ALU.add).then_inc(x_ready, 1)

        def pe(self, pe):
            self.scale_pe(pe, 0)
            pe.wait_ge(self.x_quant, 1)
            pe.wait_ge(self.wT_copied, 3)
            k = 0
            for w, j in ((0, 1), (1, 2)):
                for c in range(self.CH):
                    for b in range(B):
                        if k >= 6:
                            pe.wait_ge(self.evac, k - 5)
                        pe.matmul(PS[:, k % 6, :], self.wT[:, w, c, :], xn[:, b, :],
                                  start=True, stop=True).then_inc(self.prod, 1)
                        k += 1
                self.scale_pe(pe, j)
            self.scale_pe(pe, 3)
            self.scale_pe(pe, 4)
            pe.wait_ge(self.o_quant, 1)
            for b in range(B):
                for c in range(self.CH):
                    mm = pe.matmul(PS[:, b, :], self.wT[:, 2, c, :], self.h[:, 3, c, S * b:S * b + S],
                                   start=(c == 0), stop=(c == self.CH - 1))
                mm.then_inc(self.down, 1)

        def act(self, act):
            k = 0
            for dst in (1, 0):
                for c in range(self.CH):
                    for b in range(B):
                        act.wait_ge(self.prod, k + 1)
                        act.activation(self.h[:, dst, c, S * b:S * b + S], PS[:, k % 6, :], ACT.Copy)\
                           .then_inc(self.evac, 1)
                        k += 1
            act.wait_ge(self.gate_quant, 1)
            act.activation(self.h[:, 2, :, :], self.h[:, 1, :, :], ACT.Sigmoid).then_inc(self.sig_ready, 1)

    class ContextAttention:

        COUNTS = dict(w_in=64, mask_ready=1, pads=1, kv_prod=3, kv_ready=3, kb_ready=2, vb_prod=6, vb_ready=6, q_prod=2,
                      q_ready=2, scores=NT, scores_read=NT, centred=NT, exps=NT, rden_ready=NT, probs=NT,
                      turned=3 * NT, pT_ready=3 * NT, mixed=NT, o_ready=2, out_prod=2)
        sems = {}

        def __init__(self, tag, mask_is_int, use):
            self.tag, self.mask_is_int = tag, mask_is_int
            self.past = {k: use * v for k, v in self.COUNTS.items()}
            at = self.stack = ExitStack()
            name = lambda a: tag + "_" + a
            self.w = sb(name("w"), [P, 4, P], at=at)
            self.mraw = sb(name("mraw"), [P, NT // B, KC], I32 if mask_is_int else F32, at=at)
            self.mask = sb(name("mask"), [P, NT // B, KC], at=at)
            self.sel = sb(name("sel"), [KC, HKP], at=at)
            self.hmask = sb(name("hmask"), [P, HKC, P], at=at)
            self.k = sb(name("k"), [P, B, KC], at=at)
            self.v = sb(name("v"), [KC, B, P], at=at)
            self.kb = sb(name("kb"), [P, B, H, KC], at=at)
            self.vb = sb(name("vb"), [P, B, HKC, P], at=at)
            self.q = sb(name("q"), [P, B, S], at=at)
            self.s = sb(name("s"), [P, 3, HKP], at=at)
            self.pT = sb(name("pT"), [P, 2, HKC, P], at=at)
            self.o = sb(name("o"), [P, B, S], at=at)
            self.mx = sb(name("mx"), [P, 2, H], at=at)
            self.den = sb(name("den"), [P, 2, H], at=at)
            self.rden = sb(name("rden"), [P, 2, H], at=at)
            if not use:
                self.sems.update({k: sem("ca_" + k) for k in self.COUNTS})
            (self.w_in, self.mask_ready, self.pads, self.kv_prod, self.kv_ready, self.kb_ready, self.vb_prod,
             self.vb_ready, self.q_prod, self.q_ready, self.scores, self.scores_read, self.centred, self.exps,
             self.rden_ready, self.probs, self.turned, self.pT_ready, self.mixed, self.o_ready, self.out_prod) = [
                self.sems[what] for what in self.COUNTS]

        def sp(self, sp):
            t = self.tag
            sp.dma_start(self.w[:, :, :], io[t + "_w"]).then_inc(self.w_in, 16)
            sp.dma_start(self.mraw[:, :, :], io[t + "_mask"]).then_inc(self.w_in, 16)
            sp.dma_start(self.sel[:, :], io["sel"]).then_inc(self.w_in, 16)
            sp.dma_start(self.hmask[:, :, :], io["hmask"]).then_inc(self.w_in, 16)

        def pe_prepare(self, pe):
            pe.wait_ge(self.w_in, self.past["w_in"] + 64)
            pe.matmul(PS[:, 0, 0:B * KC], self.w[:, 1, :], ctxT[:, :], start=True, stop=True).then_inc(self.kv_prod, 1)
            a = R_AT[self.tag + "_bv"][0]
            for b in range(B):
                pe.matmul(PS[0:KC, 1 + b, 0:P], ctxT[:, KC * b:KC * b + KC], self.w[:, 2, :], start=True, stop=False)
                pe.matmul(PS[0:KC, 1 + b, 0:P], const("one")[0:1, 0:KC], row[:, a:a + P],
                          start=False, stop=True).then_inc(self.kv_prod, 1)
            pe.wait_ge(self.kv_ready, self.past["kv_ready"] + 3)
            for b in range(B):
                for c in range(HKC):
                    bank, at = 3 * b + c // 4, P * (c % 4)
                    mm = pe.matmul(PS[:, bank, at:at + P], self.sel[:, P * c:P * c + P], self.v[:, b, :],
                                   start=True, stop=True)
                    if c % 4 == 3 or c == HKC - 1:
                        mm.then_inc(self.vb_prod, 1)

        def act_prepare(self, act):
            act.wait_ge(self.kv_prod, self.past["kv_prod"] + 1)
            act.activation(self.k[:, :, :].rearrange("p b k -> p (b k)"), PS[:, 0, 0:B * KC], ACT.Identity,
                           bias=column(self.tag + "_bk")).then_inc(self.kv_ready, 1)
            for b in range(B):
                act.wait_ge(self.kv_prod, self.past["kv_prod"] + 2 + b)
                act.activation(self.v[:, b, :], PS[0:KC, 1 + b, 0:P], ACT.Copy).then_inc(self.kv_ready, 1)

        def pool(self, pool):
            pool.memset(self.s[:, :, HK:], 0.0).then_inc(self.pads, 1)
            pool.wait_ge(self.w_in, self.past["w_in"] + 64)
            pool.wait_ge(self.kv_ready, self.past["kv_ready"] + 1)
            for b in range(B):
                pool.tensor_tensor(self.kb[:, b, :, :], self.k[:, b, :].unsqueeze(1).broadcast_to([P, H, KC]),
                                   const("hm").unsqueeze(2).broadcast_to([P, H, KC]), ALU.mult)\
                    .then_inc(self.kb_ready, 1)
            for t in range(NT):
                pool.wait_ge(self.rden_ready, self.past["rden_ready"] + t + 1)
                s = self.s[:, t % 3, 0:HK].rearrange("p (h k) -> p h k", h=H)
                pool.tensor_tensor(s, s, self.rden[:, t % 2, :].unsqueeze(2).broadcast_to([P, H, KC]), ALU.mult)\
                    .then_inc(self.probs, 1)

        def dve_prepare(self, dve):
            dve.wait_ge(self.w_in, self.past["w_in"] + 64)
            if self.mask_is_int:
                dve.tensor_scalar(self.mask[:, :, :], self.mraw[:, :, :], 0, NEG, ALU.is_equal, ALU.mult)\
                   .then_inc(self.mask_ready, 1)
            else:
                dve.tensor_scalar(self.mask[:, :, :], self.mraw[:, :, :], -1e9, None, ALU.mult)\
                   .then_inc(self.mask_ready, 1)
            for b in range(B):
                for g in range(3):
                    dve.wait_ge(self.vb_prod, self.past["vb_prod"] + 3 * b + g + 1)
                    c0, c1 = 4 * g, min(4 * g + 4, HKC)
                    dve.tensor_tensor(self.vb[:, b, c0:c1, :].rearrange("p c f -> p (c f)"),
                                      PS[:, 3 * b + g, 0:P * (c1 - c0)],
                                      self.hmask[:, c0:c1, :].rearrange("p c f -> p (c f)"), ALU.mult)\
                       .then_inc(self.vb_ready, 1)

        def pe(self, pe):
            pe.wait_ge(self.vb_ready, self.past["vb_ready"] + 6)
            norm.wait(pe, "pe")
            for b in range(B):
                pe.matmul(PS[:, 6 + b, :], self.w[:, 0, :], xn[:, b, :], start=True, stop=True)\
                  .then_inc(self.q_prod, 1)
            pe.wait_ge(self.kb_ready, self.past["kb_ready"] + 2)
            for t in range(NT + 2):
                if t < NT:
                    b, j = divmod(t, NT // B)
                    if j == 0:
                        pe.wait_ge(self.q_ready, self.past["q_ready"] + b + 1)
                    if t >= 1:
                        pe.wait_ge(self.scores_read, self.past["scores_read"] + t)
                    for g, (h0, nh) in enumerate(HGROUPS):
                        mm = pe.matmul(PS[:, g, 0:nh * KC], self.q[:, b, P * j:P * j + P],
                                       self.kb[:, b, h0:h0 + nh, :].rearrange("p h k -> p (h k)"), start=True, stop=True)
                    mm.then_inc(self.scores, 1)
                if t >= 2:
                    u = t - 2
                    b, j = divmod(u, NT // B)
                    pe.wait_ge(self.probs, self.past["probs"] + u + 1)
                    for c in range(HKC):
                        if u >= 1 and c % 4 == 0:
                            pe.wait_ge(self.pT_ready, self.past["pT_ready"] + 3 * (u - 1) + c // 4 + 1)
                        mm = pe.transpose(PS[:, 3 + c // 4, P * (c % 4):P * (c % 4) + P],
                                          self.s[:, u % 3, P * c:P * c + P], ident)
                        if c % 4 == 3 or c == HKC - 1:
                            mm.then_inc(self.turned, 1)
                    if j == 0 and b == 1:
                        pe.wait_ge(self.o_ready, self.past["o_ready"] + 1)
                    for c in range(HKC):
                        if c % 4 == 0:
                            pe.wait_ge(self.pT_ready, self.past["pT_ready"] + 3 * u + c // 4 + 1)
                        mm = pe.matmul(PS[:, 6, P * j:P * j + P], self.vb[:, b, c, :], self.pT[:, u % 2, c, :],
                                       start=(c == 0), stop=(c == HKC - 1))
                    mm.then_inc(self.mixed, 1)
                    if j == NT // B - 1:
                        pe.wait_ge(self.o_ready, self.past["o_ready"] + b + 1)
                        if b == 1:
                            pe.wait_ge(self.scores_read, self.past["scores_read"] + NT)
                        pe.matmul(PS[:, 7 - 7 * b, :], self.w[:, 3, :], self.o[:, b, :], start=True, stop=True)\
                          .then_inc(self.out_prod, 1)

        def act(self, act):
            for b in range(B):
                act.wait_ge(self.q_prod, self.past["q_prod"] + b + 1)
                act.activation(self.q[:, b, :], PS[:, 6 + b, :], ACT.Identity, bias=column(self.tag + "_bq"))\
                   .then_inc(self.q_ready, 1)
            for t in range(NT + 2):
                if t >= 2:
                    u = t - 2
                    b, j = divmod(u, NT // B)
                    for g in range(3):
                        act.wait_ge(self.turned, self.past["turned"] + 3 * u + g + 1)
                        if u >= 2 and g == 0:
                            act.wait_ge(self.mixed, self.past["mixed"] + u - 1)
                        c0, c1 = 4 * g, min(4 * g + 4, HKC)
                        act.activation(self.pT[:, u % 2, c0:c1, :].rearrange("p c f -> p (c f)"),
                                       PS[:, 3 + g, 0:P * (c1 - c0)], ACT.Copy).then_inc(self.pT_ready, 1)
                if t < NT:
                    act.wait_ge(self.centred, self.past["centred"] + t + 1)
                    s = self.s[:, t % 3, 0:HK]
                    act.activation(s, s, ACT.Exp).then_inc(self.exps, 1)
                if t >= 2 and j == NT // B - 1:
                    act.wait_ge(self.mixed, self.past["mixed"] + u + 1)
                    act.activation(self.o[:, b, :], PS[:, 6, :], ACT.Copy).then_inc(self.o_ready, 1)

        def dve(self, dve):
            scale = float(1.0 / np.sqrt(np.float32(DH)))
            dve.wait_ge(self.mask_ready, self.past["mask_ready"] + 1)
            dve.wait_ge(self.pads, self.past["pads"] + 1)
            for t in range(NT + 1):
                if t < NT:
                    j = t % (NT // B)
                    s = self.s[:, t % 3, 0:HK].rearrange("p (h k) -> p h k", h=H)
                    dve.wait_ge(self.scores, self.past["scores"] + t + 1)
                    if t >= 3:
                        dve.wait_ge(self.turned, self.past["turned"] + 3 * (t - 2))
                    for g, (h0, nh) in enumerate(HGROUPS):
                        ins = dve.scalar_tensor_tensor(
                            s[:, h0:h0 + nh, :], PS[:, g, 0:nh * KC].rearrange("p (h k) -> p h k", h=nh), scale,
                            self.mask[:, j, :].unsqueeze(1).broadcast_to([P, nh, KC]), ALU.mult, ALU.add)
                    ins.then_inc(self.scores_read, 1)
                if t >= 1:
                    u = t - 1
                    su = self.s[:, u % 3, 0:HK].rearrange("p (h k) -> p h k", h=H)
                    dve.wait_ge(self.exps, self.past["exps"] + u + 1)
                    order.link(dve, dve.tensor_reduce(self.den[:, u % 2, :], su, X, ALU.add))
                    if u >= 2:
                        dve.wait_ge(self.probs, self.past["probs"] + u - 1)
                    dve.reciprocal(self.rden[:, u % 2, :], self.den[:, u % 2, :]).then_inc(self.rden_ready, 1)
                if t < NT:
                    dve.wait_ge(self.scores_read, self.past["scores_read"] + t + 1)
                    order.link(dve, dve.tensor_reduce(self.mx[:, t % 2, :], s, X, ALU.max))
                    dve.tensor_tensor(s, s, self.mx[:, t % 2, :].unsqueeze(2).broadcast_to([P, H, KC]), ALU.subtract)\
                       .then_inc(self.centred, 1)
            for b in range(B):
                dve.wait_ge(self.out_prod, self.past["out_prod"] + b + 1)
                dve.scalar_tensor_tensor(x[:, b, :], PS[:, 7 - 7 * b, :], column(self.tag + "_bo"), x[:, b, :],
                                         ALU.add, ALU.add).then_inc(x_ready, 1)

    class PairAttention:

        def __init__(self):
            at = self.stack = ExitStack()
            self.w = sb("pa_w", [P, 4, P], at=at)
            self.h0 = sb("pa_h0", [P, B, S], at=at)
            self.h2 = sb("pa_h2", [P, B, S], at=at)
            self.q = sb("pa_q", [P, S], at=at)
            self.v = sb("pa_v", [P, B, S], at=at)
            self.qk = sb("pa_qk", [P, B, S], at=at)
            self.s = sb("pa_s", [P, B, S], at=at)
            self.m = sb("pa_m", [P, S], at=at)
            (self.w_in, self.prod, self.q_ready, self.v_ready, self.qk_ready, self.scores, self.s1_ready,
             self.centred, self.exps, self.mixed, self.out_prod, self.h2_ready) = [
                sem("pa_" + what) for what in (
                "w_in prod q_ready v_ready qk_ready scores s1_ready centred exps mixed out_prod h2_ready").split()]

        def sp(self, sp):
            sp.dma_start(self.w[:, :, :], io["pa_w"]).then_inc(self.w_in, 16)

        def pe(self, pe):
            norm.wait(pe, "pe")
            norm.pe(pe, self.h0, None)
            norm.wait(pe, "pe")
            pe.wait_ge(self.w_in, 16)
            for bank, (w, b) in enumerate(((0, 1), (1, 0), (1, 1), (2, 0), (2, 1))):
                pe.matmul(PS[:, bank, :], self.w[:, w, :], xn[:, b, :], start=True, stop=True).then_inc(self.prod, 1)
            for b in range(B):
                pe.wait_ge(self.qk_ready, b + 1)
                pe.matmul(PS[:, 5 + b, :], const("blk8"), self.qk[:, b, :], start=True, stop=True)\
                  .then_inc(self.scores, 1)
            pe.wait_ge(self.v_ready, 2)
            pe.matmul(PS[:, 0, :], self.w[:, 3, :], self.v[:, 0, :], start=True, stop=True).then_inc(self.out_prod, 1)
            pe.wait_ge(self.mixed, 1)
            pe.matmul(PS[:, 1, :], self.w[:, 3, :], self.qk[:, 0, :], start=True, stop=True).then_inc(self.out_prod, 1)
            norm.pe(pe, self.h2, self.h2_ready)

        def act(self, act):
            norm.act(act)
            act.wait_ge(self.prod, 1)
            act.activation(self.q[:, :], PS[:, 0, :], ACT.Copy).then_inc(self.q_ready, 1)
            for b in range(B):
                act.wait_ge(self.prod, 4 + b)
                act.activation(self.v[:, b, :], PS[:, 3 + b, :], ACT.Copy).then_inc(self.v_ready, 1)
            act.wait_ge(self.scores, 2)
            act.activation(self.s[:, 1, :], PS[:, 6, :], ACT.Copy).then_inc(self.s1_ready, 1)
            act.wait_ge(self.centred, 1)
            act.activation(self.s[:, :, :], self.s[:, :, :], ACT.Exp, scale=float(1.0 / np.sqrt(np.float32(DH))))\
               .then_inc(self.exps, 1)
            norm.act(act)

        def dve(self, dve):
            norm.wait(dve, "dve")
            norm.dve(dve, self.h0, xn, column("pa_ln1w"), column("pa_ln1b"))
            dve.wait_ge(self.q_ready, 1)
            for b in range(B):
                dve.wait_ge(self.prod, 2 + b)
                dve.tensor_tensor(self.qk[:, b, :], PS[:, 1 + b, :], self.q[:, :], ALU.mult).then_inc(self.qk_ready, 1)
            dve.wait_ge(self.s1_ready, 1)
            order.link(dve, dve.tensor_tensor(self.m[:, :], PS[:, 5, :], self.s[:, 1, :], ALU.max))
            order.step(dve.tensor_tensor(self.s[:, 0, :], PS[:, 5, :], self.m[:, :], ALU.subtract))
            dve.tensor_tensor(self.s[:, 1, :], self.s[:, 1, :], self.m[:, :], ALU.subtract).then_inc(self.centred, 1)
            dve.wait_ge(self.exps, 1)
            order.link(dve, dve.tensor_tensor(self.m[:, :], self.s[:, 0, :], self.s[:, 1, :], ALU.add))
            order.link(dve, dve.reciprocal(self.m[:, :], self.m[:, :]))
            for b in range(B):
                order.link(dve, dve.tensor_tensor(self.s[:, b, :], self.s[:, b, :], self.m[:, :], ALU.mult))
            dve.wait_ge(self.v_ready, 2)
            for b in range(B):
                order.link(dve, dve.tensor_tensor(self.s[:, b, :], self.s[:, b, :], self.v[:, b, :], ALU.mult))
            dve.tensor_tensor(self.qk[:, 0, :], self.s[:, 0, :], self.s[:, 1, :], ALU.add).then_inc(self.mixed, 1)
            for b in range(B):
                dve.wait_ge(self.out_prod, b + 1)
                dve.tensor_tensor(self.h2[:, b, :], self.h0[:, b, :], PS[:, b, :], ALU.add).then_inc(self.h2_ready, 1)
            dve.wait_ge(self.h2_ready, 2)
            norm.dve(dve, self.h2, xn, column("pa_ln2w"), column("pa_ln2b"))

    class Experts:

        COUNTS = dict(router_in=16, rank_step=3, logits=1, g_centred=1, g_exps=1, g_ready=1, g_turned=4, wT_ready=2,
                      wb_prod=E * B, wb_ready=E * B, w_in0=16 * E, w_in1=16 * E, h_prod=E * B * FF // P,
                      h_ready=4 + E * B * FF // P, y_prod=2 + E * B, y_used=2 + E * B, y_step=E * B)
        sems = {}

        def __init__(self, tag, act_fn, temperature, capped, use):
            self.tag, self.fn, self.temperature, self.capped = tag, act_fn, temperature, capped
            self.past = {k: use * v for k, v in self.COUNTS.items()}
            at = self.stack = ExitStack()
            name = lambda a: tag + "_" + a
            self.router = sb(name("router"), [P, E], at=at)
            self.w1 = sb(name("w1"), [P, 2, FF], at=at)
            self.w2 = sb(name("w2"), [P, 2, FF // P, P], at=at)
            self.g = sb(name("g"), [P, 4, NT, E], at=at)
            self.r = sb(name("r"), [P, 2, NT], at=at)
            self.wT = sb(name("wT"), [E, T], at=at)
            self.rank = sb(name("rank"), [E, T], at=at)
            self.ones = sb(name("ones"), [E, T], at=at)
            self.wb = sb(name("wb"), [P, E, B, S], at=at)
            self.h = sb(name("h"), [P, 2, FF // P, S], at=at)
            self.y = sb(name("y"), [P, 2, S], at=at)
            if not use:
                self.sems.update({k: sem("ex_" + k) for k in self.COUNTS})
            (self.router_in, self.rank_step, self.logits, self.g_centred, self.g_exps, self.g_ready, self.g_turned,
             self.wT_ready, self.wb_prod, self.wb_ready, self.w_in0, self.w_in1, self.h_prod, self.h_ready,
             self.y_prod, self.y_used, self.y_step) = [self.sems[what] for what in self.COUNTS]
            self.w_in = (self.w_in0, self.w_in1)

        def load(self, sp, e, slot):
            sp.dma_start(self.w1[:, slot, :], io[self.tag + "_w1"][e]).then_inc(self.w_in[slot], 16)
            sp.dma_start(self.w2[:, slot, :, :], io[self.tag + "_w2"][e].rearrange("(c p) d -> p c d", p=P))\
              .then_inc(self.w_in[slot], 16)

        def sp(self, sp):
            sp.dma_start(self.router[:, :], io[self.tag + "_router"]).then_inc(self.router_in, 16)
            for e in range(2):
                self.load(sp, e, e)
            with sp.Fori(0, E // 2 - 1) as i:
                for slot in range(2):
                    sp.wait_ge(self.y_prod, self.past["y_prod"] + i * 4 + 2 * slot + 4)
                    e = i * 2 + 2 + slot
                    sp.dma_start(self.w1[:, slot, :], io[self.tag + "_w1"][bass.ds(e, 1)].rearrange("a p f -> p (a f)"))\
                      .then_inc(self.w_in[slot], 16)
                    sp.dma_start(self.w2[:, slot, :, :],
                                 io[self.tag + "_w2"][bass.ds(e, 1)].rearrange("a (c p) d -> p (a c) d", p=P))\
                      .then_inc(self.w_in[slot], 16)

        def pool(self, pool):
            pool.memset(self.ones[:, :], 1.0).then_inc(self.rank_step, 1)

        def gate_dve(self, dve):
            logits = PS[:, 6, 0:NT * E].rearrange("p (t e) -> p t e", e=E)
            w, sel, t2, ex = [self.g[:, k, :, :] for k in range(4)]
            r0, r1 = self.r[:, 0, :], self.r[:, 1, :]
            wide = lambda r: r.unsqueeze(2).broadcast_to([P, NT, E])
            kidx = const("kidx").unsqueeze(1).broadcast_to([P, NT, E])

            def pick(src, dst):
                order.link(dve, dve.tensor_reduce(r0, src, X, ALU.max))
                order.link(dve, dve.tensor_tensor(dst, src, wide(r0), ALU.is_equal))
                order.link(dve, dve.tensor_tensor(dst, dst, kidx, ALU.mult))
                order.link(dve, dve.tensor_reduce(r0, dst, X, ALU.max))
                order.link(dve, dve.tensor_tensor(dst, dst, wide(r0), ALU.is_equal))

            dve.wait_ge(self.logits, self.past["logits"] + 1)
            order.link(dve, dve.tensor_reduce(r0, logits, X, ALU.max))
            dve.tensor_tensor(ex, logits, wide(r0), ALU.subtract).then_inc(self.g_centred, 1)
            dve.wait_ge(self.g_exps, self.past["g_exps"] + 1)
            pick(ex, sel)
            order.link(dve, dve.scalar_tensor_tensor(w, sel, -2.0, ex, ALU.mult, ALU.add))
            pick(w, t2)
            order.link(dve, dve.tensor_tensor(sel, sel, t2, ALU.add))
            order.link(dve, dve.tensor_tensor(w, ex, sel, ALU.mult))
            order.link(dve, dve.tensor_reduce(r1, w if self.capped else ex, X, ALU.add))
            order.link(dve, dve.reciprocal(r1, r1))
            dve.tensor_tensor(w, w, wide(r1), ALU.mult).then_inc(self.g_ready, 1)
            if not self.capped:
                for b in range(B):
                    dve.wait_ge(self.g_turned, self.past["g_turned"] + b + 1)
                    dve.tensor_copy(self.wT[:, S * b:S * b + S], PS[0:E, 6 + b, :]).then_inc(self.wT_ready, 1)
                return
            dve.wait_ge(self.rank_step, self.past["rank_step"] + 1)
            for b in range(B):
                dve.wait_ge(self.g_turned, self.past["g_turned"] + 1 + b)
                init = self.rank[:, S - 1:S] if b else 0.0
                dve.tensor_tensor_scan(self.rank[:, S * b:S * b + S], self.ones[:, S * b:S * b + S],
                                       PS[0:E, 6 + b, :], init, ALU.mult, ALU.add).then_inc(self.rank_step, 1)
                dve.wait_ge(self.rank_step, self.past["rank_step"] + 2 + b)
            for b in range(B):
                dve.wait_ge(self.g_turned, self.past["g_turned"] + 3 + b)
                dve.scalar_tensor_tensor(self.wT[:, S * b:S * b + S], self.rank[:, S * b:S * b + S], float(CAP),
                                         PS[0:E, 6 + b, :], ALU.is_le, ALU.mult).then_inc(self.wT_ready, 1)


        def hidden_pe(self, pe, u):
            e, b = divmod(u, B)
            if b == 0:
                pe.wait_ge(self.w_in[e % 2], self.past["w_in0"] + (e // 2) * 32 + 32)
            for c in range(FF // P):
                pe.wait_ge(self.h_ready, self.past["h_ready"] + 4 * u + c + 1)
                pe.matmul(PS[:, c, :], self.w1[:, e % 2, P * c:P * c + P], xn[:, b, :], start=True, stop=True)\
                  .then_inc(self.h_prod, 1)

        def outward_pe(self, pe, u):
            e = u // B
            pe.wait_ge(self.h_ready, self.past["h_ready"] + 4 * u + 4 + 4)
            pe.wait_ge(self.y_used, self.past["y_used"] + u + 1)
            for c in range(FF // P):
                mm = pe.matmul(PS[:, 4 + u % 2, :], self.w2[:, e % 2, c, :], self.h[:, u % 2, c, :],
                               start=(c == 0), stop=(c == FF // P - 1))
            mm.then_inc(self.y_prod, 1)

        def spread_pe(self, pe, u):
            e, b = divmod(u, B)
            if u < 2:
                pe.wait_ge(self.wT_ready, self.past["wT_ready"] + 2)
            else:
                pe.wait_ge(self.wb_ready, self.past["wb_ready"] + u - 1)
            pe.matmul(PS[:, 6 + u % 2, :], cst[0:E, e:e + 1].broadcast_to([E, P]), self.wT[:, S * b:S * b + S],
                      start=True, stop=True).then_inc(self.wb_prod, 1)

        def turn_pe(self, pe, k):
            for t in range(NT):
                mm = pe.transpose(PS[0:E, 6 + t // 4, P * (t % 4):P * (t % 4) + P], self.g[:, k, t, :], ident)
                if t % 4 == 3:
                    mm.then_inc(self.g_turned, 1)

        def pe(self, pe):
            norm.wait(pe, "pe")
            pe.wait_ge(self.router_in, self.past["router_in"] + 16)
            for t in range(NT):
                mm = pe.matmul(PS[:, 6, E * t:E * t + E], xn[:, t * P // S, P * (t % (S // P)):P * (t % (S // P)) + P],
                               self.router[:, :], start=True, stop=True)
            mm.then_inc(self.logits, 1)
            pe.sem_inc(self.y_prod, 2)
            self.hidden_pe(pe, 0)
            self.hidden_pe(pe, 1)
            self.outward_pe(pe, 0)
            self.outward_pe(pe, 1)
            pe.wait_ge(self.g_ready, self.past["g_ready"] + 1)
            if self.capped:
                self.turn_pe(pe, 1)
                self.hidden_pe(pe, 2)
                pe.wait_ge(self.rank_step, self.past["rank_step"] + 1 + B)
                self.turn_pe(pe, 0)
            else:
                self.turn_pe(pe, 0)
                self.hidden_pe(pe, 2)
            self.hidden_pe(pe, 3)
            self.spread_pe(pe, 0)
            self.spread_pe(pe, 1)
            for u in range(4, E * B + 2):
                self.outward_pe(pe, u - 2)
                self.spread_pe(pe, u - 2)
                if u < E * B:
                    self.hidden_pe(pe, u)

        def hidden_act(self, act, u):
            for c in range(FF // P):
                act.wait_ge(self.h_prod, self.past["h_prod"] + 4 * u + c + 1)
                if c == 0:
                    act.wait_ge(self.y_prod, self.past["y_prod"] + u + 1)
                act.activation(self.h[:, u % 2, c, :], PS[:, c, :], self.fn).then_inc(self.h_ready, 1)

        def spread_act(self, act, u):
            e, b = divmod(u, B)
            act.wait_ge(self.wb_prod, self.past["wb_prod"] + u + 1)
            act.activation(self.wb[:, e, b, :], PS[:, 6 + u % 2, :], ACT.Copy).then_inc(self.wb_ready, 1)

        def act(self, act):
            act.sem_inc(self.h_ready, 4)
            act.wait_ge(self.g_centred, self.past["g_centred"] + 1)
            g = self.g[:, 3, :, :]
            act.activation(g, g, ACT.Exp, scale=1.0 / self.temperature).then_inc(self.g_exps, 1)
            for u in range(4):
                self.hidden_act(act, u)
            self.spread_act(act, 0)
            self.spread_act(act, 1)
            for u in range(4, E * B + 2):
                self.spread_act(act, u - 2)
                if u < E * B:
                    self.hidden_act(act, u)

        def dve(self, dve, base):
            dve.sem_inc(self.y_used, 2)
            self.gate_dve(dve)
            for b in range(B):
                order.link(dve, dve.tensor_tensor(x[:, b, :], x[:, b, :], base[:, b, :], ALU.add))
            with dve.Fori(0, E // 2) as i:
                for u in range(4):
                    slot, b = divmod(u, B)
                    dve.wait_ge(self.wb_ready, self.past["wb_ready"] + i * 4 + u + 1)
                    dve.wait_ge(self.y_prod, self.past["y_prod"] + i * 4 + u + 3)
                    dve.tensor_tensor(self.y[:, u % 2, :], PS[:, 4 + u % 2, :],
                                      self.wb[:, bass.ds(i * 2 + slot, 1), b, :].rearrange("p a s -> p (a s)"),
                                      ALU.mult).then_inc(self.y_used, 1)
                    dve.wait_ge(self.y_used, self.past["y_used"] + i * 4 + u + 3)
                    dve.tensor_tensor(x[:, b, :], x[:, b, :], self.y[:, u % 2, :], ALU.add).then_inc(self.y_step, 1)
            dve.wait_ge(self.y_step, self.past["y_step"] + 2 * E)
            dve.sem_inc(x_ready, 2)

    class Stack:

        TILES = S // P
        CHUNKS = ((0, 128), (128, 128), (256, FFI - 256))

        def __init__(self):
            at = self.stack = ExitStack()
            s = lambda name, shape, dt=F32: sb("st_" + name, shape, dt, at=at)
            self.wqkv = s("wqkv", [P, 3, INNER])
            self.wo = s("wo", [P, INNER // P, P])
            self.w1 = s("w1", [P, 2 * FFI])
            self.w2 = s("w2", [P, 3, P])
            self.sv = s("sv", [P, 9])
            self.qks = s("qks", [P, 2, 2, D2])
            self.base = s("base", [P, 2, 2, 4, D2])
            self.rot = s("rot", [P, 2, 2, 4, D2])
            self.wmask = s("wmask", [P, 2, 2 * WIN], BF16)
            self.identb = s("identb", [P, P], BF16)
            self.xs = s("xs", [P, B, S])
            self.xf = s("xf", [P, S])
            self.xfn = s("xfn", [P, S])
            self.y0 = s("y0", [P, B, S])
            self.sqh = s("sqh", [P, 2, 512])
            self.t2 = s("t2", [P, 2, 512])
            self.r = s("r", [P, 2, 4, 512])
            self.ss = s("ss", [P, 2, 32])
            self.gy = s("gy", [P, 2, 32])
            self.gt = s("gt", [P, 2, 32])
            self.qT = s("qT", [P, 8, S])
            self.kT = s("kT", [P, 8, WIN + S])
            self.v = s("v", [P, 2, INNER])
            self.v_out = dram("st_v_out", (4, P, INNER))
            self.vv = s("vv", [P, S // WIN, INNER // 2])
            self.e = s("e", [P, 8, 2, 2 * WIN])
            self.pT = s("pT", [P, 8, P])
            self.mx = s("mx", [P, 16])
            self.den = s("den", [P, 16])
            self.rden = s("rden", [P, 2, 16])
            self.on = s("on", [P, 8, 2, D2])
            self.oT = s("oT", [P, 8, S])
            self.gel = s("gel", [P, 2, S])
            self.hid = s("hid", [P, 3, S])
            (self.c_in, self.wv_in, self.wq_in, self.wk_in, self.wf_in, self.qks_in, self.set_up, self.rot_ready,
             self.xs_ready, self.proj, self.v_evac, self.squares, self.ss_done, self.qk_used, self.added,
             self.v_ready, self.guess, self.newton, self.r_ready, self.turned, self.evac, self.scores, self.mx_ready,
             self.sub_done, self.exps, self.den_ready, self.rden_ready, self.v_stored, self.pv_done, self.on_ready,
             self.wo_done, self.xu_ready, self.xf_ready, self.mean, self.centred, self.lnsq, self.var, self.std,
             self.rstd, self.spread, self.ln_tmp, self.ffn_in, self.up, self.gelu, self.act_ready, self.down) = [
                sem("st_" + what) for what in (
                "c_in wv_in wq_in wk_in wf_in qks_in set_up rot_ready xs_ready proj v_evac squares ss_done "
                "qk_used added v_ready guess newton r_ready turned evac scores mx_ready sub_done exps "
                "den_ready rden_ready v_stored pv_done on_ready wo_done xu_ready xf_ready mean centred lnsq "
                "var std rstd spread ln_tmp ffn_in up gelu act_ready down").split()]
            self.mix_begun = sem("st_mix_begun")
            self.load_begun = sem("st_load_begun")
            self.vshift = [sem("st_vshift%d" % t) for t in range(4)]

        def load_a(self, sp, l):
            for k in (2, 0, 1):
                self.load_w(sp, l, k)
            sp.dma_start(self.qks[:, :, :, :], io["st_qks"][bass.ds(l, 1)].rearrange("a q k d -> a (q k d)")
                         .broadcast_to([P, 4 * D2])).then_inc(self.qks_in, 16)

        def load_w(self, sp, l, k):
            src = io["st_wqkv"][bass.ds(l, 1), :, INNER * k:INNER * k + INNER].rearrange("a p n -> p (a n)")
            sp.dma_start(self.wqkv[:, k, :], src).then_inc((self.wq_in, self.wk_in, self.wv_in)[k], 16)

        def load_f(self, sp, l):
            one = lambda name: io[name][bass.ds(l, 1)]
            sp.dma_start(self.wo[:, :, :], one("st_wo").rearrange("a (c p) d -> p (a c) d", p=P)).then_inc(self.wf_in, 16)
            sp.dma_start(self.w1[:, :], one("st_w1").rearrange("a p n -> p (a n)")).then_inc(self.wf_in, 16)
            sp.dma_start(self.w2[:, 0:2, :], one("st_w2")[:, 0:256, :].rearrange("a (c p) d -> p (a c) d", p=P))\
              .then_inc(self.wf_in, 16)
            sp.dma_start(self.w2[0:FFI - 256, 2, :], one("st_w2")[:, 256:, :].rearrange("a p d -> p (a d)"))\
              .then_inc(self.wf_in, 16)
            sp.dma_start(self.sv[:, :], one("st_sv").rearrange("a p n -> p (a n)")).then_inc(self.wf_in, 16)

        WF = 5 * 16

        def sp_shift(self, sp, u):
            for t in range(4):
                T = 4 * u + t
                sp.wait_ge(self.pv_done, T + 1)
                sp.wait_ge(self.v_evac, T * 2 + 2)
                sp.dma_start(self.v_out[t], self.v[:, t % 2, :]).then_inc(self.v_stored, 16)
                if t < 3:
                    sp.wait_ge(self.pv_done, T + 2)
                sp.wait_ge(self.v_stored, T * 16 + 16)
                for e in range(2):
                    for h in range(2):
                        first, count = 4 * t + 1 - h, 4 - (t == 3 and h == 0)
                        rows = slice(64 * e + WIN * h, 64 * e + WIN * h + WIN)
                        src = view(self.v_out, t * P * INNER + 512 * e, [[INNER, WIN], [WIN * INNER, count], [1, 512]])
                        sp.dma_start(self.vv[rows, first:first + count, :], src).then_inc(self.vshift[t], 16)

        def sp(self, sp):
            sp.dma_start(self.base[:, :, :, :, :], io["st_base"]).then_inc(self.c_in, 16)
            sp.dma_start(self.wmask[:, :, :], io["st_wmask"]).then_inc(self.c_in, 16)
            sp.dma_start(self.identb[:, :], io["identb"]).then_inc(self.c_in, 16)
            self.load_a(sp, 0)
            self.load_f(sp, 0)
            self.sp_shift(sp, 0)
            with sp.Fori(0, DEPTH - 1) as i:
                self.sp_shift(sp, i * 2 + 1)
                sp.wait_ge(self.rot_ready, i + 1)
                sp.sem_inc(self.load_begun, 1)
                sp.dma_start(self.qks[:, :, :, :], io["st_qks"][bass.ds(i + 1, 1)].rearrange("a q k d -> a (q k d)")
                             .broadcast_to([P, 4 * D2])).then_inc(self.qks_in, 16)
                for k, done in ((2, 20), (0, 22), (1, 24)):
                    sp.wait_ge(self.proj, (i * 2 + 1) * 24 + done)
                    sp.sem_inc(self.load_begun, 1)
                    self.load_w(sp, i + 1, k)
                self.sp_shift(sp, i * 2 + 2)
                sp.wait_ge(self.xs_ready, i * 2 + 4)
                sp.sem_inc(self.load_begun, 1)
                self.load_f(sp, i + 1)
            self.sp_shift(sp, 2 * DEPTH - 1)

        def pe_proj(self, pe, u, t, ms):
            T = 4 * u + t
            b = self.b_of(u)
            l = self.l_of(u)
            for m in ms:
                if m == 0 and t == 0:
                    pe.wait_ge(self.xs_ready, u + 1)
                if m % 2 == 0 and t == 0:
                    pe.wait_ge((self.wv_in, self.wq_in, self.wk_in)[m // 2], l * 16 + 16)
                if m < 3:
                    if self.later(T):
                        pe.wait_ge(self.qk_used, T * 4 - 2 + m)
                elif m < 5:
                    pe.wait_ge(self.v_evac, T * 2 + m - 2)
                else:
                    pe.wait_ge(self.qk_used, T * 4 + 1)
                k, half = ((2, 0), (2, 1), (0, 0), (0, 1), (1, 0), (1, 1))[m]
                pe.matmul(PS[:, 4 + m % 3, :], self.xs[:, b, P * t:P * t + P],
                          self.wqkv[:, k, 512 * half:512 * half + 512], start=True, stop=True).then_inc(self.proj, 1)

        def later(self, T):
            return not isinstance(T, int) or T > 0

        def b_of(self, u):
            return self.now[0]

        def l_of(self, u):
            return self.now[1]

        def group(self, u, k):
            return u * 32 + 12 + k

        def pe_turn(self, pe, u, t, g, number):
            pe.wait_ge(self.r_ready, (4 * u + t) * 4 + g + 1)
            if not isinstance(number, int) or number > 0:
                pe.wait_ge(self.evac, number)
            for j in range(4):
                mm = pe.transpose(PS[:, 7, P * j:P * j + P], self.r[:, t % 2, g, P * j:P * j + P], ident)
            mm.then_inc(self.turned, 1)

        def act_turn(self, act, u, t, g, number):
            act.wait_ge(self.turned, number + 1)
            src = PS[:, 7, :].rearrange("p (c n) -> p c n", c=4)
            c = 4 * (g % 2)
            dst = self.qT[:, c:c + 4, P * t:P * t + P] if g < 2 else self.kT[:, c:c + 4, WIN + P * t:WIN + P * t + P]
            act.activation(dst, src, ACT.Copy).then_inc(self.evac, 1)

        def act_proj(self, act, u, t, ms):
            T = 4 * u + t
            for m in ms:
                act.wait_ge(self.proj, T * 6 + m + 1)
                if m < 2:
                    if m == 0 and (t >= 2 or self.later(u)):
                        act.wait_ge(self.v_stored, T * 16 - 16)
                    act.activation(self.v[:, t % 2, 512 * m:512 * m + 512], PS[:, 4 + m % 3, :], ACT.Copy)\
                       .then_inc(self.v_evac, 1)
                else:
                    c = m - 2
                    if c >= 2 or self.later(T):
                        act.wait_ge(self.ss_done, T * 4 + c - 1)
                    act.activation(self.sqh[:, c % 2, :], PS[:, 4 + m % 3, :], ACT.Square).then_inc(self.squares, 1)

        def dve_proj(self, dve, u, t, cs):
            T = 4 * u + t
            for c in cs:
                m, k = c + 2, c // 2
                ps = PS[:, 4 + m % 3, :]
                dve.wait_ge(self.squares, T * 4 + c + 1)
                if c == 0 and (t >= 2 or self.later(u)):
                    dve.wait_ge(self.turned, self.turned_by(u, t))
                if c == 0 and t == 0:
                    dve.wait_ge(self.rot_ready, self.l_of(u) + 1)
                h3 = lambda a: a.rearrange("p (h d) -> p h d", h=8)
                h4 = lambda a: a.rearrange("p (h s d) -> p h s d", h=8, s=2)
                table = lambda j: self.rot[:, k, j, t, :].unsqueeze(1).broadcast_to([P, 8, D2])
                dve.tensor_tensor(h3(self.r[:, t % 2, c, :]), h3(ps), table(0), ALU.mult)
                if c >= 2 or self.later(T):
                    dve.wait_ge(self.added, T * 4 + c - 1)
                for s in range(2):
                    ins = dve.tensor_tensor(h4(self.t2[:, c % 2, :])[:, :, s, :], h4(ps)[:, :, 1 - s, :],
                                            self.rot[:, k, 1, t, 32 * s:32 * s + 32].unsqueeze(1)
                                            .broadcast_to([P, 8, 32]), ALU.mult)
                ins.then_inc(self.qk_used, 1)
                if c == 0 and (t >= 2 or self.later(u)):
                    dve.wait_ge(self.r_ready, T * 4 - 4)
                dve.tensor_reduce(self.ss[:, t % 2, 8 * c:8 * c + 8], h3(self.sqh[:, c % 2, :]), X, ALU.add)\
                   .then_inc(self.ss_done, 1)
                if c == 3:
                    ss, y = self.ss[:, t % 2, :], self.gy[:, t % 2, :]
                    dve.wait_ge(self.ss_done, T * 4 + 4)
                    dve.tensor_scalar(ss, ss, 1e-24, -0.5, ALU.max, ALU.mult).then_inc(self.v_ready, 1)
                    dve.wait_ge(self.v_ready, T + 1)
                    dve.tensor_scalar(y.bitcast(I32), ss.bitcast(I32), -0.5, GUESS, ALU.mult, ALU.add)\
                       .then_inc(self.guess, 1)

        def turned_by(self, u, t):
            if t >= 2:
                if isinstance(u, int) and u == 0:
                    return 4 * (t - 1)
                return (u - 1) * 32 + 12 + (14, 22)[t - 2]
            if t == 0:
                return (u - 1) * 32 + 12 if not (isinstance(u, int) and u == 0) else 0
            return (u - 1) * 32 + 12 + 6

        def pool_proj(self, pool, u, t):
            T = 4 * u + t
            for c in range(4):
                pool.wait_ge(self.qk_used, T * 4 + c + 1)
                r = self.r[:, t % 2, c, :]
                pool.tensor_tensor(r, r, self.t2[:, c % 2, :], ALU.add).then_inc(self.added, 1)
            pool.wait_ge(self.guess, T + 1)
            ss, y, g = self.ss[:, t % 2, :], self.gy[:, t % 2, :], self.gt[:, t % 2, :]
            k = 0
            for _ in range(3):
                for f in (lambda: pool.tensor_tensor(g, y, y, ALU.mult),
                          lambda: pool.tensor_tensor(g, g, ss, ALU.mult),
                          lambda: pool.tensor_tensor(g, g, const("threehalves").broadcast_to([P, 32]), ALU.add),
                          lambda: pool.tensor_tensor(y, y, g, ALU.mult)):
                    f().then_inc(self.newton, 1)
                    k += 1
                    pool.wait_ge(self.newton, T * 12 + k)
            pool.wait_ge(self.added, T * 4 + 4)
            for c in range(4):
                r = self.r[:, t % 2, c, :].rearrange("p (h d) -> p h d", h=8)
                pool.tensor_tensor(r, r, y[:, 8 * c:8 * c + 8].unsqueeze(2).broadcast_to([P, 8, D2]), ALU.mult)\
                    .then_inc(self.r_ready, 1)

        def pe_scores(self, pe, u, t, number, between=None):
            T = 4 * u + t
            pe.wait_ge(self.evac, number)
            pe.wait_ge(self.sub_done, T + 1)
            for e in range(2):
                pe.matmul(PS[:, e, :], self.identb[:, :],
                          self.wmask[:, min(t, 1), :].unsqueeze(1).broadcast_to([P, 8, 2 * WIN]),
                          start=True, stop=False, skip_group_check=True)
            for e in range(2):
                if e == 1 and between is not None:
                    between()
                for c in range(8):
                    for w in range(4):
                        q = P * t + WIN * w
                        mm = pe.matmul(PS[WIN * w:WIN * w + WIN, e, D2 * c:D2 * c + D2],
                                       self.qT[64 * e:64 * e + 64, c, q:q + WIN],
                                       self.kT[64 * e:64 * e + 64, c, q:q + 2 * WIN],
                                       start=False, stop=(c == 7), skip_group_check=True,
                                       tile_position=(64 * e, WIN * w))
            mm.then_inc(self.scores, 1)

        def pe_turn_p(self, pe, u, t, half, number):
            if half == 0:
                pe.wait_ge(self.exps, 4 * u + t + 1)
            pe.wait_ge(self.evac, number)
            for j in range(4):
                mm = pe.transpose(PS[:, 7, P * j:P * j + P],
                                  self.e[:, 4 * half + j, :, :].rearrange("p e k -> p (e k)"), ident)
            mm.then_inc(self.turned, 1)

        def act_turn_p(self, act, u, t, half, number):
            act.wait_ge(self.turned, number + 1)
            if half == 0:
                act.wait_ge(self.pv_done, 4 * u + t + 4)
            act.activation(self.pT[:, 4 * half:4 * half + 4, :], PS[:, 7, :].rearrange("p (c n) -> p c n", c=4),
                           ACT.Copy).then_inc(self.evac, 1)

        def pe_mix(self, pe, u, t, number):
            T = 4 * u + t
            pe.wait_ge(self.evac, number)
            pe.wait_ge(self.vshift[t], (u + 1) * 64)
            pe.wait_ge(self.on_ready, T + 1)
            pe.sem_inc(self.mix_begun, 1)
            for e in range(2):
                rows = slice(64 * e, 64 * e + 64)
                for c in range(8):
                    for w in range(4):
                        g = slice(WIN * w, WIN * w + WIN)
                        mm = pe.matmul(PS[g, 2 + e, D2 * c:D2 * c + D2], self.pT[rows, c, g],
                                       self.vv[rows, 4 * t + w, D2 * c:D2 * c + D2], start=True, stop=True,
                                       tile_position=(64 * e, WIN * w), skip_group_check=True)
            mm.then_inc(self.pv_done, 1)

        def pe_turn_o(self, pe, u, t, half, number):
            pe.wait_ge(self.on_ready, 4 * u + t + 2)
            pe.wait_ge(self.evac, number)
            for j in range(4):
                c = 4 * half + j
                mm = pe.transpose(PS[:, 7, P * j:P * j + P], self.on[:, c, :, :].rearrange("p e d -> p (e d)"), ident)
            mm.then_inc(self.turned, 1)

        def act_turn_o(self, act, u, t, half, number):
            act.wait_ge(self.turned, number + 1)
            act.activation(self.oT[:, 4 * half:4 * half + 4, P * t:P * t + P],
                           PS[:, 7, :].rearrange("p (c n) -> p c n", c=4), ACT.Copy).then_inc(self.evac, 1)

        def act_exp(self, act, u, t):
            act.wait_ge(self.sub_done, 4 * u + t + 2)
            act.activation(self.e[:, :, :, :], self.e[:, :, :, :], ACT.Exp, scale=8.0).then_inc(self.exps, 1)

        def dve_max(self, dve, u, t, number):
            T = 4 * u + t
            heads = lambda a: a.rearrange("p (e c) -> p e c", e=2)
            dve.wait_ge(self.scores, T + 1)
            ps = PS[:, 0:2, :].rearrange("p e (c k) -> p e c k", c=8)
            dve.tensor_reduce(heads(self.mx[:, :]), ps, X, ALU.max).then_inc(self.mx_ready, 1)
            dve.wait_ge(self.mx_ready, T + 1)
            dve.wait_ge(self.turned, number)
            dve.wait_ge(self.den_ready, T + 1)
            dve.tensor_tensor(self.e[:, :, :, :].rearrange("p c e k -> p e c k"), ps,
                              heads(self.mx[:, :]).unsqueeze(3).broadcast_to([P, 2, 8, 2 * WIN]),
                              ALU.subtract).then_inc(self.sub_done, 1)

        def dve_sum(self, dve, u, t):
            T = 4 * u + t
            dve.wait_ge(self.exps, T + 1)
            dve.tensor_reduce(self.den[:, :].rearrange("p (e c) -> p e c", e=2),
                              self.e[:, :, :, :].rearrange("p c e k -> p e c k"), X, ALU.add)\
               .then_inc(self.den_ready, 1)
            dve.wait_ge(self.den_ready, T + 2)
            dve.reciprocal(self.rden[:, t % 2, :], self.den[:, :]).then_inc(self.rden_ready, 1)

        def dve_out(self, dve, u, t, number):
            T = 4 * u + t
            dve.wait_ge(self.pv_done, T + 1 + 4)
            dve.wait_ge(self.rden_ready, T + 1)
            dve.wait_ge(self.turned, number)
            dve.tensor_tensor(self.on[:, :, :, :].rearrange("p c e d -> p e c d"),
                              PS[:, 2:4, :].rearrange("p e (c d) -> p e c d", c=8),
                              self.rden[:, t % 2, :].rearrange("p (e c) -> p e c", e=2).unsqueeze(3)
                              .broadcast_to([P, 2, 8, D2]), ALU.mult).then_inc(self.on_ready, 1)

        def pe_wo(self, pe, u, number):
            pe.wait_ge(self.wf_in, self.l_of(u) * self.WF + self.WF)
            pe.wait_ge(self.evac, number)
            for c in range(8):
                mm = pe.matmul(PS[:, 2, :], self.wo[:, c, :], self.oT[:, c, :], start=(c == 0), stop=(c == 7))
            mm.then_inc(self.wo_done, 1)

        def pe_mean(self, pe, u):
            pe.wait_ge(self.xf_ready, u + 1)
            pe.matmul(PS[:, 3, :], const("mean"), self.xf[:, :], start=True, stop=True).then_inc(self.mean, 1)

        def pe_var(self, pe, u):
            pe.wait_ge(self.lnsq, u + 1)
            for j in range(8):
                mm = pe.matmul(PS[0:8, 3, 0:64], const("slide")[:, 15 - j:23 - j], sq[:, 0, 64 * j:64 * j + 64],
                               start=(j == 0), stop=(j == 7))
            mm.then_inc(self.var, 1)

        def pe_spread(self, pe, u):
            pe.wait_ge(self.rstd, u + 1)
            for j in range(8):
                mm = pe.matmul(PS[:, 3, 64 * j:64 * j + 64], cst[0:8, j:j + 1].broadcast_to([8, P]), rstd[0:8, 1, :],
                               start=(j == 0), stop=(j == 7))
            mm.then_inc(self.spread, 1)

        def pe_ffn(self, pe, u):
            pe.wait_ge(self.ffn_in, u + 1)
            for j, (a, w) in enumerate(self.CHUNKS):
                bank = 2 * (j % 2)
                if j == 2:
                    pe.wait_ge(self.act_ready, u * 3 + 1)
                pe.matmul(PS[0:w, bank + 1, :], self.w1[:, FFI + a:FFI + a + w], self.xfn[:, :], start=True, stop=True)
                pe.matmul(PS[0:w, bank, :], self.w1[:, a:a + w], self.xfn[:, :], start=True, stop=True)\
                  .then_inc(self.up, 1)
            for j, (a, w) in enumerate(self.CHUNKS):
                if j != 0:
                    pe.wait_ge(self.act_ready, u * 3 + j + 1)
                else:
                    pe.wait_ge(self.act_ready, u * 3 + 2)
                mm = pe.matmul(PS[:, 3, :], self.w2[0:w, j, :], self.hid[0:w, j, :], start=(j == 0), stop=(j == 2))
            mm.then_inc(self.down, 1)

        def act_ln_square(self, act, u):
            act.wait_ge(self.centred, u + 1)
            act.activation(sq[:, 0, :], xc[:, 0, :], ACT.Square).then_inc(self.lnsq, 1)

        def act_ln_root(self, act, u):
            act.wait_ge(self.var, u + 1)
            a = C_AT["eps"][0]
            act.activation(rstd[0:8, 0, :], PS[0:8, 3, 0:64], ACT.Sqrt, bias=cst[0:8, a:a + 1]).then_inc(self.std, 1)

        def act_ffn(self, act, u):
            for j, (a, w) in enumerate(self.CHUNKS):
                act.wait_ge(self.up, u * 3 + j + 1)
                if j == 2:
                    act.wait_ge(self.act_ready, u * 3 + 1)
                act.activation(self.gel[0:w, j % 2, :], PS[0:w, 2 * (j % 2) + 1, :], ACT.Gelu,
                               bias=self.sv[0:w, 6 + j:7 + j]).then_inc(self.gelu, 1)

        def shift(self, dve, b, dst, signal):
            dve.tensor_copy(dst[0:64, :], x[0:64, b, :])
            dve.tensor_copy(dst[64:P, 1:], x[64:P, b, 0:S - 1]).then_inc(signal, 1)

        def dve_wo(self, dve, u):
            b = self.b_of(u)
            dve.wait_ge(self.wo_done, u + 1)
            dve.tensor_tensor(x[:, b, :], x[:, b, :], PS[:, 2, :], ALU.add).then_inc(self.xu_ready, 1)
            dve.wait_ge(self.xu_ready, u * 2 + 1)
            self.shift(dve, b, self.xf, self.xf_ready)

        def dve_ln_centre(self, dve, u):
            dve.wait_ge(self.mean, u + 1)
            dve.wait_ge(self.xf_ready, u + 1)
            dve.tensor_tensor(xc[:, 0, :], self.xf[:, :], PS[:, 3, :], ALU.subtract).then_inc(self.centred, 1)

        def dve_ln_root(self, dve, u):
            dve.wait_ge(self.std, u + 1)
            dve.reciprocal(rstd[0:8, 1, :], rstd[0:8, 0, :]).then_inc(self.rstd, 1)

        def dve_ln_out(self, dve, u):
            dve.wait_ge(self.spread, u + 1)
            dve.wait_ge(self.centred, u + 1)
            dve.tensor_tensor(xc[:, 0, :], xc[:, 0, :], PS[:, 3, :], ALU.mult).then_inc(self.ln_tmp, 1)
            dve.wait_ge(self.ln_tmp, u + 1)
            dve.tensor_scalar(self.xfn[:, :], xc[:, 0, :], self.sv[:, 0:1], self.sv[:, 1:2], ALU.mult, ALU.add)\
               .then_inc(self.ffn_in, 1)

        def dve_ffn(self, dve, u):
            b = self.b_of(u)
            for j, (a, w) in enumerate(self.CHUNKS):
                dve.wait_ge(self.gelu, u * 3 + j + 1)
                dve.scalar_tensor_tensor(self.hid[0:w, j, :], PS[0:w, 2 * (j % 2), :], self.sv[0:w, 3 + j:4 + j],
                                         self.gel[0:w, j % 2, :], ALU.add, ALU.mult).then_inc(self.act_ready, 1)
            dve.wait_ge(self.down, u + 1)
            dve.scalar_tensor_tensor(x[:, b, :], PS[:, 3, :], self.sv[:, 2:3], x[:, b, :], ALU.add, ALU.add)\
               .then_inc(self.xu_ready, 1)
            dve.wait_ge(self.xu_ready, u * 2 + 2)
            self.shift(dve, b, self.xs[:, b, :], self.xs_ready)

        def dve_tables(self, dve, l, u):
            dve.wait_ge(self.qks_in, l * 16 + 16)
            if self.later(u):
                dve.wait_ge(self.qk_used, u * 16)
            for k in range(2):
                for j in range(2):
                    ins = dve.tensor_tensor(self.rot[:, k, j, :, :], self.base[:, k, j, :, :],
                                            self.qks[:, k, j, :].unsqueeze(1).broadcast_to([P, 4, D2]), ALU.mult)
            ins.then_inc(self.rot_ready, 1)

        def at(self, slot):
            self.now = slot[1:]
            return slot[0]

        def pe_ahead(self, pe, slot, nxt, t, ms):
            if nxt:
                self.pe_proj(pe, self.at(nxt), t, ms)
            self.at(slot)

        def act_ahead(self, act, slot, nxt, t, ms):
            if nxt:
                self.act_proj(act, self.at(nxt), t, ms)
            self.at(slot)

        def pe_slot(self, pe, slot, nxt):
            u = self.at(slot)
            g = lambda with_next, last=None: self.group(u, with_next if nxt or last is None else last)
            ahead = lambda t, *ms: self.pe_ahead(pe, slot, nxt, t, ms)
            turn_p = lambda t, half, number: self.pe_turn_p(pe, u, t, half, number)
            turn_o = lambda t, half, number: self.pe_turn_o(pe, u, t, half, number)
            turn = lambda v, t, k, number: self.pe_turn(pe, v, t, k, number)
            turn_p(0, 0, g(0))
            self.pe_scores(pe, u, 1, g(0), lambda: turn_p(0, 1, g(1)))
            pe.wait_ge(self.xs_ready, u + 2)
            self.pe_mix(pe, u, 0, g(2))
            ahead(0, 0, 1)
            for k in range(4):
                turn(u, 3, k, g(2 + k))
                ahead(0, 2 + k)
            turn_p(1, 0, g(6))
            self.pe_scores(pe, u, 2, g(0), lambda: turn_p(1, 1, g(7)))
            self.pe_mix(pe, u, 1, g(8))
            turn_o(0, 0, g(8))
            ahead(1, 0)
            turn_o(0, 1, g(9))
            ahead(1, 1)
            if nxt:
                for k in range(4):
                    turn(nxt[0], 0, k, g(10 + k))
                    ahead(1, 2 + k)
            turn_p(2, 0, g(14, 10))
            self.pe_scores(pe, u, 3, g(6), lambda: turn_p(2, 1, g(15, 11)))
            self.pe_mix(pe, u, 2, g(16, 12))
            turn_o(1, 0, g(16, 12))
            ahead(2, 0)
            turn_o(1, 1, g(17, 13))
            ahead(2, 1)
            if nxt:
                for k in range(4):
                    turn(nxt[0], 1, k, g(18 + k))
                    ahead(2, 2 + k)
            turn_p(3, 0, g(22, 14))
            ahead(3, 0)
            turn_p(3, 1, g(23, 15))
            ahead(3, 1)
            turn_o(2, 0, g(24, 16))
            ahead(3, 2)
            turn_o(2, 1, g(25, 17))
            self.pe_mix(pe, u, 3, g(24, 16))
            if nxt:
                turn(nxt[0], 2, 0, g(26))
            turn_o(3, 0, g(27, 18))
            ahead(3, 3)
            turn_o(3, 1, g(28, 19))
            self.pe_wo(pe, u, g(29, 20))
            if nxt:
                turn(nxt[0], 2, 1, g(29))
                self.pe_scores(pe, self.at(nxt), 0, g(14))
            self.at(slot)
            self.pe_mean(pe, u)
            ahead(3, 4)
            if nxt:
                turn(nxt[0], 2, 2, g(30))
            self.pe_var(pe, u)
            ahead(3, 5)
            if nxt:
                turn(nxt[0], 2, 3, g(31))
            self.pe_spread(pe, u)
            if nxt:
                pe.wait_ge(self.sub_done, 4 * u + 6)
            self.pe_ffn(pe, u)

        def pe_proj_turn(self, pe, v, t, number):
            self.pe_proj(pe, v, t, (0, 1))
            for k in range(4):
                self.pe_turn(pe, v, t - 1, k, number + k)
                self.pe_proj(pe, v, t, (2 + k,))

        def act_proj_turn(self, act, v, t, number):
            self.act_proj(act, v, t, (0, 1))
            for k in range(4):
                self.act_turn(act, v, t - 1, k, number + k)
                self.act_proj(act, v, t, (2 + k,))

        def act_slot(self, act, slot, nxt):
            u = self.at(slot)
            g = lambda with_next, last=None: self.group(u, with_next if nxt or last is None else last)
            ahead = lambda t, *ms: self.act_ahead(act, slot, nxt, t, ms)
            turn_p = lambda t, half, number: self.act_turn_p(act, u, t, half, number)
            turn_o = lambda t, half, number: self.act_turn_o(act, u, t, half, number)
            turn = lambda v, t, k, number: self.act_turn(act, v, t, k, number)
            turn_p(0, 0, g(0))
            turn_p(0, 1, g(1))
            self.act_exp(act, u, 1)
            ahead(0, 0, 1)
            for k in range(4):
                turn(u, 3, k, g(2 + k))
                ahead(0, 2 + k)
            turn_p(1, 0, g(6))
            turn_p(1, 1, g(7))
            self.act_exp(act, u, 2)
            turn_o(0, 0, g(8))
            ahead(1, 0)
            turn_o(0, 1, g(9))
            ahead(1, 1)
            if nxt:
                for k in range(4):
                    turn(nxt[0], 0, k, g(10 + k))
                    ahead(1, 2 + k)
            turn_p(2, 0, g(14, 10))
            turn_p(2, 1, g(15, 11))
            self.act_exp(act, u, 3)
            turn_o(1, 0, g(16, 12))
            ahead(2, 0)
            turn_o(1, 1, g(17, 13))
            ahead(2, 1)
            if nxt:
                for k in range(4):
                    turn(nxt[0], 1, k, g(18 + k))
                    ahead(2, 2 + k)
            turn_p(3, 0, g(22, 14))
            ahead(3, 0)
            turn_p(3, 1, g(23, 15))
            ahead(3, 1)
            turn_o(2, 0, g(24, 16))
            ahead(3, 2)
            turn_o(2, 1, g(25, 17))
            if nxt:
                turn(nxt[0], 2, 0, g(26))
            turn_o(3, 0, g(27, 18))
            ahead(3, 3)
            turn_o(3, 1, g(28, 19))
            if nxt:
                turn(nxt[0], 2, 1, g(29))
            self.act_ln_square(act, u)
            ahead(3, 4)
            if nxt:
                turn(nxt[0], 2, 2, g(30))
            self.act_ln_root(act, u)
            if nxt:
                self.act_exp(act, nxt[0], 0)
            ahead(3, 5)
            if nxt:
                turn(nxt[0], 2, 3, g(31))
            self.act_ffn(act, u)

        def dve_ahead(self, dve, slot, nxt, t, cs):
            if nxt:
                self.dve_proj(dve, self.at(nxt), t, cs)
            self.at(slot)

        def dve_slot(self, dve, slot, nxt, tables=None):
            u = self.at(slot)
            g = lambda with_next, last=None: self.group(u, with_next if nxt or last is None else last)
            ahead = lambda t, *cs: self.dve_ahead(dve, slot, nxt, t, cs)
            self.dve_sum(dve, u, 0)
            self.dve_max(dve, u, 1, g(2))
            self.dve_out(dve, u, 0, g(0))
            if tables is not None:
                self.at(nxt)
                self.dve_tables(dve, tables, nxt[0])
            ahead(0, 0, 1, 2, 3)
            self.dve_sum(dve, u, 1)
            self.dve_max(dve, u, 2, g(8))
            self.dve_out(dve, u, 1, g(10))
            self.dve_sum(dve, u, 2)
            ahead(1, 0, 1, 2, 3)
            self.dve_max(dve, u, 3, g(16, 12))
            self.dve_out(dve, u, 2, g(18, 14))
            self.dve_sum(dve, u, 3)
            ahead(2, 0, 1, 2, 3)
            self.dve_out(dve, u, 3, g(26, 18))
            if nxt:
                self.dve_proj(dve, self.at(nxt), 3, (0,))
            self.at(slot)
            self.dve_wo(dve, u)
            if nxt:
                self.dve_proj(dve, self.at(nxt), 3, (1,))
            self.at(slot)
            self.dve_ln_centre(dve, u)
            if nxt:
                self.dve_max(dve, self.at(nxt), 0, g(24))
            self.at(slot)
            self.dve_ln_root(dve, u)
            if nxt:
                self.dve_proj(dve, self.at(nxt), 3, (2,))
            self.at(slot)
            self.dve_ln_out(dve, u)
            if nxt:
                self.dve_proj(dve, self.at(nxt), 3, (3,))
            self.at(slot)
            self.dve_ffn(dve, u)

        def rounds(self, eng, body, last):
            with eng.Fori(0, DEPTH - 1) as i:
                body((i * 2, 0, i), (i * 2 + 1, 1, i), None)
                body((i * 2 + 1, 1, i), (i * 2 + 2, 0, i + 1), i + 1)
            L = DEPTH - 1
            body((2 * L, 0, L), (2 * L + 1, 1, L), None)
            last((2 * L + 1, 1, L))

        def pe(self, pe):
            pe.wait_ge(self.c_in, 48)
            pe.wait_ge(self.set_up, 5)
            pe.sem_inc(self.pv_done, 4)
            u = self.at((0, 0, 0))
            self.pe_proj(pe, u, 0, range(6))
            for t in range(1, 4):
                self.pe_proj_turn(pe, u, t, 4 * (t - 1))
            self.pe_scores(pe, u, 0, 4)
            self.rounds(pe, lambda a, b, l: self.pe_slot(pe, a, b), lambda a: self.pe_slot(pe, a, None))

        def act(self, act):
            u = self.at((0, 0, 0))
            self.act_proj(act, u, 0, range(6))
            for t in range(1, 4):
                self.act_proj_turn(act, u, t, 4 * (t - 1))
            self.act_exp(act, u, 0)
            self.rounds(act, lambda a, b, l: self.act_slot(act, a, b), lambda a: self.act_slot(act, a, None))

        def dve(self, dve):
            for b in range(B):
                order.link(dve, dve.tensor_copy(xn[:, b, :], x[:, b, :]))
                order.link(dve, dve.tensor_copy(x[:, b, :], self.y0[:, b, :]))
            dve.wait_ge(self.set_up, 5)
            for b in range(B):
                self.shift(dve, b, self.xs[:, b, :], self.xs_ready)
            self.dve_tables(dve, 0, 0)
            dve.sem_inc(self.sub_done, 1)
            dve.sem_inc(self.den_ready, 1)
            dve.sem_inc(self.on_ready, 1)
            u = self.at((0, 0, 0))
            for t in range(4):
                self.dve_proj(dve, u, t, range(4))
            self.dve_max(dve, u, 0, 12)
            self.rounds(dve, lambda a, b, l: self.dve_slot(dve, a, b, l), lambda a: self.dve_slot(dve, a, None))
            dve.wait_ge(self.xs_ready, 2 * DEPTH + 2)
            for b in range(B):
                dve.tensor_tensor(x[:, b, :], x[:, b, :], xn[:, b, :], ALU.add).then_inc(x_ready, 1)

        def pool(self, pool):
            for k, what in enumerate((self.xs[64:P, :, 0:1], self.xf[64:P, 0:1], self.kT[:, :, 0:WIN],
                                      self.vv[0:WIN, 0, :], self.vv[64:64 + WIN, 0, :])):
                pool.memset(what, 0.0).then_inc(self.set_up, 1)
                pool.wait_ge(self.set_up, k + 1)
            for t in range(4):
                self.pool_proj(pool, 0, t)
            with pool.Fori(1, 2 * DEPTH) as u:
                for t in range(4):
                    self.pool_proj(pool, u, t)

    class LatentAttention:

        KEYS = S + KC
        TK = S // P + 1
        UNITS, GROUPS, PIECES = 16, 4, 8
        WAS = dict(w_in=16, proj=5, act_took=1, dve_took=2, scores=2, maxed=1, exps=1, mixed=1, out_prod=2,
                   turned=2, pT_ready=1, mask_set=2)
        FREE = dict(exps=2, turned=2, pT_ready=1, mixed=2, oT_ready=1)

        def __init__(self):
            at = self.stack = ExitStack()
            s = lambda name, shape, dt=F32: sb("la_" + name, shape, dt, at=at)
            self.h0 = s("h0", [P, B, S])
            self.wo = s("wo", [P, INNER // P, P])
            self.wc = s("wc", [P, 3, P])
            self.mraw = s("mraw", [1, B * KC], U8)
            self.mneg = s("mneg", [1, B * KC])
            self.mnegb = s("mnegb", [1, B * KC], BF16)
            self.oneb = s("oneb", [1, P], BF16)
            self.cc = s("cc", [P, 3, B * KC])
            self.cn = s("cn", [P, B * KC])
            self.q = s("q", [P, B, S])
            self.k = s("k", [P, B, self.KEYS])
            self.v = s("v", [P, B, self.TK, P])
            self.p = s("p", [P, 2, self.KEYS])
            self.pT = s("pT", [P, 2, 2, self.TK, 2 * P])
            self.nmx = s("nmx", [P, self.UNITS])
            self.den = s("den", [P, self.UNITS])
            self.rden = s("rden", [P, self.UNITS])
            self.oT = s("oT", [P, INNER // P, B, S])
            self.w_in, self.proj, self.act_took, self.dve_took = pair.w_in, pair.prod, pair.q_ready, pair.v_ready
            self.scores, self.maxed, self.exps, self.mixed = pair.scores, pair.centred, pair.exps, pair.mixed
            self.out_prod, self.turned, self.pT_ready = pair.out_prod, pair.qk_ready, pair.s1_ready
            self.mask_set = pair.h2_ready
            self.wc_in, self.oT_ready, self.rdens, self.sums_ready = [
                sem("la_" + what) for what in ("wc_in", "oT_ready", "rdens", "sums_ready")]

        def c(self, what, k):
            return self.WAS.get(what, 0) + self.FREE.get(what, 0) + k

        def sp(self, sp):
            sp.dma_start(self.wo[:, :, :], io["la_wo"]).then_inc(self.w_in, 16)
            sp.dma_start(self.mraw[:, :], io["la_mask"]).then_inc(self.w_in, 16)
            sp.dma_start(self.wc[:, :, :], io["la_wc"][0]).then_inc(self.wc_in, 16)
            with sp.Fori(0, INNER // P - 1) as i:
                sp.wait_ge(self.proj, i * self.PIECES + self.c("proj", self.PIECES))
                sp.dma_start(self.wc[:, :, :], io["la_wc"][bass.ds(i + 1, 1)].rearrange("a p k n -> p (a k) n"))\
                  .then_inc(self.wc_in, 16)

        def ctx_pe(self, pe):
            pe.matmul(PS[:, 5, 0:B * KC], const("mean"), ctxT[:, :], start=True, stop=True).then_inc(norm.mean_ready, 1)
            pe.wait_ge(norm.squared, n("pe", norm.squared))
            pe.matmul(PS[:, 5, 0:B * KC], const("mean"), self.cc[:, 1, :], start=True, stop=True)\
              .then_inc(norm.var_ready, 1)
            pe.wait_ge(norm.rstd_ready, n("pe", norm.rstd_ready))

        def ctx_act(self, act):
            act.wait_ge(norm.centred, n("act", norm.centred))
            act.activation(self.cc[:, 1, :], self.cc[:, 0, :], ACT.Square).then_inc(norm.squared, 1)
            act.wait_ge(norm.var_ready, n("act", norm.var_ready))
            act.activation(self.cc[:, 2, :], PS[:, 5, 0:B * KC], ACT.Sqrt, bias=const("eps")).then_inc(norm.std_ready, 1)

        def ctx_dve(self, dve):
            dve.wait_ge(norm.mean_ready, n("dve", norm.mean_ready))
            dve.tensor_tensor(self.cc[:, 0, :], ctxT[:, :], PS[:, 5, 0:B * KC], ALU.subtract).then_inc(norm.centred, 1)
            dve.wait_ge(norm.std_ready, n("dve", norm.std_ready))
            order.link(dve, dve.reciprocal(self.cc[:, 2, :], self.cc[:, 2, :]))
            order.link(dve, dve.tensor_tensor(self.cc[:, 0, :], self.cc[:, 0, :], self.cc[:, 2, :], ALU.mult))
            dve.tensor_scalar(self.cn[:, :], self.cc[:, 0, :], column("la_g1"), column("la_b1"), ALU.mult, ALU.add)\
               .then_inc(norm.rstd_ready, 1)
            dve.wait_ge(self.w_in, self.WAS["w_in"] + 32)
            order.link(dve, dve.tensor_copy(self.mneg[:, :], self.mraw[:, :]))
            order.link(dve, dve.tensor_scalar(self.mneg[:, :], self.mneg[:, :], -NEG, NEG, ALU.mult, ALU.add))
            dve.tensor_copy(self.mnegb[:, :], self.mneg[:, :])
            dve.tensor_copy(self.oneb[:, :], const("one")[0:1, :]).then_inc(self.mask_set, 1)

        def unit(self, u):
            return u // 8, (u // 2) % 4, u % 2

        def span(self, u):
            return PS[:, 2 * (u % 2):2 * (u % 2) + 2, :].rearrange("p b n -> p (b n)")[:, 0:self.KEYS]

        Q0, K0, Q1, K1, KCTX, V0, V1, VCTX = range(8)
        BANK = (0, 1, 2, 3, 4, 5, 4, 5)

        def piece(self, k):
            ps = PS[:, self.BANK[k], :]
            if k in (self.Q0, self.Q1):
                return self.q[:, k // 2, :], ps, 0.125
            if k in (self.K0, self.K1):
                return self.k[:, k // 2, 0:S], ps, 1.0
            if k == self.KCTX:
                return self.k[:, :, S:], ps[:, 0:B * KC].rearrange("p (b k) -> p b k", b=B), 1.0
            if k in (self.V0, self.V1):
                return self.v[:, k - self.V0, 0:4, :], ps.rearrange("p (t n) -> p t n", t=4), 1.0
            return self.v[0:KC, :, 4, :], ps[0:KC, 0:B * P].rearrange("p (b n) -> p b n", b=B), 1.0

        def pe_piece(self, pe, k):
            wq, wk, wv = [self.wc[:, j, :] for j in range(3)]
            bank = self.BANK[k]
            if k in (self.Q0, self.Q1, self.K0, self.K1):
                mm = pe.matmul(PS[:, bank, :], (wq, wk)[k % 2], xn[:, k // 2, :], start=True, stop=True)
            elif k == self.KCTX:
                mm = pe.matmul(PS[:, bank, 0:B * KC], wk, self.cn[:, :], start=True, stop=True)
            elif k in (self.V0, self.V1):
                for t in range(4):
                    mm = pe.matmul(PS[:, bank, P * t:P * t + P], xn[:, k - self.V0, P * t:P * t + P], wv,
                                   start=True, stop=True)
            else:
                for b in range(B):
                    mm = pe.matmul(PS[0:KC, bank, P * b:P * b + P], self.cn[:, KC * b:KC * b + KC], wv,
                                   start=True, stop=True)
            mm.then_inc(self.proj, 1)

        def act_piece(self, act, i, k):
            act.wait_ge(self.proj, i * self.PIECES + self.c("proj", k + 1))
            dst, src, scale = self.piece(k)
            act.activation(dst, src, ACT.Copy, scale=scale).then_inc(self.act_took, 1)

        def dve_piece(self, dve, i, k):
            dve.wait_ge(self.proj, i * self.PIECES + self.c("proj", k + 1))
            dst, src, _ = self.piece(k)
            dve.tensor_copy(dst, src).then_inc(self.dve_took, 1)

        def pe_scores(self, pe, i, u):
            b, t, e = self.unit(u)
            at, h = 2 * (u % 2), slice(64 * e, 64 * e + 64)
            pe.wait_ge(self.exps, i * self.UNITS + self.c("exps", u - 1))
            pe.matmul(PS[:, at, :], self.q[h, b, P * t:P * t + P], self.k[h, b, 0:S], start=True, stop=True)
            pe.matmul(PS[:, at + 1, 0:KC], self.q[h, b, P * t:P * t + P], self.k[h, b, S:], start=True, stop=False)
            pe.matmul(PS[:, at + 1, 0:KC], self.oneb[:, :], self.mnegb[:, KC * b:KC * b + KC],
                      start=False, stop=True).then_inc(self.scores, 1)

        def pe_mix(self, pe, i, g):
            b, half = divmod(g, 2)
            at = 2 * P * half
            pe.wait_ge(self.rdens, i * (self.UNITS // 2) + 2 * g + 2)
            if half == 0:
                pe.wait_ge(self.oT_ready, i * B + self.c("oT_ready", b))
            pe.wait_ge(self.pT_ready, i * self.UNITS + self.c("pT_ready", 4 * g + 4))
            for k in range(2):
                for e in range(2):
                    u = 4 * g + 2 * k + e
                    pe.matmul(PS[64 * e:64 * e + 64, 7, at + P * k:at + P * k + P],
                              self.rden[:, u:u + 1].broadcast_to([P, D2]), ident, start=True, stop=True,
                              skip_group_check=True, tile_position=(0, 64 * e))
            for k in range(self.TK):
                w = P if k < self.TK - 1 else KC
                for e in range(2):
                    mm = pe.matmul(PS[64 * e:64 * e + 64, 6, at:at + 2 * P], self.v[0:w, b, k, 64 * e:64 * e + 64],
                                   self.pT[0:w, g % 2, e, k, :], start=(k == 0), stop=(k == self.TK - 1),
                                   skip_group_check=True, tile_position=(0, 64 * e))
            mm.then_inc(self.mixed, 1)

        def pe(self, pe):
            norm.wait(pe, "pe")
            pe.wait_ge(self.w_in, self.WAS["w_in"] + 32)
            pe.sem_inc(self.turned, self.FREE["turned"])
            pe.sem_inc(self.mixed, self.FREE["mixed"])
            pe.wait_ge(self.mask_set, self.c("mask_set", 1))
            pe.wait_ge(self.wc_in, 16)
            for k in range(4):
                self.pe_piece(pe, k)
            with pe.Fori(0, INNER // P - 1) as i:
                self.pe_pair(pe, i, True)
            self.pe_pair(pe, INNER // P - 1, False)
            pe.wait_ge(self.oT_ready, self.c("oT_ready", INNER // P * B))
            for b in range(B):
                for c in range(INNER // P):
                    mm = pe.matmul(PS[:, b, :], self.wo[:, c, :], self.oT[:, c, b, :],
                                   start=(c == 0), stop=(c == INNER // P - 1))
                mm.then_inc(self.out_prod, 1)

        def pe_pair(self, pe, i, more):
            pe.wait_ge(self.pT_ready, i * self.UNITS + self.c("pT_ready", 0))
            self.pe_piece(pe, self.KCTX)
            self.pe_piece(pe, self.V0)
            pe.wait_ge(self.dve_took, i * 4 + self.c("dve_took", 1))
            pe.wait_ge(self.act_took, i * 4 + self.c("act_took", 3))
            self.pe_scores(pe, i, 0)
            self.pe_piece(pe, self.V1)
            pe.wait_ge(self.dve_took, i * 4 + self.c("dve_took", 2))
            self.pe_scores(pe, i, 1)
            pe.wait_ge(self.dve_took, i * 4 + self.c("dve_took", 3))
            self.pe_piece(pe, self.VCTX)
            pe.wait_ge(self.act_took, i * 4 + self.c("act_took", 4))
            pe.wait_ge(self.dve_took, i * 4 + self.c("dve_took", 4))
            for u in range(self.UNITS):
                pe.wait_ge(self.pT_ready, i * self.UNITS + self.c("pT_ready", u))
                pe.wait_ge(self.exps, i * self.UNITS + self.c("exps", u + 1))
                for k in range(self.TK):
                    w = P if k < self.TK - 1 else KC
                    mm = pe.transpose(PS[0:w, 4 + k // 4, P * (k % 4):P * (k % 4) + P],
                                      self.p[:, u % 2, P * k:P * k + w], ident)
                mm.then_inc(self.turned, 1)
                if u + 2 < self.UNITS:
                    self.pe_scores(pe, i, u + 2)
                elif more:
                    if u == self.UNITS - 2:
                        pe.wait_ge(self.wc_in, i * 16 + 32)
                    self.pe_piece(pe, 2 * (u % 2))
                    self.pe_piece(pe, 2 * (u % 2) + 1)
                if u % 4 == 0 and u:
                    self.pe_mix(pe, i, u // 4 - 1)
            self.pe_mix(pe, i, self.GROUPS - 1)

        def act(self, act):
            act.sem_inc(self.exps, self.FREE["exps"])
            self.act_piece(act, 0, self.Q0)
            self.act_piece(act, 0, self.Q1)
            with act.Fori(0, INNER // P - 1) as i:
                self.act_pair(act, i, True)
            self.act_pair(act, INNER // P - 1, False)

        def act_pair(self, act, i, more):
            self.act_piece(act, i, self.KCTX)
            self.act_piece(act, i, self.V1)
            for u in range(self.UNITS):
                act.wait_ge(self.maxed, i * self.UNITS + self.c("maxed", u + 1))
                act.wait_ge(self.turned, i * self.UNITS + self.c("turned", u - 1))
                act.activation(self.p[:, u % 2, :], self.span(u), ACT.Exp, bias=self.nmx[:, u:u + 1],
                               accum_out=self.den[:, u:u + 1]).then_inc(self.exps, 1)
                if u == 9:
                    self.act_sums(act, i, 0)
            if more:
                self.act_piece(act, i + 1, self.Q0)
                self.act_piece(act, i + 1, self.Q1)
            self.act_sums(act, i, 1)

        def act_sums(self, act, i, b):
            act.wait_ge(self.mixed, i * self.GROUPS + self.c("mixed", 2 * b + 2))
            act.activation(sq[:, b, :], PS[:, 7, :], ACT.Copy).then_inc(self.sums_ready, 1)

        def dve(self, dve):
            dve.sem_inc(self.pT_ready, self.FREE["pT_ready"])
            dve.sem_inc(self.oT_ready, self.FREE["oT_ready"])
            self.dve_piece(dve, 0, self.K0)
            self.dve_piece(dve, 0, self.K1)
            with dve.Fori(0, INNER // P - 1) as i:
                self.dve_pair(dve, i, True)
            self.dve_pair(dve, INNER // P - 1, False)
            for b in range(B):
                dve.wait_ge(self.out_prod, self.WAS["out_prod"] + b + 1)
                dve.tensor_tensor(x[:, b, :], x[:, b, :], PS[:, b, :], ALU.add).then_inc(x_ready, 1)

        def dve_pair(self, dve, i, more):
            self.dve_piece(dve, i, self.V0)
            self.dve_max(dve, i, 0)
            self.dve_max(dve, i, 1)
            self.dve_piece(dve, i, self.VCTX)
            for u in range(self.UNITS):
                g, e = u // 4, u % 2
                dve.wait_ge(self.turned, i * self.UNITS + self.c("turned", u + 1))
                if u % 4 == 0:
                    dve.wait_ge(self.mixed, i * self.GROUPS + self.c("mixed", g - 1))
                at = P * ((u // 2) % 2)
                dve.tensor_copy(self.pT[:, g % 2, e, 0:4, at:at + P], PS[:, 4, :].rearrange("p (k q) -> p k q", k=4))
                dve.tensor_copy(self.pT[0:KC, g % 2, e, 4, at:at + P], PS[0:KC, 5, 0:P]).then_inc(self.pT_ready, 1)
                if u + 2 < self.UNITS:
                    self.dve_max(dve, i, u + 2)
                if e == 1:
                    dve.reciprocal(self.rden[:, u - 1:u + 1], self.den[:, u - 1:u + 1]).then_inc(self.rdens, 1)
                if u == 9:
                    self.dve_out(dve, i, 0)
            if more:
                self.dve_piece(dve, i + 1, self.K0)
                self.dve_piece(dve, i + 1, self.K1)
            self.dve_out(dve, i, 1)

        def dve_out(self, dve, i, b):
            dve.wait_ge(self.sums_ready, i * B + b + 1)
            dve.tensor_tensor(self.oT[:, bass.ds(i, 1), b, :].rearrange("p a s -> p (a s)"), PS[:, 6, :],
                              sq[:, b, :], ALU.mult).then_inc(self.oT_ready, 1)

        def dve_max(self, dve, i, u):
            dve.wait_ge(self.scores, i * self.UNITS + self.c("scores", u + 1))
            dve.tensor_reduce(self.nmx[:, u:u + 1], self.span(u), X, ALU.max, negate=True).then_inc(self.maxed, 1)

    align = Align()
    align.stack.close()
    quantised = Quantised()
    quantised.stack.close()
    attend1 = ContextAttention("l1", True, 0)
    attend1.stack.close()
    pair = PairAttention()
    experts1 = Experts("m1", ACT.Gelu, 1.0, True, 0)
    experts1.stack.close()
    pair.stack.close()
    attend2 = ContextAttention("l2", False, 1)
    attend2.stack.close()
    stack = Stack()
    stack.stack.close()
    latents = LatentAttention()
    latents.stack.close()
    experts3 = Experts("m3", ACT.Silu, 1.5, False, 1)
    h7 = sb("h7", [P, B, S], at=experts3.stack)
    experts3.stack.close()
    final = sem("final")
    out = io["out"]
    block = ctx.enter_context(nc.Block())

    @block.sync
    def _(sp):
        sp.dma_start(x[:, :, :], io["xT"]).then_inc(loaded, 16)
        sp.dma_start(cst[:, :], io["cst"]).then_inc(loaded, 16)
        sp.dma_start(ctxT[:, :], io["ctxT"]).then_inc(loaded, 16)
        sp.dma_start(ctxN[:, :, :], io["ctxN"]).then_inc(loaded, 16)
        sp.dma_start(vec[:, :], io["vec"]).then_inc(loaded, 16)
        sp.dma_start(row[:, :], io["row"]).then_inc(loaded, 16)
        align.sp(sp)
        sp.wait_ge(x_ready, 2)
        quantised.sp(sp)
        sp.wait_ge(x_ready, 4)
        attend1.sp(sp)
        sp.wait_ge(x_ready, 6)
        pair.sp(sp)
        experts1.sp(sp)
        sp.wait_ge(x_ready, 8)
        attend2.sp(sp)
        sp.wait_ge(x_ready, 10)
        stack.sp(sp)
        sp.wait_ge(x_ready, 12)
        latents.sp(sp)
        sp.wait_ge(x_ready, 14)
        experts3.sp(sp)
        sp.wait_ge(x_ready, 2 * PARTS)
        sp.dma_start(out, x[:, :, :]).then_inc(final, 16)
        sp.wait_ge(final, 16)

    @block.gpsimd
    def _(pool):
        align.pool(pool)
        pool.wait_ge(x_ready, 4)
        attend1.pool(pool)
        pool.wait_ge(x_ready, 6)
        experts1.pool(pool)
        pool.wait_ge(x_ready, 8)
        attend2.pool(pool)
        pool.wait_ge(x_ready, 10)
        stack.pool(pool)

    @block.scalar
    def _(act):
        act.wait_ge(loaded, 16 * LOADS)
        norm.act(act)
        align.act(act)
        norm.act(act)
        quantised.weights_act(act)
        quantised.act(act)
        attend1.act_prepare(act)
        norm.act(act)
        attend1.act(act)
        norm.act(act)
        pair.act(act)
        experts1.act(act)
        attend2.act_prepare(act)
        norm.act(act)
        attend2.act(act)
        norm.act(act)
        stack.act(act)
        norm.act(act)
        latents.ctx_act(act)
        norm.act(act)
        latents.act(act)
        norm.act(act)
        norm.act(act)
        experts3.act(act)

    @block.tensor
    def _(pe):
        pe.wait_ge(loaded, 16 * LOADS)
        norm.pe(pe, x, None)
        align.pe(pe)
        norm.pe(pe, x, x_ready)
        quantised.weights_pe(pe)
        quantised.pe(pe)
        attend1.pe_prepare(pe)
        norm.pe(pe, x, x_ready)
        attend1.pe(pe)
        norm.pe(pe, x, x_ready)
        pair.pe(pe)
        experts1.pe(pe)
        attend2.pe_prepare(pe)
        norm.pe(pe, x, x_ready)
        attend2.pe(pe)
        norm.pe(pe, x, x_ready)
        stack.pe(pe)
        norm.pe(pe, x, x_ready)
        latents.ctx_pe(pe)
        norm.wait(pe, "pe")
        norm.pe(pe, latents.h0, None)
        latents.pe(pe)
        norm.pe(pe, x, x_ready)
        norm.wait(pe, "pe")
        norm.pe(pe, h7, None)
        experts3.pe(pe)

    @block.vector
    def _(dve):
        align.strips_dve(dve)
        dve.wait_ge(loaded, 16 * LOADS)
        norm.dve(dve, x, xn)
        align.dve(dve)
        norm.dve(dve, x, xn)
        quantised.weights_dve(dve)
        quantised.dve(dve)
        attend1.dve_prepare(dve)
        norm.dve(dve, x, xn)
        attend1.dve(dve)
        norm.dve(dve, x, pair.h0)
        pair.dve(dve)
        experts1.dve(dve, pair.h2)
        attend2.dve_prepare(dve)
        norm.dve(dve, x, xn)
        attend2.dve(dve)
        norm.dve(dve, x, stack.y0)
        stack.dve(dve)
        norm.dve(dve, x, latents.h0)
        latents.ctx_dve(dve)
        norm.wait(dve, "dve")
        norm.dve(dve, latents.h0, xn, column("la_g2"), column("la_b2"))
        latents.dve(dve)
        norm.dve(dve, x, h7)
        norm.wait(dve, "dve")
        norm.dve(dve, h7, xn, column("m3_g"), column("m3_b"))
        experts3.dve(dve, h7)

    ctx.close()


def spans(parts):
    at, out = 0, {}
    for name, width in parts:
        out[name] = (at, width)
        at += width
    return out, at


C_AT, C_ALL = spans([("ident", P), ("mean", P), ("one", P), ("slide", 31), ("eps", 1), ("rinit", SC + 1),
                     ("iota", S), ("blk8", P), ("hm", H), ("kidx", E), ("threehalves", 1)])
VECTORS = {"l1_bq": "L1_xattn_bq", "l1_bk": "L1_xattn_bk", "l1_bo": "L1_xattn_bo",
           "pa_ln1w": "L1_ffn_ln1_weight", "pa_ln1b": "L1_ffn_ln1_bias",
           "pa_ln2w": "L1_ffn_ln2_weight", "pa_ln2b": "L1_ffn_ln2_bias",
           "l2_bq": "L2_xattn_bq", "l2_bk": "L2_xattn_bk", "l2_bo": "L2_xattn_bo",
           "la_g1": "L3_xattn_g1", "la_b1": "L3_xattn_b1", "la_g2": "L3_xattn_g2", "la_b2": "L3_xattn_b2",
           "m3_g": "L3_ffn_gamma", "m3_b": "L3_ffn_beta"}
V_AT, V_ALL = spans([(k, 1) for k in VECTORS])
R_AT, R_ALL = spans([("l1_bv", P), ("l2_bv", P)])


def constants():
    c = np.zeros((P, C_ALL), np.float32)

    def put(name, a):
        at, w = C_AT[name]
        c[:, at:at + w] = a
    put("ident", np.eye(P))
    put("mean", 1.0 / P)
    put("one", 1.0)
    s = np.zeros((P, 31)); s[:, 15] = 1.0 / P
    put("slide", s)
    put("eps", EPS)
    put("threehalves", 1.5)
    r = np.full((P, SC + 1), BIG); r[SEG - 1, 0] = 0; r[2 * SEG - 1, 0] = 0
    put("rinit", r)
    put("iota", np.arange(S)[None])
    head = np.arange(P) // DH
    put("blk8", head[:, None] == head[None])
    put("hm", head[:, None] == np.arange(H)[None])
    put("kidx", (E - np.arange(E))[None])
    r = np.arange(HKP)
    sel = (r[None] % KC == np.arange(KC)[:, None]) & (r[None] < HK)
    r = r.reshape(HKC, P).T
    hmask = (r[:, :, None] // KC == head[None, None]) & (r[:, :, None] < HK)
    half = np.arange(0, D2, 2, dtype=np.float32)
    token = np.arange(S, dtype=np.float32)
    freqs = token[:, None] * (1.0 / np.float32(10000.0) ** (half / D2)).astype(np.float32)[None]
    scale = ((half + 0.4 * D2) / (1.4 * D2)).astype(np.float32)[None] ** ((token - S // 2) / (WIN // 2))[:, None]
    sign = np.where(np.arange(D2) < D2 // 2, -1.0, 1.0)[None]
    both = lambda m: np.concatenate([m, m], axis=1)
    base = np.stack([np.stack([both(np.cos(freqs) * s), both(np.sin(freqs) * s) * sign])
                     for s in (scale, 1.0 / scale)])
    base = base.reshape(2, 2, 4, P, D2).transpose(3, 0, 1, 2, 4)
    i, jj = np.arange(P)[:, None] % WIN, np.arange(2 * WIN)[None]
    seen = (jj >= i) & (jj <= i + WIN)
    first = seen & ~((np.arange(P)[:, None] < WIN) & (jj < WIN))
    wmask = np.where(np.stack([first, seen], axis=1), 0.0, NEG)
    bf16 = mybir.dt.np(BF16)
    return {"st_base": np.ascontiguousarray(base, np.float32), "st_wmask": wmask.astype(bf16),
            "identb": np.eye(P).astype(bf16), "cst": c, "sel": sel.astype(np.float32), "hmask": hmask.astype(np.float32)}


def lay(inputs):
    f = lambda k: np.asarray(inputs[k])
    a = dict(constants())
    a["xT"] = np.ascontiguousarray(f("x").reshape(T, P).T.reshape(P, B, S))
    a["ctxT"] = np.ascontiguousarray(f("ctx_1024").reshape(B * KC, P).T)
    a["ctxN"] = np.ascontiguousarray(f("ctx_1024").transpose(1, 0, 2))
    for k, w in (("wg", "gate"), ("wu", "up")):
        a["q_" + k] = np.ascontiguousarray(f("L0_ffn_w_" + w).reshape(QW // P, P, P).transpose(1, 0, 2)).reshape(P, QW)
    a["q_wd"] = f("L0_ffn_w_down")
    a["vec"] = np.stack([f(k) for k in VECTORS.values()], axis=1)
    a["row"] = np.concatenate([f("L1_xattn_bv"), f("L2_xattn_bv")])[None]
    a["l1_w"] = np.stack([f("L1_xattn_W" + k).T for k in "qkvo"], axis=1)
    a["l2_w"] = np.stack([f("L2_xattn_W" + k) for k in "qkvo"], axis=1)
    for t, k in (("l1", "mask_1x1xSxS2_ik0"), ("l2", "mask_1x1xSxS2_fk1")):
        a[t + "_mask"] = np.ascontiguousarray(f(k)[0, 0].reshape(NT // B, P, KC).transpose(1, 0, 2))
    g = f("L1_ffn_qkv_weight").reshape(H // 2, 4, DH, P)
    twice = lambda k: np.repeat(g[:, k:k + 1], 2, axis=1)
    a["pa_w"] = np.stack([np.ascontiguousarray(w.reshape(P, P).T) for w in
                          (g[:, 0:2], twice(2), twice(3), f("L1_ffn_proj_weight"))], axis=1)
    a["m1_router"] = f("L1_ffn_router_weight")
    w = f("L2_ffn_Wqkv")
    wv = w[:, :, 2 * INNER:].reshape(DEPTH, P, H // 2, 2, D2).transpose(0, 1, 3, 2, 4).reshape(DEPTH, P, INNER)
    a["st_wqkv"], a["st_wo"] = np.concatenate([w[:, :, :2 * INNER], wv], axis=2), f("L2_ffn_Wo")
    a["st_w1"], a["st_w2"] = f("L2_ffn_W1"), f("L2_ffn_W2")
    scales = np.stack([f("L2_ffn_q_scale"), f("L2_ffn_k_scale")], axis=1)
    a["st_qks"] = np.stack([scales, np.roll(scales, D2 // 2, axis=2)], axis=2)
    b1 = np.zeros((DEPTH, 2, 3 * P), np.float32)
    b1[:, :, 0:FFI] = f("L2_ffn_b1").reshape(DEPTH, 2, FFI)
    a["st_sv"] = np.concatenate([np.stack([f("L2_ffn_ln_g"), f("L2_ffn_ln_b"), f("L2_ffn_b2")], axis=2),
                                 b1.reshape(DEPTH, 6, P).transpose(0, 2, 1)], axis=2)
    wkv = f("L3_xattn_Wkv")
    a["la_wc"] = np.ascontiguousarray(np.stack([f("L3_xattn_Wq"), wkv[:, 0:INNER], wkv[:, INNER:]])
                                      .reshape(3, P, INNER // P, P).transpose(2, 1, 0, 3))
    a["la_wo"] = np.ascontiguousarray(f("L3_xattn_Wout").reshape(INNER // P, P, P).transpose(1, 0, 2))
    a["la_mask"] = f("mask_BxS2_bk0").reshape(1, B * KC)
    a["m3_router"] = np.ascontiguousarray(f("L3_ffn_router_w").T)
    a["m3_w1"], a["m3_w2"] = f("L3_ffn_W1"), f("L3_ffn_W2")
    a["m1_w1"], a["m1_w2"] = f("L1_ffn_moe_w1"), f("L1_ffn_moe_w2")
    return a


def kernel(**inputs):
    import concourse.bacc as bacc
    from concourse.bass_utils import run_bass_kernel_spmd

    nc = bacc.Bacc("TRN2", target_bir_lowering=False, num_devices=1)
    arrays = lay(inputs)
    io = {k: nc.dram_tensor("in_" + k, a.shape, mybir.dt.from_np(a.dtype), kind="ExternalInput").ap()
          for k, a in arrays.items()}
    io["out"] = nc.dram_tensor("out_x", (P, B, S), F32, kind="ExternalOutput").ap()
    build(nc, io)
    r = run_bass_kernel_spmd(nc, [{"in_" + k: a for k, a in arrays.items()}], core_ids=[0])
    got = r.results[0]["out_x"]
    return np.ascontiguousarray(got.reshape(P, T).T.reshape(B, S, P))
```
